# Optimizing a Trainium2 kernel written in Bass

```python
import numpy as np
import jax
import jax.numpy as jnp

def _softmax(x, axis=-1):
    return jax.nn.softmax(x, axis=axis)

def _gelu(x):
    return jax.nn.gelu(x, approximate=True)

def _silu(x):
    return jax.nn.silu(x)

def _sigmoid(x):
    return jax.nn.sigmoid(x)

def _layernorm(x, axis=-1, eps=1e-05):
    m = jnp.mean(x, axis=axis, keepdims=True)
    v = jnp.var(x, axis=axis, keepdims=True)
    return (x - m) / jnp.sqrt(v + eps)

def _scatter_add(tgt, idx, src, axis=0):
    return tgt.at[idx].add(src)

def _segment_sum(src, seg, n):
    return jax.ops.segment_sum(src, seg, n)
kernel_name = 'mk_perceiver_d4_seqx_r8_8bc615'

def setup_inputs(seed: int=0):
    np.random.seed(seed)
    _w = jnp.asarray

    def _rec_inputs():
        import jax
        import jax.numpy as jnp
        _rk = jax.random.key(seed)
        x = -0.0002928 + 1 * jax.random.normal(jax.random.fold_in(_rk, 1), (64, 32, 128), jnp.float32)
        _lenS = 32 - jax.random.randint(jax.random.fold_in(_rk, 7), (64,), 0, max(1, 32 // 4) + 1, jnp.int32)
        _lenS2 = 257 - jax.random.randint(jax.random.fold_in(_rk, 8), (64,), 0, max(1, 257 // 4) + 1, jnp.int32)
        _ctx_1024P = jax.random.normal(jax.random.fold_in(_rk, 11), (64, 16, 128), jnp.float32)
        _ctx_1024c = jax.random.dirichlet(jax.random.fold_in(_rk, 511), 0.3 * jnp.ones((16,), jnp.float32), (64, 257))
        _ctx_1024t = jnp.einsum('bsk,bkd->bsd', _ctx_1024c, _ctx_1024P)
        _ctx_1024t = _ctx_1024t * jax.lax.rsqrt(jnp.mean(jnp.square(_ctx_1024t)) + 1e-12) * 0.953939
        ctx_1024 = -1.39393e-06 + 0.999914 * (_ctx_1024t + 0.3 * jax.random.normal(jax.random.fold_in(_rk, 611), (64, 257, 128), jnp.float32))
        _validS = jnp.arange(32)[None, :] < _lenS[:, None]
        _validS2 = jnp.arange(257)[None, :] < _lenS2[:, None]
        _causal = jnp.tril(jnp.ones((32, 32), dtype=bool))
        mask_BxSxS2_bk1 = jnp.broadcast_to(_validS2[:, None, :], (64, 32, 257))
        mask_Bx1xSxS2_bf1 = jnp.ones((64, 1, 32, 257), dtype=bool)
        return (x, ctx_1024, mask_BxSxS2_bk1, mask_Bx1xSxS2_bf1)
    x, ctx_1024, mask_BxSxS2_bk1, mask_Bx1xSxS2_bf1 = _rec_inputs()

    def _L0_xattn_setup():
        import jax, jax.numpy as jnp
        import numpy as np
        D_MODEL = 128
        NUM_HEADS = 16
        D_K = 64
        D_V = 64
        B, L = (2, 256)
        key = jax.random.key(seed)
        ks = jax.random.split(key, 12)
        std_qk = np.sqrt(2.0 / (D_MODEL + D_K)).astype(np.float32)
        std_v = np.sqrt(2.0 / (D_MODEL + D_V)).astype(np.float32)
        return {'input_Q': jax.random.normal(ks[0], (B, L, D_MODEL), jnp.float32), 'input_K': jax.random.normal(ks[1], (B, L, D_MODEL), jnp.float32), 'input_V': jax.random.normal(ks[2], (B, L, D_MODEL), jnp.float32), 'attn_mask': jax.random.randint(ks[3], (B, L, L), 0, 2).astype(jnp.bool_), 'W_Q': std_qk * jax.random.normal(ks[4], (NUM_HEADS * D_K, D_MODEL), jnp.float32), 'b_Q': jnp.zeros((NUM_HEADS * D_K,), jnp.float32), 'W_K': std_qk * jax.random.normal(ks[5], (NUM_HEADS * D_K, D_MODEL), jnp.float32), 'b_K': jnp.zeros((NUM_HEADS * D_K,), jnp.float32), 'W_V': std_v * jax.random.normal(ks[6], (NUM_HEADS * D_V, D_MODEL), jnp.float32), 'b_V': jnp.zeros((NUM_HEADS * D_V,), jnp.float32), 'W_out': std_v * jax.random.normal(ks[7], (D_MODEL, NUM_HEADS * D_V), jnp.float32), 'b_out': jnp.zeros((D_MODEL,), jnp.float32)}
    _L0_xattn_all = _L0_xattn_setup()
    _L0_xattn_in = {k: v for k, v in _L0_xattn_all.items() if k in ('W_Q', 'b_Q', 'W_K', 'b_K', 'W_V', 'b_V', 'W_out', 'b_out')}
    del _L0_xattn_all

    def _L0_attn_setup():
        import jax, jax.numpy as jnp
        import numpy as np
        B, S, D, H, DH, FF = (4, 512, 128, 16, 64, 512)
        EPS = 1e-06

        def _layer_norm(x, g, b):
            m = jnp.mean(x, axis=-1, keepdims=True)
            v = jnp.mean(jnp.square(x - m), axis=-1, keepdims=True)
            return (x - m) * jax.lax.rsqrt(v + 1e-05) * g + b
        key = jax.random.key(seed)
        ks = jax.random.split(key, 8)
        s = 0.02
        return {'src': jax.random.normal(ks[0], (B, S, D), dtype=jnp.float32), 'Wq': jax.random.normal(ks[1], (D, H * DH), dtype=jnp.float32) * s, 'bq': jnp.zeros((H * DH,), jnp.float32), 'Wk': jax.random.normal(ks[2], (D, H * DH), dtype=jnp.float32) * s, 'bk': jnp.zeros((H * DH,), jnp.float32), 'Wv': jax.random.normal(ks[3], (D, H * DH), dtype=jnp.float32) * s, 'bv': jnp.zeros((H * DH,), jnp.float32), 'Wo': jax.random.normal(ks[4], (H * DH, D), dtype=jnp.float32) * s, 'bo': jnp.zeros((D,), jnp.float32), 'W1': jax.random.normal(ks[5], (D, FF), dtype=jnp.float32) * s, 'b1': jnp.zeros((FF,), jnp.float32), 'W2': jax.random.normal(ks[6], (FF, D), dtype=jnp.float32) * s, 'b2': jnp.zeros((D,), jnp.float32), 'g1': jnp.ones((D,), jnp.float32), 'be1': jnp.zeros((D,), jnp.float32), 'g2': jnp.ones((D,), jnp.float32), 'be2': jnp.zeros((D,), jnp.float32)}
    _L0_attn_all = _L0_attn_setup()
    _L0_attn_in = {k: v for k, v in _L0_attn_all.items() if k in ('Wq', 'bq', 'Wk', 'bk', 'Wv', 'bv', 'Wo', 'bo', 'W1', 'b1', 'W2', 'b2', 'g1', 'be1', 'g2', 'be2')}
    del _L0_attn_all

    def _L0_ffn_setup():
        import jax, jax.numpy as jnp
        import numpy as np
        import math
        D_IN = 128
        FEATURES = (512, 512, 128)
        BATCH, SEQ = (8, 256)

        def _conn_dense(kernel_bool, x):
            w = jnp.where(kernel_bool, jnp.float32(1.0), jnp.float32(-1.0))
            return x @ w
        key = jax.random.key(seed)
        kx, kk0, kk1, kk2 = jax.random.split(key, 4)
        x = jax.random.normal(kx, (BATCH, SEQ, D_IN), dtype=jnp.float32)
        k0 = jax.random.randint(kk0, (2 * D_IN, FEATURES[0]), 0, 2).astype(jnp.bool_)
        k1 = jax.random.randint(kk1, (FEATURES[0], FEATURES[1]), 0, 2).astype(jnp.bool_)
        k2 = jax.random.randint(kk2, (FEATURES[1], FEATURES[2]), 0, 2).astype(jnp.bool_)
        s0 = jnp.asarray(1.0 / math.sqrt(2 * D_IN), dtype=jnp.float32)
        s1 = jnp.asarray(1.0 / math.sqrt(FEATURES[0]), dtype=jnp.float32)
        s2 = jnp.asarray(1.0 / math.sqrt(FEATURES[1]), dtype=jnp.float32)
        return {'x': x, 'k0': k0, 'k1': k1, 'k2': k2, 's0': s0, 's1': s1, 's2': s2}
    _L0_ffn_all = _L0_ffn_setup()
    _L0_ffn_in = {k: v for k, v in _L0_ffn_all.items() if k in ('k0', 'k1', 'k2', 's0', 's1', 's2')}
    del _L0_ffn_all

    def _L1_xattn_setup():
        import jax, jax.numpy as jnp
        import numpy as np
        D_MODEL = 128
        NUM_HEADS = 16
        D_K = D_MODEL // NUM_HEADS
        B, S = (2, 256)
        key = jax.random.key(seed)
        ks = jax.random.split(key, 12)
        sc = 1.0 / np.sqrt(D_MODEL)
        inp = {'q': jax.random.normal(ks[0], (B, S, D_MODEL), jnp.float32), 'k': jax.random.normal(ks[1], (B, S, D_MODEL), jnp.float32), 'v': jax.random.normal(ks[2], (B, S, D_MODEL), jnp.float32), 'mask': jnp.ones((B, 1, S, S), dtype=bool), 'Wq': jax.random.normal(ks[3], (D_MODEL, D_MODEL), jnp.float32) * sc, 'bq': jnp.zeros((D_MODEL,), jnp.float32), 'Wk': jax.random.normal(ks[4], (D_MODEL, D_MODEL), jnp.float32) * sc, 'bk': jnp.zeros((D_MODEL,), jnp.float32), 'Wv': jax.random.normal(ks[5], (D_MODEL, D_MODEL), jnp.float32) * sc, 'bv': jnp.zeros((D_MODEL,), jnp.float32), 'Wo': jax.random.normal(ks[6], (D_MODEL, D_MODEL), jnp.float32) * sc, 'bo': jnp.zeros((D_MODEL,), jnp.float32)}
        return inp
    _L1_xattn_all = _L1_xattn_setup()
    _L1_xattn_in = {k: v for k, v in _L1_xattn_all.items() if k in ('Wq', 'bq', 'Wk', 'bk', 'Wv', 'bv', 'Wo', 'bo')}
    del _L1_xattn_all

    def _L1_attn_setup():
        import jax, jax.numpy as jnp
        import numpy as np
        DIM = 128
        EPS = 1e-05

        def _layernorm(x, w, b):
            mu = jnp.mean(x, axis=-1, keepdims=True)
            var = jnp.mean(jnp.square(x - mu), axis=-1, keepdims=True)
            return (x - mu) * jax.lax.rsqrt(var + EPS) * w + b
        key = jax.random.key(seed)
        ks = jax.random.split(key, 7)
        C = DIM
        x = jax.random.normal(ks[0], (4, 512, C), dtype=jnp.float32)
        norm_w = jnp.ones((C,), dtype=jnp.float32)
        norm_b = jnp.zeros((C,), dtype=jnp.float32)
        s = 1.0 / np.sqrt(C)
        qkv_w = jax.random.uniform(ks[1], (3 * C, C), dtype=jnp.float32, minval=-s, maxval=s)
        qkv_b = jax.random.uniform(ks[2], (3 * C,), dtype=jnp.float32, minval=-s, maxval=s)
        proj_w = jax.random.uniform(ks[3], (C, C), dtype=jnp.float32, minval=-s, maxval=s)
        proj_b = jax.random.uniform(ks[4], (C,), dtype=jnp.float32, minval=-s, maxval=s)
        return {'x': x, 'norm_w': norm_w, 'norm_b': norm_b, 'qkv_w': qkv_w, 'qkv_b': qkv_b, 'proj_w': proj_w, 'proj_b': proj_b}
    _L1_attn_all = _L1_attn_setup()
    _L1_attn_in = {k: v for k, v in _L1_attn_all.items() if k in ('norm_w', 'norm_b', 'qkv_w', 'qkv_b', 'proj_w', 'proj_b')}
    del _L1_attn_all

    def _L1_ffn_setup():
        import jax, jax.numpy as jnp
        import numpy as np
        import math
        GOLDEN_CENTER = 1.0 / math.e
        GOLDEN_LOWER = 0.5 - math.log(4.0 / 3.0)
        GOLDEN_UPPER = 0.5
        B, T, D = (4, 256, 128)
        E = 8
        I = 512 // (E // 2)

        def _routing_weights(x, Wr, temperature):
            inh = jax.nn.sigmoid(x @ Wr / temperature)
            in_zone = (inh >= GOLDEN_LOWER) & (inh <= GOLDEN_UPPER)
            dist = jnp.abs(inh - GOLDEN_CENTER)
            w = jnp.exp(-dist / 0.1) * in_zone.astype(x.dtype)
            wsum = w.sum(axis=-1, keepdims=True)
            no_expert = wsum < 1e-08
            fb = jnp.exp(-dist / 0.3)
            _, top2 = jax.lax.top_k(fb, 2)
            fb_mask = jax.nn.one_hot(top2, E, dtype=x.dtype).sum(axis=-2)
            fb_w = fb * fb_mask
            fb_w = fb_w / jnp.clip(fb_w.sum(axis=-1, keepdims=True), 1e-08)
            w = jnp.where(no_expert, fb_w, w)
            wsum = w.sum(axis=-1, keepdims=True)
            return w / jnp.clip(wsum, 1e-08)
        key = jax.random.key(seed)
        k = jax.random.split(key, 6)
        s_d = 1.0 / math.sqrt(D)
        s_i = 1.0 / math.sqrt(I)
        return {'x': jax.random.normal(k[0], (B, T, D), jnp.float32), 'Wg': jax.random.normal(k[1], (E, D, I), jnp.float32) * s_d, 'Wu': jax.random.normal(k[2], (E, D, I), jnp.float32) * s_d, 'Wd': jax.random.normal(k[3], (E, I, D), jnp.float32) * s_i, 'Wr': jax.random.normal(k[4], (D, E), jnp.float32) * s_d, 'temperature': jnp.ones((1,), jnp.float32)}
    _L1_ffn_all = _L1_ffn_setup()
    _L1_ffn_in = {k: v for k, v in _L1_ffn_all.items() if k in ('Wg', 'Wu', 'Wd', 'Wr', 'temperature')}
    del _L1_ffn_all

    def _L2_xattn_setup():
        import jax, jax.numpy as jnp
        import numpy as np
        DIM = 128
        SCALE_DIM = 4
        QK_DIM = DIM // SCALE_DIM
        B, S = (4, 512)
        key = jax.random.key(seed)
        ks = jax.random.split(key, 8)
        std = 1.0 / np.sqrt(DIM)
        return {'q': jax.random.normal(ks[0], (B, S, DIM), jnp.float32), 'k': jax.random.normal(ks[1], (B, S, DIM), jnp.float32), 'v': jax.random.normal(ks[2], (B, S, DIM), jnp.float32), 'Wq': jax.random.normal(ks[3], (QK_DIM, DIM), jnp.float32) * std, 'bq': jnp.zeros((QK_DIM,), jnp.float32), 'Wk': jax.random.normal(ks[4], (QK_DIM, DIM), jnp.float32) * std, 'bk': jnp.zeros((QK_DIM,), jnp.float32), 'Wv': jax.random.normal(ks[5], (DIM, DIM), jnp.float32) * std, 'bv': jnp.zeros((DIM,), jnp.float32)}
    _L2_xattn_all = _L2_xattn_setup()
    _L2_xattn_in = {k: v for k, v in _L2_xattn_all.items() if k in ('Wq', 'bq', 'Wk', 'bk', 'Wv', 'bv')}
    del _L2_xattn_all

    def _L2_attn_setup():
        import jax, jax.numpy as jnp
        import numpy as np
        D_MODEL, N_HEADS, D_LATENT = (128, 16, 32)
        HEAD_DIM = D_MODEL // N_HEADS
        B, T = (2, 256)

        def apply_rope(x):
            Tn, D = (x.shape[1], x.shape[3])
            inv_freq = 1.0 / 10000.0 ** (jnp.arange(0, D, 2, dtype=jnp.float32) / D)
            t = jnp.arange(Tn, dtype=jnp.float32)
            freqs = jnp.outer(t, inv_freq)
            sin_f = jnp.sin(freqs)[None, :, None, :]
            cos_f = jnp.cos(freqs)[None, :, None, :]
            x1, x2 = jnp.split(x, 2, axis=-1)
            return jnp.concatenate([x1 * cos_f - x2 * sin_f, x1 * sin_f + x2 * cos_f], axis=-1)
        key = jax.random.key(seed)
        ks = jax.random.split(key, 5)
        s = lambda fan_in: 1.0 / np.sqrt(fan_in)
        return {'x': jax.random.normal(ks[0], (B, T, D_MODEL), jnp.float32), 'Wq': jax.random.normal(ks[1], (D_MODEL, D_MODEL), jnp.float32) * s(D_MODEL), 'bq': jnp.zeros((D_MODEL,), jnp.float32), 'Wkv_down': jax.random.normal(ks[2], (D_MODEL, D_LATENT), jnp.float32) * s(D_MODEL), 'bkv_down': jnp.zeros((D_LATENT,), jnp.float32), 'Wkv_up': jax.random.normal(ks[3], (D_LATENT, 2 * D_MODEL), jnp.float32) * s(D_LATENT), 'bkv_up': jnp.zeros((2 * D_MODEL,), jnp.float32), 'Wo': jax.random.normal(ks[4], (D_MODEL, D_MODEL), jnp.float32) * s(D_MODEL), 'bo': jnp.zeros((D_MODEL,), jnp.float32)}
    _L2_attn_all = _L2_attn_setup()
    _L2_attn_in = {k: v for k, v in _L2_attn_all.items() if k in ('Wq', 'bq', 'Wkv_down', 'bkv_down', 'Wkv_up', 'bkv_up', 'Wo', 'bo')}
    del _L2_attn_all

    def _L2_ffn_setup():
        import jax, jax.numpy as jnp
        import numpy as np
        DM, NEXPERTS, SETS, ESIZE = (128, 32, 4, 32)
        B, S = (2, 1024)
        key = jax.random.key(seed)
        ks = jax.random.split(key, 7)
        sc = 0.02
        return {'x': jax.random.normal(ks[0], (B, S, DM), jnp.float32), 'Wc': jax.random.normal(ks[1], (DM, NEXPERTS, SETS), jnp.float32) * sc, 'bc': jax.random.normal(ks[2], (NEXPERTS, SETS), jnp.float32) * sc, 'W1': jax.random.normal(ks[3], (NEXPERTS, SETS, DM, ESIZE), jnp.float32) * sc, 'b1': jax.random.normal(ks[4], (NEXPERTS, SETS, ESIZE), jnp.float32) * sc, 'W2': jax.random.normal(ks[5], (NEXPERTS, SETS, DM, ESIZE), jnp.float32) * sc, 'b2': jax.random.normal(ks[6], (NEXPERTS, SETS, DM), jnp.float32) * sc}
    _L2_ffn_all = _L2_ffn_setup()
    _L2_ffn_in = {k: v for k, v in _L2_ffn_all.items() if k in ('Wc', 'bc', 'W1', 'b1', 'W2', 'b2')}
    del _L2_ffn_all

    def _L3_xattn_setup():
        import jax, jax.numpy as jnp
        import numpy as np
        D_MODEL = 128
        N_HEAD = 16
        HEAD_DIM = D_MODEL // N_HEAD
        key = jax.random.key(seed)
        ks = jax.random.split(key, 8)
        B, T, C = (4, 256, D_MODEL)
        s = 0.02
        return {'q': jax.random.normal(ks[0], (B, T, C), jnp.float32), 'k': jax.random.normal(ks[1], (B, T, C), jnp.float32), 'v': jax.random.normal(ks[2], (B, T, C), jnp.float32), 'Wq': jax.random.normal(ks[3], (C, C), jnp.float32) * s, 'Wk': jax.random.normal(ks[4], (C, HEAD_DIM), jnp.float32) * s, 'Wv': jax.random.normal(ks[5], (C, HEAD_DIM), jnp.float32) * s, 'Wp': jax.random.normal(ks[6], (C, C), jnp.float32) * s, 'bp': jnp.zeros((C,), jnp.float32)}
    _L3_xattn_all = _L3_xattn_setup()
    _L3_xattn_in = {k: v for k, v in _L3_xattn_all.items() if k in ('Wq', 'Wk', 'Wv', 'Wp', 'bp')}
    del _L3_xattn_all

    def _L3_attn_setup():
        import jax, jax.numpy as jnp
        import numpy as np
        import math
        B, S, D, H, R, DFF = (4, 128, 128, 16, 64, 512)

        def _layernorm(x, g, b, eps=1e-05):
            m = jnp.mean(x, axis=-1, keepdims=True)
            v = jnp.var(x, axis=-1, keepdims=True)
            return (x - m) / jnp.sqrt(v + eps) * g + b
        key = jax.random.key(seed)
        ks = jax.random.split(key, 12)
        sc = 0.02
        return {'src': jax.random.normal(ks[0], (B, S, D), jnp.float32), 'in_proj_w': jax.random.normal(ks[1], (3 * D, D), jnp.float32) * sc, 'in_proj_b': jnp.zeros((3 * D,), jnp.float32), 'out_proj_w': jax.random.normal(ks[2], (D, D), jnp.float32) * sc, 'out_proj_b': jnp.zeros((D,), jnp.float32), 'Qp_w': jax.random.normal(ks[3], (R, D), jnp.float32) * sc, 'Qp_b': jnp.zeros((R,), jnp.float32), 'Kp_w': jax.random.normal(ks[4], (R, D), jnp.float32) * sc, 'Kp_b': jnp.zeros((R,), jnp.float32), 'Vp_w': jax.random.normal(ks[5], (D, D), jnp.float32) * sc, 'Vp_b': jnp.zeros((D,), jnp.float32), 'lam': jnp.float32(0.5), 'ff1_w': jax.random.normal(ks[6], (DFF, D), jnp.float32) * sc, 'ff1_b': jnp.zeros((DFF,), jnp.float32), 'ff2_w': jax.random.normal(ks[7], (D, DFF), jnp.float32) * sc, 'ff2_b': jnp.zeros((D,), jnp.float32), 'ln1_g': jnp.ones((D,), jnp.float32), 'ln1_b': jnp.zeros((D,), jnp.float32), 'ln2_g': jnp.ones((D,), jnp.float32), 'ln2_b': jnp.zeros((D,), jnp.float32)}
    _L3_attn_all = _L3_attn_setup()
    _L3_attn_in = {k: v for k, v in _L3_attn_all.items() if k in ('in_proj_w', 'in_proj_b', 'out_proj_w', 'out_proj_b', 'Qp_w', 'Qp_b', 'Kp_w', 'Kp_b', 'Vp_w', 'Vp_b', 'lam', 'ff1_w', 'ff1_b', 'ff2_w', 'ff2_b', 'ln1_g', 'ln1_b', 'ln2_g', 'ln2_b')}
    del _L3_attn_all

    def _L3_ffn_setup():
        import jax, jax.numpy as jnp
        import numpy as np
        E, D, TOP_K = (8, 128, 2)
        EPS_NORM, EPS_COS = (1e-12, 1e-08)

        def _l2norm(v, eps):
            return v / jnp.maximum(jnp.linalg.norm(v, axis=-1, keepdims=True), eps)

        def _mlp(x, gw, uw, dw):
            return jax.nn.silu(x @ gw.T) * (x @ uw.T) @ dw.T
        key = jax.random.key(seed)
        ks = jax.random.split(key, 12)
        B, S, H, F_ = (2, 256, 128, 256)
        G = E * D
        w = lambda k, shp: jax.random.normal(k, shp, dtype=jnp.float32) * 0.02
        return {'hidden_states': jax.random.normal(ks[0], (B, S, H), dtype=jnp.float32), 'gru_w_ih': w(ks[1], (3 * G, H)), 'gru_w_hh': w(ks[2], (3 * G, G)), 'expr_w': w(ks[3], (G, H)), 'ctx_w': w(ks[4], (G, H)), 'ctx_b': jnp.zeros((G,), dtype=jnp.float32), 'gate_w': w(ks[5], (E, F_, H)), 'up_w': w(ks[6], (E, F_, H)), 'down_w': w(ks[7], (E, H, F_)), 'shared_gate_w': w(ks[8], (F_, H)), 'shared_up_w': w(ks[9], (F_, H)), 'shared_down_w': w(ks[10], (H, F_))}
    _L3_ffn_all = _L3_ffn_setup()
    _L3_ffn_in = {k: v for k, v in _L3_ffn_all.items() if k in ('gru_w_ih', 'gru_w_hh', 'expr_w', 'ctx_w', 'ctx_b', 'gate_w', 'up_w', 'down_w', 'shared_gate_w', 'shared_up_w', 'shared_down_w')}
    del _L3_ffn_all
    return {'x': x, 'ctx_1024': ctx_1024, 'mask_BxSxS2_bk1': mask_BxSxS2_bk1, 'mask_Bx1xSxS2_bf1': mask_Bx1xSxS2_bf1, 'L0_xattn_W_Q': _L0_xattn_in['W_Q'], 'L0_xattn_b_Q': _L0_xattn_in['b_Q'], 'L0_xattn_W_K': _L0_xattn_in['W_K'], 'L0_xattn_b_K': _L0_xattn_in['b_K'], 'L0_xattn_W_V': _L0_xattn_in['W_V'], 'L0_xattn_b_V': _L0_xattn_in['b_V'], 'L0_xattn_W_out': _L0_xattn_in['W_out'], 'L0_xattn_b_out': _L0_xattn_in['b_out'], 'L0_attn_Wq': _L0_attn_in['Wq'], 'L0_attn_bq': _L0_attn_in['bq'], 'L0_attn_Wk': _L0_attn_in['Wk'], 'L0_attn_bk': _L0_attn_in['bk'], 'L0_attn_Wv': _L0_attn_in['Wv'], 'L0_attn_bv': _L0_attn_in['bv'], 'L0_attn_Wo': _L0_attn_in['Wo'], 'L0_attn_bo': _L0_attn_in['bo'], 'L0_attn_W1': _L0_attn_in['W1'], 'L0_attn_b1': _L0_attn_in['b1'], 'L0_attn_W2': _L0_attn_in['W2'], 'L0_attn_b2': _L0_attn_in['b2'], 'L0_attn_g1': _L0_attn_in['g1'], 'L0_attn_be1': _L0_attn_in['be1'], 'L0_attn_g2': _L0_attn_in['g2'], 'L0_attn_be2': _L0_attn_in['be2'], 'L0_ffn_k0': _L0_ffn_in['k0'], 'L0_ffn_k1': _L0_ffn_in['k1'], 'L0_ffn_k2': _L0_ffn_in['k2'], 'L0_ffn_s0': _L0_ffn_in['s0'], 'L0_ffn_s1': _L0_ffn_in['s1'], 'L0_ffn_s2': _L0_ffn_in['s2'], 'L1_xattn_Wq': _L1_xattn_in['Wq'], 'L1_xattn_bq': _L1_xattn_in['bq'], 'L1_xattn_Wk': _L1_xattn_in['Wk'], 'L1_xattn_bk': _L1_xattn_in['bk'], 'L1_xattn_Wv': _L1_xattn_in['Wv'], 'L1_xattn_bv': _L1_xattn_in['bv'], 'L1_xattn_Wo': _L1_xattn_in['Wo'], 'L1_xattn_bo': _L1_xattn_in['bo'], 'L1_attn_norm_w': _L1_attn_in['norm_w'], 'L1_attn_norm_b': _L1_attn_in['norm_b'], 'L1_attn_qkv_w': _L1_attn_in['qkv_w'], 'L1_attn_qkv_b': _L1_attn_in['qkv_b'], 'L1_attn_proj_w': _L1_attn_in['proj_w'], 'L1_attn_proj_b': _L1_attn_in['proj_b'], 'L1_ffn_Wg': _L1_ffn_in['Wg'], 'L1_ffn_Wu': _L1_ffn_in['Wu'], 'L1_ffn_Wd': _L1_ffn_in['Wd'], 'L1_ffn_Wr': _L1_ffn_in['Wr'], 'L1_ffn_temperature': _L1_ffn_in['temperature'], 'L2_xattn_Wq': _L2_xattn_in['Wq'], 'L2_xattn_bq': _L2_xattn_in['bq'], 'L2_xattn_Wk': _L2_xattn_in['Wk'], 'L2_xattn_bk': _L2_xattn_in['bk'], 'L2_xattn_Wv': _L2_xattn_in['Wv'], 'L2_xattn_bv': _L2_xattn_in['bv'], 'L2_attn_Wq': _L2_attn_in['Wq'], 'L2_attn_bq': _L2_attn_in['bq'], 'L2_attn_Wkv_down': _L2_attn_in['Wkv_down'], 'L2_attn_bkv_down': _L2_attn_in['bkv_down'], 'L2_attn_Wkv_up': _L2_attn_in['Wkv_up'], 'L2_attn_bkv_up': _L2_attn_in['bkv_up'], 'L2_attn_Wo': _L2_attn_in['Wo'], 'L2_attn_bo': _L2_attn_in['bo'], 'L2_ffn_Wc': _L2_ffn_in['Wc'], 'L2_ffn_bc': _L2_ffn_in['bc'], 'L2_ffn_W1': _L2_ffn_in['W1'], 'L2_ffn_b1': _L2_ffn_in['b1'], 'L2_ffn_W2': _L2_ffn_in['W2'], 'L2_ffn_b2': _L2_ffn_in['b2'], 'L3_xattn_Wq': _L3_xattn_in['Wq'], 'L3_xattn_Wk': _L3_xattn_in['Wk'], 'L3_xattn_Wv': _L3_xattn_in['Wv'], 'L3_xattn_Wp': _L3_xattn_in['Wp'], 'L3_xattn_bp': _L3_xattn_in['bp'], 'L3_attn_in_proj_w': _L3_attn_in['in_proj_w'], 'L3_attn_in_proj_b': _L3_attn_in['in_proj_b'], 'L3_attn_out_proj_w': _L3_attn_in['out_proj_w'], 'L3_attn_out_proj_b': _L3_attn_in['out_proj_b'], 'L3_attn_Qp_w': _L3_attn_in['Qp_w'], 'L3_attn_Qp_b': _L3_attn_in['Qp_b'], 'L3_attn_Kp_w': _L3_attn_in['Kp_w'], 'L3_attn_Kp_b': _L3_attn_in['Kp_b'], 'L3_attn_Vp_w': _L3_attn_in['Vp_w'], 'L3_attn_Vp_b': _L3_attn_in['Vp_b'], 'L3_attn_lam': _L3_attn_in['lam'], 'L3_attn_ff1_w': _L3_attn_in['ff1_w'], 'L3_attn_ff1_b': _L3_attn_in['ff1_b'], 'L3_attn_ff2_w': _L3_attn_in['ff2_w'], 'L3_attn_ff2_b': _L3_attn_in['ff2_b'], 'L3_attn_ln1_g': _L3_attn_in['ln1_g'], 'L3_attn_ln1_b': _L3_attn_in['ln1_b'], 'L3_attn_ln2_g': _L3_attn_in['ln2_g'], 'L3_attn_ln2_b': _L3_attn_in['ln2_b'], 'L3_ffn_gru_w_ih': _L3_ffn_in['gru_w_ih'], 'L3_ffn_gru_w_hh': _L3_ffn_in['gru_w_hh'], 'L3_ffn_expr_w': _L3_ffn_in['expr_w'], 'L3_ffn_ctx_w': _L3_ffn_in['ctx_w'], 'L3_ffn_ctx_b': _L3_ffn_in['ctx_b'], 'L3_ffn_gate_w': _L3_ffn_in['gate_w'], 'L3_ffn_up_w': _L3_ffn_in['up_w'], 'L3_ffn_down_w': _L3_ffn_in['down_w'], 'L3_ffn_shared_gate_w': _L3_ffn_in['shared_gate_w'], 'L3_ffn_shared_up_w': _L3_ffn_in['shared_up_w'], 'L3_ffn_shared_down_w': _L3_ffn_in['shared_down_w']}

def reference(x, ctx_1024, mask_BxSxS2_bk1, mask_Bx1xSxS2_bf1, L0_xattn_W_Q, L0_xattn_b_Q, L0_xattn_W_K, L0_xattn_b_K, L0_xattn_W_V, L0_xattn_b_V, L0_xattn_W_out, L0_xattn_b_out, L0_attn_Wq, L0_attn_bq, L0_attn_Wk, L0_attn_bk, L0_attn_Wv, L0_attn_bv, L0_attn_Wo, L0_attn_bo, L0_attn_W1, L0_attn_b1, L0_attn_W2, L0_attn_b2, L0_attn_g1, L0_attn_be1, L0_attn_g2, L0_attn_be2, L0_ffn_k0, L0_ffn_k1, L0_ffn_k2, L0_ffn_s0, L0_ffn_s1, L0_ffn_s2, L1_xattn_Wq, L1_xattn_bq, L1_xattn_Wk, L1_xattn_bk, L1_xattn_Wv, L1_xattn_bv, L1_xattn_Wo, L1_xattn_bo, L1_attn_norm_w, L1_attn_norm_b, L1_attn_qkv_w, L1_attn_qkv_b, L1_attn_proj_w, L1_attn_proj_b, L1_ffn_Wg, L1_ffn_Wu, L1_ffn_Wd, L1_ffn_Wr, L1_ffn_temperature, L2_xattn_Wq, L2_xattn_bq, L2_xattn_Wk, L2_xattn_bk, L2_xattn_Wv, L2_xattn_bv, L2_attn_Wq, L2_attn_bq, L2_attn_Wkv_down, L2_attn_bkv_down, L2_attn_Wkv_up, L2_attn_bkv_up, L2_attn_Wo, L2_attn_bo, L2_ffn_Wc, L2_ffn_bc, L2_ffn_W1, L2_ffn_b1, L2_ffn_W2, L2_ffn_b2, L3_xattn_Wq, L3_xattn_Wk, L3_xattn_Wv, L3_xattn_Wp, L3_xattn_bp, L3_attn_in_proj_w, L3_attn_in_proj_b, L3_attn_out_proj_w, L3_attn_out_proj_b, L3_attn_Qp_w, L3_attn_Qp_b, L3_attn_Kp_w, L3_attn_Kp_b, L3_attn_Vp_w, L3_attn_Vp_b, L3_attn_lam, L3_attn_ff1_w, L3_attn_ff1_b, L3_attn_ff2_w, L3_attn_ff2_b, L3_attn_ln1_g, L3_attn_ln1_b, L3_attn_ln2_g, L3_attn_ln2_b, L3_ffn_gru_w_ih, L3_ffn_gru_w_hh, L3_ffn_expr_w, L3_ffn_ctx_w, L3_ffn_ctx_b, L3_ffn_gate_w, L3_ffn_up_w, L3_ffn_down_w, L3_ffn_shared_gate_w, L3_ffn_shared_up_w, L3_ffn_shared_down_w):
    import jax
    import jax.numpy as jnp

    def _L0_xattn_ref(input_Q, input_K, input_V, attn_mask, W_Q, b_Q, W_K, b_K, W_V, b_V, W_out, b_out):
        import jax, jax.numpy as jnp
        import numpy as np
        D_MODEL = 128
        NUM_HEADS = 16
        D_K = 64
        D_V = 64
        B, L = (2, 256)
        batch = input_Q.shape[0]
        Q = (input_Q @ W_Q.T + b_Q).reshape(batch, -1, NUM_HEADS, D_K).transpose(0, 2, 1, 3)
        K = (input_K @ W_K.T + b_K).reshape(batch, -1, NUM_HEADS, D_K).transpose(0, 2, 1, 3)
        V = (input_V @ W_V.T + b_V).reshape(batch, -1, NUM_HEADS, D_V).transpose(0, 2, 1, 3)
        scores = jnp.einsum('bhqd,bhkd->bhqk', Q, K) / np.sqrt(D_K).astype(np.float32)
        scores = jnp.where(attn_mask[:, None, :, :], jnp.float32(-10000.0), scores)
        attn = jax.nn.softmax(scores, axis=-1)
        out = jnp.einsum('bhqk,bhkd->bhqd', attn, V)
        out = out.transpose(0, 2, 1, 3).reshape(batch, -1, NUM_HEADS * D_V)
        return out @ W_out.T + b_out

    def _L0_attn_ref(src, Wq, bq, Wk, bk, Wv, bv, Wo, bo, W1, b1, W2, b2, g1, be1, g2, be2):
        import jax, jax.numpy as jnp
        import numpy as np
        B, S, D, H, DH, FF = (4, 512, 128, 16, 64, 512)
        EPS = 1e-06

        def _layer_norm(x, g, b):
            m = jnp.mean(x, axis=-1, keepdims=True)
            v = jnp.mean(jnp.square(x - m), axis=-1, keepdims=True)
            return (x - m) * jax.lax.rsqrt(v + 1e-05) * g + b
        b, s = (src.shape[0], src.shape[1])
        q = (src @ Wq + bq).reshape(b, s, H, DH)
        k = (src @ Wk + bk).reshape(b, s, H, DH)
        v = (src @ Wv + bv).reshape(b, s, H, DH)
        Q = jax.nn.elu(q) + 1.0
        K = jax.nn.elu(k) + 1.0
        KV = jnp.einsum('bshd,bshm->bhdm', K, v)
        Z = 1.0 / (jnp.einsum('bshd,bhd->bsh', Q, K.sum(axis=1)) + EPS)
        o = jnp.einsum('bshd,bhdm,bsh->bshm', Q, KV, Z).reshape(b, s, H * DH)
        attn_out = o @ Wo + bo
        x = _layer_norm(src + attn_out, g1, be1)
        y = jax.nn.gelu(x @ W1 + b1, approximate=False) @ W2 + b2
        return _layer_norm(x + y, g2, be2)

    def _L0_ffn_ref(x, k0, k1, k2, s0, s1, s2):
        import jax, jax.numpy as jnp
        import numpy as np
        import math
        D_IN = 128
        FEATURES = (512, 512, 128)
        BATCH, SEQ = (8, 256)

        def _conn_dense(kernel_bool, x):
            w = jnp.where(kernel_bool, jnp.float32(1.0), jnp.float32(-1.0))
            return x @ w
        h = jnp.concatenate([x, -x], axis=-1)
        h = s0 * _conn_dense(k0, h)
        h = jax.nn.relu(h) * 2
        h = s1 * _conn_dense(k1, h)
        h = jax.nn.relu(h) * 2
        h = s2 * _conn_dense(k2, h)
        return h

    def _L1_xattn_ref(q, k, v, mask, Wq, bq, Wk, bk, Wv, bv, Wo, bo):
        import jax, jax.numpy as jnp
        import numpy as np
        D_MODEL = 128
        NUM_HEADS = 16
        D_K = D_MODEL // NUM_HEADS
        B, S = (2, 256)
        b = q.shape[0]

        def proj(x, W, bias):
            y = jnp.einsum('bsd,ed->bse', x, W) + bias
            return y.reshape(b, -1, NUM_HEADS, D_K).transpose(0, 2, 1, 3)
        qh = proj(q, Wq, bq)
        kh = proj(k, Wk, bk)
        vh = proj(v, Wv, bv)
        scores = jnp.einsum('bhqd,bhkd->bhqk', qh, kh) / np.sqrt(D_K)
        scores = jnp.where(mask, scores, jnp.float32(-1000000000.0))
        attn = jax.nn.softmax(scores, axis=-1)
        out = jnp.einsum('bhqk,bhkd->bhqd', attn, vh)
        out = out.transpose(0, 2, 1, 3).reshape(b, -1, D_MODEL)
        return jnp.einsum('bsd,ed->bse', out, Wo) + bo

    def _L1_attn_ref(x, norm_w, norm_b, qkv_w, qkv_b, proj_w, proj_b):
        import jax, jax.numpy as jnp
        import numpy as np
        DIM = 128
        EPS = 1e-05

        def _layernorm(x, w, b):
            mu = jnp.mean(x, axis=-1, keepdims=True)
            var = jnp.mean(jnp.square(x - mu), axis=-1, keepdims=True)
            return (x - mu) * jax.lax.rsqrt(var + EPS) * w + b
        B, T, C = x.shape
        residual = x
        h = _layernorm(x, norm_w, norm_b)
        qkv = jnp.einsum('btc,oc->bto', h, qkv_w) + qkv_b
        q, k, v = (qkv[..., :C], qkv[..., C:2 * C], qkv[..., 2 * C:])
        attn = jnp.einsum('btc,bsc->bts', q, k) / jnp.sqrt(jnp.float32(C))
        o = jnp.einsum('bts,bsc->btc', attn, v)
        o = jnp.einsum('btc,oc->bto', o, proj_w) + proj_b
        return residual + o

    def _L1_ffn_ref(x, Wg, Wu, Wd, Wr, temperature):
        import jax, jax.numpy as jnp
        import numpy as np
        import math
        GOLDEN_CENTER = 1.0 / math.e
        GOLDEN_LOWER = 0.5 - math.log(4.0 / 3.0)
        GOLDEN_UPPER = 0.5
        B, T, D = (4, 256, 128)
        E = 8
        I = 512 // (E // 2)

        def _routing_weights(x, Wr, temperature):
            inh = jax.nn.sigmoid(x @ Wr / temperature)
            in_zone = (inh >= GOLDEN_LOWER) & (inh <= GOLDEN_UPPER)
            dist = jnp.abs(inh - GOLDEN_CENTER)
            w = jnp.exp(-dist / 0.1) * in_zone.astype(x.dtype)
            wsum = w.sum(axis=-1, keepdims=True)
            no_expert = wsum < 1e-08
            fb = jnp.exp(-dist / 0.3)
            _, top2 = jax.lax.top_k(fb, 2)
            fb_mask = jax.nn.one_hot(top2, E, dtype=x.dtype).sum(axis=-2)
            fb_w = fb * fb_mask
            fb_w = fb_w / jnp.clip(fb_w.sum(axis=-1, keepdims=True), 1e-08)
            w = jnp.where(no_expert, fb_w, w)
            wsum = w.sum(axis=-1, keepdims=True)
            return w / jnp.clip(wsum, 1e-08)
        weights = _routing_weights(x, Wr, temperature)
        gate = jnp.einsum('btd,edi->beti', x, Wg)
        up = jnp.einsum('btd,edi->beti', x, Wu)
        h = jax.nn.silu(gate) * up
        e_out = jnp.einsum('beti,eid->betd', h, Wd)
        out = jnp.einsum('bte,betd->btd', weights, e_out)
        return out

    def _L2_xattn_ref(q, k, v, Wq, bq, Wk, bk, Wv, bv):
        import jax, jax.numpy as jnp
        import numpy as np
        DIM = 128
        SCALE_DIM = 4
        QK_DIM = DIM // SCALE_DIM
        B, S = (4, 512)
        scale = jnp.asarray(np.sqrt(QK_DIM), q.dtype)
        qp = jnp.einsum('bsd,ed->bse', q, Wq) + bq
        kp = jnp.einsum('bsd,ed->bse', k, Wk) + bk
        vp = jnp.einsum('bsd,ed->bse', v, Wv) + bv
        z = jnp.einsum('bqe,bke->bqk', qp, kp)
        z = jax.nn.sigmoid(z / scale)
        return jnp.einsum('bqk,bkd->bqd', z, vp)

    def _L2_attn_ref(x, Wq, bq, Wkv_down, bkv_down, Wkv_up, bkv_up, Wo, bo):
        import jax, jax.numpy as jnp
        import numpy as np
        D_MODEL, N_HEADS, D_LATENT = (128, 16, 32)
        HEAD_DIM = D_MODEL // N_HEADS
        B, T = (2, 256)

        def apply_rope(x):
            Tn, D = (x.shape[1], x.shape[3])
            inv_freq = 1.0 / 10000.0 ** (jnp.arange(0, D, 2, dtype=jnp.float32) / D)
            t = jnp.arange(Tn, dtype=jnp.float32)
            freqs = jnp.outer(t, inv_freq)
            sin_f = jnp.sin(freqs)[None, :, None, :]
            cos_f = jnp.cos(freqs)[None, :, None, :]
            x1, x2 = jnp.split(x, 2, axis=-1)
            return jnp.concatenate([x1 * cos_f - x2 * sin_f, x1 * sin_f + x2 * cos_f], axis=-1)
        Bn, Tn = (x.shape[0], x.shape[1])
        q = x @ Wq + bq
        kv = (x @ Wkv_down + bkv_down) @ Wkv_up + bkv_up
        q = q.reshape(Bn, Tn, N_HEADS, HEAD_DIM)
        kv = kv.reshape(Bn, Tn, N_HEADS, 2 * HEAD_DIM)
        k, v = jnp.split(kv, 2, axis=-1)
        q = apply_rope(q)
        k = apply_rope(k)
        q = q.transpose(0, 2, 1, 3)
        k = k.transpose(0, 2, 1, 3)
        v = v.transpose(0, 2, 1, 3)
        att = jnp.einsum('bhqd,bhkd->bhqk', q, k) / jnp.sqrt(jnp.float32(HEAD_DIM))
        idx = jnp.arange(Tn, dtype=jnp.float32)
        dist_signed = idx[:, None] - idx[None, :]
        log_sparse = -0.1 * jnp.log(jnp.abs(dist_signed) + 1.0)
        decay = jnp.exp(-jnp.maximum(dist_signed, 0.0) * 0.01)
        att = att + (log_sparse + jnp.log(decay + 1e-09))[None, None]
        att = jax.nn.softmax(att, axis=-1)
        out = jnp.einsum('bhqk,bhkd->bhqd', att, v)
        memory_k = jnp.mean(k, axis=2, keepdims=True)
        memory_v = jnp.mean(v, axis=2, keepdims=True)
        memory_scores = jnp.einsum('bhqd,bhkd->bhqk', q, memory_k)
        infini_out = jax.nn.sigmoid(memory_scores) * memory_v
        out = out + 0.2 * infini_out
        out = out.transpose(0, 2, 1, 3).reshape(Bn, Tn, D_MODEL)
        return out @ Wo + bo

    def _L2_ffn_ref(x, Wc, bc, W1, b1, W2, b2):
        import jax, jax.numpy as jnp
        import numpy as np
        DM, NEXPERTS, SETS, ESIZE = (128, 32, 4, 32)
        B, S = (2, 1024)
        b, s, d = x.shape
        g = Wc.shape[1]
        grouped = x.reshape(b, s // g, g, d)
        logits = jnp.einsum('bntd,des->bntes', grouped, Wc) + bc
        tie = jnp.linspace(0.0, 1e-06, g, dtype=x.dtype).reshape(-1, 1, 1)
        logits = logits + tie
        perm = (logits == jnp.max(logits, axis=-3, keepdims=True)).astype(x.dtype)
        permuted = jnp.einsum('bntd,bntes->bnesd', grouped, perm)
        inner = jax.nn.relu(jnp.einsum('bnesd,esdf->bnesf', permuted, W1) + b1)
        result_permuted = jnp.einsum('bnesf,esdf->bnesd', inner, W2) + b2
        result = jnp.einsum('bnesd,bntes->bntd', result_permuted, perm)
        return result.reshape(b, s, d)

    def _L3_xattn_ref(q, k, v, Wq, Wk, Wv, Wp, bp):
        import jax, jax.numpy as jnp
        import numpy as np
        D_MODEL = 128
        N_HEAD = 16
        HEAD_DIM = D_MODEL // N_HEAD
        B, T, C = q.shape
        scale = 1.0 / jnp.sqrt(jnp.asarray(HEAD_DIM, q.dtype))
        q_proj = (q @ Wq).reshape(B, T, N_HEAD, HEAD_DIM)
        k_proj = k @ Wk
        v_proj = v @ Wv
        wei = jnp.einsum('bqhd,bkd->bhqk', q_proj, k_proj) * scale
        p = jax.nn.softmax(wei, axis=-1)
        out = jnp.einsum('bhqk,bkd->bqhd', p, v_proj).reshape(B, T, C)
        return out @ Wp + bp

    def _L3_attn_ref(src, in_proj_w, in_proj_b, out_proj_w, out_proj_b, Qp_w, Qp_b, Kp_w, Kp_b, Vp_w, Vp_b, lam, ff1_w, ff1_b, ff2_w, ff2_b, ln1_g, ln1_b, ln2_g, ln2_b):
        import jax, jax.numpy as jnp
        import numpy as np
        import math
        B, S, D, H, R, DFF = (4, 128, 128, 16, 64, 512)

        def _layernorm(x, g, b, eps=1e-05):
            m = jnp.mean(x, axis=-1, keepdims=True)
            v = jnp.var(x, axis=-1, keepdims=True)
            return (x - m) / jnp.sqrt(v + eps) * g + b
        b, s, d = src.shape
        dh = d // H
        qkv = src @ in_proj_w.T + in_proj_b
        q, k, v = jnp.split(qkv, 3, axis=-1)
        q = q.reshape(b, s, H, dh).transpose(0, 2, 1, 3)
        k = k.reshape(b, s, H, dh).transpose(0, 2, 1, 3)
        v = v.reshape(b, s, H, dh).transpose(0, 2, 1, 3)
        scores = jnp.einsum('bhqd,bhkd->bhqk', q, k) / math.sqrt(dh)
        attn = jax.nn.softmax(scores, axis=-1)
        ctx = jnp.einsum('bhqk,bhkd->bhqd', attn, v)
        ctx = ctx.transpose(0, 2, 1, 3).reshape(b, s, d)
        dense_output = ctx @ out_proj_w.T + out_proj_b
        Q = src @ Qp_w.T + Qp_b
        K = src @ Kp_w.T + Kp_b
        V = src @ Vp_w.T + Vp_b
        QK = jnp.einsum('bqr,bkr->bqk', Q, K) / math.sqrt(R)
        aw = jax.nn.softmax(QK, axis=-1)
        kk = max(1, int(s * 0.2))
        topv, topi = jax.lax.top_k(aw, kk)
        bi = jnp.arange(b)[:, None, None]
        si = jnp.arange(s)[None, :, None]
        sparse_attn = jnp.zeros_like(aw).at[bi, si, topi].set(topv)
        sparse_attn = sparse_attn / (jnp.sum(sparse_attn, axis=-1, keepdims=True) + 1e-09)
        sparse_output = jnp.einsum('bqk,bkd->bqd', sparse_attn, V)
        sig = jax.nn.sigmoid(lam)
        fused = sig * dense_output + (1.0 - sig) * sparse_output
        x = _layernorm(src + fused, ln1_g, ln1_b)
        ff = jax.nn.relu(x @ ff1_w.T + ff1_b) @ ff2_w.T + ff2_b
        return _layernorm(x + ff, ln2_g, ln2_b)

    def _L3_ffn_ref(hidden_states, gru_w_ih, gru_w_hh, expr_w, ctx_w, ctx_b, gate_w, up_w, down_w, shared_gate_w, shared_up_w, shared_down_w):
        import jax, jax.numpy as jnp
        import numpy as np
        E, D, TOP_K = (8, 128, 2)
        EPS_NORM, EPS_COS = (1e-12, 1e-08)

        def _l2norm(v, eps):
            return v / jnp.maximum(jnp.linalg.norm(v, axis=-1, keepdims=True), eps)

        def _mlp(x, gw, uw, dw):
            return jax.nn.silu(x @ gw.T) * (x @ uw.T) @ dw.T
        B, S, H = hidden_states.shape
        h0 = hidden_states.mean(axis=1) @ ctx_w.T + ctx_b
        xw = hidden_states @ gru_w_ih.T

        def step(h, xw_t):
            hw = h @ gru_w_hh.T
            xr, xz, xn = jnp.split(xw_t, 3, axis=-1)
            hr, hz, hnn = jnp.split(hw, 3, axis=-1)
            r = jax.nn.sigmoid(xr + hr)
            z = jax.nn.sigmoid(xz + hz)
            n = jnp.tanh(xn + r * hnn)
            h_new = (1.0 - z) * n + z * h
            return (h_new, h_new)
        _, hs = jax.lax.scan(step, h0, jnp.swapaxes(xw, 0, 1))
        routing = jnp.swapaxes(hs, 0, 1).reshape(B, S, E, D)
        routing = _l2norm(routing, EPS_NORM)
        expr = (hidden_states @ expr_w.T).reshape(B, S, E, D)
        gram = jnp.einsum('bsed,bsfd->bsef', routing, routing)
        diff = gram - jnp.eye(E, dtype=routing.dtype)
        diff_n = _l2norm(diff, EPS_NORM)
        penalty = jnp.mean(jnp.sum(diff_n ** 2, axis=(-2, -1)))
        num = jnp.sum(expr * routing, axis=-1)
        den = jnp.maximum(jnp.linalg.norm(expr, axis=-1), EPS_COS) * jnp.maximum(jnp.linalg.norm(routing, axis=-1), EPS_COS)
        cos_dist = 1.0 - num / den
        scores = (cos_dist * (1.0 + penalty)).reshape(B * S, E)
        top_v, top_i = jax.lax.top_k(scores, TOP_K)
        mult = jax.nn.softmax(top_v, axis=-1)
        onehot = jax.nn.one_hot(top_i, E, dtype=mult.dtype)
        cw = jnp.einsum('tk,tke->te', mult, onehot)
        xf = hidden_states.reshape(B * S, H)
        out = jnp.zeros_like(xf)
        for e in range(E):
            out = out + cw[:, e:e + 1] * _mlp(xf, gate_w[e], up_w[e], down_w[e])
        moe = out.reshape(B, S, H)
        shared = jax.lax.stop_gradient(_mlp(hidden_states, shared_gate_w, shared_up_w, shared_down_w))
        return moe + shared
    x = x + _L0_xattn_ref(_layernorm(x, axis=-1), ctx_1024, ctx_1024, mask_BxSxS2_bk1, L0_xattn_W_Q, L0_xattn_b_Q, L0_xattn_W_K, L0_xattn_b_K, L0_xattn_W_V, L0_xattn_b_V, L0_xattn_W_out, L0_xattn_b_out)
    x = x + _L0_attn_ref(_layernorm(x, axis=-1), L0_attn_Wq, L0_attn_bq, L0_attn_Wk, L0_attn_bk, L0_attn_Wv, L0_attn_bv, L0_attn_Wo, L0_attn_bo, L0_attn_W1, L0_attn_b1, L0_attn_W2, L0_attn_b2, L0_attn_g1, L0_attn_be1, L0_attn_g2, L0_attn_be2)
    x = x + _L0_ffn_ref(_layernorm(x, axis=-1), L0_ffn_k0, L0_ffn_k1, L0_ffn_k2, L0_ffn_s0, L0_ffn_s1, L0_ffn_s2)
    x = x + _L1_xattn_ref(_layernorm(x, axis=-1), ctx_1024, ctx_1024, mask_Bx1xSxS2_bf1, L1_xattn_Wq, L1_xattn_bq, L1_xattn_Wk, L1_xattn_bk, L1_xattn_Wv, L1_xattn_bv, L1_xattn_Wo, L1_xattn_bo)
    x = x + _L1_attn_ref(_layernorm(x, axis=-1), L1_attn_norm_w, L1_attn_norm_b, L1_attn_qkv_w, L1_attn_qkv_b, L1_attn_proj_w, L1_attn_proj_b)
    x = x + _L1_ffn_ref(_layernorm(x, axis=-1), L1_ffn_Wg, L1_ffn_Wu, L1_ffn_Wd, L1_ffn_Wr, L1_ffn_temperature)
    x = x + _L2_xattn_ref(_layernorm(x, axis=-1), ctx_1024, ctx_1024, L2_xattn_Wq, L2_xattn_bq, L2_xattn_Wk, L2_xattn_bk, L2_xattn_Wv, L2_xattn_bv)
    x = x + _L2_attn_ref(_layernorm(x, axis=-1), L2_attn_Wq, L2_attn_bq, L2_attn_Wkv_down, L2_attn_bkv_down, L2_attn_Wkv_up, L2_attn_bkv_up, L2_attn_Wo, L2_attn_bo)
    x = x + _L2_ffn_ref(_layernorm(x, axis=-1), L2_ffn_Wc, L2_ffn_bc, L2_ffn_W1, L2_ffn_b1, L2_ffn_W2, L2_ffn_b2)
    x = x + _L3_xattn_ref(_layernorm(x, axis=-1), ctx_1024, ctx_1024, L3_xattn_Wq, L3_xattn_Wk, L3_xattn_Wv, L3_xattn_Wp, L3_xattn_bp)
    x = x + _L3_attn_ref(_layernorm(x, axis=-1), L3_attn_in_proj_w, L3_attn_in_proj_b, L3_attn_out_proj_w, L3_attn_out_proj_b, L3_attn_Qp_w, L3_attn_Qp_b, L3_attn_Kp_w, L3_attn_Kp_b, L3_attn_Vp_w, L3_attn_Vp_b, L3_attn_lam, L3_attn_ff1_w, L3_attn_ff1_b, L3_attn_ff2_w, L3_attn_ff2_b, L3_attn_ln1_g, L3_attn_ln1_b, L3_attn_ln2_g, L3_attn_ln2_b)
    x = x + _L3_ffn_ref(_layernorm(x, axis=-1), L3_ffn_gru_w_ih, L3_ffn_gru_w_hh, L3_ffn_expr_w, L3_ffn_ctx_w, L3_ffn_ctx_b, L3_ffn_gate_w, L3_ffn_up_w, L3_ffn_down_w, L3_ffn_shared_gate_w, L3_ffn_shared_up_w, L3_ffn_shared_down_w)
    return x

_drawn_inputs = setup_inputs


def setup_inputs(seed=0):
    import zlib

    import numpy as np

    out = dict(_drawn_inputs(seed))
    spreads = {'L0_xattn_b_Q': (0.0, 0.529),
     'L0_xattn_b_K': (0.0, 2.0),
     'L0_xattn_b_V': (0.0, 0.1),
     'L0_xattn_b_out': (0.0, 0.586),
     'L0_attn_bq': (0.0, 2.0),
     'L0_attn_bk': (0.0, 2.0),
     'L0_attn_bv': (0.0, 0.8),
     'L0_attn_bo': (0.0, 0.8),
     'L0_attn_b1': (0.0, 0.8),
     'L0_attn_b2': (0.0, 0.8),
     'L0_attn_g1': (1.0, 0.6),
     'L0_attn_be1': (0.0, 0.8),
     'L0_attn_g2': (1.0, 0.6),
     'L0_attn_be2': (0.0, 0.8),
     'L1_xattn_bq': (0.0, 0.8),
     'L1_xattn_bk': (0.0, 2.0),
     'L1_xattn_bv': (0.0, 0.8),
     'L1_xattn_bo': (0.0, 0.8),
     'L1_attn_norm_w': (1.0, 0.2),
     'L1_attn_norm_b': (0.0, 0.388),
     'L2_xattn_bq': (0.0, 0.309),
     'L2_xattn_bk': (0.0, 0.1),
     'L2_xattn_bv': (0.0, 0.1),
     'L2_attn_bq': (0.0, 0.8),
     'L2_attn_bkv_down': (0.0, 0.8),
     'L2_attn_bkv_up': (0.0, 0.8),
     'L2_attn_bo': (0.0, 2.0),
     'L3_xattn_bp': (0.0, 2.0),
     'L3_attn_in_proj_b': (0.0, 2.0),
     'L3_attn_out_proj_b': (0.0, 2.0),
     'L3_attn_Qp_b': (0.0, 2.0),
     'L3_attn_Kp_b': (0.0, 2.0),
     'L3_attn_Vp_b': (0.0, 2.0),
     'L3_attn_ff1_b': (0.0, 2.0),
     'L3_attn_ff2_b': (0.0, 2.0),
     'L3_attn_ln1_g': (1.0, 0.6),
     'L3_attn_ln1_b': (0.0, 2.0),
     'L3_attn_ln2_g': (1.0, 0.6),
     'L3_attn_ln2_b': (0.0, 2.0),
     'L3_ffn_ctx_b': (0.0, 0.8)}
    factors = {'L0_attn_Wq': 8.0,
     'L0_attn_Wk': 8.0,
     'L0_attn_Wv': 5.822,
     'L0_attn_Wo': 4.54,
     'L0_attn_W1': 8.0,
     'L0_attn_W2': 8.0,
     'L1_xattn_Wq': 3.464,
     'L1_xattn_Wk': 3.326,
     'L1_attn_proj_b': 8.0,
     'L1_ffn_Wg': 3.371,
     'L1_ffn_Wu': 3.123,
     'L1_ffn_Wd': 3.075,
     'L1_ffn_Wr': 3.696,
     'L2_attn_Wq': 8.0,
     'L2_attn_Wkv_down': 3.726,
     'L2_attn_Wkv_up': 3.649,
     'L2_attn_Wo': 3.68,
     'L2_ffn_Wc': 8.0,
     'L2_ffn_W1': 8.0,
     'L2_ffn_b1': 64.0,
     'L2_ffn_W2': 8.0,
     'L2_ffn_b2': 64.0,
     'L3_xattn_Wq': 8.0,
     'L3_xattn_Wk': 8.0,
     'L3_xattn_Wv': 8.0,
     'L3_xattn_Wp': 8.0,
     'L3_attn_in_proj_w': 27.577,
     'L3_attn_out_proj_w': 27.443,
     'L3_attn_Qp_w': 64.0,
     'L3_attn_Kp_w': 64.0,
     'L3_attn_Vp_w': 47.214,
     'L3_attn_ff1_w': 24.795,
     'L3_attn_ff2_w': 22.061,
     'L3_ffn_gru_w_ih': 8.0,
     'L3_ffn_gru_w_hh': 8.0,
     'L3_ffn_expr_w': 8.0,
     'L3_ffn_ctx_w': 8.0,
     'L3_ffn_gate_w': 8.0,
     'L3_ffn_up_w': 8.0,
     'L3_ffn_down_w': 8.0,
     'L3_ffn_shared_gate_w': 8.0,
     'L3_ffn_shared_up_w': 8.0,
     'L3_ffn_shared_down_w': 8.0}
    for name, (base, spread) in spreads.items():
        noise = np.random.default_rng([zlib.crc32(name.encode()), seed]).standard_normal(out[name].shape)
        drawn = base * np.exp(spread * noise) if base else spread * noise
        out[name] = jnp.asarray(drawn.astype(out[name].dtype))
    for name, factor in factors.items():
        out[name] = (out[name] * factor).astype(out[name].dtype)
    return out
```

```python
from contextlib import ExitStack
import numpy as np
import concourse.bass as bass
from concourse import mybir

F32 = mybir.dt.float32
U8 = mybir.dt.uint8
ALU = mybir.AluOpType
ACT = mybir.ActivationFunctionType
AX = mybir.AxisListType

P = 128
BATCH = 64
SEQ = 32
CTX = 257
NTOK = BATCH * SEQ
NT = NTOK // P
BPT = P // SEQ
H = 16


class Token:

    def __init__(self, seg, sem, unit):
        self.seg, self.sem, self.unit, self.used, self.order = seg, sem, unit, False, None

    def value(self, i):
        return self.seg.base[self.sem] + i * self.seg.per.get(self.sem, 0) + self.order


class Prev:

    def __init__(self, token):
        self.token = token


class Buffer:

    def __init__(self, *readers):
        self.readers, self.by_segment = list(readers), {}

    def read_by(self, *tokens):
        self.readers = [t for t in tokens if t is not None]
        self.by_segment[self.readers[0].seg] = self.readers
        return tokens[0]

    @property
    def free(self):
        return Free(self, self.readers)


class Free:
    def __init__(self, buffer, readers):
        self.buffer, self.readers = buffer, readers

    def tokens(self, seg):
        if any(t.seg is seg for t in self.readers):
            return self.readers
        again = self.buffer.by_segment.get(seg, []) if seg.rounds > 1 else []
        return self.readers + [Prev(t) for t in again]


class Segment:
    def __init__(self, rounds):
        self.rounds, self.ops, self.per, self.base = rounds, {}, {}, {}
        self.first = 0


class Queues:

    ENGINES = ("pe", "act", "dve", "pool", "sp")

    def __init__(self, nc, ctx):
        self.nc, self.ctx = nc, ctx
        self.sems, self.segments, self.tokens = {}, [], []
        for e in self.ENGINES:
            self.sems[e] = ctx.enter_context(nc.semaphore("done_" + e))
        self.spare = ctx.enter_context(nc.semaphore("spare"))
        self.seg = None
        self.names = 0

    def sb(self, stack, name, shape, dt=F32):
        self.names += 1
        return stack.enter_context(self.nc.sbuf_tensor(f"{name}_{self.names}", shape, dt))

    def straight(self):
        self.seg = Segment(1)
        self.segments.append(self.seg)

    def loop(self, rounds):
        self.seg = Segment(rounds)
        self.segments.append(self.seg)

    def barrier(self):
        last = {}
        for seg in self.segments:
            for ops in seg.ops.values():
                for _, _, t in ops:
                    if t is not None:
                        last[t.sem] = t
        self.straight()
        for e in self.ENGINES:
            for sem, t in last.items():
                t.used = True
            self.seg.ops.setdefault(e, []).append((None, list(last.values()), None))

    def put(self, engine, fn, waits, sem=None, unit=1, alone=False):
        t = Token(self.seg, sem or engine, unit)
        t.alone = alone
        if unit == 16:
            t.used = True
        flat = self.flat(waits)
        self.seg.ops.setdefault(engine, []).append((fn, flat, t))
        return t

    def flat(self, waits):
        out = []
        for w in waits:
            out += self.flat(w) if isinstance(w, (list, tuple)) else [] if w is None else [w]
        return out

    def pe(self, fn, *w, alone=False):
        return self.put("pe", fn, w, alone=alone)

    def act(self, fn, *w, alone=False):
        return self.put("act", fn, w, alone=alone)

    def dve(self, fn, *w, alone=False):
        return self.put("dve", fn, w, alone=alone)

    def pool(self, fn, *w, alone=False):
        return self.put("pool", fn, w, alone=alone)

    def dma(self, sem, fn, *w, q="sp"):
        if sem not in self.sems:
            self.sems[sem] = self.ctx.enter_context(self.nc.semaphore("dma_" + sem))
        return self.put(q, fn, w, sem=sem, unit=16)

    def finish(self):
        for seg in self.segments:
            for ops in seg.ops.values():
                for n, (fn, waits, t) in enumerate(ops):
                    waits = [x for w in waits for x in (w.tokens(seg) if isinstance(w, Free) else [w])]
                    ops[n] = (fn, waits, t)
                    for w in waits:
                        (w.token if isinstance(w, Prev) else w).used = True
        total = {s: 0 for s in self.sems}
        for seg in self.segments:
            seg.base = dict(total)
            per = {}
            for ops in seg.ops.values():
                for _, _, t in ops:
                    if t is not None and t.used:
                        per[t.sem] = per.get(t.sem, 0) + t.unit
                        t.order = per[t.sem]
            seg.per = per
            for s, n in per.items():
                total[s] += n * seg.rounds
        lead = {s: max([seg.per.get(s, 0) for seg in self.segments]) for s in self.sems}
        owner = {}
        for seg in self.segments:
            for e, ops in seg.ops.items():
                for _, _, t in ops:
                    if t is not None and t.used:
                        owner.setdefault(t.sem, e)

        def emit(name, eng):
            for s in self.sems:
                if owner.get(s) == name and lead[s]:
                    eng.sem_inc(self.sems[s], lead[s])
            known = {}
            for seg in self.segments:
                ops = seg.ops.get(name, [])
                if not ops:
                    continue
                if seg.rounds == 1:
                    self.run(seg, ops, eng, seg.first, lead, known)
                    continue
                for _, waits, _ in ops:
                    for w in waits:
                        if not isinstance(w, Prev) and w.seg is not seg:
                            self.wait(eng, w.sem, lead[w.sem] + w.value(w.seg.rounds - 1), known)
                with eng.Fori(0, seg.rounds) as i:
                    self.run(seg, ops, eng, i, lead, None)
                known.clear()

        block = self.ctx.enter_context(self.nc.Block())

        @block.tensor
        def _(e):
            emit("pe", e)

        @block.scalar
        def _(e):
            emit("act", e)

        @block.vector
        def _(e):
            emit("dve", e)

        @block.gpsimd
        def _(e):
            emit("pool", e)

        @block.sync
        def _(e):
            emit("sp", e)
            for s in self.sems:
                if s not in self.ENGINES and total[s]:
                    e.wait_ge(self.sems[s], lead[s] + total[s])

    def wait(self, eng, sem, value, known):
        if known.get(sem, -1) < value:
            eng.wait_ge(self.sems[sem], value)
            known[sem] = value

    def run(self, seg, ops, eng, i, lead, known):
        inside = {}
        for fn, waits, t in ops:
            need, waited = {}, False
            for w in waits:
                if isinstance(w, Prev):
                    r = w.token.order - seg.per[w.token.sem]
                    need[w.token.sem] = max(need.get(w.token.sem, -1 << 30), r)
                elif w.seg is seg:
                    need[w.sem] = max(need.get(w.sem, -1 << 30), w.order)
                elif seg.rounds == 1:
                    self.wait(eng, w.sem, lead[w.sem] + w.value(w.seg.rounds - 1), known)
            for s, r in need.items():
                if inside.get(s, -1 << 30) < r:
                    inside[s] = r
                    v = lead[s] + seg.base[s] + r
                    if seg.rounds == 1:
                        self.wait(eng, s, v, known)
                    else:
                        eng.wait_ge(self.sems[s], v + i * seg.per[s])
                        waited = True
            if fn is None:
                continue
            if waited and t.alone:
                eng.sem_inc(self.spare, 1)
            ins = fn(eng, i)
            if t is not None and t.used:
                ins.then_inc(self.sems[t.sem], t.unit)


class Env:

    def __init__(self, k, ctx):
        nc = k.nc
        self.k, self.ctx = k, ctx
        self.X = k.sb(ctx, "X", [P, NT * P])
        self.yT = k.sb(ctx, "yT", [P, NTOK])
        self.ident = k.sb(ctx, "ident", [P, P])
        self.ones = k.sb(ctx, "ones", [P, P])
        self.mean_var = k.sb(ctx, "mean_var", [P, 2 * NT])
        self.rstd = k.sb(ctx, "rstd", [P, NT])
        self.stats = k.sb(ctx, "stats", [P, 6])
        self.moments = k.sb(ctx, "moments", [P, 2])
        self.ytile = k.sb(ctx, "ytile", [P, 4 * P])
        self.prep_banks = [Buffer() for _ in range(8)]
        self.bank = [ctx.enter_context(nc.psum_tensor(f"bank{n}", [P, 512], F32)) for n in range(8)]

    def constants(self):
        k = self.k
        a = k.pool(lambda e, i: e.memset(self.ident[:, :], 0.0))
        k.pool(lambda e, i: e.affine_select(out=self.ident[:, :], in_=self.ident[:, :], compare_op=ALU.not_equal,
                                            fill=1.0, base=0, pattern=[[-1, P]], channel_multiplier=1), a)
        k.dve(lambda e, i: e.memset(self.ones[:, :], 1.0))


def norm_tiles(env, y=None):
    k, X, mv, rstd = env.k, env.X, env.mean_var, env.rstd
    k.barrier()
    k.loop(NT)
    stats, moments = Buffer(), Buffer()
    st = k.dve(lambda e, i: e.bn_stats(env.stats[:, :], X[:, bass.ts(i, P)]), stats.free)
    ag = stats.read_by(k.dve(lambda e, i: e.bn_aggr(env.moments[:, :], env.stats[:, :]), st, moments.free, alone=True))
    last = moments.read_by(k.dve(lambda e, i: e.tensor_copy(mv[:, bass.ts(i, 2)], env.moments[:, :]), ag))
    k.straight()
    var = mv[:, :].rearrange("p (t two) -> p t two", two=2)[:, :, 1]
    a = k.dve(lambda e, i: e.tensor_scalar(rstd[:, :], var, 1e-5, None, ALU.add), last)
    b = k.act(lambda e, i: e.activation(rstd[:, :], rstd[:, :], ACT.Sqrt), a)
    r = k.dve(lambda e, i: e.reciprocal(rstd[:, :], rstd[:, :]), b)
    k.loop(NT // 4)
    ytile = [Buffer() for _ in range(4)]
    bank = Buffer()
    turned = []
    for u in range(4):
        yt = env.ytile[:, u * P:(u + 1) * P]
        n = k.dve(lambda e, i, u=u, yt=yt: e.tensor_scalar(
            yt, X[:, bass.ts(4 * i + u, P)], mv[:, bass.ds(8 * i + 2 * u, 1)],
            rstd[:, bass.ds(4 * i + u, 1)], ALU.subtract, ALU.mult), r, ytile[u].free)
        c = None
        if y is not None:
            c = k.pool(lambda e, i, u=u, yt=yt: e.tensor_copy(y[:, bass.ts(4 * i + u, P)], yt), n)
        t = k.pe(lambda e, i, u=u, yt=yt: e.transpose(env.bank[0][:, u * P:(u + 1) * P], yt,
                                                     env.ident[:, :]), n, bank.free)
        ytile[u].read_by(t, c)
        turned.append(t)
    bank.read_by(k.act(lambda e, i: e.copy(env.yT[:, bass.ts(i, 512)], env.bank[0][:, :]), turned))
    k.barrier()


def load_x(env, x):
    env.k.dma("x", lambda e, i: e.dma_start(env.X[:, :].rearrange("p (t d) -> p t d", d=P),
                                            x.rearrange("(t p) d -> p t d", p=P)))


def store_x(env, out):
    env.k.barrier()
    env.k.straight()
    env.k.dma("out", lambda e, i: e.dma_start(out.rearrange("(t p) d -> p t d", p=P),
                                              env.X[:, :].rearrange("p (t d) -> p t d", d=P)))


def heads_last(w):
    return w.rearrange("(h j) d -> j h d", h=H)


def softmax_cross_attention(env, ctx_kv, dk, Wq, Wk, Wv, Wo, scale, bq=None, bk=None, bv=None, bo=None,
                            mask=None, masked_where=None, masked_to=None, shared=False):
    k, nc = env.k, env.k.nc
    bank = env.bank
    with ExitStack() as st:
        sb = lambda name, shape, dt=F32: k.sb(st, name, shape, dt)
        A = sb("A", [P, H * P])
        M = sb("M", [P, H * P])
        bo_eff = sb("bo_eff", [1, P])
        if bq is not None:
            c = sb("c", [P, H])
            g = sb("g", [P, H])
            g0 = sb("g0", [P, H // 4])
        k.barrier()
        with ExitStack() as pre:
            wsb = lambda name, shape: k.sb(pre, name, shape)
            wq, wk, wv, wo = (wsb(n, [dk, H * P]) for n in ("wq", "wk", "wv", "wo"))
            as_heads = lambda t: t[:, :].rearrange("j (h d) -> j h d", h=H)
            lw = []
            done = []
            if not shared:
                for t, src in ((wq, Wq), (wk, Wk), (wv, Wv)):
                    lw.append(k.dma("w", lambda e, i, t=t, src=src: e.dma_start(as_heads(t), heads_last(src))))
                wo_rows = wsb("wo_rows", [P, H * dk])
                lo = k.dma("w", lambda e, i: e.dma_start(wo_rows[:, :], Wo))
                brow = wsb("brow", [1, P])
                bcol = [wsb("bcol", [dk, H]) for _ in range(3)]
                lb = [k.dma("w", lambda e, i: e.dma_start(brow[:, :], bo.rearrange("(a d) -> a d", a=1)))]
                for t, src in zip(bcol, (bq, bk, bv)):
                    lb.append(k.dma("w", lambda e, i, t=t, src=src: e.dma_start(
                        t[:, :], src.rearrange("(h j) -> j h", h=H))))
                lw = [lb[-1]]
                for q in range(4):
                    for r in range(4):
                        h = 4 * q + r
                        tt = k.pe(lambda e, i, q=q, r=r, h=h: e.transpose(
                            bank[q][0:dk, r * P:(r + 1) * P], wo_rows[:, h * dk:(h + 1) * dk], env.ident[:, :]), lb[-1])
                    cp = k.act(lambda e, i, q=q: e.copy(wo[:, q * 512:(q + 1) * 512], bank[q][0:dk, :]), tt)
                    done.append(cp)
                wkh = lambda h: wk[:, h * P:(h + 1) * P]
                wvh = lambda h: wv[:, h * P:(h + 1) * P]
            else:
                rows = [wsb("rows", [P, w]) for w in (P, dk, dk)]
                for t, src in zip(rows, (Wq, Wk, Wv)):
                    k.dma("w", lambda e, i, t=t, src=src: e.dma_start(t[:, :], src))
                brow = wsb("brow", [1, P])
                k.dma("w", lambda e, i: e.dma_start(brow[:, :], bo.rearrange("(a d) -> a d", a=1)))
                lw = [k.dma("w", lambda e, i: e.dma_start(as_heads(wo), heads_last(Wo)))]
                for q in range(4):
                    for r in range(4):
                        h = 4 * q + r
                        tt = k.pe(lambda e, i, q=q, r=r, h=h: e.transpose(
                            bank[q][0:dk, r * P:(r + 1) * P], rows[0][:, h * dk:(h + 1) * dk], env.ident[:, :]), lw)
                    done.append(k.act(lambda e, i, q=q: e.copy(wq[:, q * 512:(q + 1) * 512], bank[q][0:dk, :]), tt))
                for n, t in ((1, wk), (2, wv)):
                    tt = k.pe(lambda e, i, n=n: e.transpose(bank[3 + n][0:dk, 0:P], rows[n][:, :], env.ident[:, :]), lw)
                    done.append(k.act(lambda e, i, n=n, t=t: e.copy(t[:, 0:P], bank[3 + n][0:dk, 0:P]), tt))
                wkh = lambda h: wk[:, 0:P]
                wvh = lambda h: wv[:, 0:P]
            wqh = lambda h: wq[:, h * P:(h + 1) * P]
            woh = lambda h: wo[:, h * P:(h + 1) * P]
            for dst, left, right, first in ((A, wqh, wkh, 0), (M, wvh, woh, 4)):
                for q in range(4):
                    for r in range(4):
                        h = 4 * q + r
                        mm = k.pe(lambda e, i, h=h, r=r, b=bank[first + q], left=left, right=right: e.matmul(
                            b[:, r * P:(r + 1) * P], left(h), right(h), start=True, stop=True), done, lw)
                    cp = k.dve(lambda e, i, q=q, b=bank[first + q], dst=dst: e.tensor_copy(
                        dst[:, q * 512:(q + 1) * 512], b[:, :]), mm)
                    last = cp
                    if first == 0 and q == 0:
                        free0 = cp
                    if first == 0 and q == 1:
                        free1 = cp
            free = [free0, free1]
            if bq is not None:
                for h in range(H):
                    k.pe(lambda e, i, h=h: e.matmul(bank[0][:, h:h + 1], wkh(h), bcol[0][:, h:h + 1], start=True, stop=True), free)
                    mm = k.pe(lambda e, i, h=h: e.matmul(bank[0][:, H + h:H + h + 1], wqh(h), bcol[1][:, h:h + 1], start=True, stop=True))
                c1 = k.dve(lambda e, i: e.tensor_copy(c[:, :], bank[0][:, 0:H]), mm)
                c2 = k.dve(lambda e, i: e.tensor_copy(g[:, :], bank[0][:, H:2 * H]), mm)
                m1 = k.dve(lambda e, i: e.tensor_tensor(bcol[0][:, :], bcol[0][:, :], bcol[1][:, :], ALU.mult), mm)
                gq = bcol[0][:, :].rearrange("j (g f) -> j g f", f=4)
                for f in range(4):
                    mm = k.pe(lambda e, i, f=f: e.matmul(bank[2][32 * f:32 * f + 32, 0:4], env.ones[0:dk, 0:32], gq[:, :, f],
                                                         start=True, stop=True, tile_position=(0, 32 * f)), m1, done)
                c3 = k.dve(lambda e, i: e.tensor_copy(g0[:, :], bank[2][:, 0:4]), mm)
            mm = k.pe(lambda e, i: e.matmul(bank[1][0:1, 0:P], env.ones[0:1, 0:1], brow[:, :], start=True, stop=bq is None), free, lw)
            if bq is not None:
                for h in range(H):
                    mm = k.pe(lambda e, i, h=h: e.matmul(bank[1][0:1, 0:P], bcol[2][:, h:h + 1], woh(h),
                                                         start=False, stop=h == H - 1))
            k.dve(lambda e, i: e.tensor_copy(bo_eff[:, :], bank[1][0:1, 0:P]), mm)
            k.barrier()
        NB = 2
        qh = sb("qh", [P, BPT * H * SEQ])
        r_all = sb("r_all", [P, BPT * 4])
        kv = [sb("kv", [P, 2 * P]) for _ in range(NB)]
        kv_last = [sb("kv_last", [1, P]) for _ in range(NB)]
        kvT = [sb("kvT", [P, CTX]) for _ in range(NB)]
        maxes = [sb("maxes", [P, 4]) for _ in range(NB)]
        nbias = [sb("nbias", [P, 4]) for _ in range(NB)]
        rows_sum = [sb("rows_sum", [P, 4]) for _ in range(NB)]
        rinv = [sb("rinv", [P, 4]) for _ in range(NB)]
        probs = [sb("probs", [P, 4 * CTX]) for _ in range(NB)]
        pT = [sb("pT", [P, 2 * 512]) for _ in range(NB)]
        pT_last = [sb("pT_last", [1, 512]) for _ in range(NB)]
        U = sb("U", [P, H * P])
        y_tile = sb("y_tile", [P, P])
        if mask is not None:
            mask_u8 = sb("mask_u8", [P, BPT * CTX], U8)
            keep = sb("keep", [P, BPT * CTX])
            fill = sb("fill", [P, BPT * CTX])
        B = lambda: Buffer()
        f_q, f_r, f_U, f_y, f_mask, f_keep = B(), B(), B(), B(), B(), B()
        f_kv, f_kvT, f_mx, f_nb, f_rs, f_ri, f_pr, f_pT, f_pTl = ([B() for _ in range(NB)] for _ in range(9))
        f_bank = [B() for _ in range(8)]
        k.loop(NT)
        mapped = None
        if mask is not None:
            for f in range(4):
                lm = k.dma("mask", lambda e, i, f=f: e.dma_start(
                    mask_u8[32 * f:32 * f + 32, :].rearrange("q (b s) -> q b s", b=BPT),
                    mask[bass.ts(i, BPT), :, :].rearrange("b q s -> q b s")), f_mask.free)
            keep_mul, keep_add = (-1.0, 1.0) if masked_where else (1.0, 0.0)
            k1 = k.pool(lambda e, i: e.tensor_scalar(keep[:, :], mask_u8[:, :], keep_mul, keep_add, ALU.mult, ALU.add), lm, f_keep.free, alone=True)
            fill_mul, fill_add = (masked_to / scale, 0.0) if masked_where else (-masked_to / scale, masked_to / scale)
            mapped = k.pool(lambda e, i: e.tensor_scalar(fill[:, :], mask_u8[:, :], fill_mul, fill_add, ALU.mult, ALU.add), lm, f_keep.free, alone=True)
            f_mask.read_by(mapped)
        evq = []
        q_out = qh[:, :].rearrange("p (b h q) -> p h b q", b=BPT, h=H)
        for n in range(4):
            for r in range(4):
                h = 4 * n + r
                mm = k.pe(lambda e, i, n=n, r=r, h=h: e.matmul(
                    bank[1 + n][:, r * P:(r + 1) * P], A[:, h * P:(h + 1) * P], env.yT[:, bass.ts(i, P)],
                    start=True, stop=True), f_bank[1 + n].free)
            if bq is not None and n % 2:
                cp = k.dve(lambda e, i, n=n: e.tensor_tensor(
                    q_out[:, 4 * n:4 * n + 4], bank[1 + n][:, :].rearrange("p (h b q) -> p h b q", h=4, b=BPT),
                    c[:, 4 * n:4 * n + 4].unsqueeze(2).unsqueeze(3).to_broadcast([P, 4, BPT, SEQ]), ALU.add), mm, f_q.free)
            elif bq is None:
                for r in range(4):
                    cp = k.act(lambda e, i, n=n, r=r: e.copy(
                        q_out[:, 4 * n + r], bank[1 + n][:, r * P:(r + 1) * P].rearrange("p (b q) -> p b q", b=BPT)), mm, f_q.free)
            else:
                for r in range(4):
                    h = 4 * n + r
                    cp = k.act(lambda e, i, h=h, n=n, r=r: e.activation(
                        q_out[:, h], bank[1 + n][:, r * P:(r + 1) * P].rearrange("p (b q) -> p b q", b=BPT),
                        ACT.Identity, bias=c[:, h:h + 1]), mm, f_q.free)
            evq.append(cp)
            f_bank[1 + n].read_by(cp)
        rr = None
        if bq is not None:
            yc = k.dve(lambda e, i: e.tensor_copy(y_tile[:, :], env.yT[:, bass.ts(i, P)]), f_y.free)
            gf = g[:, :].rearrange("p (g f) -> p g f", f=4)
            for b in range(BPT):
                for f in range(4):
                    mm = k.pe(lambda e, i, b=b, f=f: e.matmul(
                        bank[7][32 * f:32 * f + 32, 4 * b:4 * b + 4], y_tile[:, 32 * b:32 * b + 32], gf[:, :, f],
                        start=True, stop=True, tile_position=(0, 32 * f)), yc, f_bank[7].free)
            f_y.read_by(mm)
            rr = k.dve(lambda e, i: e.tensor_tensor(
                r_all[:, :].rearrange("p (b g) -> p b g", b=BPT), bank[7][:, 0:16].rearrange("p (b g) -> p b g", b=BPT),
                g0[:, :].unsqueeze(1).to_broadcast([P, BPT, 4]), ALU.add), mm, f_r.free)
            f_bank[7].read_by(rr)
        exps = {}

        def scores(b):
            z = b % NB
            l1 = k.dma(f"kv{z}", lambda e, i: e.dma_start(kv[z][:, :].rearrange("p (c d) -> p c d", c=2),
                       ctx_kv[bass.ds(BPT * i + b, 1), 0:2 * P, :].rearrange("a (c p) d -> p (a c) d", p=P)), f_kv[z].free)
            l2 = k.dma(f"kv{z}", lambda e, i: e.dma_start(kv_last[z][:, :],
                       ctx_kv[bass.ds(BPT * i + b, 1), 2 * P:CTX, :].rearrange("a c d -> a (c d)")), f_kv[z].free)
            k.pe(lambda e, i: e.transpose(bank[0][:, 0:P], kv[z][:, 0:P], env.ident[:, :]), l2, f_bank[0].free)
            k.pe(lambda e, i: e.transpose(bank[0][:, P:2 * P], kv[z][:, P:2 * P], env.ident[:, :]))
            t = k.pe(lambda e, i: e.transpose(bank[0][:, 2 * P:CTX], kv_last[z][:, :], env.ident[0:1, 0:1]))
            ct = k.act(lambda e, i: e.copy(kvT[z][:, :], bank[0][:, 0:CTX]), t, f_kvT[z].free)
            f_bank[0].read_by(ct)
            mx, sc = [], []
            for n in range(4):
                bk_ = bank[1 + n]
                mm = k.pe(lambda e, i, n=n, bk_=bk_: e.matmul(
                    bk_[:, 0:CTX], qh[:, (4 * b + n) * P:(4 * b + n + 1) * P], kvT[z][:, :], start=True, stop=True),
                    ct, evq, f_bank[1 + n].free)
                if mask is not None:
                    w1 = k.dve(lambda e, i, n=n, bk_=bk_: e.scalar_tensor_tensor(
                        bk_[:, 0:CTX], bk_[:, 0:CTX], r_all[:, 4 * b + n:4 * b + n + 1], keep[:, b * CTX:(b + 1) * CTX],
                        ALU.add, ALU.mult), mm, rr, mapped)
                    w2 = k.dve(lambda e, i, n=n, bk_=bk_: e.tensor_tensor_reduce(
                        bk_[:, 0:CTX], bk_[:, 0:CTX], fill[:, b * CTX:(b + 1) * CTX], 1.0, -3.0e38, ALU.add, ALU.max,
                        maxes[z][:, n:n + 1]), w1, f_mx[z].free if n == 0 else None, alone=True)
                else:
                    w2 = k.dve(lambda e, i, n=n, bk_=bk_: e.tensor_reduce(
                        maxes[z][:, n:n + 1], bk_[:, 0:CTX], AX.X, ALU.max), mm, f_mx[z].free if n == 0 else None)
                mx.append(w2)
            if b == BPT - 1:
                f_q.read_by(mm)
                if bq is not None:
                    f_r.read_by(w1)
                if mask is not None:
                    f_keep.read_by(w2)
            f_kvT[z].read_by(mm)
            nb = k.dve(lambda e, i: e.tensor_scalar(nbias[z][:, :], maxes[z][:, :], -scale, None, ALU.mult), w2, f_nb[z].free)
            f_mx[z].read_by(nb)
            for n in range(4):
                ex = k.act(lambda e, i, n=n: e.activation(
                    probs[z][:, n * CTX:(n + 1) * CTX], bank[1 + n][:, 0:CTX], ACT.Exp, bias=nbias[z][:, n:n + 1], scale=scale,
                    accum_out=rows_sum[z][:, n:n + 1]), nb, f_pr[z].free if n == 0 else None, f_rs[z].free if n == 0 else None)
                f_bank[1 + n].read_by(ex)
            f_nb[z].read_by(ex)
            ri = k.dve(lambda e, i: e.reciprocal(rinv[z][:, :], rows_sum[z][:, :]), ex, f_ri[z].free)
            f_rs[z].read_by(ri)
            for n in range(4):
                eng = k.pool if n < 3 else k.dve
                nm = eng(lambda e, i, n=n: e.tensor_scalar(
                    probs[z][:, n * CTX:(n + 1) * CTX], probs[z][:, n * CTX:(n + 1) * CTX], rinv[z][:, n:n + 1], 1.0,
                    ALU.mult, ALU.mult), ri, alone=True)
                exps[b, n] = nm
            f_ri[z].read_by(exps[b, 2], exps[b, 3])

        def attend(b):
            z = b % NB
            for n in range(4):
                for c_ in range(2):
                    t = k.pe(lambda e, i, n=n, c_=c_: e.transpose(
                        bank[5 + c_][:, n * P:(n + 1) * P], probs[z][:, n * CTX + c_ * P:n * CTX + (c_ + 1) * P],
                        env.ident[:, :]), exps[b, n], f_bank[5 + c_].free)
            for n in range(4):
                t2 = k.pe(lambda e, i, n=n: e.transpose(
                    bank[0][0:1, n * P:(n + 1) * P], probs[z][:, n * CTX + 2 * P:(n + 1) * CTX], env.ident[:, :]),
                    f_bank[0].free)
            f_pr[z].read_by(t2)
            e0 = k.act(lambda e, i: e.copy(pT[z][:, 0:512], bank[5][:, :]), t, f_pT[z].free)
            e1 = k.dve(lambda e, i: e.tensor_copy(pT[z][:, 512:1024], bank[6][:, :]), t, f_pT[z].free)
            e2 = k.act(lambda e, i: e.copy(pT_last[z][:, :], bank[0][0:1, :]), t2, f_pTl[z].free)
            f_bank[5].read_by(e0)
            f_bank[6].read_by(e1)
            f_bank[0].read_by(e2)
            k.pe(lambda e, i: e.matmul(bank[7][:, :], kv[z][:, 0:P], pT[z][:, 0:512], start=True, stop=False),
                 e0, f_bank[7].free)
            k.pe(lambda e, i: e.matmul(bank[7][:, :], kv[z][:, P:2 * P], pT[z][:, 512:1024], start=False, stop=False), e1)
            mm = k.pe(lambda e, i: e.matmul(bank[7][:, :], kv_last[z][:, :], pT_last[z][:, :], start=False, stop=True), e2)
            f_kv[z].read_by(mm)
            f_pT[z].read_by(mm)
            f_pTl[z].read_by(mm)
            uo = k.act(lambda e, i: e.copy(
                U[:, :].rearrange("p (h b q) -> p h b q", h=H, b=BPT)[:, :, b], bank[7][:, :].rearrange("p (h q) -> p h q", h=H)),
                mm, f_U.free if b == 0 else None)
            f_bank[7].read_by(uo)
            return uo

        scores(0)
        for b in range(1, BPT):
            scores(b)
            attend(b - 1)
        uo = attend(BPT - 1)
        for h in range(H):
            k.pe(lambda e, i, h=h: e.matmul(bank[5][:, 0:P], U[:, h * P:(h + 1) * P], M[:, h * P:(h + 1) * P],
                                            start=h == 0, stop=False), uo, f_bank[5].free)
        mm = k.pe(lambda e, i: e.matmul(bank[5][:, 0:P], env.ones[0:1, :], bo_eff[:, :], start=False, stop=True))
        f_U.read_by(mm)
        ad = k.dve(lambda e, i: e.tensor_tensor(env.X[:, bass.ts(i, P)], env.X[:, bass.ts(i, P)], bank[5][:, 0:P], ALU.add), mm)
        f_bank[5].read_by(ad)
        k.barrier()

R4 = 4 * P


def columns(k, st, name, src, width=P):
    n = src.shape[0] // width
    t = k.sb(st, name, [width, n])
    return t, k.dma("w", lambda e, i: e.dma_start(t[:, :], src.rearrange("(c p) -> p c", p=width)))


def broadcast_row(k, st, name, src):
    t = k.sb(st, name, [P, src.shape[0]])
    return t, k.dma("w", lambda e, i: e.dma_start(t[:, :], src.partition_broadcast(P)))


def rows(k, st, name, src):
    c = src.shape[0] // P
    t = k.sb(st, name, [P, c * src.shape[1]])
    return t, k.dma("w", lambda e, i: e.dma_start(t[:, :].rearrange("p (c n) -> p c n", c=c),
                                                  src.rearrange("(c p) n -> p c n", p=P)))


def transpose_blocks(env, src, dst, count, ready, src_at=None, dst_at=None, first_bank=0):
    k = env.k
    src_at = src_at or (lambda n: src[:, n * P:(n + 1) * P])
    out = []
    for q in range(0, count, 4):
        b = first_bank + (q // 4) % 4
        m = min(4, count - q)
        for r in range(m):
            t = k.pe(lambda e, i, q=q, r=r, b=b: e.transpose(env.bank[b][:, r * P:(r + 1) * P], src_at(q + r),
                                                             env.ident[:, :]), ready, env.prep_banks[b].free)
        if dst_at is None:
            c = k.dve(lambda e, i, q=q, m=m, b=b: e.tensor_copy(dst[:, q * P:(q + m) * P], env.bank[b][:, 0:m * P]), t)
        else:
            c = k.dve(lambda e, i, q=q, m=m, b=b: e.tensor_copy(dst_at(q, m), env.bank[b][:, 0:m * P]), t)
        env.prep_banks[b].read_by(c)
        out.append(c)
    return out


def block_diagonal(env, st, value):
    k = env.k
    t = k.sb(st, "same_batch", [P, P])
    a = k.dve(lambda e, i: e.memset(t[:, :], 0.0))
    for b in range(BPT):
        a2 = k.dve(lambda e, i, b=b: e.memset(t[b * SEQ:(b + 1) * SEQ, b * SEQ:(b + 1) * SEQ], value), a)
    return t


class Norm4:

    def __init__(self, env, st):
        self.env, k = env, env.k
        self.stats = k.sb(st, "stats4", [P, 4 * 6])
        self.mv = k.sb(st, "mv4", [P, 8])
        self.rstd = k.sb(st, "rstd4", [P, 4])
        self.f_stats, self.f_mv, self.f_rstd = Buffer(), Buffer(), Buffer()

    def __call__(self, src, dst, gain, offset, ready):
        k = self.env.k
        s = []
        for u in range(4):
            s.append(k.dve(lambda e, i, u=u: e.bn_stats(self.stats[:, u * 6:u * 6 + 6], src[:, u * P:(u + 1) * P]), ready,
                           self.f_stats.free))
        for u in range(4):
            a = k.dve(lambda e, i, u=u: e.bn_aggr(self.mv[:, 2 * u:2 * u + 2], self.stats[:, u * 6:u * 6 + 6]), s[-1],
                      self.f_mv.free, alone=True)
        self.f_stats.read_by(a)
        var = self.mv[:, :].rearrange("p (t two) -> p t two", two=2)[:, :, 1]
        v = k.dve(lambda e, i: e.tensor_scalar(self.rstd[:, :], var, 1e-5, None, ALU.add), a, self.f_rstd.free)
        q = k.act(lambda e, i: e.activation(self.rstd[:, :], self.rstd[:, :], ACT.Sqrt), v)
        r = k.dve(lambda e, i: e.reciprocal(self.rstd[:, :], self.rstd[:, :]), q)
        for u in range(4):
            n = k.dve(lambda e, i, u=u: e.tensor_scalar(
                dst[:, u * P:(u + 1) * P], src[:, u * P:(u + 1) * P], self.mv[:, 2 * u:2 * u + 1],
                self.rstd[:, u:u + 1], ALU.subtract, ALU.mult), r)
        self.f_mv.read_by(n)
        self.f_rstd.read_by(n)
        four = lambda t: t[:, :].rearrange("p (t d) -> p t d", d=P)
        row = lambda t: t[:, :].unsqueeze(1).to_broadcast([P, 4, P])
        g = k.dve(lambda e, i: e.tensor_tensor(four(dst), four(dst), row(gain), ALU.mult), n)
        return k.dve(lambda e, i: e.tensor_tensor(four(dst), four(dst), row(offset), ALU.add), g)


def l0_attention(env, w):
    k, bank = env.k, env.bank
    DH, C = 64, 8
    with ExitStack() as st:
        sb = lambda name, shape, dt=F32: k.sb(st, name, shape, dt)
        y = sb("y", [P, NTOK])
        norm_tiles(env, y)
        k.straight()
        Wq, _ = rows(k, st, "Wq", w["Wq"])
        Wk, _ = rows(k, st, "Wk", w["Wk"])
        Wv, _ = rows(k, st, "Wv", w["Wv"])
        Wo, _ = rows(k, st, "Wo", w["Wo"])
        W1, _ = rows(k, st, "W1", w["W1"])
        W2, _ = rows(k, st, "W2", w["W2"])
        bq, _ = columns(k, st, "bq", w["bq"])
        bk, _ = columns(k, st, "bk", w["bk"])
        b1, _ = columns(k, st, "b1", w["b1"])
        bv, _ = broadcast_row(k, st, "bv", w["bv"])
        bo, _ = broadcast_row(k, st, "bo", w["bo"])
        b2, _ = broadcast_row(k, st, "b2", w["b2"])
        g1, _ = broadcast_row(k, st, "g1", w["g1"])
        be1, _ = broadcast_row(k, st, "be1", w["be1"])
        g2, _ = broadcast_row(k, st, "g2", w["g2"])
        be2, _ = broadcast_row(k, st, "be2", w["be2"])
        same = block_diagonal(env, st, 1.0)
        y_static = sb("y_static", [P, R4])
        feat = [sb("qf", [P, C * R4]), sb("kf", [P, C * R4])]
        ex = [sb("ex", [P, R4]) for _ in range(2)]
        re = [sb("re", [P, R4]) for _ in range(2)]
        vext = [sb("vext", [P, H * (DH + 1)]) for _ in range(2)]
        att = [sb("att", [P, 512]) for _ in range(2)]
        rec = [sb("rec", [P, H]) for _ in range(2)]
        o_tok = sb("o_tok", [P, H * DH])
        oT = sb("oT", [P, H * DH])
        s1 = sb("s1", [P, R4])
        x1T = sb("x1T", [P, R4])
        hT = sb("hT", [P, 4 * R4])
        s2 = s1b = sb("s2", [P, R4])
        for t in vext:
            k.dve(lambda e, i, t=t: e.memset(t[:, :], 1.0))
        norm = Norm4(env, st)
        k.barrier()
        f_ys, f_y, f_oT, f_ot, f_s1, f_x1T, f_hT, f_s2 = (Buffer() for _ in range(8))
        f_feat = [Buffer(), Buffer()]
        f_ex, f_re, f_v, f_att, f_rec = ([Buffer(), Buffer()] for _ in range(5))
        f_bank = [Buffer() for _ in range(8)]
        k.loop(NT // 4)
        yc = k.pool(lambda e, i: e.tensor_copy(y_static[:, :], env.yT[:, bass.ts(i, R4)]), f_ys.free)
        made = [[], []]
        for c in range(C):
            for t, (W, b) in enumerate(((Wq, bq), (Wk, bk))):
                n = (2 * c + t) % 2
                mm = k.pe(lambda e, i, c=c, W=W, n=n: e.matmul(bank[n][:, :], W[:, c * P:(c + 1) * P], y_static[:, :],
                                                               start=True, stop=True), yc, f_bank[n].free)
                a = k.act(lambda e, i, c=c, b=b, n=n: e.activation(ex[n][:, :], bank[n][:, :], ACT.Exp, bias=b[:, c:c + 1]),
                          mm, f_ex[n].free)
                r = k.act(lambda e, i, c=c, b=b, n=n: e.activation(re[n][:, :], bank[n][:, :], ACT.Relu, bias=b[:, c:c + 1]),
                          f_re[n].free)
                f_bank[n].read_by(r)
                m = k.dve(lambda e, i, c=c, t=t, n=n: e.scalar_tensor_tensor(
                    feat[t][:, c * R4:(c + 1) * R4], ex[n][:, :], 1.0, re[n][:, :], ALU.min, ALU.add), r, f_feat[t].free)
                f_ex[n].read_by(m)
                f_re[n].read_by(m)
                made[t].append(m)
        for s in range(4):
            z = s % 2
            for n in range(2):
                mm = k.pe(lambda e, i, s=s, n=n: e.matmul(bank[2 + n][:, :], y_static[:, s * P:(s + 1) * P],
                                                          Wv[:, n * 512:(n + 1) * 512], start=True, stop=True), f_bank[2 + n].free)
                va = k.dve(lambda e, i, z=z, n=n: e.tensor_tensor(
                    vext[z][:, :].rearrange("p (h j) -> p h j", h=H)[:, 8 * n:8 * n + 8, 0:DH],
                    bank[2 + n][:, :].rearrange("p (h j) -> p h j", h=8),
                    bv[:, n * 512:(n + 1) * 512].rearrange("p (h j) -> p h j", h=8), ALU.add), mm, f_v[z].free)
                f_bank[2 + n].read_by(va)
            f_ys.read_by(mm)
            outs = []
            for j in range(2):
                for r in range(4):
                    for odd in range(2):
                        lo = odd * DH
                        col = (4 * j + r) * R4 + s * P
                        mm = k.pe(lambda e, i, r=r, lo=lo, col=col, odd=odd: e.matmul(
                            bank[4 + odd][:, r * P:(r + 1) * P], feat[1][lo:lo + DH, col:col + P], feat[0][lo:lo + DH, col:col + P],
                            start=True, stop=True), made, f_bank[4 + odd].free)
                for odd in range(2):
                    g = 2 * j + odd
                    ma = k.dve(lambda e, i, odd=odd: e.tensor_tensor(
                        att[odd][:, :].rearrange("p (h q) -> p h q", h=4), bank[4 + odd][:, :].rearrange("p (h q) -> p h q", h=4),
                        same[:, :].unsqueeze(1).to_broadcast([P, 4, P]), ALU.mult), mm, f_att[odd].free)
                    f_bank[4 + odd].read_by(ma)
                    for r in range(4):
                        h = 8 * j + 2 * r + odd
                        mo = k.pe(lambda e, i, r=r, h=h, odd=odd, z=z: e.matmul(
                            bank[6 + odd][:, r * 65:(r + 1) * 65], att[odd][:, r * P:(r + 1) * P], vext[z][:, h * 65:(h + 1) * 65],
                            start=True, stop=True), ma, va, f_bank[6 + odd].free)
                    f_att[odd].read_by(mo)
                    view = bank[6 + odd][:, 0:4 * 65].rearrange("p (h j) -> p h j", h=4)
                    r1 = k.dve(lambda e, i, z=z, g=g, view=view: e.tensor_scalar(
                        rec[z][:, 4 * g:4 * g + 4], view[:, :, DH], 1e-6, None, ALU.add), mo, f_rec[z].free)
                    r2 = k.dve(lambda e, i, z=z, g=g: e.reciprocal(rec[z][:, 4 * g:4 * g + 4], rec[z][:, 4 * g:4 * g + 4]), r1)
                    oo = k.dve(lambda e, i, z=z, g=g, j=j, odd=odd, view=view: e.tensor_tensor(
                        o_tok[:, :].rearrange("p (j r o d) -> p j o r d", j=2, r=4, o=2)[:, j, odd], view[:, :, 0:DH],
                        rec[z][:, 4 * g:4 * g + 4].unsqueeze(2).to_broadcast([P, 4, DH]), ALU.mult), r2, f_ot.free)
                    f_bank[6 + odd].read_by(oo)
                    outs.append(oo)
            f_v[z].read_by(mo)
            f_rec[z].read_by(oo)
            for n in range(2):
                for r in range(4):
                    t = k.pe(lambda e, i, n=n, r=r: e.transpose(bank[2 + n][:, r * P:(r + 1) * P],
                                                                o_tok[:, (4 * n + r) * P:(4 * n + r + 1) * P], env.ident[:, :]),
                             outs, f_bank[2 + n].free)
                ec = k.act(lambda e, i, n=n: e.copy(oT[:, n * 512:(n + 1) * 512], bank[2 + n][:, :]), t, f_oT.free)
                f_bank[2 + n].read_by(ec)
            f_ot.read_by(t)
            for c in range(8):
                mm = k.pe(lambda e, i, c=c: e.matmul(bank[1][:, 0:P], oT[:, c * P:(c + 1) * P], Wo[:, c * P:(c + 1) * P],
                                                     start=c == 0, stop=c == 7), ec, f_bank[1].free)
            f_oT.read_by(mm)
            a1 = k.dve(lambda e, i, s=s: e.tensor_tensor(s1[:, s * P:(s + 1) * P], bank[1][:, 0:P], bo[:, :], ALU.add), mm, f_s1.free)
            f_bank[1].read_by(a1)
            a2 = k.dve(lambda e, i, s=s: e.tensor_tensor(s1[:, s * P:(s + 1) * P], s1[:, s * P:(s + 1) * P],
                                                         y[:, bass.ts(4 * i + s, P)], ALU.add), a1)
        for f in f_feat:
            f.read_by(mo)
        n1 = norm(s1, s1, g1, be1, a2)
        for s in range(4):
            t = k.pe(lambda e, i, s=s: e.transpose(bank[0][:, s * P:(s + 1) * P], s1[:, s * P:(s + 1) * P], env.ident[:, :]),
                     n1, f_bank[0].free)
        xc = k.act(lambda e, i: e.copy(x1T[:, :], bank[0][:, :]), t, f_x1T.free)
        f_bank[0].read_by(xc)
        hs = []
        for c in range(4):
            n = 4 + c % 2
            mm = k.pe(lambda e, i, c=c, n=n: e.matmul(bank[n][:, :], W1[:, c * P:(c + 1) * P], x1T[:, :], start=True, stop=True),
                      xc, f_bank[n].free)
            ge = k.act(lambda e, i, c=c, n=n: e.activation(hT[:, c * R4:(c + 1) * R4], bank[n][:, :], ACT.Gelu, bias=b1[:, c:c + 1]),
                       mm, f_hT.free)
            f_bank[n].read_by(ge)
        f_x1T.read_by(mm)
        for s in range(4):
            for c in range(4):
                mm = k.pe(lambda e, i, s=s, c=c: e.matmul(bank[6][:, s * P:(s + 1) * P], hT[:, c * R4 + s * P:c * R4 + (s + 1) * P],
                                                          W2[:, c * P:(c + 1) * P], start=c == 0, stop=c == 3), ge, f_bank[6].free)
        f_hT.read_by(mm)
        a = k.dve(lambda e, i: e.tensor_tensor(s2[:, :], bank[6][:, :], s1[:, :], ALU.add), mm, f_s2.free)
        f_bank[6].read_by(a)
        f_s1.read_by(a)
        a = k.dve(lambda e, i: e.tensor_tensor(s2[:, :].rearrange("p (t d) -> p t d", d=P), s2[:, :].rearrange("p (t d) -> p t d", d=P),
                                               b2[:, :].unsqueeze(1).to_broadcast([P, 4, P]), ALU.add), a)
        n2 = norm(s2, s2, g2, be2, a)
        f_s2.read_by(k.dve(lambda e, i: e.tensor_tensor(env.X[:, bass.ts(i, R4)], env.X[:, bass.ts(i, R4)], s2[:, :], ALU.add), n2))
        k.barrier()


def l0_ffn(env, w):
    k, bank = env.k, env.bank
    FC = 4
    norm_tiles(env)
    with ExitStack() as st:
        sb = lambda name, shape, dt=F32: k.sb(st, name, shape, dt)
        k.straight()
        raw = [sb(f"k{n}", [P, c * wd], U8) for n, c, wd in ((0, 2, 512), (1, 4, 512), (2, 4, 128))]
        W = [sb(f"W{n}", [P, c * wd]) for n, c, wd in ((0, 2, 512), (1, 4, 512), (2, 4, 128))]
        scales = sb("scales", [P, 3])
        for n, c in ((0, 2), (1, 4), (2, 4)):
            k.dma("w", lambda e, i, n=n, c=c: e.dma_start(raw[n][:, :].rearrange("p (c n) -> p c n", c=c),
                                                          w[f"k{n}"].rearrange("(c p) n -> p c n", p=P)))
        for n in range(3):
            l = k.dma("w", lambda e, i, n=n: e.dma_start(scales[:, n:n + 1], w[f"s{n}"].partition_broadcast(P)))
        for n in range(3):
            c = k.dve(lambda e, i, n=n: e.tensor_scalar(W[n][:, :], raw[n][:, :], 2.0, -1.0, ALU.mult, ALU.add), l)
        k.dve(lambda e, i: e.tensor_tensor(W[0][:, 0:512], W[0][:, 0:512], W[0][:, 512:1024], ALU.subtract), c)
        k.dve(lambda e, i: e.tensor_scalar(scales[:, 1:3], scales[:, 1:3], 2.0, None, ALU.mult), l)
        h = [sb("h0", [P, FC * R4]), sb("h1", [P, FC * R4])]
        f_h = [Buffer(), Buffer()]
        f_bank = [Buffer() for _ in range(8)]
        k.barrier()
        k.loop(NT // 4)
        r0 = []
        for c in range(FC):
            n = c % 2
            mm = k.pe(lambda e, i, c=c, n=n: e.matmul(bank[n][:, :], W[0][:, c * P:(c + 1) * P], env.yT[:, bass.ts(i, R4)],
                                                      start=True, stop=True), f_bank[n].free)
            a = k.act(lambda e, i, c=c, n=n: e.activation(h[0][:, c * R4:(c + 1) * R4], bank[n][:, :], ACT.Relu, scale=scales[:, 0:1]),
                      mm, f_h[0].free)
            f_bank[n].read_by(a)
        r0 = a
        for c in range(FC):
            n = 2 + c % 2
            for kc in range(FC):
                mm = k.pe(lambda e, i, c=c, kc=kc, n=n: e.matmul(bank[n][:, :], W[1][:, kc * 512 + c * P:kc * 512 + (c + 1) * P],
                                                                 h[0][:, kc * R4:(kc + 1) * R4], start=kc == 0, stop=kc == FC - 1),
                          r0, f_bank[n].free)
            a = k.act(lambda e, i, c=c, n=n: e.activation(h[1][:, c * R4:(c + 1) * R4], bank[n][:, :], ACT.Relu, scale=scales[:, 1:2]),
                      mm, f_h[1].free)
            f_bank[n].read_by(a)
        f_h[0].read_by(mm)
        for s in range(4):
            for c in range(FC):
                mm = k.pe(lambda e, i, s=s, c=c: e.matmul(bank[4][:, s * P:(s + 1) * P], h[1][:, c * R4 + s * P:c * R4 + (s + 1) * P],
                                                          W[2][:, c * P:(c + 1) * P], start=c == 0, stop=c == FC - 1), a, f_bank[4].free)
        f_h[1].read_by(mm)
        f_bank[4].read_by(k.dve(lambda e, i: e.scalar_tensor_tensor(
            env.X[:, bass.ts(i, R4)], bank[4][:, :], scales[:, 2:3], env.X[:, bass.ts(i, R4)], ALU.mult, ALU.add), mm))
        k.barrier()


def l1_attention(env, w):
    k, bank = env.k, env.bank
    with ExitStack() as st:
        sb = lambda name, shape, dt=F32: k.sb(st, name, shape, dt)
        y = sb("y", [P, NTOK])
        norm_tiles(env, y)
        k.straight()
        qkv_rows, _ = rows(k, st, "qkv_rows", w["qkv_w"])
        proj_rows, _ = rows(k, st, "proj_rows", w["proj_w"])
        bqk, _ = columns(k, st, "bqk", w["qkv_b"][0:2 * P])
        bv, _ = broadcast_row(k, st, "bv", w["qkv_b"][2 * P:3 * P])
        bp, _ = broadcast_row(k, st, "bp", w["proj_b"])
        gw, _ = broadcast_row(k, st, "gw", w["norm_w"])
        gb, l = broadcast_row(k, st, "gb", w["norm_b"])
        qkvT = sb("qkvT", [P, 3 * P])
        projT = sb("projT", [P, P])
        transpose_blocks(env, qkv_rows, qkvT, 3, l)
        transpose_blocks(env, proj_rows, projT, 1, l, first_bank=1)
        same = block_diagonal(env, st, P ** -0.5)
        hn, hT, v, att, oT, t1 = (sb(n, [P, R4]) for n in ("hn", "hT", "v", "att", "oT", "t1"))
        qk = [sb("qT", [P, R4]), sb("kT", [P, R4])]
        norm = Norm4(env, st)
        f_hn, f_hT, f_v, f_att, f_oT, f_t1 = (Buffer() for _ in range(6))
        f_qk = [Buffer(), Buffer()]
        f_bank = [Buffer() for _ in range(8)]
        k.barrier()
        k.loop(NT // 4)
        ycp = k.dve(lambda e, i: e.tensor_copy(t1[:, :], y[:, bass.ts(i, R4)]), f_t1.free)
        n1 = norm(t1, hn, gw, gb, [ycp, f_hn.free])
        for s in range(4):
            t = k.pe(lambda e, i, s=s: e.transpose(bank[0][:, s * P:(s + 1) * P], hn[:, s * P:(s + 1) * P], env.ident[:, :]),
                     n1, f_bank[0].free)
        f_hn.read_by(t)
        hc = k.act(lambda e, i: e.copy(hT[:, :], bank[0][:, :]), t, f_hT.free)
        f_bank[0].read_by(hc)
        for n in range(2):
            mm = k.pe(lambda e, i, n=n: e.matmul(bank[1 + n][:, :], qkvT[:, n * P:(n + 1) * P], hT[:, :], start=True, stop=True),
                      hc, f_bank[1 + n].free)
            qa = k.act(lambda e, i, n=n: e.activation(qk[n][:, :], bank[1 + n][:, :], ACT.Identity, bias=bqk[:, n:n + 1]),
                       mm, f_qk[n].free)
            f_bank[1 + n].read_by(qa)
        for s in range(4):
            mm = k.pe(lambda e, i, s=s: e.matmul(bank[3][:, s * P:(s + 1) * P], hT[:, s * P:(s + 1) * P], qkvT[:, 2 * P:3 * P],
                                                 start=True, stop=True), f_bank[3].free)
        f_hT.read_by(mm)
        four = lambda t: t[:, :].rearrange("p (t d) -> p t d", d=P)
        row = lambda t: t[:, :].unsqueeze(1).to_broadcast([P, 4, P])
        va = k.dve(lambda e, i: e.tensor_tensor(four(v), four(bank[3]), row(bv), ALU.add), mm, f_v.free)
        f_bank[3].read_by(va)
        for s in range(4):
            mm = k.pe(lambda e, i, s=s: e.matmul(bank[4][:, s * P:(s + 1) * P], qk[1][:, s * P:(s + 1) * P], qk[0][:, s * P:(s + 1) * P],
                                                 start=True, stop=True), qa, f_bank[4].free)
        f_qk[0].read_by(mm)
        f_qk[1].read_by(mm)
        aa = k.dve(lambda e, i: e.tensor_tensor(four(att), four(bank[4]), row(same), ALU.mult), mm, f_att.free)
        f_bank[4].read_by(aa)
        for s in range(4):
            mm = k.pe(lambda e, i, s=s: e.matmul(bank[5][:, s * P:(s + 1) * P], v[:, s * P:(s + 1) * P], att[:, s * P:(s + 1) * P],
                                                 start=True, stop=True), aa, va, f_bank[5].free)
        f_v.read_by(mm)
        f_att.read_by(mm)
        oc = k.act(lambda e, i: e.copy(oT[:, :], bank[5][:, :]), mm, f_oT.free)
        f_bank[5].read_by(oc)
        for s in range(4):
            mm = k.pe(lambda e, i, s=s: e.matmul(bank[6][:, s * P:(s + 1) * P], oT[:, s * P:(s + 1) * P], projT[:, :],
                                                 start=True, stop=True), oc, f_bank[6].free)
        f_oT.read_by(mm)
        a = k.dve(lambda e, i: e.tensor_tensor(t1[:, :], bank[6][:, :], t1[:, :], ALU.add), mm)
        f_bank[6].read_by(a)
        a = k.dve(lambda e, i: e.tensor_tensor(four(t1), four(t1), row(bp), ALU.add), a)
        f_t1.read_by(k.dve(lambda e, i: e.tensor_tensor(env.X[:, bass.ts(i, R4)], env.X[:, bass.ts(i, R4)], t1[:, :], ALU.add), a))
        k.barrier()


def l1_ffn(env, w):
    k, bank = env.k, env.bank
    E, I = 8, 128
    CENTER, LOWER, UPPER = 1.0 / np.e, 0.5 - np.log(4.0 / 3.0), 0.5
    norm_tiles(env)
    with ExitStack() as st:
        sb = lambda name, shape, dt=F32: k.sb(st, name, shape, dt)
        k.straight()
        Wg, Wu, Wd = (sb(n, [P, E * P]) for n in ("Wg", "Wu", "Wd"))
        for t, s in ((Wg, "Wg"), (Wu, "Wu"), (Wd, "Wd")):
            k.dma("w", lambda e, i, t=t, s=s: e.dma_start(t[:, :].rearrange("p (e n) -> p e n", e=E), w[s].rearrange("e p n -> p e n")))
        Wr, _ = rows(k, st, "Wr", w["Wr"])
        temp, l = broadcast_row(k, st, "temp", w["temperature"])
        last = [k.dve(lambda e, i: e.reciprocal(temp[:, :], temp[:, :]), l)]
        for t in range(NT):
            mm = k.pe(lambda e, i, t=t: e.matmul(bank[0][:, t * E:(t + 1) * E], env.yT[:, t * P:(t + 1) * P], Wr[:, :],
                                                 start=True, stop=True), l)
        NE = NT * E
        names = {n: sb(n, [P, NE]) for n in ("inh", "dist", "zone", "hot", "wz", "fb", "left", "key", "pick", "order")}
        small = {n: sb(n, [P, NT]) for n in ("wsum", "none", "top", "fsum")}
        A = {n: t[:, :] for n, t in {**names, **small}.items()}
        te = lambda n: A[n].rearrange("p (t e) -> p t e", e=E)
        col = lambda n: A[n].unsqueeze(2).to_broadcast([P, NT, E])
        last.append(mm)

        def step(eng, fn):
            last[:] = [eng(fn, last)]

        TS = lambda o, a, s1, s2, p1, p2=None: step(k.dve, lambda e, i: (
            e.tensor_scalar(A[o], A[a], s1, s2, p1, p2) if p2 is not None else e.tensor_scalar(A[o], A[a], s1, s2, p1)))
        TT = lambda o, a, b, p: step(k.dve, lambda e, i: e.tensor_tensor(A[o], A[a], A[b], p))
        TC = lambda o, a, c, p: step(k.dve, lambda e, i: e.tensor_tensor(te(o), te(a), col(c), p))
        RD = lambda o, a, p: step(k.dve, lambda e, i: e.tensor_reduce(A[o], te(a), AX.X, p))
        for n in range(E):
            step(k.dve, lambda e, i, n=n: e.memset(te("order")[:, :, n], float(E - n)))
        step(k.act, lambda e, i: e.activation(A["inh"], bank[0][:, 0:NE], ACT.Sigmoid, scale=temp[:, 0:1]))
        TS("zone", "inh", LOWER, None, ALU.is_ge)
        TS("hot", "inh", UPPER, None, ALU.is_le)
        TT("zone", "zone", "hot", ALU.mult)
        TS("dist", "inh", CENTER, None, ALU.subtract)
        step(k.act, lambda e, i: e.activation(A["dist"], A["dist"], ACT.Abs))
        step(k.act, lambda e, i: e.activation(A["wz"], A["dist"], ACT.Exp, scale=-1.0 / 0.1))
        step(k.act, lambda e, i: e.activation(A["fb"], A["dist"], ACT.Exp, scale=-1.0 / 0.3))
        TT("wz", "wz", "zone", ALU.mult)
        RD("wsum", "wz", ALU.add)
        TS("none", "wsum", 1e-8, None, ALU.is_lt)
        TS("left", "fb", 1.0, None, ALU.mult)
        TS("pick", "fb", 0.0, None, ALU.mult)
        for _ in range(2):
            RD("top", "left", ALU.max)
            TC("key", "left", "top", ALU.is_equal)
            TT("key", "key", "order", ALU.mult)
            RD("top", "key", ALU.max)
            TC("key", "key", "top", ALU.is_equal)
            TT("pick", "pick", "key", ALU.add)
            TS("key", "key", -4.0, None, ALU.mult)
            TT("left", "left", "key", ALU.add)
        TT("fb", "fb", "pick", ALU.mult)
        RD("fsum", "fb", ALU.add)
        TS("fsum", "fsum", 1e-8, None, ALU.max)
        step(k.dve, lambda e, i: e.reciprocal(A["fsum"], A["fsum"]))
        TC("fb", "fb", "fsum", ALU.mult)
        TT("fb", "fb", "wz", ALU.subtract)
        TC("fb", "fb", "none", ALU.mult)
        TT("wz", "wz", "fb", ALU.add)
        RD("wsum", "wz", ALU.add)
        TS("wsum", "wsum", 1e-8, None, ALU.max)
        step(k.dve, lambda e, i: e.reciprocal(A["wsum"], A["wsum"]))
        TC("wz", "wz", "wsum", ALU.mult)
        weights = names["wz"]
        hs = [sb("h", [P, R4]) for _ in range(2)]
        wt = sb("wt", [P, 4 * E])
        f_h, f_bank, f_wt = [Buffer(), Buffer()], [Buffer() for _ in range(8)], Buffer()
        k.barrier()
        k.loop(NT // 4)
        wc = k.dve(lambda e, i: e.tensor_copy(wt[:, :], weights[:, bass.ts(i, 4 * E)]), f_wt.free)
        for x in range(E):
            z = x % 2
            g = k.pe(lambda e, i, x=x, z=z: e.matmul(bank[z][:, :], Wg[:, x * P:(x + 1) * P], env.yT[:, bass.ts(i, R4)],
                                                     start=True, stop=True), f_bank[z].free)
            u = k.pe(lambda e, i, x=x, z=z: e.matmul(bank[2 + z][:, :], Wu[:, x * P:(x + 1) * P], env.yT[:, bass.ts(i, R4)],
                                                     start=True, stop=True), f_bank[2 + z].free)
            a = k.act(lambda e, i, z=z: e.activation(hs[z][:, :], bank[z][:, :], ACT.Silu), g, f_h[z].free)
            f_bank[z].read_by(a)
            m = k.dve(lambda e, i, z=z: e.tensor_tensor(hs[z][:, :], hs[z][:, :], bank[2 + z][:, :], ALU.mult), a, u)
            f_bank[2 + z].read_by(m)
            for s in range(4):
                mm = k.pe(lambda e, i, x=x, z=z, s=s: e.matmul(bank[4 + z][:, s * P:(s + 1) * P], hs[z][:, s * P:(s + 1) * P],
                                                               Wd[:, x * P:(x + 1) * P], start=True, stop=True), m, f_bank[4 + z].free)
            f_h[z].read_by(mm)
            for s in range(4):
                prior = f_bank[4 + (x + 1) % 2].readers if x else None
                ad = k.dve(lambda e, i, x=x, z=z, s=s: e.scalar_tensor_tensor(
                    env.X[:, bass.ts(4 * i + s, P)], bank[4 + z][:, s * P:(s + 1) * P], wt[:, s * E + x:s * E + x + 1],
                    env.X[:, bass.ts(4 * i + s, P)], ALU.mult, ALU.add), mm, wc, prior)
            f_bank[4 + z].read_by(ad)
        f_wt.read_by(ad)
        k.barrier()


def l2_cross_attention(env, w, ctx_kv):
    k, bank = env.k, env.bank
    DQ = 32
    norm_tiles(env)
    with ExitStack() as st:
        sb = lambda name, shape, dt=F32: k.sb(st, name, shape, dt)
        k.straight()
        Wq, Wk, Wv = sb("Wq", [DQ, P]), sb("Wk", [DQ, P]), sb("Wv", [P, P])
        for t, n in ((Wq, "Wq"), (Wk, "Wk"), (Wv, "Wv")):
            k.dma("w", lambda e, i, t=t, n=n: e.dma_start(t[:, :], w[n]))
        bq, _ = columns(k, st, "bq", w["bq"], DQ)
        bk, _ = columns(k, st, "bk", w["bk"], DQ)
        bv = sb("bv", [1, P])
        l = k.dma("w", lambda e, i: e.dma_start(bv[:, :], w["bv"].rearrange("(a d) -> a d", a=1)))
        A, WvT, cg, g0 = sb("A", [P, P]), sb("WvT", [P, P]), sb("cg", [P, 2]), sb("g0", [1, 1])
        k.pe(lambda e, i: e.matmul(bank[0][:, 0:P], Wq[:, :], Wk[:, :], start=True, stop=True), l)
        k.pe(lambda e, i: e.matmul(bank[0][:, P:P + 1], Wk[:, :], bq[:, :], start=True, stop=True))
        k.pe(lambda e, i: e.matmul(bank[0][:, P + 1:P + 2], Wq[:, :], bk[:, :], start=True, stop=True))
        k.pe(lambda e, i: e.matmul(bank[0][0:1, P + 2:P + 3], bq[:, :], bk[:, :], start=True, stop=True))
        t = k.pe(lambda e, i: e.transpose(bank[0][:, 2 * P:3 * P], Wv[:, :], env.ident[:, :]))
        k.dve(lambda e, i: e.tensor_copy(A[:, :], bank[0][:, 0:P]), t)
        k.dve(lambda e, i: e.tensor_copy(cg[:, :], bank[0][:, P:P + 2]), t)
        k.dve(lambda e, i: e.tensor_copy(g0[:, :], bank[0][0:1, P + 2:P + 3]), t)
        k.dve(lambda e, i: e.tensor_copy(WvT[:, :], bank[0][:, 2 * P:3 * P]), t)
        ND = 2
        per = lambda n, s: [sb(n, s) for _ in range(ND)]
        kv, kv_last, kvT = per("kv", [P, BPT * 2 * P]), per("kv_last", [1, BPT * P]), [sb("kvT", [P, CTX]) for _ in range(2)]
        qf, r, zT, zT_last = per("qf", [P, P]), per("r", [1, P]), per("zT", [P, BPT * 64]), per("zT_last", [1, P])
        U, zs = per("U", [P, P]), per("zs", [1, P])
        mk = lambda: [Buffer() for _ in range(ND)]
        f_kv, f_kvT, f_qf, f_r, f_z, f_zl, f_U, f_zs = (mk() for _ in range(8))
        f_bank = [Buffer() for _ in range(8)]
        k.barrier()
        k.loop(NT // ND)
        for d in range(ND):
            batch = lambda i, d=d: bass.ts(ND * i + d, BPT)
            for c in range(2):
                k.dma(f"kv{d}", lambda e, i, d=d, c=c, batch=batch: e.dma_start(
                    kv[d][:, :].rearrange("p (b c d) -> p c b d", b=BPT, c=2)[:, c],
                    ctx_kv[batch(i), c * P:(c + 1) * P, :].rearrange("b p d -> p b d")), f_kv[d].free)
            ld = k.dma(f"kv{d}", lambda e, i, d=d, batch=batch: e.dma_start(
                kv_last[d][:, :].rearrange("a (b d) -> a b d", b=BPT),
                ctx_kv[batch(i), 2 * P:CTX, :].rearrange("b c d -> c b d")), f_kv[d].free)
            mm = k.pe(lambda e, i, d=d: e.matmul(bank[0][:, 0:P], A[:, :], env.yT[:, bass.ts(ND * i + d, P)], start=True, stop=True),
                      f_bank[0].free)
            mr = k.pe(lambda e, i, d=d: e.matmul(bank[0][0:1, P:2 * P], cg[:, 1:2], env.yT[:, bass.ts(ND * i + d, P)],
                                                 start=True, stop=True))
            q1 = k.dve(lambda e, i, d=d: e.tensor_scalar(qf[d][:, :], bank[0][:, 0:P], cg[:, 0:1], None, ALU.add), mr, f_qf[d].free)
            q2 = k.dve(lambda e, i, d=d: e.tensor_scalar(r[d][:, :], bank[0][0:1, P:2 * P], g0[:, :], None, ALU.add), mr, f_r[d].free)
            f_bank[0].read_by(q2)
            S = bank[3 + d]
            for b in range(BPT):
                z = b % 2
                o = 2 * P * b
                k.pe(lambda e, i, d=d, z=z, o=o: e.transpose(bank[1 + z][:, 0:P], kv[d][:, o:o + P], env.ident[:, :]),
                     ld, f_bank[1 + z].free)
                k.pe(lambda e, i, d=d, z=z, o=o: e.transpose(bank[1 + z][:, P:2 * P], kv[d][:, o + P:o + 2 * P], env.ident[:, :]))
                t = k.pe(lambda e, i, d=d, z=z, b=b: e.transpose(bank[1 + z][:, 2 * P:CTX], kv_last[d][:, b * P:(b + 1) * P],
                                                                 env.ident[0:1, 0:1]))
                cp = (k.act if z else k.dve)(lambda e, i, z=z: (e.copy if z else e.tensor_copy)(
                    kvT[z][:, :], bank[1 + z][:, 0:CTX]), t, f_kvT[z].free)
                f_bank[1 + z].read_by(cp)
                for c in range(3):
                    m = P if c < 2 else 1
                    dst = S[0:m, b * 96 + c * 32:b * 96 + c * 32 + 32]
                    k.pe(lambda e, i, d=d, z=z, b=b, c=c, m=m, dst=dst: e.matmul(
                        dst, kvT[z][:, c * P:c * P + m], qf[d][:, b * SEQ:(b + 1) * SEQ], start=True, stop=False), cp, q1, f_bank[3 + d].free)
                    mm = k.pe(lambda e, i, d=d, b=b, m=m, dst=dst: e.matmul(
                        dst, env.ones[0:1, 0:m], r[d][:, b * SEQ:(b + 1) * SEQ], start=False, stop=True), q2)
                f_kvT[z].read_by(mm)
            f_qf[d].read_by(mm)
            f_r[d].read_by(mm)
            scale = DQ ** -0.5
            s1 = k.act(lambda e, i, d=d, S=S: e.activation(
                zT[d][:, :].rearrange("p (b q) -> p b q", b=BPT), S[:, 0:BPT * 96].rearrange("p (b q) -> p b q", b=BPT)[:, :, 0:64],
                ACT.Sigmoid, scale=scale), mm, f_z[d].free)
            s2 = k.act(lambda e, i, d=d, S=S: e.activation(
                zT_last[d][:, :].rearrange("p (b q) -> p b q", b=BPT), S[0:1, 0:BPT * 96].rearrange("p (b q) -> p b q", b=BPT)[:, :, 64:96],
                ACT.Sigmoid, scale=scale), mm, f_zl[d].free)
            f_bank[3 + d].read_by(s2)
            for b in range(BPT):
                for c in range(3):
                    src = (kv[d][:, (2 * b + c) * P:(2 * b + c + 1) * P] if c < 2 else kv_last[d][:, b * P:(b + 1) * P])
                    zz = (zT[d][:, b * 64 + c * 32:b * 64 + c * 32 + 32] if c < 2 else zT_last[d][:, b * 32:b * 32 + 32])
                    k.pe(lambda e, i, b=b, c=c, src=src, zz=zz: e.matmul(
                        bank[5][:, b * SEQ:(b + 1) * SEQ], src, zz, start=c == 0, stop=c == 2), s2, f_bank[5].free)
            zv = zT[d][:, :].rearrange("p (b c q) -> p b c q", b=BPT, c=2)
            for c in range(3):
                zz = zv[:, :, c] if c < 2 else zT_last[d][:, :]
                m = P if c < 2 else 1
                mm = k.pe(lambda e, i, c=c, zz=zz, m=m: e.matmul(bank[6][0:1, 0:P], env.ones[0:m, 0:1], zz, start=c == 0, stop=c == 2),
                          f_bank[6].free)
            f_kv[d].read_by(mm)
            f_z[d].read_by(mm)
            f_zl[d].read_by(mm)
            u1 = k.act(lambda e, i, d=d: e.copy(U[d][:, :], bank[5][:, 0:P]), mm, f_U[d].free)
            f_bank[5].read_by(u1)
            u2 = k.act(lambda e, i, d=d: e.copy(zs[d][:, :], bank[6][0:1, 0:P]), mm, f_zs[d].free)
            f_bank[6].read_by(u2)
            k.pe(lambda e, i, d=d: e.matmul(bank[7][:, 0:P], U[d][:, :], WvT[:, :], start=True, stop=False), u2, f_bank[7].free)
            mm = k.pe(lambda e, i, d=d: e.matmul(bank[7][:, 0:P], zs[d][:, :], bv[:, :], start=False, stop=True))
            f_U[d].read_by(mm)
            f_zs[d].read_by(mm)
            f_bank[7].read_by(k.dve(lambda e, i, d=d: e.tensor_tensor(
                env.X[:, bass.ts(ND * i + d, P)], env.X[:, bass.ts(ND * i + d, P)], bank[7][:, 0:P], ALU.add), mm))
        k.barrier()


class HeadAttention:

    def __init__(self, env, st, head_mask):
        k = env.k
        self.env, self.head_mask = env, head_mask
        sb = lambda n, s: k.sb(st, n, s)
        self.kh = [sb("kh", [P, BPT * H * SEQ]) for _ in range(2)]
        self.s = [sb("s", [P, 512]) for _ in range(2)]
        self.mx = [sb("mx", [P, H]) for _ in range(2)]
        self.sum = [sb("sum", [P, H]) for _ in range(2)]
        self.pT = [sb("pT", [P, H * P]) for _ in range(2)]
        for t in self.pT:
            k.pool(lambda e, i, t=t: e.memset(t[:, :], 0.0))
        self.f = {n: [Buffer(), Buffer()] for n in ("kh", "s", "mx", "sum", "pT")}

    def __call__(self, s, qT, kT, v, out, ready, f_bank, banks, scale, table=None, out_free=None):
        k, bank, z, f = self.env.k, self.env.bank, s % 2, self.f
        kh, S, mx, sm, pT = self.kh[z], self.s[z], self.mx[z], self.sum[z], self.pT[z]
        sbank, obank = banks
        hb = lambda t: t.rearrange("p (h q) -> p h q", h=H)
        tok = slice(s * P, (s + 1) * P)
        for half in range(2):
            eng = (k.dve, k.pool)[half]
            kc = eng(lambda e, i, half=half: e.tensor_tensor(
                kh[:, :].rearrange("p (b h q) -> p b h q", b=BPT, h=H)[:, 2 * half:2 * half + 2],
                kT[:, tok].rearrange("p (b q) -> p b q", b=BPT)[:, 2 * half:2 * half + 2].unsqueeze(2).to_broadcast([P, 2, H, SEQ]),
                self.head_mask[:, :].unsqueeze(1).unsqueeze(3).to_broadcast([P, 2, H, SEQ]), ALU.mult), ready, f["kh"][z].free)
            if half == 0:
                k0 = kc
        for b in range(BPT):
            mm = k.pe(lambda e, i, b=b: e.matmul(
                bank[sbank][b * SEQ:(b + 1) * SEQ, :], qT[:, s * P + b * SEQ:s * P + (b + 1) * SEQ], kh[:, b * 512:(b + 1) * 512],
                start=True, stop=True, tile_position=(0, b * SEQ)), k0, kc, f_bank[sbank].free)
        f["kh"][z].read_by(mm)
        if table is not None:
            a = k.dve(lambda e, i: e.scalar_tensor_tensor(hb(S[:, :]), hb(bank[sbank][:, :]), scale,
                                                          table[:, :].unsqueeze(1).to_broadcast([P, H, SEQ]), ALU.mult, ALU.add),
                      mm, f["s"][z].free)
            f_bank[sbank].read_by(a)
            src, escale = S, 1.0
        else:
            a, src, escale = mm, bank[sbank], scale
        m = k.dve(lambda e, i: e.tensor_reduce(mx[:, :], hb(src[:, :]), AX.X, ALU.max), a, f["mx"][z].free)
        d = k.dve(lambda e, i: e.tensor_tensor(hb(S[:, :]), hb(src[:, :]), mx[:, :].unsqueeze(2).to_broadcast([P, H, SEQ]), ALU.subtract),
                  m, f["s"][z].free if table is None else None)
        f["mx"][z].read_by(d)
        if table is None:
            f_bank[sbank].read_by(d)
        x = k.act(lambda e, i: e.activation(S[:, :], S[:, :], ACT.Exp, scale=escale), d)
        sr = k.dve(lambda e, i: e.tensor_reduce(sm[:, :], hb(S[:, :]), AX.X, ALU.add), x, f["sum"][z].free)
        rc = k.dve(lambda e, i: e.reciprocal(sm[:, :], sm[:, :]), sr)
        for b in range(BPT):
            t = k.dve(lambda e, i, b=b: e.transpose(
                pT[:, :].rearrange("p (h b q) -> p b h q", h=H, b=BPT)[b * SEQ:(b + 1) * SEQ, b],
                hb(S[:, :])[b * SEQ:(b + 1) * SEQ]), x, f["pT"][z].free)
        f["s"][z].read_by(t)
        for h in range(H):
            mm = k.pe(lambda e, i, h=h: e.matmul(bank[obank][:, h * 8:(h + 1) * 8], pT[:, h * P:(h + 1) * P],
                                                 v[:, s * P + h * 8:s * P + (h + 1) * 8], start=True, stop=True), t, f_bank[obank].free)
        f["pT"][z].read_by(mm)
        o = k.dve(lambda e, i: e.tensor_tensor(
            out[:, tok].rearrange("p (h j) -> p h j", h=H), bank[obank][:, 0:P].rearrange("p (h j) -> p h j", h=H),
            sm[:, :].unsqueeze(2).to_broadcast([P, H, 8]), ALU.mult), mm, rc, out_free)
        f["sum"][z].read_by(o)
        f_bank[obank].read_by(o)
        return o


def l2_tables():
    f = np.float32
    t = np.arange(SEQ, dtype=f)
    freq = (1.0 / 10000.0 ** (np.arange(0, 8, 2, dtype=f) / f(8))).astype(f)
    angle = np.outer(t, freq).astype(f)
    cos, sin = np.cos(angle).astype(f), np.sin(angle).astype(f)
    cos8 = np.concatenate([cos, cos], 1)
    sin8 = np.concatenate([-sin, sin], 1)
    d = t[:, None] - t[None, :]
    bias = -0.1 * np.log(np.abs(d) + 1.0) + np.log(np.exp(-np.maximum(d, 0.0) * 0.01) + 1e-9)
    return {"rope_cos": np.tile(cos8, (BPT, H)).astype(f), "rope_sin": np.tile(sin8, (BPT, H)).astype(f),
            "distance_bias": np.tile(bias, (BPT, 1)).astype(f)}


def head_constants(env, st):
    k = env.k
    hm, sh = k.sb(st, "head_mask", [P, H]), k.sb(st, "same_head", [P, P])
    a = k.pool(lambda e, i: e.memset(hm[:, :], 1.0))
    b = k.pool(lambda e, i: e.affine_select(out=hm[:, :], in_=hm[:, :], compare_op=ALU.is_ge, fill=0.0, base=0,
                                            pattern=[[-8, H]], channel_multiplier=1), a)
    c = k.pool(lambda e, i: e.affine_select(out=hm[:, :], in_=hm[:, :], compare_op=ALU.is_ge, fill=0.0, base=7,
                                            pattern=[[8, H]], channel_multiplier=-1), b)
    d = k.dve(lambda e, i: e.tensor_copy(sh[:, :].rearrange("p (h j) -> p h j", h=H), hm[:, :].unsqueeze(2).to_broadcast([P, H, 8])), c)
    return hm, sh, d


def l2_attention(env, w, tables):
    k, bank = env.k, env.bank
    DL = 32
    norm_tiles(env)
    with ExitStack() as st:
        sb = lambda name, shape, dt=F32: k.sb(st, name, shape, dt)
        k.straight()
        Wq, _ = rows(k, st, "Wq", w["Wq"])
        Wd, _ = rows(k, st, "Wd", w["Wkv_down"])
        Wo, _ = rows(k, st, "Wo", w["Wo"])
        bd, _ = columns(k, st, "bd", w["bkv_down"], DL)
        bias = sb("bias", [P, 3 * P])
        k.dma("w", lambda e, i: e.dma_start(bias[:, 0:P], w["bq"].partition_broadcast(P)))
        for t in range(2):
            k.dma("w", lambda e, i, t=t: e.dma_start(
                bias[:, (1 + t) * P:(2 + t) * P].rearrange("p (h j) -> p h j", h=H),
                w["bkv_up"].rearrange("(h two j) -> two h j", two=2, h=H)[t].partition_broadcast(P)))
        Wup = sb("Wup", [DL, 2 * P])
        for t in range(2):
            k.dma("w", lambda e, i, t=t: e.dma_start(
                Wup[:, t * P:(t + 1) * P].rearrange("l (h j) -> l h j", h=H),
                w["Wkv_up"].rearrange("l (h two j) -> l h two j", two=2, h=H)[:, :, t]))
        bo, _ = broadcast_row(k, st, "bo", w["bo"])
        cos, sin, dist = sb("cos", [P, P]), sb("sin", [P, P]), sb("dist", [P, SEQ])
        for t, n in ((cos, "rope_cos"), (sin, "rope_sin"), (dist, "distance_bias")):
            k.dma("w", lambda e, i, t=t, n=n: e.dma_start(t[:, :], tables[n]))
        hm, sh, _ = head_constants(env, st)
        mean = sb("mean", [P, BPT])
        a = k.dve(lambda e, i: e.memset(mean[:, :], 0.0))
        for b in range(BPT):
            k.dve(lambda e, i, b=b: e.memset(mean[b * SEQ:(b + 1) * SEQ, b:b + 1], 1.0 / SEQ), a)
        attn = HeadAttention(env, st, hm)
        ys, lat = sb("ys", [P, R4]), sb("lat", [DL, R4])
        q, kk, v, t1, t2 = (sb(n, [P, R4]) for n in ("q", "kk", "v", "t1", "t2"))
        qT, kT, o, oT, gate, rot = (sb(n, [P, R4]) for n in ("qT", "kT", "o", "oT", "gate", "rot"))
        mem = sb("mem", [P, 8 * BPT])
        f_ys, f_lat, f_q, f_k, f_v, f_t1, f_t2, f_qT, f_kT, f_o, f_oT, f_g, f_mem = (Buffer() for _ in range(13))
        f_bank = [Buffer() for _ in range(8)]
        k.barrier()
        k.loop(NT // 4)
        yc = k.pool(lambda e, i: e.tensor_copy(ys[:, :], env.yT[:, bass.ts(i, R4)]), f_ys.free)
        mm = k.pe(lambda e, i: e.matmul(bank[0][0:DL, :], Wd[:, :], ys[:, :], start=True, stop=True), yc, f_bank[0].free)
        la = k.act(lambda e, i: e.activation(lat[:, :], bank[0][0:DL, :], ACT.Identity, bias=bd[:, 0:1]), mm, f_lat.free)
        f_bank[0].read_by(la)
        for s in range(4):
            z = 1 + s % 2
            k.pe(lambda e, i, s=s, z=z: e.matmul(bank[z][:, 0:P], ys[:, s * P:(s + 1) * P], Wq[:, :], start=True, stop=True),
                 f_bank[z].free)
            mm = k.pe(lambda e, i, s=s, z=z: e.matmul(bank[z][:, P:3 * P], lat[:, s * P:(s + 1) * P], Wup[:, :], start=True, stop=True), la)
            for n, (t, f) in enumerate(((q, f_q), (kk, f_k), (v, f_v))):
                e3 = k.dve(lambda e, i, n=n, t=t, s=s, z=z: e.tensor_tensor(
                    t[:, s * P:(s + 1) * P], bank[z][:, n * P:(n + 1) * P], bias[:, n * P:(n + 1) * P], ALU.add), mm, f.free)
            f_bank[z].read_by(e3)
        f_ys.read_by(mm)
        f_lat.read_by(mm)
        four = lambda t: t[:, :].rearrange("p (t d) -> p t d", d=P)
        row = lambda t: t[:, :].unsqueeze(1).to_broadcast([P, 4, P])
        halves = lambda t, n: t[:, :].rearrange("p (g two j) -> p g two j", two=2, j=4)[:, :, n]
        swap_sin = lambda n: sin[:, :].rearrange("p (h two j) -> p h two j", two=2, j=4)[:, :, n].unsqueeze(1).to_broadcast([P, 4, H, 4])
        hv = lambda t, n: t[:, :].rearrange("p (s h two j) -> p s h two j", s=4, two=2, j=4)[:, :, :, n]
        roped = []
        for t, f in ((q, f_q), (kk, f_k)):
            swaps = []
            for n in range(2):
                swaps.append(k.pool(lambda e, i, t=t, n=n: e.tensor_tensor(hv(t1, n), hv(t, 1 - n), swap_sin(n), ALU.mult), e3, f_t1.free))
            a = k.dve(lambda e, i, t=t: e.tensor_tensor(four(t2), four(t), row(cos), ALU.mult), e3, f_t2.free)
            b = k.dve(lambda e, i, t=t: e.tensor_tensor(t[:, :], t1[:, :], t2[:, :], ALU.add), a, swaps)
            f_t1.read_by(b)
            f_t2.read_by(b)
            roped.append(b)
        for s in range(4):
            k.pe(lambda e, i, s=s: e.transpose(bank[3][:, s * P:(s + 1) * P], q[:, s * P:(s + 1) * P], env.ident[:, :]),
                 roped, f_bank[3].free)
            t = k.pe(lambda e, i, s=s: e.transpose(bank[4][:, s * P:(s + 1) * P], kk[:, s * P:(s + 1) * P], env.ident[:, :]),
                     f_bank[4].free)
        c1 = k.act(lambda e, i: e.copy(qT[:, :], bank[3][:, :]), t, f_qT.free)
        c2 = k.act(lambda e, i: e.copy(kT[:, :], bank[4][:, :]), t, f_kT.free)
        f_bank[3].read_by(c1)
        f_bank[4].read_by(c2)
        f_q.read_by(t)
        for s in range(4):
            k.pe(lambda e, i, s=s: e.matmul(bank[7][:, s * BPT:(s + 1) * BPT], kk[:, s * P:(s + 1) * P], mean[:, :], start=True, stop=True),
                 f_bank[7].free)
            mm = k.pe(lambda e, i, s=s: e.matmul(bank[7][:, (4 + s) * BPT:(5 + s) * BPT], v[:, s * P:(s + 1) * P], mean[:, :],
                                                 start=True, stop=True))
        f_k.read_by(mm)
        mc = k.dve(lambda e, i: e.tensor_copy(mem[:, :], bank[7][:, 0:8 * BPT]), mm, f_mem.free)
        f_bank[7].read_by(mc)
        outs = []
        for s in range(4):
            outs.append(attn(s, qT, kT, v, o, [c2], f_bank, (5 + s % 2, 1 + s % 2), 8 ** -0.5, dist, f_o.free))
        f_v.read_by(mm, *[t for t in f_bank[2].readers])
        f_kT.read_by(outs[-1])
        bq_ = lambda t: t[:, :].rearrange("p (b q) -> p b q", q=SEQ)
        a = k.dve(lambda e, i: e.tensor_tensor(bq_(gate), bq_(qT), mem[:, 0:16].unsqueeze(2).to_broadcast([P, 16, SEQ]), ALU.mult),
                  c1, mc, f_g.free)
        mm = k.pe(lambda e, i: e.matmul(bank[3][:, :], sh[:, :], gate[:, :], start=True, stop=True), a, f_bank[3].free)
        x = k.act(lambda e, i: e.activation(gate[:, :], bank[3][:, :], ACT.Sigmoid), mm)
        f_bank[3].read_by(x)
        a = k.dve(lambda e, i: e.tensor_tensor(bq_(gate), bq_(gate), mem[:, 16:32].unsqueeze(2).to_broadcast([P, 16, SEQ]), ALU.mult), x)
        f_qT.read_by(a)
        f_mem.read_by(a)
        for s in range(4):
            t = k.pe(lambda e, i, s=s: e.transpose(bank[4][:, s * P:(s + 1) * P], o[:, s * P:(s + 1) * P], env.ident[:, :]),
                     outs, f_bank[4].free)
        f_o.read_by(t)
        a = k.dve(lambda e, i: e.scalar_tensor_tensor(oT[:, :], gate[:, :], 0.2, bank[4][:, :], ALU.mult, ALU.add), a, t, f_oT.free)
        f_bank[4].read_by(a)
        f_g.read_by(a)
        for s in range(4):
            mm = k.pe(lambda e, i, s=s: e.matmul(bank[0][:, s * P:(s + 1) * P], oT[:, s * P:(s + 1) * P], Wo[:, :], start=True, stop=True),
                      a, f_bank[0].free)
        f_oT.read_by(mm)
        xs = lambda i: env.X[:, bass.ts(i, R4)]
        a = k.dve(lambda e, i: e.tensor_tensor(xs(i), xs(i), bank[0][:, :], ALU.add), mm)
        f_bank[0].read_by(a)
        k.dve(lambda e, i: e.tensor_tensor(xs(i).rearrange("p (t d) -> p t d", d=P), xs(i).rearrange("p (t d) -> p t d", d=P), row(bo), ALU.add), a)
        k.barrier()


def l3_attention(env, w):
    k, bank = env.k, env.bank
    R, TOP = 64, 6
    with ExitStack() as st:
        sb = lambda name, shape, dt=F32: k.sb(st, name, shape, dt)
        y = sb("y", [P, NTOK])
        norm_tiles(env, y)
        k.straight()
        in_rows, _ = rows(k, st, "in_rows", w["in_proj_w"])
        QK_rows = sb("QK_rows", [P, P])
        k.dma("w", lambda e, i: e.dma_start(QK_rows[0:R, :], w["Qp_w"]))
        k.dma("w", lambda e, i: e.dma_start(QK_rows[R:2 * R, :], w["Kp_w"]))
        out_rows, _ = rows(k, st, "out_rows", w["out_proj_w"])
        V_rows, _ = rows(k, st, "V_rows", w["Vp_w"])
        f1_rows, _ = rows(k, st, "f1_rows", w["ff1_w"])
        f2_rows, _ = rows(k, st, "f2_rows", w["ff2_w"])
        b_qk, _ = columns(k, st, "b_qk", w["in_proj_b"][0:2 * P])
        b_Q, _ = columns(k, st, "b_Q", w["Qp_b"], R)
        b_K, _ = columns(k, st, "b_K", w["Kp_b"], R)
        b_f1, _ = columns(k, st, "b_f1", w["ff1_b"])
        b_vV = sb("b_vV", [P, 2 * P])
        k.dma("w", lambda e, i: e.dma_start(b_vV[:, 0:P], w["in_proj_b"][2 * P:3 * P].partition_broadcast(P)))
        k.dma("w", lambda e, i: e.dma_start(b_vV[:, P:2 * P], w["Vp_b"].partition_broadcast(P)))
        b_out, _ = broadcast_row(k, st, "b_out", w["out_proj_b"])
        b_f2, _ = broadcast_row(k, st, "b_f2", w["ff2_b"])
        lam, _ = broadcast_row(k, st, "lam", w["lam"])
        g1, _ = broadcast_row(k, st, "g1", w["ln1_g"])
        be1, _ = broadcast_row(k, st, "be1", w["ln1_b"])
        g2, _ = broadcast_row(k, st, "g2", w["ln2_g"])
        be2, l = broadcast_row(k, st, "be2", w["ln2_b"])
        inT, outT, QKT, vVT, f1T, f2T = (sb(n, [P, c * P]) for n, c in
                                         (("inT", 2), ("outT", 1), ("QKT", 1), ("vVT", 2), ("f1T", 4), ("f2T", 4)))
        transpose_blocks(env, in_rows, inT, 2, l)
        transpose_blocks(env, None, vVT, 2, l, src_at=lambda n: in_rows[:, 2 * P:3 * P] if n == 0 else V_rows[:, :], first_bank=1)
        transpose_blocks(env, out_rows, outT, 1, l, first_bank=2)
        transpose_blocks(env, QK_rows, QKT, 1, l, first_bank=3)
        transpose_blocks(env, f1_rows, f1T, 4, l)
        transpose_blocks(env, f2_rows, f2T, 4, l, first_bank=1)
        sig = k.act(lambda e, i: e.activation(lam[:, :], lam[:, :], ACT.Sigmoid), l)
        one_minus = sb("one_minus", [P, 1])
        k.dve(lambda e, i: e.tensor_scalar(one_minus[:, :], lam[:, :], -1.0, 1.0, ALU.mult, ALU.add), sig)
        hm, _, _ = head_constants(env, st)
        attn = HeadAttention(env, st, hm)
        norm = Norm4(env, st)
        ys, v, V2, o, oT, s1, x1T, mix = (sb(n, [P, R4]) for n in ("ys", "v", "V2", "o", "oT", "s1", "x1T", "mix"))
        qk = [sb("qT", [P, R4]), sb("kT", [P, R4])]
        QK = [sb("QT", [R, R4]), sb("KT", [R, R4])]
        W34 = SEQ + 2
        aw, rest, top = sb("aw", [P, 4 * W34]), sb("rest", [P, 4 * W34]), sb("top", [P, 32])
        amx, asm, sp = sb("amx", [P, 4]), sb("asm", [P, 4]), sb("sp", [P, 4 * SEQ])
        spT = sb("spT", [P, R4])
        hT = sb("hT", [P, 4 * R4])
        k.dve(lambda e, i: e.memset(aw[:, :], 2.0))
        k.dve(lambda e, i: e.memset(spT[:, :], 0.0))
        names = "ys v V2 o oT s1 x1T mix q k Q K aw rest top amx asm sp spT hT".split()
        f = {n: Buffer() for n in names}
        f_bank = [Buffer() for _ in range(8)]
        four = lambda t: t[:, :].rearrange("p (t d) -> p t d", d=P)
        row = lambda t: t[:, :].unsqueeze(1).to_broadcast([P, 4, P])
        k.barrier()
        k.loop(NT // 4)
        yc = k.pool(lambda e, i: e.tensor_copy(ys[:, :], env.yT[:, bass.ts(i, R4)]), f["ys"].free)
        made = []
        for n in range(4):
            wide = n < 2
            rows_ = P if wide else R
            lhs = inT[:, n * P:(n + 1) * P] if wide else QKT[:, (n - 2) * R:(n - 1) * R]
            dst = qk[n] if wide else QK[n - 2]
            b = b_qk[:, n:n + 1] if wide else (b_Q, b_K)[n - 2][:, 0:1]
            mm = k.pe(lambda e, i, n=n, lhs=lhs, rows_=rows_: e.matmul(bank[n][0:rows_, :], lhs, ys[:, :], start=True, stop=True),
                      yc, f_bank[n].free)
            a = k.act(lambda e, i, n=n, dst=dst, b=b, rows_=rows_: e.activation(dst[:, :], bank[n][0:rows_, :], ACT.Identity, bias=b),
                      mm, f["qkQK"[n]].free)
            f_bank[n].read_by(a)
            made.append(a)
        for s in range(4):
            z = 4 + s % 2
            mm = k.pe(lambda e, i, s=s, z=z: e.matmul(bank[z][:, 0:2 * P], ys[:, s * P:(s + 1) * P], vVT[:, :], start=True, stop=True),
                      f_bank[z].free)
            for n, t in ((0, v), (1, V2)):
                vb = k.dve(lambda e, i, s=s, z=z, n=n, t=t: e.tensor_tensor(
                    t[:, s * P:(s + 1) * P], bank[z][:, n * P:(n + 1) * P], b_vV[:, n * P:(n + 1) * P], ALU.add), mm,
                    f["v" if n == 0 else "V2"].free)
            f_bank[z].read_by(vb)
        f["ys"].read_by(mm)
        for s in range(4):
            for b in range(BPT):
                c = s * P + b * SEQ
                mm = k.pe(lambda e, i, s=s, b=b, c=c: e.matmul(
                    bank[3][b * SEQ:(b + 1) * SEQ, s * SEQ:(s + 1) * SEQ], QK[0][:, c:c + SEQ], QK[1][:, c:c + SEQ],
                    start=True, stop=True, tile_position=(0, b * SEQ)), made, f_bank[3].free, alone=True)
        f["Q"].read_by(mm)
        f["K"].read_by(mm)
        S3 = bank[3][:, 0:P].rearrange("p (s k) -> p s k", s=4)
        A3 = aw[:, :].rearrange("p (s k) -> p s k", s=4)[:, :, 0:SEQ]
        R3 = rest[:, :].rearrange("p (s k) -> p s k", s=4)[:, :, 0:SEQ]
        P3 = sp[:, :].rearrange("p (s k) -> p s k", s=4)
        wide4 = lambda t: t[:, :].unsqueeze(2).to_broadcast([P, 4, SEQ])
        a = k.dve(lambda e, i: e.tensor_reduce(amx[:, :], S3, AX.X, ALU.max), mm, f["amx"].free)
        a = k.dve(lambda e, i: e.tensor_tensor(A3, S3, wide4(amx), ALU.subtract), a, f["aw"].free)
        f_bank[3].read_by(a)
        f["amx"].read_by(a)
        a = k.act(lambda e, i: e.activation(A3, A3, ACT.Exp, scale=R ** -0.5), a)
        a = k.dve(lambda e, i: e.tensor_reduce(asm[:, :], A3, AX.X, ALU.add), a, f["asm"].free)
        a = k.dve(lambda e, i: e.reciprocal(asm[:, :], asm[:, :]), a)
        a = k.dve(lambda e, i: e.tensor_tensor(A3, A3, wide4(asm), ALU.mult), a)
        for s in range(4):
            t = k.dve(lambda e, i, s=s: e.max(top[:, 8 * s:8 * s + 8], aw[:, s * W34:(s + 1) * W34]), a, f["top"].free, alone=True)
        for s in range(4):
            m = k.dve(lambda e, i, s=s: e.match_replace(rest[:, s * W34:(s + 1) * W34], top[:, 8 * s:8 * s + 8],
                                                        aw[:, s * W34:(s + 1) * W34], 0.0), t, f["rest"].free, alone=True)
        f["top"].read_by(m)
        a = k.dve(lambda e, i: e.tensor_tensor(P3, A3, R3, ALU.subtract), m, f["sp"].free)
        f["aw"].read_by(a)
        f["rest"].read_by(a)
        a = k.dve(lambda e, i: e.tensor_reduce(asm[:, :], P3, AX.X, ALU.add), a)
        a = k.dve(lambda e, i: e.tensor_scalar(asm[:, :], asm[:, :], 1e-9, None, ALU.add), a)
        a = k.dve(lambda e, i: e.reciprocal(asm[:, :], asm[:, :]), a)
        a = k.dve(lambda e, i: e.tensor_tensor(P3, P3, wide4(asm), ALU.mult), a)
        f["asm"].read_by(a)
        for b in range(BPT):
            t = k.dve(lambda e, i, b=b: e.transpose(
                spT[:, :].rearrange("p (s b q) -> p b s q", s=4, b=BPT)[b * SEQ:(b + 1) * SEQ, b],
                P3[b * SEQ:(b + 1) * SEQ]), a, f["spT"].free)
        f["sp"].read_by(t)
        outs = []
        for s in range(4):
            outs.append(attn(s, qk[0], qk[1], v, o, [made, vb], f_bank, (6 + s % 2, 4 + s % 2), 8 ** -0.5, None, f["o"].free))
        for n in "qkv":
            f[n].read_by(outs[-1])
        for s in range(4):
            mm = k.pe(lambda e, i, s=s: e.matmul(bank[0][:, s * P:(s + 1) * P], spT[:, s * P:(s + 1) * P], V2[:, s * P:(s + 1) * P],
                                                 start=True, stop=True), t, f_bank[0].free)
        f["spT"].read_by(mm)
        f["V2"].read_by(mm)
        for s in range(4):
            t = k.pe(lambda e, i, s=s: e.transpose(bank[1][:, s * P:(s + 1) * P], o[:, s * P:(s + 1) * P], env.ident[:, :]),
                     outs, f_bank[1].free)
        f["o"].read_by(t)
        oc = k.act(lambda e, i: e.copy(oT[:, :], bank[1][:, :]), t, f["oT"].free)
        f_bank[1].read_by(oc)
        for s in range(4):
            md = k.pe(lambda e, i, s=s: e.matmul(bank[2][:, s * P:(s + 1) * P], oT[:, s * P:(s + 1) * P], outT[:, :], start=True, stop=True),
                      oc, f_bank[2].free)
        f["oT"].read_by(md)
        a = k.dve(lambda e, i: e.tensor_tensor(four(mix), four(bank[2]), row(b_out), ALU.add), md, f["mix"].free)
        f_bank[2].read_by(a)
        b = k.dve(lambda e, i: e.scalar_tensor_tensor(s1[:, :], bank[0][:, :], one_minus[:, 0:1], y[:, bass.ts(i, R4)], ALU.mult, ALU.add),
                  mm, f["s1"].free)
        f_bank[0].read_by(b)
        a = k.dve(lambda e, i: e.scalar_tensor_tensor(s1[:, :], mix[:, :], lam[:, 0:1], s1[:, :], ALU.mult, ALU.add), a, b)
        f["mix"].read_by(a)
        n1 = norm(s1, s1, g1, be1, a)
        for s in range(4):
            t = k.pe(lambda e, i, s=s: e.transpose(bank[1][:, s * P:(s + 1) * P], s1[:, s * P:(s + 1) * P], env.ident[:, :]),
                     n1, f_bank[1].free)
        xc = k.act(lambda e, i: e.copy(x1T[:, :], bank[1][:, :]), t, f["x1T"].free)
        f_bank[1].read_by(xc)
        for c in range(4):
            n = 4 + c % 2
            mm = k.pe(lambda e, i, c=c, n=n: e.matmul(bank[n][:, :], f1T[:, c * P:(c + 1) * P], x1T[:, :], start=True, stop=True),
                      xc, f_bank[n].free)
            re = k.act(lambda e, i, c=c, n=n: e.activation(hT[:, c * R4:(c + 1) * R4], bank[n][:, :], ACT.Relu, bias=b_f1[:, c:c + 1]),
                       mm, f["hT"].free)
            f_bank[n].read_by(re)
        f["x1T"].read_by(mm)
        for s in range(4):
            for c in range(4):
                mm = k.pe(lambda e, i, s=s, c=c: e.matmul(bank[6][:, s * P:(s + 1) * P], hT[:, c * R4 + s * P:c * R4 + (s + 1) * P],
                                                          f2T[:, c * P:(c + 1) * P], start=c == 0, stop=c == 3), re, f_bank[6].free)
        f["hT"].read_by(mm)
        a = k.dve(lambda e, i: e.tensor_tensor(s1[:, :], bank[6][:, :], s1[:, :], ALU.add), mm)
        f_bank[6].read_by(a)
        a = k.dve(lambda e, i: e.tensor_tensor(four(s1), four(s1), row(b_f2), ALU.add), a)
        n2 = norm(s1, s1, g2, be2, a)
        f["s1"].read_by(k.dve(lambda e, i: e.tensor_tensor(env.X[:, bass.ts(i, R4)], env.X[:, bass.ts(i, R4)], s1[:, :], ALU.add), n2))
        k.barrier()


def l2_ffn(env, w, tables):
    k, bank = env.k, env.bank
    E, SETS, F = 32, 4, 32
    ES = E * SETS
    with ExitStack() as st:
        sb = lambda name, shape, dt=F32: k.sb(st, name, shape, dt)
        y = sb("y", [P, NTOK])
        norm_tiles(env, y)
        k.straight()
        Wc, _ = rows(k, st, "Wc", w["Wc"].rearrange("d e s -> d (e s)"))
        bc = sb("bc", [P, 1])
        k.dma("w", lambda e, i: e.dma_start(bc[:, :], w["bc"].rearrange("e (s a) -> (e s) a", a=1)))
        b1 = sb("b1", [P, E])
        k.dma("w", lambda e, i: e.dma_start(b1[:, :], w["b1"].rearrange("e s f -> (s f) e")))
        b2 = sb("b2", [P, P])
        k.dma("w", lambda e, i: e.dma_start(b2[:, :], w["b2"].rearrange("e s d -> (e s) d")))
        tie = sb("tie", [P, SEQ])
        k.dma("w", lambda e, i: e.dma_start(tie[:, :], tables["tie"].partition_broadcast(P)))
        pick = sb("pick", [P, NTOK])
        G = sb("G", [P, ES * BATCH])
        G3 = G[:, :].rearrange("p (x b) -> p x b", b=BATCH)
        lg, mx = sb("lg", [P, R4]), sb("mx", [P, 16])
        pk = sb("pk", [P, R4])
        pick_tok, ys = sb("pick_tok", [P, R4]), sb("ys", [P, R4])
        f_lg, f_mx, f_pk, f_pt, f_ys = (Buffer() for _ in range(5))
        f_bank = [Buffer() for _ in range(8)]
        k.barrier()
        k.loop(NT // 4)
        b32 = lambda t: t[:, :].rearrange("p (b t) -> p b t", t=SEQ)
        mm = k.pe(lambda e, i: e.matmul(bank[0][:, :], Wc[:, :], env.yT[:, bass.ts(i, R4)], start=True, stop=True), f_bank[0].free)
        a = k.dve(lambda e, i: e.tensor_scalar(lg[:, :], bank[0][:, :], bc[:, 0:1], None, ALU.add), mm, f_lg.free)
        f_bank[0].read_by(a)
        a = k.dve(lambda e, i: e.tensor_tensor(b32(lg), b32(lg), tie[:, :].unsqueeze(1).to_broadcast([P, 16, SEQ]), ALU.add), a)
        a = k.dve(lambda e, i: e.tensor_reduce(mx[:, :], b32(lg), AX.X, ALU.max), a, f_mx.free)
        a = k.dve(lambda e, i: e.tensor_tensor(b32(pk), b32(lg), mx[:, :].unsqueeze(2).to_broadcast([P, 16, SEQ]), ALU.is_equal), a, f_pk.free)
        f_lg.read_by(a)
        f_mx.read_by(a)
        pc = k.pool(lambda e, i: e.tensor_copy(pick[:, bass.ts(i, R4)], pk[:, :]), a)
        yc = k.pool(lambda e, i: e.tensor_copy(ys[:, :], y[:, bass.ts(i, R4)]), f_ys.free)
        for s in range(4):
            t = k.pe(lambda e, i, s=s: e.transpose(bank[1][:, s * P:(s + 1) * P], pk[:, s * P:(s + 1) * P], env.ident[:, :]),
                     a, f_bank[1].free)
        f_pk.read_by(t, pc)
        c = k.act(lambda e, i: e.copy(pick_tok[:, :], bank[1][:, :]), t, f_pt.free)
        f_bank[1].read_by(c)
        for s in range(4):
            for b in range(BPT):
                lo = b * SEQ
                mm = k.pe(lambda e, i, s=s, b=b, lo=lo: e.matmul(
                    bank[2 + b][:, s * P:(s + 1) * P], ys[lo:lo + SEQ, s * P:(s + 1) * P], pick_tok[lo:lo + SEQ, s * P:(s + 1) * P],
                    start=True, stop=True), c, yc, f_bank[2 + b].free)
        f_pt.read_by(mm)
        f_ys.read_by(mm)
        for b in range(BPT):
            eng = (k.dve, k.act)[b % 2]
            for s in range(4):
                op = eng(lambda e, i, b=b, s=s: (e.copy if b % 2 else e.tensor_copy)(
                    G3[:, :, bass.ds(16 * i + 4 * s + b, 1)].rearrange("p x a -> p (x a)"), bank[2 + b][:, s * P:(s + 1) * P]), mm)
            f_bank[2 + b].read_by(op)
        k.barrier()
        ND = 2
        dd = lambda n, s: [sb(n, s) for _ in range(ND)]
        W1, W2, W2T, Gs, inner = dd("W1", [P, P]), dd("W2", [P, P]), dd("W2T", [P, P]), dd("Gs", [P, 256]), dd("inner", [P, 256])
        for t in inner:
            k.dve(lambda e, i, t=t: e.memset(t[:, :], 0.0))
        mk = lambda: [Buffer() for _ in range(ND)]
        f_W1, f_W2, f_W2T, f_Gs, f_in = (mk() for _ in range(5))
        f_bank = [Buffer() for _ in range(8)]
        k.barrier()
        k.loop(E // ND)
        for d in range(ND):
            xp = lambda i, d=d: bass.ds(ND * i + d, 1)
            l1 = k.dma(f"kv{d}", lambda e, i, d=d, xp=xp: e.dma_start(
                W1[d][:, :].rearrange("p (s f) -> p s f", s=SETS), w["W1"][xp(i)].rearrange("a s d f -> d (a s) f")), f_W1[d].free)
            l2 = k.dma(f"kv{d}", lambda e, i, d=d, xp=xp: e.dma_start(
                W2[d][:, :].rearrange("p (s f) -> p s f", s=SETS), w["W2"][xp(i)].rearrange("a s d f -> d (a s) f")), f_W2[d].free)
            gc = k.pool(lambda e, i, d=d: e.tensor_copy(Gs[d][:, :], G[:, bass.ts(ND * i + d, 256)]), f_Gs[d].free)
            t = k.pe(lambda e, i, d=d: e.transpose(bank[d][:, 0:P], W2[d][:, :], env.ident[:, :]), l2, f_bank[d].free)
            f_W2[d].read_by(t)
            wc = k.dve(lambda e, i, d=d: e.tensor_copy(W2T[d][:, :], bank[d][:, 0:P]), t, f_W2T[d].free)
            f_bank[d].read_by(wc)
            for s in range(SETS):
                mm = k.pe(lambda e, i, d=d, s=s: e.matmul(
                    bank[2 + d][32 * s:32 * s + 32, 0:BATCH], W1[d][:, s * F:(s + 1) * F], Gs[d][:, s * BATCH:(s + 1) * BATCH],
                    start=True, stop=True, tile_position=(0, 32 * s)), gc, f_bank[2 + d].free)
            f_W1[d].read_by(mm)
            f_Gs[d].read_by(mm)
            for s in range(SETS):
                ra = k.act(lambda e, i, d=d, s=s: e.activation(
                    inner[d][32 * s:32 * s + 32, s * BATCH:(s + 1) * BATCH], bank[2 + d][32 * s:32 * s + 32, 0:BATCH], ACT.Relu,
                    bias=b1[32 * s:32 * s + 32, bass.ds(ND * i + d, 1)]), mm, f_in[d].free)
            f_bank[2 + d].read_by(ra)
            mm = k.pe(lambda e, i, d=d: e.matmul(bank[4 + d][:, 0:256], W2T[d][:, :], inner[d][:, :], start=True, stop=True),
                      ra, wc, f_bank[4 + d].free)
            f_W2T[d].read_by(mm)
            f_in[d].read_by(mm)
            f_bank[4 + d].read_by(k.dve(lambda e, i, d=d: e.tensor_copy(G[:, bass.ts(ND * i + d, 256)], bank[4 + d][:, 0:256]), mm, gc))
        k.barrier()
        Rb, rb, pt = dd("Rb", [P, 512]), dd("rb", [P, 512]), dd("pt", [P, P])
        f_Rb, f_rb, f_pt = (mk() for _ in range(3))
        f_bank = [Buffer() for _ in range(8)]
        k.loop(NT // ND)
        for d in range(ND):
            cps = [k.pool(lambda e, i, d=d: e.tensor_copy(pt[d][:, :], pick[:, bass.ts(ND * i + d, P)]), f_pt[d].free)]
            for b in range(BPT):
                cps.append((k.pool, k.dve)[b % 2](lambda e, i, d=d, b=b: e.tensor_copy(
                    Rb[d][:, b * P:(b + 1) * P], G3[:, :, bass.ds(4 * (ND * i + d) + b, 1)].rearrange("p x a -> p (x a)")), f_Rb[d].free))
            for b in range(BPT):
                t = k.pe(lambda e, i, d=d, b=b: e.transpose(bank[d][:, b * P:(b + 1) * P], Rb[d][:, b * P:(b + 1) * P], env.ident[:, :]),
                         cps, f_bank[d].free)
            f_Rb[d].read_by(t)
            a = k.dve(lambda e, i, d=d: e.tensor_tensor(
                rb[d][:, :].rearrange("p (b d) -> p b d", b=4), bank[d][:, :].rearrange("p (b d) -> p b d", b=4),
                b2[:, :].unsqueeze(1).to_broadcast([P, 4, P]), ALU.add), t, f_rb[d].free)
            f_bank[d].read_by(a)
            for b in range(BPT):
                mm = k.pe(lambda e, i, d=d, b=b: e.matmul(
                    bank[2 + d][b * SEQ:(b + 1) * SEQ, 0:P], pt[d][:, b * SEQ:(b + 1) * SEQ], rb[d][:, b * P:(b + 1) * P],
                    start=True, stop=True, tile_position=(0, b * SEQ)), a, f_bank[2 + d].free)
            f_rb[d].read_by(mm)
            f_pt[d].read_by(mm)
            f_bank[2 + d].read_by(k.dve(lambda e, i, d=d: e.tensor_tensor(
                env.X[:, bass.ts(ND * i + d, P)], env.X[:, bass.ts(ND * i + d, P)], bank[2 + d][:, 0:P], ALU.add), mm))
        k.barrier()


def tie_table():
    return {"tie": np.linspace(0.0, 1e-6, SEQ, dtype=np.float32)}


def l3_ffn(env, w, out):
    k, nc, bank = env.k, env.k.nc, env.bank
    E, F = 8, 256
    HID = E * P
    ex_dram = nc.dram_tensor("x_scratch", (NTOK, P), F32, kind="Internal").ap()
    pos = lambda c: (c % 4) * 2 + c // 4
    k.barrier()
    k.straight()
    a = k.dma("turn", lambda e, i: e.dma_start(ex_dram.rearrange("(t p) d -> p t d", p=P),
                                               env.X[:, :].rearrange("p (t d) -> p t d", d=P)))
    by_time = lambda dram: [dram.rearrange("(b j t) d -> t b j d", b=BATCH, t=2)[t] for t in range(2)]
    tiles = lambda t: env.X[t * BATCH:(t + 1) * BATCH, :].rearrange("b (j d) -> b j d", d=P)
    for t in range(2):
        k.dma("turn", lambda e, i, t=t: e.dma_start(tiles(t), by_time(ex_dram)[t]), a)
    norm_tiles(env)
    with ExitStack() as outer:
        slots = SEQ + 1
        s_num, s_expr, s_state = (k.sb(outer, n, [P, slots * 4]) for n in ("s_num", "s_expr", "s_state"))
        gram = k.sb(outer, "gram", [P, slots * 4 * E])
        same = k.sb(outer, "same_token", [P, P])
        same_expert = k.sb(outer, "same_expert", [P, E])
        a = k.pool(lambda e, i: e.memset(same[:, :], 1.0))
        s3 = same[:, :].rearrange("p (b e) -> p b e", e=E)
        a = k.pool(lambda e, i: e.affine_select(out=s3, in_=s3, compare_op=ALU.is_ge, fill=0.0, base=0,
                                                pattern=[[-E, 16], [0, E]], channel_multiplier=1), a)
        a = k.pool(lambda e, i: e.affine_select(out=s3, in_=s3, compare_op=ALU.is_ge, fill=0.0, base=E - 1,
                                                pattern=[[E, 16], [0, E]], channel_multiplier=-1), a)
        k.dve(lambda e, i: e.tensor_reduce(same_expert[:, :], env.ident[:, :].rearrange("p (b e) -> p e b", e=E), AX.X, ALU.add))
        with ExitStack() as st:
            sb = lambda name, shape, dt=F32: k.sb(st, name, shape, dt)
            WhhT = sb("WhhT", [P, E * 3 * HID])
            W3 = WhhT[:, :].rearrange("p (c g) -> p c g", c=E)
            WihT = sb("WihT", [P, 3 * HID])
            ctxT = sb("ctxT", [P, HID])
            ctx_b = sb("ctx_b", [P, E])
            raw = [sb("raw", [P, HID]) for _ in range(2)]
            rawi = [sb("rawi", [P, P]) for _ in range(2)]
            k.straight()
            k.dma("w", lambda e, i: e.dma_start(ctx_b[:, :], w["ctx_b"].rearrange("(c p) -> p c", p=P)))
            f_raw, f_rawi = [Buffer(), Buffer()], [Buffer(), Buffer()]
            f_bank = [Buffer() for _ in range(8)]
            k.loop(3 * E // 2)
            for d in range(2):
                q = lambda i, d=d: 2 * i + d
                l = k.dma(f"kv{d}", lambda e, i, d=d, q=q: e.dma_start(raw[d][:, :], w["gru_w_hh"][bass.ts(q(i), P), :]), f_raw[d].free)
                l = k.dma(f"kv{d}", lambda e, i, d=d, q=q: e.dma_start(rawi[d][:, :], w["gru_w_ih"][bass.ts(q(i), P), :]), f_rawi[d].free)
                for half in range(2):
                    b = 2 * d + half
                    for r in range(4):
                        t = k.pe(lambda e, i, d=d, b=b, r=r, half=half: e.transpose(
                            bank[b][:, r * P:(r + 1) * P], raw[d][:, (4 * half + r) * P:(4 * half + r + 1) * P], env.ident[:, :]),
                            l, f_bank[b].free)
                    eng, op = ((k.dve, "dve"), (k.act, "act"))[half]
                    c = eng(lambda e, i, b=b, half=half, q=q, op=op: (e.tensor_copy if op == "dve" else e.copy)(
                        W3[:, 4 * half:4 * half + 4, bass.ts(q(i), P)], bank[b][:, :].rearrange("p (c g) -> p c g", c=4)), t)
                    f_bank[b].read_by(c)
                f_raw[d].read_by(t)
                t = k.pe(lambda e, i, d=d: e.transpose(bank[4 + d][:, 0:P], rawi[d][:, :], env.ident[:, :]), f_bank[4 + d].free)
                f_rawi[d].read_by(t)
                f_bank[4 + d].read_by(k.dve(lambda e, i, d=d, q=q: e.tensor_copy(WihT[:, bass.ts(q(i), P)], bank[4 + d][:, 0:P]), t))
            k.barrier()
            HALF = HID // 2
            k.straight()
            l = k.dma("w0", lambda e, i: e.dma_start(raw[0][:, :].rearrange("p (c h) -> p c h", c=E),
                                                    w["ctx_w"].rearrange("(c p) h -> p c h", p=P)))
            hb = sb("hb", [P, HALF])
            hT = sb("hT", [P, HID * BATCH // P])
            b0 = sb("b0", [P, HALF])
            for hf in range(2):
                lb = k.dma("w1", lambda e, i, hf=hf: e.dma_start(
                    b0[hf * BATCH:(hf + 1) * BATCH, :], w["ctx_b"][hf * HALF:(hf + 1) * HALF].partition_broadcast(BATCH)))
            done = transpose_blocks(env, raw[0], ctxT, E, l)
            mean = sb("mean", [P, BATCH])
            m = k.dve(lambda e, i: e.tensor_reduce(mean[:, :], env.yT[:, :].rearrange("p (t b) -> p b t", b=BATCH), AX.X, ALU.add))
            m = k.dve(lambda e, i: e.tensor_scalar(mean[:, :], mean[:, :], 1.0 / SEQ, None, ALU.mult), m)
            for hf in range(2):
                mm = k.pe(lambda e, i, hf=hf: e.matmul(bank[5][hf * BATCH:(hf + 1) * BATCH, :], mean[:, :], ctxT[:, hf * HALF:(hf + 1) * HALF],
                                                       start=True, stop=True, tile_position=(0, hf * BATCH)), m, done)
            k.dve(lambda e, i: e.tensor_tensor(hb[:, :], bank[5][:, :], b0[:, :], ALU.add), mm, lb)
            r_, z_, n_, d_, t_ = (sb(nm, [P, HALF]) for nm in ("r", "z", "n", "d", "t"))
            xt = sb("xt", [P, BATCH])
            R, HN, XN, ZA, ZB, TA, TB, GR = range(8)
            f = {nm: Buffer() for nm in ("r", "z", "n", "d", "t", "xt", "xp", "hT", "rb", "dv", "pr", "sq")}
            made = [Buffer(), Buffer()]
            f_bank = [Buffer() for _ in range(8)]
            Q = HALF // 2
            exprT = sb("exprT", [P, HID])
            xp = sb("xp", [P, BATCH])
            rb, dv, pr, sq = (sb(nm, [P, HALF]) for nm in ("rb", "dv", "pr", "sq"))
            l = k.dma("w2", lambda e, i: e.dma_start(raw[1][:, :].rearrange("p (c h) -> p c h", c=E),
                                                    w["expr_w"].rearrange("(c p) h -> p c h", p=P)))
            transpose_blocks(env, raw[1], exprT, E, l)
            k.dve(lambda e, i: e.memset(xt[:, :], 0.0))
            four = lambda t: t[:, :].rearrange("p (c d) -> p c d", c=4)

            def routing_work(made, EX, GR, turned, f_bank, tt):
                done = []
                pc = k.pool(lambda e, i: e.tensor_copy(rb[:, :].rearrange("p (b q) -> p q b", q=E),
                                                       hT[:, :].rearrange("p (q b) -> p q b", q=E)), turned, f["rb"].free, alone=True)
                for hf in range(2):
                    mx = k.pe(lambda e, i, hf=hf: e.matmul(bank[EX][hf * BATCH:(hf + 1) * BATCH, :], xp[:, :], exprT[:, hf * HALF:(hf + 1) * HALF],
                                                           start=True, stop=True, tile_position=(0, hf * BATCH)), xo, turned)
                f["xp"].read_by(mx)
                for g in range(4):
                    mg = k.pe(lambda e, i, g=g: e.matmul(bank[GR][:, g * P:(g + 1) * P], rb[:, g * P:(g + 1) * P], rb[:, g * P:(g + 1) * P],
                                                         start=True, stop=True), pc, f_bank[GR].free)
                f["rb"].read_by(mg)
                a = k.dve(lambda e, i: e.tensor_tensor(pr[:, :], hb[:, :], bank[EX][:, :], ALU.mult), mx, f["pr"].free, [b.free for b in made])
                done.append(a)
                b = k.act(lambda e, i: e.activation(sq[:, :], bank[EX][:, :], ACT.Square), a, f["sq"].free)
                f_bank[EX].read_by(b)
                f["pr"].read_by(k.dve(lambda e, i: e.tensor_reduce(s_num[:, bass.ts(i, 4)], four(pr), AX.X, ALU.add), a))
                b = k.dve(lambda e, i: e.tensor_reduce(s_expr[:, bass.ts(i, 4)], four(sq), AX.X, ALU.add), b)
                b = k.act(lambda e, i: e.activation(sq[:, :], hb[:, :], ACT.Square), b)
                done.append(b)
                f["sq"].read_by(k.dve(lambda e, i: e.tensor_reduce(s_state[:, bass.ts(i, 4)], four(sq), AX.X, ALU.add), b))
                a = k.dve(lambda e, i: e.tensor_tensor(four(dv), four(bank[GR]), same[:, :].unsqueeze(1).to_broadcast([P, 4, P]), ALU.mult),
                          mg, f["dv"].free)
                f_bank[GR].read_by(a)
                f["dv"].read_by(k.dve(lambda e, i: e.tensor_reduce(
                    gram[:, bass.ts(i, 4 * E)].rearrange("p (g f) -> p g f", g=4),
                    dv[:, :].rearrange("p (g b f) -> p g f b", g=4, f=E), AX.X, ALU.add), a))
                return done

            k.barrier()
            k.loop(SEQ)
            xo = k.pool(lambda e, i: e.tensor_copy(xp[:, :], xt[:, :]), f["xt"].free, f["xp"].free, alone=True)
            xc = k.pool(lambda e, i: e.tensor_copy(xt[:, :], env.yT[:, bass.ts(i, BATCH)]), f["xt"].free, xo, alone=True)

            def product(b, gate, kc, cols, start, stop, *waits):
                for hf in range(2):
                    lhs = xt[:, :] if kc is None else hT[:, pos(kc) * BATCH:(pos(kc) + 1) * BATCH]
                    g = gate * HID + hf * HALF
                    rhs = (WihT[:, g + cols.start:g + cols.stop] if kc is None else W3[:, kc, g + cols.start:g + cols.stop])
                    mm = k.pe(lambda e, i, hf=hf, lhs=lhs, rhs=rhs, n=cols.stop - cols.start: e.matmul(
                        bank[b][hf * BATCH:(hf + 1) * BATCH, 0:n], lhs, rhs, start=start, stop=stop, tile_position=(0, hf * BATCH)),
                        *waits)
                return mm

            every, cA, cB = slice(0, HALF), slice(0, Q), slice(Q, HALF)
            xm = product(XN, 2, None, every, True, True, xc, f_bank[XN].free)
            product(R, 0, None, every, True, False, f_bank[R].free)
            product(ZA, 1, None, cA, True, False, f_bank[ZA].free)
            xl = product(ZB, 1, None, cB, True, False, f_bank[ZB].free)
            f["xt"].read_by(xl)
            turned = []
            for half, (b, order) in enumerate(((TA, (0, 4, 1, 5)), (TB, (2, 6, 3, 7)))):
                for c in range(2):
                    tt = k.pe(lambda e, i, b=b, c=c, half=half: e.transpose(
                        bank[b][:, c * P:(c + 1) * P], hb[:, half * Q + c * P:half * Q + (c + 1) * P], env.ident[:, :]),
                        made[half].free, f_bank[b].free)
                ev = k.act(lambda e, i, b=b, half=half: e.copy(hT[:, half * Q:(half + 1) * Q], bank[b][:, 0:Q]), tt,
                           f["hT"].free)
                f_bank[b].read_by(ev)
                turned.append(ev)
                for kc in order:
                    rm = product(R, 0, kc, every, False, kc == 7, ev)
            hb_read = routing_work(made, TA, GR, turned, f_bank, tt)
            for kc in range(E):
                hm = product(HN, 2, kc, every, kc == 0, kc == 7, f_bank[HN].free)
            for kc in range(E):
                zA = product(ZA, 1, kc, cA, False, kc == 7)
            for kc in range(E):
                zB = product(ZB, 1, kc, cB, False, kc == 7)
            f["hT"].read_by(zB)
            a = k.act(lambda e, i: e.activation(r_[:, :], bank[R][:, :], ACT.Tanh, scale=0.5), rm, f["r"].free)
            f_bank[R].read_by(a)
            a = k.dve(lambda e, i: e.scalar_tensor_tensor(t_[:, :], r_[:, :], 1.0, bank[HN][:, :], ALU.add, ALU.mult), a, hm, f["t"].free)
            f_bank[HN].read_by(a)
            f["r"].read_by(a)
            a = k.dve(lambda e, i: e.scalar_tensor_tensor(t_[:, :], t_[:, :], 0.5, bank[XN][:, :], ALU.mult, ALU.add), a, xm)
            f_bank[XN].read_by(a)
            nn = k.act(lambda e, i: e.activation(n_[:, :], t_[:, :], ACT.Tanh), a, f["n"].free)
            f["t"].read_by(nn)
            dd = k.dve(lambda e, i: e.tensor_tensor(d_[:, :], hb[:, :], n_[:, :], ALU.subtract), nn, f["d"].free,
                       [b.free for b in made])
            for half, (b, zm, s) in enumerate(((ZA, zA, cA), (ZB, zB, cB))):
                a = k.act(lambda e, i, s=s, b=b: e.activation(z_[:, s], bank[b][:, 0:Q], ACT.Tanh, scale=0.5), zm, f["z"].free)
                f_bank[b].read_by(a)
                a = k.dve(lambda e, i, s=s: e.scalar_tensor_tensor(d_[:, s], z_[:, s], 1.0, d_[:, s], ALU.add, ALU.mult), a, dd)
                a = k.dve(lambda e, i, s=s: e.scalar_tensor_tensor(hb[:, s], d_[:, s], 0.5, n_[:, s], ALU.mult, ALU.add), a, tt, hb_read)
                made[half].read_by(a)
            for nm in ("z", "n", "d"):
                f[nm].read_by(a)
            k.barrier()
            k.loop(1)
            k.seg.first = SEQ
            for c in range(4):
                tt = k.pe(lambda e, i, c=c: e.transpose(bank[TB][:, c * P:(c + 1) * P], hb[:, c * P:(c + 1) * P], env.ident[:, :]))
            ev = k.act(lambda e, i: e.copy(hT[:, :], bank[TB][:, :]), tt)
            xo = k.pool(lambda e, i: e.tensor_copy(xp[:, :], xt[:, :]))
            f = {nm: Buffer() for nm in f}
            routing_work([Buffer(), Buffer()], TA, GR, [ev], [Buffer() for _ in range(8)], tt)
            k.barrier()
        with ExitStack() as st:
            sb = lambda name, shape, dt=F32: k.sb(st, name, shape, dt)
            k.straight()
            NE = NT * E
            NG = SEQ * 4
            nm = {n: sb(n, [P, NE]) for n in ("num", "den", "tmp", "cos", "key", "pick", "one", "order", "expr2", "state2")}
            sm = {n: sb(n, [P, NT]) for n in ("top", "first", "second")}
            pen = {n: sb(n, [P, NG]) for n in ("inv", "dev2", "pb")}
            gw = {n: sb(n, [P, NG * E]) for n in ("own", "norm")}
            one = sb("pen1", [P, 1])
            A = {n: t[:, :] for n, t in {**nm, **sm, **pen, **gw, "pen1": one}.items()}
            G = gram[:, 4 * E:].rearrange("p (m f) -> p m f", f=E)
            gx = lambda n: A[n].rearrange("p (m f) -> p m f", f=E)
            expert = same_expert[:, :].unsqueeze(1).to_broadcast([P, NG, E])
            by_row = lambda n: A[n].unsqueeze(2).to_broadcast([P, NG, E])
            te = lambda n: A[n].rearrange("p (t e) -> p t e", e=E)
            col = lambda n: A[n].unsqueeze(2).to_broadcast([P, NT, E])
            last = []

            def step(eng, fn):
                last[:] = [eng(fn, last)]

            TS = lambda o, a, s1, s2, p1, p2=None: step(k.dve, lambda e, i: (
                e.tensor_scalar(A[o], A[a], s1, s2, p1, p2) if p2 is not None else e.tensor_scalar(A[o], A[a], s1, s2, p1)))
            TT = lambda o, a, b, p: step(k.dve, lambda e, i: e.tensor_tensor(A[o], A[a], A[b], p))
            TC = lambda o, a, c, p: step(k.dve, lambda e, i: e.tensor_tensor(te(o), te(a), col(c), p))
            RD = lambda o, a, p: step(k.dve, lambda e, i: e.tensor_reduce(A[o], te(a), AX.X, p))
            RC = lambda o: step(k.dve, lambda e, i: e.reciprocal(A[o], A[o]))
            AC = lambda o, a, fn, scale=1.0: step(k.act, lambda e, i: e.activation(A[o], A[a], fn, scale=scale))
            step(k.dve, lambda e, i: e.tensor_tensor(gx("own"), G, expert, ALU.mult))
            step(k.dve, lambda e, i: e.tensor_reduce(A["inv"], gx("own"), AX.X, ALU.add))
            AC("inv", "inv", ACT.Sqrt)
            TS("inv", "inv", 1e-12, None, ALU.max)
            RC("inv")
            step(k.dve, lambda e, i: e.tensor_tensor(gx("own"), by_row("inv"), expert, ALU.mult))
            step(k.dve, lambda e, i: e.tensor_tensor(gx("norm"), G, by_row("inv"), ALU.mult))
            for n in range(2):
                s = slice(n * 512, (n + 1) * 512)
                step(k.pe, lambda e, i, s=s, n=n: e.matmul(bank[n][:, :], same[:, :], A["own"][:, s], start=True, stop=True))
                step(k.dve, lambda e, i, s=s, n=n: e.tensor_tensor(A["norm"][:, s], A["norm"][:, s], bank[n][:, :], ALU.mult))
            step(k.dve, lambda e, i: e.tensor_tensor(gx("norm"), gx("norm"), expert, ALU.subtract))
            AC("norm", "norm", ACT.Square)
            step(k.dve, lambda e, i: e.tensor_reduce(A["dev2"], gx("norm"), AX.X, ALU.add))
            AC("inv", "dev2", ACT.Sqrt)
            TS("inv", "inv", 1e-12, None, ALU.max)
            RC("inv")
            TT("pb", "inv", "inv", ALU.mult)
            TT("pb", "pb", "dev2", ALU.mult)
            step(k.dve, lambda e, i: e.tensor_reduce(A["pen1"], A["pb"], AX.X, ALU.add))
            step(k.pe, lambda e, i: e.matmul(bank[0][:, 0:1], env.ones[:, :], one[:, :], start=True, stop=True))
            step(k.dve, lambda e, i: e.tensor_scalar(one[:, :], bank[0][:, 0:1], 1.0 / NTOK, 1.0, ALU.mult, ALU.add))
            for name, src in (("num", s_num), ("expr2", s_expr), ("state2", s_state)):
                for t in range(2):
                    for hf in range(2):
                        step(k.dve, lambda e, i, name=name, src=src, t=t, hf=hf: e.tensor_copy(
                            te(name)[t * BATCH:(t + 1) * BATCH, :, hf * 4:hf * 4 + 4],
                            src[hf * BATCH:(hf + 1) * BATCH, 4:].rearrange("p (j t c) -> p t j c", t=2, c=4)[:, t]))
            AC("one", "state2", ACT.Sqrt)
            TS("one", "one", 1e-12, None, ALU.max)
            RC("one")
            TT("num", "num", "one", ALU.mult)
            TT("state2", "state2", "one", ALU.mult)
            TT("state2", "state2", "one", ALU.mult)
            for src, dst in (("expr2", "den"), ("state2", "tmp")):
                AC(dst, src, ACT.Sqrt)
                TS(dst, dst, 1e-8, None, ALU.max)
            TT("den", "den", "tmp", ALU.mult)
            RC("den")
            TT("cos", "num", "den", ALU.mult)
            TS("cos", "cos", -1.0, 1.0, ALU.mult, ALU.add)
            step(k.dve, lambda e, i: e.tensor_scalar(A["cos"], A["cos"], one[:, 0:1], None, ALU.mult))
            for n in range(E):
                step(k.dve, lambda e, i, n=n: e.memset(te("order")[:, :, n], float(E - n)))
            for n, name in enumerate(("first", "second")):
                RD(name, "cos", ALU.max)
                TC("key", "cos", name, ALU.is_equal)
                TT("key", "key", "order", ALU.mult)
                RD("top", "key", ALU.max)
                TC("key" if n else "pick", "key", "top", ALU.is_equal)
                if n == 0:
                    TS("tmp", "pick", -3.0e38, None, ALU.mult)
                    TT("cos", "cos", "tmp", ALU.add)
            TT("second", "second", "first", ALU.subtract)
            AC("second", "second", ACT.Exp)
            TC("key", "key", "second", ALU.mult)
            TT("pick", "pick", "key", ALU.add)
            TS("second", "second", 1.0, None, ALU.add)
            RC("second")
            TC("pick", "pick", "second", ALU.mult)
            share = nm["pick"]
            NX = E + 1
            up, gate_, down = (sb(n, [P, NX * F]) for n in ("upT", "gateT", "downT"))
            rawg, rawu, rawd = (sb(n, [P, NX * F]) for n in ("rawg", "rawu", "rawd"))
            for t, a, b in ((rawg, "gate_w", "shared_gate_w"), (rawu, "up_w", "shared_up_w")):
                v = t[:, :].rearrange("p (c h) -> p c h", h=P)
                k.dma("w", lambda e, i, v=v, a=a: e.dma_start(v[:, 0:2 * E], w[a].rearrange("x (c p) h -> p (x c) h", p=P)))
                k.dma("w", lambda e, i, v=v, b=b: e.dma_start(v[:, 2 * E:2 * NX], w[b].rearrange("(c p) h -> p c h", p=P)))
            k.dma("w", lambda e, i: e.dma_start(rawd[:, 0:E * F].rearrange("p (x f) -> p x f", f=F), w["down_w"].rearrange("x p f -> p x f")))
            l = k.dma("w", lambda e, i: e.dma_start(rawd[:, E * F:NX * F], w["shared_down_w"]))
            for src, dst in ((rawg, gate_), (rawu, up), (rawd, down)):
                transpose_blocks(env, src, dst, 2 * NX, [l, last])
            hs = [[sb("h", [P, R4]) for _ in range(2)] for _ in range(2)]
            wt = sb("wt", [P, 4 * E])
            f_h, f_bank, f_wt = [Buffer(), Buffer()], [Buffer() for _ in range(8)], Buffer()
            k.barrier()
            k.loop(NT // 4)
            wc = k.dve(lambda e, i: e.tensor_copy(wt[:, :], share[:, bass.ts(i, 4 * E)]), f_wt.free)
            ad = None
            for x in range(NX):
                z = x % 2
                ms = []
                for c in range(2):
                    o = (2 * x + c) * P
                    g = k.pe(lambda e, i, c=c, o=o: e.matmul(bank[c][:, :], gate_[:, o:o + P], env.yT[:, bass.ts(i, R4)],
                                                             start=True, stop=True), f_bank[c].free)
                    u = k.pe(lambda e, i, c=c, o=o: e.matmul(bank[2 + c][:, :], up[:, o:o + P], env.yT[:, bass.ts(i, R4)],
                                                             start=True, stop=True), f_bank[2 + c].free)
                    a = k.act(lambda e, i, c=c, z=z: e.activation(hs[z][c][:, :], bank[c][:, :], ACT.Silu), g, f_h[z].free)
                    f_bank[c].read_by(a)
                    m = k.dve(lambda e, i, c=c, z=z: e.tensor_tensor(hs[z][c][:, :], hs[z][c][:, :], bank[2 + c][:, :], ALU.mult), a, u)
                    f_bank[2 + c].read_by(m)
                    ms.append(m)
                for s in range(4):
                    for c in range(2):
                        o = (2 * x + c) * P
                        mm = k.pe(lambda e, i, c=c, o=o, z=z, s=s: e.matmul(
                            bank[4 + z][:, s * P:(s + 1) * P], hs[z][c][:, s * P:(s + 1) * P], down[:, o:o + P],
                            start=c == 0, stop=c == 1), ms, f_bank[4 + z].free)
                f_h[z].read_by(mm)
                if x < E:
                    prior = ad
                    for s in range(4):
                        ad = k.dve(lambda e, i, x=x, z=z, s=s: e.scalar_tensor_tensor(
                            env.X[:, bass.ts(4 * i + s, P)], bank[4 + z][:, s * P:(s + 1) * P], wt[:, s * E + x:s * E + x + 1],
                            env.X[:, bass.ts(4 * i + s, P)], ALU.mult, ALU.add), mm, wc, prior)
                else:
                    f_wt.read_by(ad)
                    ad = k.dve(lambda e, i, z=z: e.tensor_tensor(env.X[:, bass.ts(i, R4)], env.X[:, bass.ts(i, R4)], bank[4 + z][:, :], ALU.add), mm, ad)
                f_bank[4 + z].read_by(ad)
            k.barrier()
            k.straight()
            for t in range(2):
                k.dma("out", lambda e, i, t=t: e.dma_start(by_time(out)[t], tiles(t)))




def perceiver(nc, a, out):
    with ExitStack() as ctx:
        ctx.enter_context(nc.allow_non_contiguous_dma(reason="bias columns and head-major weights are small"))
        k = Queues(nc, ctx)
        k.straight()
        env = Env(k, ctx)
        env.constants()
        load_x(env, a["x"].rearrange("b t d -> (b t) d"))

        def of(prefix):
            return {name[len(prefix) + 1:]: v for name, v in a.items() if name.startswith(prefix + "_")}

        kv = a["ctx_1024"]
        w = of("L0_xattn")
        norm_tiles(env)
        softmax_cross_attention(env, kv, 64, w["W_Q"], w["W_K"], w["W_V"], w["W_out"], 64 ** -0.5,
                                w["b_Q"], w["b_K"], w["b_V"], w["b_out"], a["mask_BxSxS2_bk1"], True, -10000.0)
        l0_attention(env, of("L0_attn"))
        l0_ffn(env, of("L0_ffn"))
        w = of("L1_xattn")
        norm_tiles(env)
        softmax_cross_attention(env, kv, 8, w["Wq"], w["Wk"], w["Wv"], w["Wo"], 8 ** -0.5,
                                w["bq"], w["bk"], w["bv"], w["bo"],
                                a["mask_Bx1xSxS2_bf1"].rearrange("b a q s -> (b a) q s"), False, -1.0e9)
        l1_attention(env, of("L1_attn"))
        l1_ffn(env, of("L1_ffn"))
        l2_cross_attention(env, of("L2_xattn"), kv)
        l2_attention(env, of("L2_attn"), a)
        l2_ffn(env, of("L2_ffn"), a)
        w = of("L3_xattn")
        norm_tiles(env)
        softmax_cross_attention(env, kv, 8, w["Wq"], w["Wk"], w["Wv"], w["Wp"], 8 ** -0.5, bo=w["bp"], shared=True)
        l3_attention(env, of("L3_attn"))
        l3_ffn(env, of("L3_ffn"), out.rearrange("b t d -> (b t) d"))
        k.finish()


def kernel(**inputs):
    import concourse.bacc as bacc
    from concourse.bass_utils import run_bass_kernel_spmd

    nc = bacc.Bacc("TRN2", target_bir_lowering=False, num_devices=1)
    arrays, args = {}, {}
    for name, v in {**inputs, **l2_tables(), **tie_table()}.items():
        v = np.ascontiguousarray(v)
        if v.ndim == 0:
            v = v.reshape(1)
        arrays["in_" + name] = v
        args[name] = nc.dram_tensor("in_" + name, v.shape, mybir.dt.from_np(v.dtype), kind="ExternalInput").ap()
    out = nc.dram_tensor("out_0", (BATCH, SEQ, P), F32, kind="ExternalOutput").ap()
    perceiver(nc, args, out)
    r = run_bass_kernel_spmd(nc, [arrays], core_ids=[0])
    return r.results[0]["out_0"]
```

```python
from contextlib import ExitStack
import numpy as np
import concourse.bass as bass
from concourse import mybir

F32 = mybir.dt.float32
U8 = mybir.dt.uint8
ALU = mybir.AluOpType
ACT = mybir.ActivationFunctionType
AX = mybir.AxisListType

P = 128
BATCH = 64
SEQ = 32
CTX = 257
NTOK = BATCH * SEQ
NT = NTOK // P
BPT = P // SEQ
H = 16


class Token:

    def __init__(self, seg, sem, unit):
        self.seg, self.sem, self.unit, self.used, self.order = seg, sem, unit, False, None

    def value(self, i):
        return self.seg.base[self.sem] + i * self.seg.per.get(self.sem, 0) + self.order


class Prev:

    def __init__(self, token):
        self.token = token


class Buffer:

    def __init__(self, *readers):
        self.readers, self.by_segment = list(readers), {}

    def read_by(self, *tokens):
        self.readers = [t for t in tokens if t is not None]
        self.by_segment[self.readers[0].seg] = self.readers
        return tokens[0]

    @property
    def free(self):
        return Free(self, self.readers)

    made_by = read_by
    made = free


class Free:
    def __init__(self, buffer, readers):
        self.buffer, self.readers = buffer, readers

    def tokens(self, seg):
        if any(t.seg is seg for t in self.readers):
            return self.readers
        again = self.buffer.by_segment.get(seg, []) if seg.rounds > 1 else []
        return self.readers + [Prev(t) for t in again]


class Segment:
    def __init__(self, rounds):
        self.rounds, self.ops, self.per, self.base = rounds, {}, {}, {}
        self.first = 0


class Queues:

    ENGINES = ("pe", "act", "dve", "pool", "sp")

    def __init__(self, nc, ctx):
        self.nc, self.ctx = nc, ctx
        self.sems, self.segments, self.tokens = {}, [], []
        for e in self.ENGINES:
            self.sems[e] = ctx.enter_context(nc.semaphore("done_" + e))
        self.spare = ctx.enter_context(nc.semaphore("spare"))
        self.seg = None
        self.names = 0

    def sb(self, stack, name, shape, dt=F32):
        self.names += 1
        return stack.enter_context(self.nc.sbuf_tensor(f"{name}_{self.names}", shape, dt))

    def straight(self):
        self.seg = Segment(1)
        self.segments.append(self.seg)

    def loop(self, rounds):
        self.seg = Segment(rounds)
        self.segments.append(self.seg)

    def barrier(self):
        last = {}
        for seg in self.segments:
            for ops in seg.ops.values():
                for _, _, t in ops:
                    if t is not None:
                        last[t.sem] = t
        self.straight()
        for e in self.ENGINES:
            for sem, t in last.items():
                t.used = True
            self.seg.ops.setdefault(e, []).append((None, list(last.values()), None))

    def put(self, engine, fn, waits, sem=None, unit=1, alone=False):
        t = Token(self.seg, sem or engine, unit)
        t.alone = alone
        if unit == 16:
            t.used = True
        flat = self.flat(waits)
        self.seg.ops.setdefault(engine, []).append((fn, flat, t))
        return t

    def flat(self, waits):
        out = []
        for w in waits:
            out += self.flat(w) if isinstance(w, (list, tuple)) else [] if w is None else [w]
        return out

    def pe(self, fn, *w, alone=False):
        return self.put("pe", fn, w, alone=alone)

    def act(self, fn, *w, alone=False):
        return self.put("act", fn, w, alone=alone)

    def dve(self, fn, *w, alone=False):
        return self.put("dve", fn, w, alone=alone)

    def pool(self, fn, *w, alone=False):
        return self.put("pool", fn, w, alone=alone)

    def dma(self, sem, fn, *w, q="sp"):
        if sem not in self.sems:
            self.sems[sem] = self.ctx.enter_context(self.nc.semaphore("dma_" + sem))
        return self.put(q, fn, w, sem=sem, unit=16)

    def finish(self):
        for seg in self.segments:
            for ops in seg.ops.values():
                for n, (fn, waits, t) in enumerate(ops):
                    waits = [x for w in waits for x in (w.tokens(seg) if isinstance(w, Free) else [w])]
                    ops[n] = (fn, waits, t)
                    for w in waits:
                        (w.token if isinstance(w, Prev) else w).used = True
        total = {s: 0 for s in self.sems}
        for seg in self.segments:
            seg.base = dict(total)
            per = {}
            for ops in seg.ops.values():
                for _, _, t in ops:
                    if t is not None and t.used:
                        per[t.sem] = per.get(t.sem, 0) + t.unit
                        t.order = per[t.sem]
            seg.per = per
            for s, n in per.items():
                total[s] += n * seg.rounds
        lead = {s: max([seg.per.get(s, 0) for seg in self.segments]) for s in self.sems}
        owner = {}
        for seg in self.segments:
            for e, ops in seg.ops.items():
                for _, _, t in ops:
                    if t is not None and t.used:
                        owner.setdefault(t.sem, e)

        def emit(name, eng):
            for s in self.sems:
                if owner.get(s) == name and lead[s]:
                    eng.sem_inc(self.sems[s], lead[s])
            known = {}
            for seg in self.segments:
                ops = seg.ops.get(name, [])
                if not ops:
                    continue
                if seg.rounds == 1:
                    self.run(seg, ops, eng, seg.first, lead, known)
                    continue
                for _, waits, _ in ops:
                    for w in waits:
                        if not isinstance(w, Prev) and w.seg is not seg:
                            self.wait(eng, w.sem, lead[w.sem] + w.value(w.seg.rounds - 1), known)
                with eng.Fori(0, seg.rounds) as i:
                    self.run(seg, ops, eng, i, lead, None)
                known.clear()

        block = self.ctx.enter_context(self.nc.Block())

        @block.tensor
        def _(e):
            emit("pe", e)

        @block.scalar
        def _(e):
            emit("act", e)

        @block.vector
        def _(e):
            emit("dve", e)

        @block.gpsimd
        def _(e):
            emit("pool", e)

        @block.sync
        def _(e):
            emit("sp", e)
            for s in self.sems:
                if s not in self.ENGINES and total[s]:
                    e.wait_ge(self.sems[s], lead[s] + total[s])

    def wait(self, eng, sem, value, known):
        if known.get(sem, -1) < value:
            eng.wait_ge(self.sems[sem], value)
            known[sem] = value

    def run(self, seg, ops, eng, i, lead, known):
        inside = {}
        for fn, waits, t in ops:
            need, waited = {}, False
            for w in waits:
                if isinstance(w, Prev):
                    r = w.token.order - seg.per[w.token.sem]
                    need[w.token.sem] = max(need.get(w.token.sem, -1 << 30), r)
                elif w.seg is seg:
                    need[w.sem] = max(need.get(w.sem, -1 << 30), w.order)
                elif seg.rounds == 1:
                    self.wait(eng, w.sem, lead[w.sem] + w.value(w.seg.rounds - 1), known)
            for s, r in need.items():
                if inside.get(s, -1 << 30) < r:
                    inside[s] = r
                    v = lead[s] + seg.base[s] + r
                    if seg.rounds == 1:
                        self.wait(eng, s, v, known)
                    else:
                        eng.wait_ge(self.sems[s], v + i * seg.per[s])
                        waited = True
            if fn is None:
                continue
            if waited and t.alone:
                eng.sem_inc(self.spare, 1)
            ins = fn(eng, i)
            if t is not None and t.used:
                ins.then_inc(self.sems[t.sem], t.unit)


class Env:

    def __init__(self, k, ctx):
        nc = k.nc
        self.k, self.ctx = k, ctx
        self.X = k.sb(ctx, "X", [P, NT * P])
        self.yT = k.sb(ctx, "yT", [P, NTOK])
        self.ident = k.sb(ctx, "ident", [P, P])
        self.ones = k.sb(ctx, "ones", [P, P])
        self.rstd = k.sb(ctx, "rstd", [P, 8])
        self.stats = k.sb(ctx, "stats", [P, 8 * 6])
        self.moments = k.sb(ctx, "moments", [P, 8 * 2])
        self.ytile = k.sb(ctx, "ytile", [P, 8 * P])
        self.prep_banks = [Buffer() for _ in range(8)]
        self.bank = [ctx.enter_context(nc.psum_tensor(f"bank{n}", [P, 512], F32)) for n in range(8)]

    def constants(self):
        k = self.k
        a = k.pool(lambda e, i: e.memset(self.ident[:, :], 0.0))
        k.pool(lambda e, i: e.affine_select(out=self.ident[:, :], in_=self.ident[:, :], compare_op=ALU.not_equal,
                                            fill=1.0, base=0, pattern=[[-1, P]], channel_multiplier=1), a)
        k.dve(lambda e, i: e.memset(self.ones[:, :], 1.0))


def norm_tiles(env, y=None):
    k, X, mv, rstd = env.k, env.X, env.moments, env.rstd
    N = 8
    k.loop(NT // N)
    f_stats, f_mv, f_rstd = Buffer(), Buffer(), Buffer()
    f_tile, f_bank = [Buffer() for _ in range(N)], [Buffer(), Buffer()]
    for u in range(N):
        st = k.dve(lambda e, i, u=u: e.bn_stats(env.stats[:, 6 * u:6 * u + 6], X[:, bass.ts(N * i + u, P)]), f_stats.free)
    for u in range(N):
        ag = k.dve(lambda e, i, u=u: e.bn_aggr(mv[:, 2 * u:2 * u + 2], env.stats[:, 6 * u:6 * u + 6]), st, f_mv.free, alone=True)
    f_stats.read_by(ag)
    var = mv[:, :].rearrange("p (t two) -> p t two", two=2)[:, :, 1]
    a = k.dve(lambda e, i: e.tensor_scalar(rstd[:, :], var, 1e-5, None, ALU.add), ag, f_rstd.free)
    b = k.act(lambda e, i: e.activation(rstd[:, :], rstd[:, :], ACT.Sqrt), a)
    r = k.dve(lambda e, i: e.reciprocal(rstd[:, :], rstd[:, :]), b)
    for q in range(2):
        for v in range(4):
            u = 4 * q + v
            yt = env.ytile[:, u * P:(u + 1) * P]
            n = k.dve(lambda e, i, u=u, yt=yt: e.tensor_scalar(yt, X[:, bass.ts(N * i + u, P)], mv[:, 2 * u:2 * u + 1], rstd[:, u:u + 1],
                                                               ALU.subtract, ALU.mult), r, f_tile[u].free)
            c = None
            if y is not None:
                c = k.pool(lambda e, i, u=u, yt=yt: e.tensor_copy(y[:, bass.ts(N * i + u, P)], yt), n, alone=True)
            t = k.pe(lambda e, i, q=q, v=v, yt=yt: e.transpose(env.bank[q][:, v * P:(v + 1) * P], yt, env.ident[:, :]), n, f_bank[q].free)
            f_tile[u].read_by(t, c)
        f_bank[q].read_by(k.act(lambda e, i, q=q: e.copy(env.yT[:, bass.ts(2 * i + q, 512)], env.bank[q][:, :]), t))
    f_mv.read_by(n)
    f_rstd.read_by(n)
    k.barrier()


def load_x(env, x):
    env.k.dma("x", lambda e, i: e.dma_start(env.X[:, :].rearrange("p (t d) -> p t d", d=P),
                                            x.rearrange("(t p) d -> p t d", p=P)))


def store_x(env, out):
    env.k.barrier()
    env.k.straight()
    env.k.dma("out", lambda e, i: e.dma_start(out.rearrange("(t p) d -> p t d", p=P),
                                              env.X[:, :].rearrange("p (t d) -> p t d", d=P)))


def heads_last(w):
    return w.rearrange("(h j) d -> j h d", h=H)


def softmax_cross_attention(env, ctx_kv, dk, Wq, Wk, Wv, Wo, scale, bq=None, bk=None, bv=None, bo=None,
                            mask=None, masked_where=None, masked_to=None, shared=False):
    k, nc = env.k, env.k.nc
    bank = env.bank
    with ExitStack() as st:
        sb = lambda name, shape, dt=F32: k.sb(st, name, shape, dt)
        A = sb("A", [P, H * P])
        M = sb("M", [P, H * P])
        bo_eff = sb("bo_eff", [1, P])
        if bq is not None:
            c = sb("c", [P, H])
            g = sb("g", [P, H])
            g0 = sb("g0", [P, H // 4])
        k.straight()
        with ExitStack() as pre:
            wsb = lambda name, shape: k.sb(pre, name, shape)
            wq, wk, wv, wo = (wsb(n, [dk, H * P]) for n in ("wq", "wk", "wv", "wo"))
            as_heads = lambda t: t[:, :].rearrange("j (h d) -> j h d", h=H)
            lw = []
            done = []
            if not shared:
                for t, src in ((wq, Wq), (wk, Wk), (wv, Wv)):
                    lw.append(k.dma("w", lambda e, i, t=t, src=src: e.dma_start(as_heads(t), heads_last(src))))
                wo_rows = wsb("wo_rows", [P, H * dk])
                lo = k.dma("w", lambda e, i: e.dma_start(wo_rows[:, :], Wo))
                brow = wsb("brow", [1, P])
                bcol = [wsb("bcol", [dk, H]) for _ in range(3)]
                lb = [k.dma("w", lambda e, i: e.dma_start(brow[:, :], bo.rearrange("(a d) -> a d", a=1)))]
                for t, src in zip(bcol, (bq, bk, bv)):
                    lb.append(k.dma("w", lambda e, i, t=t, src=src: e.dma_start(
                        t[:, :], src.rearrange("(h j) -> j h", h=H))))
                lw = [lb[-1]]
                norm_tiles(env)
                for q in range(4):
                    for r in range(4):
                        h = 4 * q + r
                        tt = k.pe(lambda e, i, q=q, r=r, h=h: e.transpose(
                            bank[q][0:dk, r * P:(r + 1) * P], wo_rows[:, h * dk:(h + 1) * dk], env.ident[:, :]), lb[-1])
                    cp = k.act(lambda e, i, q=q: e.copy(wo[:, q * 512:(q + 1) * 512], bank[q][0:dk, :]), tt)
                    done.append(cp)
                wkh = lambda h: wk[:, h * P:(h + 1) * P]
                wvh = lambda h: wv[:, h * P:(h + 1) * P]
            else:
                rows = [wsb("rows", [P, w]) for w in (P, dk, dk)]
                for t, src in zip(rows, (Wq, Wk, Wv)):
                    k.dma("w", lambda e, i, t=t, src=src: e.dma_start(t[:, :], src))
                brow = wsb("brow", [1, P])
                k.dma("w", lambda e, i: e.dma_start(brow[:, :], bo.rearrange("(a d) -> a d", a=1)))
                lw = [k.dma("w", lambda e, i: e.dma_start(as_heads(wo), heads_last(Wo)))]
                norm_tiles(env)
                for q in range(4):
                    for r in range(4):
                        h = 4 * q + r
                        tt = k.pe(lambda e, i, q=q, r=r, h=h: e.transpose(
                            bank[q][0:dk, r * P:(r + 1) * P], rows[0][:, h * dk:(h + 1) * dk], env.ident[:, :]), lw)
                    done.append(k.act(lambda e, i, q=q: e.copy(wq[:, q * 512:(q + 1) * 512], bank[q][0:dk, :]), tt))
                for n, t in ((1, wk), (2, wv)):
                    tt = k.pe(lambda e, i, n=n: e.transpose(bank[3 + n][0:dk, 0:P], rows[n][:, :], env.ident[:, :]), lw)
                    done.append(k.act(lambda e, i, n=n, t=t: e.copy(t[:, 0:P], bank[3 + n][0:dk, 0:P]), tt))
                wkh = lambda h: wk[:, 0:P]
                wvh = lambda h: wv[:, 0:P]
            wqh = lambda h: wq[:, h * P:(h + 1) * P]
            woh = lambda h: wo[:, h * P:(h + 1) * P]
            for dst, left, right, first in ((A, wqh, wkh, 0), (M, wvh, woh, 4)):
                for q in range(4):
                    for r in range(4):
                        h = 4 * q + r
                        mm = k.pe(lambda e, i, h=h, r=r, b=bank[first + q], left=left, right=right: e.matmul(
                            b[:, r * P:(r + 1) * P], left(h), right(h), start=True, stop=True), done, lw)
                    cp = k.dve(lambda e, i, q=q, b=bank[first + q], dst=dst: e.tensor_copy(
                        dst[:, q * 512:(q + 1) * 512], b[:, :]), mm)
                    last = cp
                    if first == 0 and q == 0:
                        free0 = cp
                    if first == 0 and q == 1:
                        free1 = cp
            free = [free0, free1]
            if bq is not None:
                for h in range(H):
                    k.pe(lambda e, i, h=h: e.matmul(bank[0][:, h:h + 1], wkh(h), bcol[0][:, h:h + 1], start=True, stop=True), free)
                    mm = k.pe(lambda e, i, h=h: e.matmul(bank[0][:, H + h:H + h + 1], wqh(h), bcol[1][:, h:h + 1], start=True, stop=True))
                c1 = k.dve(lambda e, i: e.tensor_copy(c[:, :], bank[0][:, 0:H]), mm)
                c2 = k.dve(lambda e, i: e.tensor_copy(g[:, :], bank[0][:, H:2 * H]), mm)
                m1 = k.dve(lambda e, i: e.tensor_tensor(bcol[0][:, :], bcol[0][:, :], bcol[1][:, :], ALU.mult), mm)
                gq = bcol[0][:, :].rearrange("j (g f) -> j g f", f=4)
                for f in range(4):
                    mm = k.pe(lambda e, i, f=f: e.matmul(bank[2][32 * f:32 * f + 32, 0:4], env.ones[0:dk, 0:32], gq[:, :, f],
                                                         start=True, stop=True, tile_position=(0, 32 * f)), m1, done)
                c3 = k.dve(lambda e, i: e.tensor_copy(g0[:, :], bank[2][:, 0:4]), mm)
            mm = k.pe(lambda e, i: e.matmul(bank[1][0:1, 0:P], env.ones[0:1, 0:1], brow[:, :], start=True, stop=bq is None), free, lw)
            if bq is not None:
                for h in range(H):
                    mm = k.pe(lambda e, i, h=h: e.matmul(bank[1][0:1, 0:P], bcol[2][:, h:h + 1], woh(h),
                                                         start=False, stop=h == H - 1))
            k.dve(lambda e, i: e.tensor_copy(bo_eff[:, :], bank[1][0:1, 0:P]), mm)
            k.barrier()
        v_dram = nc.dram_tensor(f"v_last_{k.names}", (BATCH * 4, 4 * P), F32, kind="Internal").ap()
        with ExitStack() as pre:
            last_rows, last_T = k.sb(pre, "last_rows", [BATCH, P]), k.sb(pre, "last_T", [P, BATCH])
            v_rows = k.sb(pre, "v_rows", [BATCH, H * P])
            l = k.dma("w3", lambda e, i: e.dma_start(last_rows[:, :], ctx_kv[:, 2 * P:CTX, :].rearrange("b c d -> b (c d)")))
            t = k.pe(lambda e, i: e.transpose(bank[0][:, 0:BATCH], last_rows[:, :], env.ident[0:BATCH, 0:BATCH]), l)
            lT = k.act(lambda e, i: e.copy(last_T[:, :], bank[0][:, 0:BATCH]), t)
            cps = []
            for q in range(4):
                mm = k.pe(lambda e, i, q=q: e.matmul(bank[1 + q][0:BATCH, :], last_T[:, :], M[:, q * 512:(q + 1) * 512], start=True, stop=True), lT)
                cps.append(k.dve(lambda e, i, q=q: e.tensor_copy(v_rows[:, q * 512:(q + 1) * 512], bank[1 + q][0:BATCH, :]), mm))
            k.dma("w3", lambda e, i: e.dma_start(v_dram.rearrange("(b n) d -> b (n d)", n=4), v_rows[:, :]), cps)
            k.barrier()
        AHEAD, RING = 3, 4
        UNITS = 2 * BPT
        G = 2 * P
        qh = [sb("qh", [P, BPT * H * SEQ]) for _ in range(2)]
        p_last = [sb("p_last", [P, BPT * 4]) for _ in range(2)]
        p_diag = sb("p_diag", [BPT * 4, 4 * P])
        of_batch = sb("of_batch", [BPT * 4, 4 * P])
        v_last = [sb("v_last", [BPT * 4, 4 * P]) for _ in range(2)]
        kv = [sb("kv", [P, 2 * P]) for _ in range(BPT)]
        kv_last = [sb("kv_last", [1, P]) for _ in range(BPT)]
        kvT = [sb("kvT", [P, CTX]) for _ in range(2)]
        maxes, nbias, rows_sum, rinv = ([sb(n, [P, 2]) for _ in range(RING)] for n in ("maxes", "nbias", "rows_sum", "rinv"))
        probs = [sb("probs", [P, 2 * CTX]) for _ in range(RING)]
        pT = [sb("pT", [P, 2 * G]) for _ in range(2)]
        U = sb("U", [P, H * P])
        if bq is not None:
            y_tile = sb("y_tile", [P, P])
            r_all = [sb("r_all", [P, BPT * 4]) for _ in range(2)]
        if mask is not None:
            mask_u8 = sb("mask_u8", [P, BPT * CTX], U8)
            keep, fill = ([sb(n, [P, BPT * CTX]) for _ in range(2)] for n in ("keep", "fill"))
        pair = lambda: [Buffer(), Buffer()]
        ring = lambda: [Buffer() for _ in range(RING)]
        f_q, f_r, f_keep, f_plast, f_vlast, f_kvT, f_pT = (pair() for _ in range(7))
        f_mx, f_nb, f_rs, f_ri, f_pr = (ring() for _ in range(5))
        f_y, f_mask, f_U, f_diag = (Buffer() for _ in range(4))
        f_kv = [Buffer() for _ in range(BPT)]
        f_bank = [Buffer() for _ in range(8)]
        m_q, m_r, m_keep, m_vlast, m_kvT, m_plast = (pair() for _ in range(6))
        m_exp, m_prob, m_aside = (ring() for _ in range(3))
        m_mask = Buffer()
        m_kv = [Buffer() for _ in range(BPT)]
        S_BANK, T_BANK, AV, X_BANK = 1, 5, 7, 0
        k.straight()
        ob = of_batch[:, :].rearrange("p (r b q) -> p r b q", r=4, b=BPT)
        a = k.pool(lambda e, i: e.memset(of_batch[:, :], 1.0))
        a = k.pool(lambda e, i: e.affine_select(out=ob, in_=ob, compare_op=ALU.is_ge, fill=0.0, base=0,
                                                pattern=[[0, 4], [-4, BPT], [0, SEQ]], channel_multiplier=1), a)
        a = k.pool(lambda e, i: e.affine_select(out=ob, in_=ob, compare_op=ALU.is_ge, fill=0.0, base=3,
                                                pattern=[[0, 4], [4, BPT], [0, SEQ]], channel_multiplier=-1), a)
        ob_made = a

        def load_context(tile, b):
            p, at = tile
            l = k.dma(f"kv{b}", lambda e, i: e.dma_start(kv[b][:, :].rearrange("p (c d) -> p c d", c=2),
                      ctx_kv[bass.ds(BPT * at(i) + b, 1), 0:2 * P, :].rearrange("a (c p) d -> p (a c) d", p=P)), f_kv[b].free)
            l = k.dma(f"kv{b}", lambda e, i: e.dma_start(kv_last[b][:, :],
                      ctx_kv[bass.ds(BPT * at(i) + b, 1), 2 * P:CTX, :].rearrange("a c d -> a (c d)")), f_kv[b].free)
            m_kv[b].made_by(l)

        def load_mask(tile):
            p, at = tile
            if mask is not None:
                for f in range(4):
                    lm = k.dma("mask", lambda e, i, f=f: e.dma_start(
                        mask_u8[32 * f:32 * f + 32, :].rearrange("q (b s) -> q b s", b=BPT),
                        mask[bass.ts(at(i), BPT), :, :].rearrange("b q s -> q b s")), f_mask.free)
                m_mask.made_by(lm)

        def map_mask(tile):
            p = tile[0]
            if mask is not None:
                lm = m_mask.made
                keep_mul, keep_add = (-1.0, 1.0) if masked_where else (1.0, 0.0)
                fill_mul, fill_add = (masked_to / scale, 0.0) if masked_where else (-masked_to / scale, masked_to / scale)
                k.pool(lambda e, i: e.tensor_scalar(keep[p][:, :], mask_u8[:, :], keep_mul, keep_add, ALU.mult, ALU.add),
                       lm, f_keep[p].free, alone=True)
                mapped = k.pool(lambda e, i: e.tensor_scalar(fill[p][:, :], mask_u8[:, :], fill_mul, fill_add, ALU.mult, ALU.add),
                                lm, f_keep[p].free, alone=True)
                f_mask.read_by(mapped)
                m_keep[p].made_by(mapped)

        def load_values(tile):
            p, at = tile
            m_vlast[p].made_by(k.dma(f"v{p}", lambda e, i: e.dma_start(v_last[p][:, :], v_dram[bass.ts(at(i), BPT * 4), :]), f_vlast[p].free))

        def fold_queries(tile, n):
            p, at = tile
            for r in range(4):
                h = 4 * n + r
                mm = k.pe(lambda e, i, r=r, h=h: e.matmul(bank[X_BANK][:, r * P:(r + 1) * P], A[:, h * P:(h + 1) * P],
                                                          env.yT[:, bass.ts(at(i), P)], start=True, stop=True), f_bank[X_BANK].free)
            out = qh[p][:, :].rearrange("p (b h q) -> p h b q", b=BPT, h=H)[:, 4 * n:4 * n + 4]
            src = bank[X_BANK][:, :].rearrange("p (h b q) -> p h b q", h=4, b=BPT)
            if bq is not None:
                cp = k.dve(lambda e, i: e.tensor_tensor(
                    out, src, c[:, 4 * n:4 * n + 4].unsqueeze(2).unsqueeze(3).to_broadcast([P, 4, BPT, SEQ]), ALU.add), mm, f_q[p].free)
            else:
                cp = k.dve(lambda e, i: e.tensor_copy(out, src), mm, f_q[p].free)
            f_bank[X_BANK].read_by(cp)
            m_q[p].made_by(cp)

        def offsets(tile):
            p, at = tile
            yc = k.dve(lambda e, i: e.tensor_copy(y_tile[:, :], env.yT[:, bass.ts(at(i), P)]), f_y.free)
            gf = g[:, :].rearrange("p (g f) -> p g f", f=4)
            for b in range(BPT):
                for f in range(4):
                    mm = k.pe(lambda e, i, b=b, f=f: e.matmul(
                        bank[X_BANK][32 * f:32 * f + 32, 4 * b:4 * b + 4], y_tile[:, 32 * b:32 * b + 32], gf[:, :, f],
                        start=True, stop=True, tile_position=(0, 32 * f)), yc, f_bank[X_BANK].free)
            f_y.read_by(mm)
            rr = k.dve(lambda e, i: e.tensor_tensor(
                r_all[p][:, :].rearrange("p (b g) -> p b g", b=BPT), bank[X_BANK][:, 0:16].rearrange("p (b g) -> p b g", b=BPT),
                g0[:, :].unsqueeze(1).to_broadcast([P, BPT, 4]), ALU.add), mm, f_r[p].free)
            f_bank[X_BANK].read_by(rr)
            m_r[p].made_by(rr)

        def turn_context(b):
            z, w = b % 2, m_kv[b].made
            k.pe(lambda e, i: e.transpose(bank[X_BANK][:, 0:P], kv[b][:, 0:P], env.ident[:, :]), w, f_bank[X_BANK].free)
            k.pe(lambda e, i: e.transpose(bank[X_BANK][:, P:2 * P], kv[b][:, P:2 * P], env.ident[:, :]))
            t = k.pe(lambda e, i: e.transpose(bank[X_BANK][:, 2 * P:CTX], kv_last[b][:, :], env.ident[0:1, 0:1]))
            ct = k.act(lambda e, i: e.copy(kvT[z][:, :], bank[X_BANK][:, 0:CTX]), t, f_kvT[z].free)
            f_bank[X_BANK].read_by(ct)
            m_kvT[z].made_by(ct)

        def scores(tile, u):
            p, b, z = tile[0], u // 2, u % 2
            made = []
            for j in range(2):
                n = 2 * z + j
                bk_ = bank[S_BANK + 2 * z + j]
                mm = k.pe(lambda e, i, n=n, bk_=bk_: e.matmul(
                    bk_[:, 0:CTX], qh[p][:, (4 * b + n) * P:(4 * b + n + 1) * P], kvT[b % 2][:, :], start=True, stop=True),
                    m_kvT[b % 2].made, m_q[p].made, f_bank[S_BANK + 2 * z + j].free)
                made.append(mm)
            if u == UNITS - 1:
                f_q[p].read_by(mm)
            if z:
                f_kvT[b % 2].read_by(mm)
            return made

        def exponentials(tile, u, made):
            p, b, z, v = tile[0], u // 2, u % 2, u % RING
            banks = [bank[S_BANK + 2 * z + j] for j in range(2)]
            top = lambda j: maxes[v][:, j:j + 1]
            if mask is not None:
                kept = [k.dve(lambda e, i, j=j: e.scalar_tensor_tensor(
                    banks[j][:, 0:CTX], banks[j][:, 0:CTX], r_all[p][:, 4 * b + 2 * z + j:4 * b + 2 * z + j + 1], keep[p][:, b * CTX:(b + 1) * CTX],
                    ALU.add, ALU.mult), made[j], m_r[p].made, m_keep[p].made) for j in range(2)]
                mx = [k.dve(lambda e, i, j=j: e.tensor_tensor_reduce(
                    banks[j][:, 0:CTX], banks[j][:, 0:CTX], fill[p][:, b * CTX:(b + 1) * CTX], 1.0, -3.0e38, ALU.add, ALU.max,
                    top(j)), kept[j], f_mx[v].free if j == 0 else None, alone=True) for j in range(2)]
                if u == UNITS - 1:
                    f_r[p].read_by(kept[1])
                    f_keep[p].read_by(mx[1])
            else:
                mx = [k.dve(lambda e, i, j=j: e.tensor_reduce(top(j), banks[j][:, 0:CTX], AX.X, ALU.max),
                            made[j], f_mx[v].free if j == 0 else None) for j in range(2)]
            nb = k.dve(lambda e, i: e.tensor_scalar(nbias[v][:, :], maxes[v][:, :], -scale, None, ALU.mult), mx, f_nb[v].free)
            f_mx[v].read_by(nb)
            for j in range(2):
                ex = k.act(lambda e, i, j=j: e.activation(
                    probs[v][:, j * CTX:(j + 1) * CTX], banks[j][:, 0:CTX], ACT.Exp, bias=nbias[v][:, j:j + 1], scale=scale,
                    accum_out=rows_sum[v][:, j:j + 1]), nb, [f_pr[v].free, m_aside[v].made] if j == 0 else None, f_rs[v].free if j == 0 else None)
                f_bank[S_BANK + 2 * z + j].read_by(ex)
            f_nb[v].read_by(ex)
            m_exp[v].made_by(ex)

        def normalise(tile, u):
            p, v = tile[0], u % RING
            ri = k.dve(lambda e, i: e.reciprocal(rinv[v][:, :], rows_sum[v][:, :]), m_exp[v].made, f_ri[v].free)
            f_rs[v].read_by(ri)
            for j in range(2):
                nm = k.pool(lambda e, i, j=j: e.tensor_scalar(
                    probs[v][:, j * CTX:(j + 1) * CTX], probs[v][:, j * CTX:(j + 1) * CTX], rinv[v][:, j:j + 1], 1.0,
                    ALU.mult, ALU.mult), ri, alone=True)
            f_ri[v].read_by(nm)
            pl = k.pool(lambda e, i: e.tensor_copy(p_last[p][:, 2 * u:2 * u + 2],
                                                   probs[v][:, :].rearrange("p (j s) -> p j s", j=2)[:, :, CTX - 1]), nm, f_plast[p].free, alone=True)
            m_prob[v].made_by(nm)
            m_plast[p].made_by(pl)
            m_aside[v].made_by(pl)

        def turn_probs(u):
            z, v = u % 2, u % RING
            for c_ in range(2):
                for j in range(2):
                    t = k.pe(lambda e, i, c_=c_, j=j: e.transpose(
                        bank[T_BANK + z][:, c_ * G + j * P:c_ * G + (j + 1) * P], probs[v][:, j * CTX + c_ * P:j * CTX + (c_ + 1) * P],
                        env.ident[:, :]), m_prob[v].made, f_bank[T_BANK + z].free)
            f_pr[v].read_by(t)
            cp = k.act(lambda e, i: e.copy(pT[z][:, :], bank[T_BANK + z][:, :]), t, f_pT[z].free)
            f_bank[T_BANK + z].read_by(cp)
            return cp

        def attend(tile, u, turned):
            b, z = u // 2, u % 2
            k.pe(lambda e, i: e.matmul(bank[AV][:, 0:G], kv[b][:, 0:P], pT[z][:, 0:G], start=True, stop=False), turned, f_bank[AV].free)
            mm = k.pe(lambda e, i: e.matmul(bank[AV][:, 0:G], kv[b][:, P:2 * P], pT[z][:, G:2 * G], start=False, stop=True))
            f_pT[z].read_by(mm)
            if z:
                f_kv[b].read_by(mm)
            uo = k.act(lambda e, i: e.copy(
                U[:, :].rearrange("p (h b q) -> p h b q", h=H, b=BPT)[:, 8 * z:8 * z + 8, b], bank[AV][:, 0:G].rearrange("p (h q) -> p h q", h=8)),
                mm, f_U.free if u < 2 else None)
            f_bank[AV].read_by(uo)
            return uo

        def turn_last(tile):
            p = tile[0]
            t = k.pe(lambda e, i: e.transpose(bank[X_BANK][0:BPT * 4, 0:P], p_last[p][:, :], env.ident[:, :]), m_plast[p].made, f_bank[X_BANK].free)
            f_plast[p].read_by(t)
            d = k.dve(lambda e, i: e.tensor_tensor(
                p_diag[:, :].rearrange("p (r b q) -> p r b q", r=4, b=BPT),
                bank[X_BANK][0:BPT * 4, 0:P].rearrange("p (r q) -> p r q", r=4).unsqueeze(2).to_broadcast([BPT * 4, 4, BPT, SEQ]),
                ob, ALU.mult), t, ob_made, f_diag.free)
            f_bank[X_BANK].read_by(d)
            return d

        def output(tile, uo, diag):
            p, at = tile
            for h in range(H):
                k.pe(lambda e, i, h=h: e.matmul(bank[X_BANK][:, 0:P], U[:, h * P:(h + 1) * P], M[:, h * P:(h + 1) * P],
                                                start=h == 0, stop=False), uo[h // 8], f_bank[X_BANK].free)
            for r in range(4):
                vm = k.pe(lambda e, i, r=r: e.matmul(bank[X_BANK][:, 0:P], p_diag[:, r * P:(r + 1) * P], v_last[p][:, r * P:(r + 1) * P],
                                                     start=False, stop=False), diag, m_vlast[p].made)
            mm = k.pe(lambda e, i: e.matmul(bank[X_BANK][:, 0:P], env.ones[0:1, :], bo_eff[:, :], start=False, stop=True))
            f_U.read_by(mm)
            f_diag.read_by(vm)
            f_vlast[p].read_by(vm)
            ad = k.dve(lambda e, i: e.tensor_tensor(env.X[:, bass.ts(at(i), P)], env.X[:, bass.ts(at(i), P)], bank[X_BANK][:, 0:P], ALU.add), mm)
            f_bank[X_BANK].read_by(ad)

        def attention(tile, following):
            uo = [None, None]
            for u in range(UNITS):
                ahead = [(tile, u + d) if u + d < UNITS else (following, u + d - UNITS) for d in range(AHEAD + 2)]
                turned = turn_probs(u)
                if ahead[1][0]:
                    normalise(*ahead[1])
                if u == UNITS - 1:
                    diag = turn_last(tile)
                made = scores(*ahead[AHEAD]) if ahead[AHEAD][0] else None
                if u % 2 == 0 and ahead[AHEAD + 1][0]:
                    turn_context(ahead[AHEAD + 1][1] // 2)
                uo[u % 2] = attend(tile, u, turned)
                if made:
                    exponentials(*ahead[AHEAD], made)
                if following:
                    if u == 0:
                        load_mask(following)
                        load_values(following)
                    if u == 2:
                        map_mask(following)
                    if u < 4:
                        fold_queries(following, u)
                    if u == 4 and bq is not None:
                        offsets(following)
                    if u % 2:
                        load_context(following, u // 2)
            output(tile, uo, diag)

        first = (0, lambda i: 0)
        load_mask(first)
        load_values(first)
        for b in range(BPT):
            load_context(first, b)
        map_mask(first)
        for n in range(4):
            fold_queries(first, n)
        if bq is not None:
            offsets(first)
        for u in range(AHEAD):
            if u % 2 == 0:
                turn_context(u // 2)
            exponentials(first, u, scores(first, u))
            if u == 0:
                normalise(first, 0)
        even, odd = (0, lambda i: 2 * i), (1, lambda i: 2 * i + 1)
        k.loop(NT // 2 - 1)
        attention(even, odd)
        attention(odd, (0, lambda i: 2 * i + 2))
        k.loop(1)
        k.seg.first = NT // 2 - 1
        attention(even, odd)
        attention(odd, None)
        k.barrier()

R4 = 4 * P


def columns(k, st, name, src, width=P):
    n = src.shape[0] // width
    t = k.sb(st, name, [width, n])
    return t, k.dma("w", lambda e, i: e.dma_start(t[:, :], src.rearrange("(c p) -> p c", p=width)))


def broadcast_row(k, st, name, src):
    t = k.sb(st, name, [P, src.shape[0]])
    return t, k.dma("w", lambda e, i: e.dma_start(t[:, :], src.partition_broadcast(P)))


def rows(k, st, name, src):
    c = src.shape[0] // P
    t = k.sb(st, name, [P, c * src.shape[1]])
    return t, k.dma("w", lambda e, i: e.dma_start(t[:, :].rearrange("p (c n) -> p c n", c=c),
                                                  src.rearrange("(c p) n -> p c n", p=P)))


def transpose_blocks(env, src, dst, count, ready, src_at=None, dst_at=None, first_bank=0):
    k = env.k
    src_at = src_at or (lambda n: src[:, n * P:(n + 1) * P])
    out = []
    for q in range(0, count, 4):
        b = first_bank + (q // 4) % 4
        m = min(4, count - q)
        for r in range(m):
            t = k.pe(lambda e, i, q=q, r=r, b=b: e.transpose(env.bank[b][:, r * P:(r + 1) * P], src_at(q + r),
                                                             env.ident[:, :]), ready, env.prep_banks[b].free)
        if dst_at is None:
            c = k.dve(lambda e, i, q=q, m=m, b=b: e.tensor_copy(dst[:, q * P:(q + m) * P], env.bank[b][:, 0:m * P]), t)
        else:
            c = k.dve(lambda e, i, q=q, m=m, b=b: e.tensor_copy(dst_at(q, m), env.bank[b][:, 0:m * P]), t)
        env.prep_banks[b].read_by(c)
        out.append(c)
    return out


def block_diagonal(env, st, value):
    k = env.k
    t = k.sb(st, "same_batch", [P, P])
    a = k.dve(lambda e, i: e.memset(t[:, :], 0.0))
    for b in range(BPT):
        a2 = k.dve(lambda e, i, b=b: e.memset(t[b * SEQ:(b + 1) * SEQ, b * SEQ:(b + 1) * SEQ], value), a)
    return t


def alternate(*streams):
    streams = list(streams)
    while streams:
        for s in list(streams):
            if next(s, streams) is streams:
                streams.remove(s)


class Norm4:

    def __init__(self, env, st):
        self.env, k = env, env.k
        self.stats = k.sb(st, "stats4", [P, 4 * 6])
        self.mv = k.sb(st, "mv4", [P, 8])
        self.rstd = k.sb(st, "rstd4", [P, 4])
        self.f_stats, self.f_mv, self.f_rstd = Buffer(), Buffer(), Buffer()

    def __call__(self, src, dst, gain, offset, ready):
        k = self.env.k
        s = []
        for u in range(4):
            s.append(k.dve(lambda e, i, u=u: e.bn_stats(self.stats[:, u * 6:u * 6 + 6], src[:, u * P:(u + 1) * P]), ready,
                           self.f_stats.free))
        for u in range(4):
            a = k.dve(lambda e, i, u=u: e.bn_aggr(self.mv[:, 2 * u:2 * u + 2], self.stats[:, u * 6:u * 6 + 6]), s[-1],
                      self.f_mv.free, alone=True)
        self.f_stats.read_by(a)
        var = self.mv[:, :].rearrange("p (t two) -> p t two", two=2)[:, :, 1]
        v = k.dve(lambda e, i: e.tensor_scalar(self.rstd[:, :], var, 1e-5, None, ALU.add), a, self.f_rstd.free)
        q = k.act(lambda e, i: e.activation(self.rstd[:, :], self.rstd[:, :], ACT.Sqrt), v)
        r = k.dve(lambda e, i: e.reciprocal(self.rstd[:, :], self.rstd[:, :]), q)
        for u in range(4):
            n = k.dve(lambda e, i, u=u: e.tensor_scalar(
                dst[:, u * P:(u + 1) * P], src[:, u * P:(u + 1) * P], self.mv[:, 2 * u:2 * u + 1],
                self.rstd[:, u:u + 1], ALU.subtract, ALU.mult), r)
        self.f_mv.read_by(n)
        self.f_rstd.read_by(n)
        four = lambda t: t[:, :].rearrange("p (t d) -> p t d", d=P)
        row = lambda t: t[:, :].unsqueeze(1).to_broadcast([P, 4, P])
        g = k.dve(lambda e, i: e.tensor_tensor(four(dst), four(dst), row(gain), ALU.mult), n)
        return k.dve(lambda e, i: e.tensor_tensor(four(dst), four(dst), row(offset), ALU.add), g)


def l0_attention(env, w):
    k, bank = env.k, env.bank
    DH, C = 64, 8
    with ExitStack() as st:
        sb = lambda name, shape, dt=F32: k.sb(st, name, shape, dt)
        y = sb("y", [P, NTOK])
        k.straight()
        Wq, _ = rows(k, st, "Wq", w["Wq"])
        Wk, _ = rows(k, st, "Wk", w["Wk"])
        Wv, _ = rows(k, st, "Wv", w["Wv"])
        Wo, _ = rows(k, st, "Wo", w["Wo"])
        W1, _ = rows(k, st, "W1", w["W1"])
        W2, _ = rows(k, st, "W2", w["W2"])
        bq, _ = columns(k, st, "bq", w["bq"])
        bk, _ = columns(k, st, "bk", w["bk"])
        b1, _ = columns(k, st, "b1", w["b1"])
        bv, _ = broadcast_row(k, st, "bv", w["bv"])
        bo, _ = broadcast_row(k, st, "bo", w["bo"])
        b2, _ = broadcast_row(k, st, "b2", w["b2"])
        g1, _ = broadcast_row(k, st, "g1", w["g1"])
        be1, _ = broadcast_row(k, st, "be1", w["be1"])
        g2, _ = broadcast_row(k, st, "g2", w["g2"])
        be2, _ = broadcast_row(k, st, "be2", w["be2"])
        norm_tiles(env, y)
        same = block_diagonal(env, st, 1.0)
        y_static = sb("y_static", [P, R4])
        feat = [sb("qf", [P, C * R4]), sb("kf", [P, C * R4])]
        ex = [sb("ex", [P, R4]) for _ in range(2)]
        vext, o_tok = ([sb(n, [P, wd]) for _ in range(2)] for n, wd in (("vext", H * (DH + 1)), ("o_tok", H * DH)))
        att = [[sb("att", [P, 512]) for _ in range(2)] for _ in range(2)]
        rec = [sb("rec", [P, H]) for _ in range(2)]
        oT = [sb("oT", [P, H * DH]) for _ in range(2)]
        s1, x1T, s2 = (sb(n, [P, R4]) for n in ("s1", "x1T", "s2"))
        hT = sb("hT", [P, 4 * R4])
        for t in vext:
            k.dve(lambda e, i, t=t: e.memset(t[:, :], 1.0))
        norm = Norm4(env, st)
        k.barrier()
        f_ys, f_s1, f_x1T, f_hT, f_s2 = (Buffer() for _ in range(5))
        pair = lambda: [Buffer(), Buffer()]
        f_feat, f_ex, f_v, f_ot, f_oT, f_rec = (pair() for _ in range(6))
        f_att = [pair(), pair()]
        f_bank = [Buffer() for _ in range(8)]
        m_feat, m_ys = pair(), Buffer()

        def features(at):
            yc = k.pool(lambda e, i: e.tensor_copy(y_static[:, :], env.yT[:, bass.ts(at(i), R4)]), f_ys.free, alone=True)
            m_ys.made_by(yc)
            for c in range(C):
                for t, (W, b) in enumerate(((Wq, bq), (Wk, bk))):
                    n = t
                    mm = k.pe(lambda e, i, c=c, W=W, n=n: e.matmul(bank[n][:, :], W[:, c * P:(c + 1) * P], y_static[:, :],
                                                                   start=True, stop=True), yc, f_bank[n].free)
                    a = k.act(lambda e, i, c=c, b=b, n=n: e.activation(ex[n][:, :], bank[n][:, :], ACT.Exp, bias=b[:, c:c + 1]),
                              mm, f_ex[n].free)
                    if t:
                        r = k.act(lambda e, i, c=c, b=b, n=n: e.activation(bank[n][:, :], bank[n][:, :], ACT.Relu, bias=b[:, c:c + 1]), a)
                    else:
                        r = k.dve(lambda e, i, c=c, b=b, n=n: e.tensor_scalar(bank[n][:, :], bank[n][:, :], b[:, c:c + 1], 0.0, ALU.add, ALU.max), a)
                    m = k.dve(lambda e, i, c=c, t=t, n=n: e.scalar_tensor_tensor(
                        feat[t][:, c * R4:(c + 1) * R4], ex[n][:, :], 1.0, bank[n][:, :], ALU.min, ALU.add), r, f_feat[t].free)
                    f_bank[n].read_by(m)
                    f_ex[n].read_by(m)
                    m_feat[t].made_by(m)
                yield

        def values(s):
            z = s % 2
            for n in range(2):
                mm = k.pe(lambda e, i, s=s, n=n: e.matmul(bank[2 + n][:, :], y_static[:, s * P:(s + 1) * P],
                                                          Wv[:, n * 512:(n + 1) * 512], start=True, stop=True), m_ys.made, f_bank[2 + n].free)
                va = k.dve(lambda e, i, z=z, n=n: e.tensor_tensor(
                    vext[z][:, :].rearrange("p (h j) -> p h j", h=H)[:, 8 * n:8 * n + 8, 0:DH],
                    bank[2 + n][:, :].rearrange("p (h j) -> p h j", h=8),
                    bv[:, n * 512:(n + 1) * 512].rearrange("p (h j) -> p h j", h=8), ALU.add), mm, f_v[z].free)
                f_bank[2 + n].read_by(va)
            f_ys.read_by(mm)
            return va

        def weights(u):
            s, j = u // 2, u % 2
            for r in range(4):
                for odd in range(2):
                    lo, col = odd * DH, (4 * j + r) * R4 + s * P
                    mm = k.pe(lambda e, i, r=r, lo=lo, col=col, odd=odd: e.matmul(
                        bank[4 + odd][:, r * P:(r + 1) * P], feat[1][lo:lo + DH, col:col + P], feat[0][lo:lo + DH, col:col + P],
                        start=True, stop=True), [m.made for m in m_feat], f_bank[4 + odd].free)
            if u == 7:
                for f in f_feat:
                    f.read_by(mm)
            return mm

        def within_batch(u, mm):
            out = []
            for odd in range(2):
                ma = k.dve(lambda e, i, odd=odd, t=att[u % 2][odd]: e.tensor_tensor(
                    t[:, :].rearrange("p (h q) -> p h q", h=4), bank[4 + odd][:, :].rearrange("p (h q) -> p h q", h=4),
                    same[:, :].unsqueeze(1).to_broadcast([P, 4, P]), ALU.mult), mm, f_att[u % 2][odd].free)
                f_bank[4 + odd].read_by(ma)
                out.append(ma)
            return out

        def apply(u, ma, va):
            s, j, z = u // 2, u % 2, (u // 2) % 2
            outs = []
            for odd in range(2):
                for r in range(4):
                    h = 8 * j + 2 * r + odd
                    mo = k.pe(lambda e, i, r=r, h=h, odd=odd: e.matmul(
                        bank[6 + odd][:, r * 65:(r + 1) * 65], att[u % 2][odd][:, r * P:(r + 1) * P], vext[z][:, h * 65:(h + 1) * 65],
                        start=True, stop=True), ma[odd], va, f_bank[6 + odd].free)
                f_att[u % 2][odd].read_by(mo)
                outs.append(mo)
            if j:
                f_v[z].read_by(mo)
            return outs

        def over_sums(u, outs):
            s, j, z = u // 2, u % 2, (u // 2) % 2
            views = [bank[6 + odd][:, 0:4 * 65].rearrange("p (h j) -> p h j", h=4) for odd in range(2)]
            at = lambda odd: slice(4 * (2 * j + odd), 4 * (2 * j + odd) + 4)
            for odd in range(2):
                r1 = k.dve(lambda e, i, odd=odd: e.tensor_scalar(rec[z][:, at(odd)], views[odd][:, :, DH], 1e-6, None, ALU.add),
                           outs[odd], f_rec[z].free)
            r2 = k.dve(lambda e, i: e.reciprocal(rec[z][:, 8 * j:8 * j + 8], rec[z][:, 8 * j:8 * j + 8]), r1)
            for odd in range(2):
                oo = k.dve(lambda e, i, odd=odd: e.tensor_tensor(
                    o_tok[z][:, :].rearrange("p (j r o d) -> p j o r d", j=2, r=4, o=2)[:, j, odd], views[odd][:, :, 0:DH],
                    rec[z][:, at(odd)].unsqueeze(2).to_broadcast([P, 4, DH]), ALU.mult), r2, f_ot[z].free)
                f_bank[6 + odd].read_by(oo)
            if j:
                f_rec[z].read_by(oo)
            return oo

        def project(s, oo):
            z = s % 2
            for n in range(2):
                for r in range(4):
                    t = k.pe(lambda e, i, n=n, r=r: e.transpose(bank[n][:, r * P:(r + 1) * P],
                                                                o_tok[z][:, (4 * n + r) * P:(4 * n + r + 1) * P], env.ident[:, :]),
                             oo, f_bank[n].free)
                ec = k.act(lambda e, i, n=n: e.copy(oT[z][:, n * 512:(n + 1) * 512], bank[n][:, :]), t, f_oT[z].free)
                f_bank[n].read_by(ec)
            f_ot[z].read_by(t)
            return ec

        def onto_y(s, ec, at):
            z = s % 2
            for c in range(8):
                mm = k.pe(lambda e, i, c=c: e.matmul(bank[0][:, 0:P], oT[z][:, c * P:(c + 1) * P], Wo[:, c * P:(c + 1) * P],
                                                     start=c == 0, stop=c == 7), ec, f_bank[0].free)
            f_oT[z].read_by(mm)
            a1 = k.dve(lambda e, i: e.tensor_tensor(s1[:, s * P:(s + 1) * P], bank[0][:, 0:P], bo[:, :], ALU.add), mm, f_s1.free)
            f_bank[0].read_by(a1)
            return k.dve(lambda e, i: e.tensor_tensor(s1[:, s * P:(s + 1) * P], s1[:, s * P:(s + 1) * P],
                                                      y[:, bass.ts(4 * at(i) + s, P)], ALU.add), a1)

        def attention(at):
            va = {0: values(0)}
            mm = weights(0)
            ma = within_batch(0, mm)
            turned = done = None
            for u in range(8):
                s, j = u // 2, u % 2
                if u < 7:
                    mm = weights(u + 1)
                if j == 1 and s < 3:
                    va[s + 1] = values(s + 1)
                if turned:
                    done = onto_y(s - 1, turned, at)
                    turned = None
                outs = apply(u, ma, va[s])
                if u < 7:
                    ma = within_batch(u + 1, mm)
                oo = over_sums(u, outs)
                if j == 0 and s:
                    turned = project(s - 1, before)
                if j:
                    before = oo
            return onto_y(3, project(3, before), at)

        def mlp(at, done):
            n1 = norm(s1, s1, g1, be1, done)
            yield
            for s in range(4):
                t = k.pe(lambda e, i, s=s: e.transpose(bank[2][:, s * P:(s + 1) * P], s1[:, s * P:(s + 1) * P], env.ident[:, :]),
                         n1, f_bank[2].free)
            xc = k.act(lambda e, i: e.copy(x1T[:, :], bank[2][:, :]), t, f_x1T.free)
            f_bank[2].read_by(xc)
            yield
            for c in range(4):
                n = 4 + c
                mm = k.pe(lambda e, i, c=c, n=n: e.matmul(bank[n][:, :], W1[:, c * P:(c + 1) * P], x1T[:, :], start=True, stop=True),
                          xc, f_bank[n].free)
                ge = k.act(lambda e, i, c=c, n=n: e.activation(hT[:, c * R4:(c + 1) * R4], bank[n][:, :], ACT.Gelu, bias=b1[:, c:c + 1]),
                           mm, f_hT.free)
                f_bank[n].read_by(ge)
            f_x1T.read_by(mm)
            yield
            for s in range(4):
                for c in range(4):
                    mm = k.pe(lambda e, i, s=s, c=c: e.matmul(bank[3][:, s * P:(s + 1) * P], hT[:, c * R4 + s * P:c * R4 + (s + 1) * P],
                                                              W2[:, c * P:(c + 1) * P], start=c == 0, stop=c == 3), ge, f_bank[3].free)
            f_hT.read_by(mm)
            a = k.dve(lambda e, i: e.tensor_tensor(s2[:, :], bank[3][:, :], s1[:, :], ALU.add), mm, f_s2.free)
            f_bank[3].read_by(a)
            f_s1.read_by(a)
            yield
            a = k.dve(lambda e, i: e.tensor_tensor(s2[:, :].rearrange("p (t d) -> p t d", d=P), s2[:, :].rearrange("p (t d) -> p t d", d=P),
                                                   b2[:, :].unsqueeze(1).to_broadcast([P, 4, P]), ALU.add), a)
            n2 = norm(s2, s2, g2, be2, a)
            yield
            f_s2.read_by(k.dve(lambda e, i: e.tensor_tensor(env.X[:, bass.ts(at(i), R4)], env.X[:, bass.ts(at(i), R4)], s2[:, :], ALU.add), n2))

        k.straight()
        alternate(features(lambda i: 0))
        k.loop(NT // 4 - 1)
        same_round, next_round = (lambda i: i), (lambda i: i + 1)
        alternate(features(next_round), mlp(same_round, attention(same_round)))
        k.loop(1)
        k.seg.first = NT // 4 - 1
        alternate(mlp(same_round, attention(same_round)))
        k.barrier()


def l0_ffn(env, w):
    k, bank = env.k, env.bank
    FC = 4
    with ExitStack() as st:
        sb = lambda name, shape, dt=F32: k.sb(st, name, shape, dt)
        k.straight()
        raw = [sb(f"k{n}", [P, c * wd], U8) for n, c, wd in ((0, 2, 512), (1, 4, 512), (2, 4, 128))]
        W = [sb(f"W{n}", [P, c * wd]) for n, c, wd in ((0, 2, 512), (1, 4, 512), (2, 4, 128))]
        scales = sb("scales", [P, 3])
        for n, c in ((0, 2), (1, 4), (2, 4)):
            k.dma("w", lambda e, i, n=n, c=c: e.dma_start(raw[n][:, :].rearrange("p (c n) -> p c n", c=c),
                                                          w[f"k{n}"].rearrange("(c p) n -> p c n", p=P)))
        for n in range(3):
            l = k.dma("w", lambda e, i, n=n: e.dma_start(scales[:, n:n + 1], w[f"s{n}"].partition_broadcast(P)))
        norm_tiles(env)
        for n in range(3):
            c = k.dve(lambda e, i, n=n: e.tensor_scalar(W[n][:, :], raw[n][:, :], 2.0, -1.0, ALU.mult, ALU.add), l)
        k.dve(lambda e, i: e.tensor_tensor(W[0][:, 0:512], W[0][:, 0:512], W[0][:, 512:1024], ALU.subtract), c)
        k.dve(lambda e, i: e.tensor_scalar(scales[:, 1:3], scales[:, 1:3], 2.0, None, ALU.mult), l)
        h = [sb("h0", [P, FC * R4]), sb("h1", [P, FC * R4])]
        f_h = [Buffer(), Buffer()]
        f_bank = [Buffer() for _ in range(8)]
        k.barrier()
        k.loop(NT // 4)
        r0 = []
        for c in range(FC):
            n = c % 2
            mm = k.pe(lambda e, i, c=c, n=n: e.matmul(bank[n][:, :], W[0][:, c * P:(c + 1) * P], env.yT[:, bass.ts(i, R4)],
                                                      start=True, stop=True), f_bank[n].free)
            a = k.act(lambda e, i, c=c, n=n: e.activation(h[0][:, c * R4:(c + 1) * R4], bank[n][:, :], ACT.Relu, scale=scales[:, 0:1]),
                      mm, f_h[0].free)
            f_bank[n].read_by(a)
        r0 = a
        for c in range(FC):
            n = 2 + c % 2
            for kc in range(FC):
                mm = k.pe(lambda e, i, c=c, kc=kc, n=n: e.matmul(bank[n][:, :], W[1][:, kc * 512 + c * P:kc * 512 + (c + 1) * P],
                                                                 h[0][:, kc * R4:(kc + 1) * R4], start=kc == 0, stop=kc == FC - 1),
                          r0, f_bank[n].free)
            a = k.act(lambda e, i, c=c, n=n: e.activation(h[1][:, c * R4:(c + 1) * R4], bank[n][:, :], ACT.Relu, scale=scales[:, 1:2]),
                      mm, f_h[1].free)
            f_bank[n].read_by(a)
        f_h[0].read_by(mm)
        for s in range(4):
            for c in range(FC):
                mm = k.pe(lambda e, i, s=s, c=c: e.matmul(bank[4][:, s * P:(s + 1) * P], h[1][:, c * R4 + s * P:c * R4 + (s + 1) * P],
                                                          W[2][:, c * P:(c + 1) * P], start=c == 0, stop=c == FC - 1), a, f_bank[4].free)
        f_h[1].read_by(mm)
        f_bank[4].read_by(k.dve(lambda e, i: e.scalar_tensor_tensor(
            env.X[:, bass.ts(i, R4)], bank[4][:, :], scales[:, 2:3], env.X[:, bass.ts(i, R4)], ALU.mult, ALU.add), mm))
        k.barrier()


def l1_attention(env, w):
    k, bank = env.k, env.bank
    with ExitStack() as st:
        sb = lambda name, shape, dt=F32: k.sb(st, name, shape, dt)
        y = sb("y", [P, NTOK])
        k.straight()
        qkv_rows, _ = rows(k, st, "qkv_rows", w["qkv_w"])
        proj_rows, _ = rows(k, st, "proj_rows", w["proj_w"])
        bqk, _ = columns(k, st, "bqk", w["qkv_b"][0:2 * P])
        bv, _ = broadcast_row(k, st, "bv", w["qkv_b"][2 * P:3 * P])
        bp, _ = broadcast_row(k, st, "bp", w["proj_b"])
        gw, _ = broadcast_row(k, st, "gw", w["norm_w"])
        gb, l = broadcast_row(k, st, "gb", w["norm_b"])
        norm_tiles(env, y)
        qkvT = sb("qkvT", [P, 3 * P])
        projT = sb("projT", [P, P])
        transpose_blocks(env, qkv_rows, qkvT, 3, l)
        transpose_blocks(env, proj_rows, projT, 1, l, first_bank=1)
        same = block_diagonal(env, st, P ** -0.5)
        hn, hT, v, att, oT, t1 = (sb(n, [P, R4]) for n in ("hn", "hT", "v", "att", "oT", "t1"))
        qk = [sb("qT", [P, R4]), sb("kT", [P, R4])]
        norm = Norm4(env, st)
        f_hn, f_hT, f_v, f_att, f_oT, f_t1 = (Buffer() for _ in range(6))
        f_qk = [Buffer(), Buffer()]
        f_bank = [Buffer() for _ in range(8)]
        k.barrier()
        k.loop(NT // 4)
        ycp = k.dve(lambda e, i: e.tensor_copy(t1[:, :], y[:, bass.ts(i, R4)]), f_t1.free)
        n1 = norm(t1, hn, gw, gb, [ycp, f_hn.free])
        for s in range(4):
            t = k.pe(lambda e, i, s=s: e.transpose(bank[0][:, s * P:(s + 1) * P], hn[:, s * P:(s + 1) * P], env.ident[:, :]),
                     n1, f_bank[0].free)
        f_hn.read_by(t)
        hc = k.act(lambda e, i: e.copy(hT[:, :], bank[0][:, :]), t, f_hT.free)
        f_bank[0].read_by(hc)
        for n in range(2):
            mm = k.pe(lambda e, i, n=n: e.matmul(bank[1 + n][:, :], qkvT[:, n * P:(n + 1) * P], hT[:, :], start=True, stop=True),
                      hc, f_bank[1 + n].free)
            qa = k.act(lambda e, i, n=n: e.activation(qk[n][:, :], bank[1 + n][:, :], ACT.Identity, bias=bqk[:, n:n + 1]),
                       mm, f_qk[n].free)
            f_bank[1 + n].read_by(qa)
        for s in range(4):
            mm = k.pe(lambda e, i, s=s: e.matmul(bank[3][:, s * P:(s + 1) * P], hT[:, s * P:(s + 1) * P], qkvT[:, 2 * P:3 * P],
                                                 start=True, stop=True), f_bank[3].free)
        f_hT.read_by(mm)
        four = lambda t: t[:, :].rearrange("p (t d) -> p t d", d=P)
        row = lambda t: t[:, :].unsqueeze(1).to_broadcast([P, 4, P])
        va = k.dve(lambda e, i: e.tensor_tensor(four(v), four(bank[3]), row(bv), ALU.add), mm, f_v.free)
        f_bank[3].read_by(va)
        for s in range(4):
            mm = k.pe(lambda e, i, s=s: e.matmul(bank[4][:, s * P:(s + 1) * P], qk[1][:, s * P:(s + 1) * P], qk[0][:, s * P:(s + 1) * P],
                                                 start=True, stop=True), qa, f_bank[4].free)
        f_qk[0].read_by(mm)
        f_qk[1].read_by(mm)
        aa = k.dve(lambda e, i: e.tensor_tensor(four(att), four(bank[4]), row(same), ALU.mult), mm, f_att.free)
        f_bank[4].read_by(aa)
        for s in range(4):
            mm = k.pe(lambda e, i, s=s: e.matmul(bank[5][:, s * P:(s + 1) * P], v[:, s * P:(s + 1) * P], att[:, s * P:(s + 1) * P],
                                                 start=True, stop=True), aa, va, f_bank[5].free)
        f_v.read_by(mm)
        f_att.read_by(mm)
        oc = k.act(lambda e, i: e.copy(oT[:, :], bank[5][:, :]), mm, f_oT.free)
        f_bank[5].read_by(oc)
        for s in range(4):
            mm = k.pe(lambda e, i, s=s: e.matmul(bank[6][:, s * P:(s + 1) * P], oT[:, s * P:(s + 1) * P], projT[:, :],
                                                 start=True, stop=True), oc, f_bank[6].free)
        f_oT.read_by(mm)
        a = k.dve(lambda e, i: e.tensor_tensor(t1[:, :], bank[6][:, :], t1[:, :], ALU.add), mm)
        f_bank[6].read_by(a)
        a = k.dve(lambda e, i: e.tensor_tensor(four(t1), four(t1), row(bp), ALU.add), a)
        f_t1.read_by(k.dve(lambda e, i: e.tensor_tensor(env.X[:, bass.ts(i, R4)], env.X[:, bass.ts(i, R4)], t1[:, :], ALU.add), a))
        k.barrier()


def l1_ffn(env, w):
    k, bank = env.k, env.bank
    E, I = 8, 128
    CENTER, LOWER, UPPER = 1.0 / np.e, 0.5 - np.log(4.0 / 3.0), 0.5
    with ExitStack() as st:
        sb = lambda name, shape, dt=F32: k.sb(st, name, shape, dt)
        k.straight()
        Wg, Wu, Wd = (sb(n, [P, E * P]) for n in ("Wg", "Wu", "Wd"))
        for t, s in ((Wg, "Wg"), (Wu, "Wu"), (Wd, "Wd")):
            k.dma("w", lambda e, i, t=t, s=s: e.dma_start(t[:, :].rearrange("p (e n) -> p e n", e=E), w[s].rearrange("e p n -> p e n")))
        Wr, _ = rows(k, st, "Wr", w["Wr"])
        temp, l = broadcast_row(k, st, "temp", w["temperature"])
        norm_tiles(env)
        last = [k.dve(lambda e, i: e.reciprocal(temp[:, :], temp[:, :]), l)]
        for t in range(NT):
            mm = k.pe(lambda e, i, t=t: e.matmul(bank[0][:, t * E:(t + 1) * E], env.yT[:, t * P:(t + 1) * P], Wr[:, :],
                                                 start=True, stop=True), l)
        NE = NT * E
        names = {n: sb(n, [P, NE]) for n in ("inh", "dist", "zone", "hot", "wz", "fb", "left", "key", "pick", "order")}
        small = {n: sb(n, [P, NT]) for n in ("wsum", "none", "top", "fsum")}
        A = {n: t[:, :] for n, t in {**names, **small}.items()}
        te = lambda n: A[n].rearrange("p (t e) -> p t e", e=E)
        col = lambda n: A[n].unsqueeze(2).to_broadcast([P, NT, E])
        last.append(mm)

        def step(eng, fn):
            last[:] = [eng(fn, last)]

        TS = lambda o, a, s1, s2, p1, p2=None: step(k.dve, lambda e, i: (
            e.tensor_scalar(A[o], A[a], s1, s2, p1, p2) if p2 is not None else e.tensor_scalar(A[o], A[a], s1, s2, p1)))
        TT = lambda o, a, b, p: step(k.dve, lambda e, i: e.tensor_tensor(A[o], A[a], A[b], p))
        TC = lambda o, a, c, p: step(k.dve, lambda e, i: e.tensor_tensor(te(o), te(a), col(c), p))
        RD = lambda o, a, p: step(k.dve, lambda e, i: e.tensor_reduce(A[o], te(a), AX.X, p))
        for n in range(E):
            step(k.dve, lambda e, i, n=n: e.memset(te("order")[:, :, n], float(E - n)))
        step(k.act, lambda e, i: e.activation(A["inh"], bank[0][:, 0:NE], ACT.Sigmoid, scale=temp[:, 0:1]))
        TS("zone", "inh", LOWER, None, ALU.is_ge)
        TS("hot", "inh", UPPER, None, ALU.is_le)
        TT("zone", "zone", "hot", ALU.mult)
        TS("dist", "inh", CENTER, None, ALU.subtract)
        step(k.act, lambda e, i: e.activation(A["dist"], A["dist"], ACT.Abs))
        step(k.act, lambda e, i: e.activation(A["wz"], A["dist"], ACT.Exp, scale=-1.0 / 0.1))
        step(k.act, lambda e, i: e.activation(A["fb"], A["dist"], ACT.Exp, scale=-1.0 / 0.3))
        TT("wz", "wz", "zone", ALU.mult)
        RD("wsum", "wz", ALU.add)
        TS("none", "wsum", 1e-8, None, ALU.is_lt)
        TS("left", "fb", 1.0, None, ALU.mult)
        TS("pick", "fb", 0.0, None, ALU.mult)
        for _ in range(2):
            RD("top", "left", ALU.max)
            TC("key", "left", "top", ALU.is_equal)
            TT("key", "key", "order", ALU.mult)
            RD("top", "key", ALU.max)
            TC("key", "key", "top", ALU.is_equal)
            TT("pick", "pick", "key", ALU.add)
            TS("key", "key", -4.0, None, ALU.mult)
            TT("left", "left", "key", ALU.add)
        TT("fb", "fb", "pick", ALU.mult)
        RD("fsum", "fb", ALU.add)
        TS("fsum", "fsum", 1e-8, None, ALU.max)
        step(k.dve, lambda e, i: e.reciprocal(A["fsum"], A["fsum"]))
        TC("fb", "fb", "fsum", ALU.mult)
        TT("fb", "fb", "wz", ALU.subtract)
        TC("fb", "fb", "none", ALU.mult)
        TT("wz", "wz", "fb", ALU.add)
        RD("wsum", "wz", ALU.add)
        TS("wsum", "wsum", 1e-8, None, ALU.max)
        step(k.dve, lambda e, i: e.reciprocal(A["wsum"], A["wsum"]))
        TC("wz", "wz", "wsum", ALU.mult)
        weights = names["wz"]
        hs = [sb("h", [P, R4]) for _ in range(2)]
        wt = sb("wt", [P, 4 * E])
        f_h, f_bank, f_wt = [Buffer(), Buffer()], [Buffer() for _ in range(8)], Buffer()
        k.barrier()
        k.loop(NT // 4)
        wc = k.dve(lambda e, i: e.tensor_copy(wt[:, :], weights[:, bass.ts(i, 4 * E)]), f_wt.free)
        for x in range(E):
            z = x % 2
            g = k.pe(lambda e, i, x=x, z=z: e.matmul(bank[z][:, :], Wg[:, x * P:(x + 1) * P], env.yT[:, bass.ts(i, R4)],
                                                     start=True, stop=True), f_bank[z].free)
            u = k.pe(lambda e, i, x=x, z=z: e.matmul(bank[2 + z][:, :], Wu[:, x * P:(x + 1) * P], env.yT[:, bass.ts(i, R4)],
                                                     start=True, stop=True), f_bank[2 + z].free)
            a = k.act(lambda e, i, z=z: e.activation(hs[z][:, :], bank[z][:, :], ACT.Silu), g, f_h[z].free)
            f_bank[z].read_by(a)
            m = k.dve(lambda e, i, z=z: e.tensor_tensor(hs[z][:, :], hs[z][:, :], bank[2 + z][:, :], ALU.mult), a, u)
            f_bank[2 + z].read_by(m)
            for s in range(4):
                mm = k.pe(lambda e, i, x=x, z=z, s=s: e.matmul(bank[4 + z][:, s * P:(s + 1) * P], hs[z][:, s * P:(s + 1) * P],
                                                               Wd[:, x * P:(x + 1) * P], start=True, stop=True), m, f_bank[4 + z].free)
            f_h[z].read_by(mm)
            for s in range(4):
                prior = f_bank[4 + (x + 1) % 2].readers if x else None
                ad = k.dve(lambda e, i, x=x, z=z, s=s: e.scalar_tensor_tensor(
                    env.X[:, bass.ts(4 * i + s, P)], bank[4 + z][:, s * P:(s + 1) * P], wt[:, s * E + x:s * E + x + 1],
                    env.X[:, bass.ts(4 * i + s, P)], ALU.mult, ALU.add), mm, wc, prior)
            f_bank[4 + z].read_by(ad)
        f_wt.read_by(ad)
        k.barrier()


def l2_cross_attention(env, w, ctx_kv):
    k, bank = env.k, env.bank
    DQ = 32
    with ExitStack() as st:
        sb = lambda name, shape, dt=F32: k.sb(st, name, shape, dt)
        k.straight()
        Wq, Wk, Wv = sb("Wq", [DQ, P]), sb("Wk", [DQ, P]), sb("Wv", [P, P])
        for t, n in ((Wq, "Wq"), (Wk, "Wk"), (Wv, "Wv")):
            k.dma("w", lambda e, i, t=t, n=n: e.dma_start(t[:, :], w[n]))
        bq, _ = columns(k, st, "bq", w["bq"], DQ)
        bk, _ = columns(k, st, "bk", w["bk"], DQ)
        bv = sb("bv", [1, P])
        l = k.dma("w", lambda e, i: e.dma_start(bv[:, :], w["bv"].rearrange("(a d) -> a d", a=1)))
        norm_tiles(env)
        A, WvT, cg, g0 = sb("A", [P, P]), sb("WvT", [P, P]), sb("cg", [P, 2]), sb("g0", [1, 1])
        k.pe(lambda e, i: e.matmul(bank[0][:, 0:P], Wq[:, :], Wk[:, :], start=True, stop=True), l)
        k.pe(lambda e, i: e.matmul(bank[0][:, P:P + 1], Wk[:, :], bq[:, :], start=True, stop=True))
        k.pe(lambda e, i: e.matmul(bank[0][:, P + 1:P + 2], Wq[:, :], bk[:, :], start=True, stop=True))
        k.pe(lambda e, i: e.matmul(bank[0][0:1, P + 2:P + 3], bq[:, :], bk[:, :], start=True, stop=True))
        t = k.pe(lambda e, i: e.transpose(bank[0][:, 2 * P:3 * P], Wv[:, :], env.ident[:, :]))
        k.dve(lambda e, i: e.tensor_copy(A[:, :], bank[0][:, 0:P]), t)
        k.dve(lambda e, i: e.tensor_copy(cg[:, :], bank[0][:, P:P + 2]), t)
        k.dve(lambda e, i: e.tensor_copy(g0[:, :], bank[0][0:1, P + 2:P + 3]), t)
        k.dve(lambda e, i: e.tensor_copy(WvT[:, :], bank[0][:, 2 * P:3 * P]), t)
        ND = 2
        per = lambda n, s: [sb(n, s) for _ in range(ND)]
        kv, kv_last, kvT = per("kv", [P, BPT * 2 * P]), per("kv_last", [1, BPT * P]), [sb("kvT", [P, CTX]) for _ in range(2)]
        qf, r, zT, zT_last = per("qf", [P, P]), per("r", [1, P]), per("zT", [P, BPT * 64]), per("zT_last", [1, P])
        U, zs = per("U", [P, P]), per("zs", [1, P])
        mk = lambda: [Buffer() for _ in range(ND)]
        f_kv, f_kvT, f_qf, f_r, f_z, f_zl, f_U, f_zs = (mk() for _ in range(8))
        f_bank = [Buffer() for _ in range(8)]
        k.barrier()
        k.loop(NT // ND)
        for d in range(ND):
            batch = lambda i, d=d: bass.ts(ND * i + d, BPT)
            for c in range(2):
                k.dma(f"kv{d}", lambda e, i, d=d, c=c, batch=batch: e.dma_start(
                    kv[d][:, :].rearrange("p (b c d) -> p c b d", b=BPT, c=2)[:, c],
                    ctx_kv[batch(i), c * P:(c + 1) * P, :].rearrange("b p d -> p b d")), f_kv[d].free)
            ld = k.dma(f"kv{d}", lambda e, i, d=d, batch=batch: e.dma_start(
                kv_last[d][:, :].rearrange("a (b d) -> a b d", b=BPT),
                ctx_kv[batch(i), 2 * P:CTX, :].rearrange("b c d -> c b d")), f_kv[d].free)
            mm = k.pe(lambda e, i, d=d: e.matmul(bank[0][:, 0:P], A[:, :], env.yT[:, bass.ts(ND * i + d, P)], start=True, stop=True),
                      f_bank[0].free)
            mr = k.pe(lambda e, i, d=d: e.matmul(bank[0][0:1, P:2 * P], cg[:, 1:2], env.yT[:, bass.ts(ND * i + d, P)],
                                                 start=True, stop=True))
            q1 = k.dve(lambda e, i, d=d: e.tensor_scalar(qf[d][:, :], bank[0][:, 0:P], cg[:, 0:1], None, ALU.add), mr, f_qf[d].free)
            q2 = k.dve(lambda e, i, d=d: e.tensor_scalar(r[d][:, :], bank[0][0:1, P:2 * P], g0[:, :], None, ALU.add), mr, f_r[d].free)
            f_bank[0].read_by(q2)
            S = bank[3 + d]
            for b in range(BPT):
                z = b % 2
                o = 2 * P * b
                k.pe(lambda e, i, d=d, z=z, o=o: e.transpose(bank[1 + z][:, 0:P], kv[d][:, o:o + P], env.ident[:, :]),
                     ld, f_bank[1 + z].free)
                k.pe(lambda e, i, d=d, z=z, o=o: e.transpose(bank[1 + z][:, P:2 * P], kv[d][:, o + P:o + 2 * P], env.ident[:, :]))
                t = k.pe(lambda e, i, d=d, z=z, b=b: e.transpose(bank[1 + z][:, 2 * P:CTX], kv_last[d][:, b * P:(b + 1) * P],
                                                                 env.ident[0:1, 0:1]))
                cp = (k.act if z else k.dve)(lambda e, i, z=z: (e.copy if z else e.tensor_copy)(
                    kvT[z][:, :], bank[1 + z][:, 0:CTX]), t, f_kvT[z].free)
                f_bank[1 + z].read_by(cp)
                for c in range(3):
                    m = P if c < 2 else 1
                    dst = S[0:m, b * 96 + c * 32:b * 96 + c * 32 + 32]
                    k.pe(lambda e, i, d=d, z=z, b=b, c=c, m=m, dst=dst: e.matmul(
                        dst, kvT[z][:, c * P:c * P + m], qf[d][:, b * SEQ:(b + 1) * SEQ], start=True, stop=False), cp, q1, f_bank[3 + d].free)
                    mm = k.pe(lambda e, i, d=d, b=b, m=m, dst=dst: e.matmul(
                        dst, env.ones[0:1, 0:m], r[d][:, b * SEQ:(b + 1) * SEQ], start=False, stop=True), q2)
                f_kvT[z].read_by(mm)
            f_qf[d].read_by(mm)
            f_r[d].read_by(mm)
            scale = DQ ** -0.5
            s1 = k.act(lambda e, i, d=d, S=S: e.activation(
                zT[d][:, :].rearrange("p (b q) -> p b q", b=BPT), S[:, 0:BPT * 96].rearrange("p (b q) -> p b q", b=BPT)[:, :, 0:64],
                ACT.Sigmoid, scale=scale), mm, f_z[d].free)
            s2 = k.act(lambda e, i, d=d, S=S: e.activation(
                zT_last[d][:, :].rearrange("p (b q) -> p b q", b=BPT), S[0:1, 0:BPT * 96].rearrange("p (b q) -> p b q", b=BPT)[:, :, 64:96],
                ACT.Sigmoid, scale=scale), mm, f_zl[d].free)
            f_bank[3 + d].read_by(s2)
            for b in range(BPT):
                for c in range(3):
                    src = (kv[d][:, (2 * b + c) * P:(2 * b + c + 1) * P] if c < 2 else kv_last[d][:, b * P:(b + 1) * P])
                    zz = (zT[d][:, b * 64 + c * 32:b * 64 + c * 32 + 32] if c < 2 else zT_last[d][:, b * 32:b * 32 + 32])
                    k.pe(lambda e, i, b=b, c=c, src=src, zz=zz: e.matmul(
                        bank[5][:, b * SEQ:(b + 1) * SEQ], src, zz, start=c == 0, stop=c == 2), s2, f_bank[5].free)
            zv = zT[d][:, :].rearrange("p (b c q) -> p b c q", b=BPT, c=2)
            for c in range(3):
                zz = zv[:, :, c] if c < 2 else zT_last[d][:, :]
                m = P if c < 2 else 1
                mm = k.pe(lambda e, i, c=c, zz=zz, m=m: e.matmul(bank[6][0:1, 0:P], env.ones[0:m, 0:1], zz, start=c == 0, stop=c == 2),
                          f_bank[6].free)
            f_kv[d].read_by(mm)
            f_z[d].read_by(mm)
            f_zl[d].read_by(mm)
            u1 = k.act(lambda e, i, d=d: e.copy(U[d][:, :], bank[5][:, 0:P]), mm, f_U[d].free)
            f_bank[5].read_by(u1)
            u2 = k.act(lambda e, i, d=d: e.copy(zs[d][:, :], bank[6][0:1, 0:P]), mm, f_zs[d].free)
            f_bank[6].read_by(u2)
            k.pe(lambda e, i, d=d: e.matmul(bank[7][:, 0:P], U[d][:, :], WvT[:, :], start=True, stop=False), u2, f_bank[7].free)
            mm = k.pe(lambda e, i, d=d: e.matmul(bank[7][:, 0:P], zs[d][:, :], bv[:, :], start=False, stop=True))
            f_U[d].read_by(mm)
            f_zs[d].read_by(mm)
            f_bank[7].read_by(k.dve(lambda e, i, d=d: e.tensor_tensor(
                env.X[:, bass.ts(ND * i + d, P)], env.X[:, bass.ts(ND * i + d, P)], bank[7][:, 0:P], ALU.add), mm))
        k.barrier()


class HeadAttention:

    def __init__(self, env, st, head_mask):
        k = env.k
        self.env, self.head_mask = env, head_mask
        sb = lambda n, s: k.sb(st, n, s)
        self.kh = [sb("kh", [P, BPT * H * SEQ]) for _ in range(2)]
        self.s = [sb("s", [P, 512]) for _ in range(2)]
        self.mx = [sb("mx", [P, H]) for _ in range(2)]
        self.sum = [sb("sum", [P, H]) for _ in range(2)]
        self.pT = [sb("pT", [P, H * P]) for _ in range(2)]
        for t in self.pT:
            k.pool(lambda e, i, t=t: e.memset(t[:, :], 0.0))
        self.f = {n: [Buffer(), Buffer()] for n in ("kh", "s", "mx", "sum", "pT")}

    def __call__(self, qT, kT, v, out, ready, f_bank, score_banks, out_banks, scale, table=None, out_free=None):
        k, bank, f = self.env.k, self.env.bank, self.f
        hb = lambda t: t.rearrange("p (h q) -> p h q", h=H)
        wide = lambda t: t[:, :].unsqueeze(2).to_broadcast([P, H, SEQ])

        def scores(s):
            z, sbank, kh = s % 2, score_banks[s % 2], self.kh[s % 2]
            masked = []
            for half in range(2):
                masked.append((k.dve, k.pool)[half](lambda e, i, half=half: e.tensor_tensor(
                    kh[:, :].rearrange("p (b h q) -> p b h q", b=BPT, h=H)[:, 2 * half:2 * half + 2],
                    kT[:, s * P:(s + 1) * P].rearrange("p (b q) -> p b q", b=BPT)[:, 2 * half:2 * half + 2].unsqueeze(2).to_broadcast([P, 2, H, SEQ]),
                    self.head_mask[:, :].unsqueeze(1).unsqueeze(3).to_broadcast([P, 2, H, SEQ]), ALU.mult), ready, f["kh"][z].free))
            for b in range(BPT):
                mm = k.pe(lambda e, i, b=b: e.matmul(
                    bank[sbank][b * SEQ:(b + 1) * SEQ, :], qT[:, s * P + b * SEQ:s * P + (b + 1) * SEQ], kh[:, b * 512:(b + 1) * 512],
                    start=True, stop=True, tile_position=(0, b * SEQ)), masked, f_bank[sbank].free)
            f["kh"][z].read_by(mm)
            return mm

        def exponentials(s, mm):
            z, sbank, S, mx = s % 2, score_banks[s % 2], self.s[s % 2], self.mx[s % 2]
            if table is not None:
                a = k.dve(lambda e, i: e.scalar_tensor_tensor(hb(bank[sbank][:, :]), hb(bank[sbank][:, :]), scale,
                                                              table[:, :].unsqueeze(1).to_broadcast([P, H, SEQ]), ALU.mult, ALU.add), mm)
            else:
                a = mm
            m = k.dve(lambda e, i: e.tensor_reduce(mx[:, :], hb(bank[sbank][:, :]), AX.X, ALU.max), a, f["mx"][z].free)
            d = k.dve(lambda e, i: e.tensor_tensor(hb(S[:, :]), hb(bank[sbank][:, :]), wide(mx), ALU.subtract), m, f["s"][z].free)
            f["mx"][z].read_by(d)
            f_bank[sbank].read_by(d)
            return k.act(lambda e, i: e.activation(S[:, :], S[:, :], ACT.Exp, scale=scale if table is None else 1.0), d)

        def turn(s, x):
            z, S, sm, pT = s % 2, self.s[s % 2], self.sum[s % 2], self.pT[s % 2]
            for b in range(BPT):
                t = k.dve(lambda e, i, b=b: e.transpose(
                    pT[:, :].rearrange("p (h b q) -> p b h q", h=H, b=BPT)[b * SEQ:(b + 1) * SEQ, b],
                    hb(S[:, :])[b * SEQ:(b + 1) * SEQ]), x, f["pT"][z].free)
            sr = k.dve(lambda e, i: e.tensor_reduce(sm[:, :], hb(S[:, :]), AX.X, ALU.add), x, f["sum"][z].free)
            rc = k.dve(lambda e, i: e.reciprocal(sm[:, :], sm[:, :]), sr)
            f["s"][z].read_by(sr)
            return t, rc

        def apply(s, t, rc):
            z, obank, sm, pT = s % 2, out_banks[s % 2], self.sum[s % 2], self.pT[s % 2]
            for h in range(H):
                mm = k.pe(lambda e, i, h=h: e.matmul(bank[obank][:, h * 8:(h + 1) * 8], pT[:, h * P:(h + 1) * P],
                                                     v[:, s * P + h * 8:s * P + (h + 1) * 8], start=True, stop=True), t, f_bank[obank].free)
            f["pT"][z].read_by(mm)
            o = k.dve(lambda e, i: e.tensor_tensor(
                out[:, s * P:(s + 1) * P].rearrange("p (h j) -> p h j", h=H), bank[obank][:, 0:P].rearrange("p (h j) -> p h j", h=H),
                sm[:, :].unsqueeze(2).to_broadcast([P, H, 8]), ALU.mult), mm, rc, out_free)
            f["sum"][z].read_by(o)
            f_bank[obank].read_by(o)
            return o

        made, raised, turned, outs = {0: scores(0), 1: scores(1)}, {}, {}, []
        raised[0] = exponentials(0, made[0])
        for s in range(4):
            if s + 1 < 4:
                raised[s + 1] = exponentials(s + 1, made[s + 1])
            turned[s] = turn(s, raised[s])
            if s + 2 < 4:
                made[s + 2] = scores(s + 2)
            if s:
                outs.append(apply(s - 1, *turned[s - 1]))
        outs.append(apply(3, *turned[3]))
        return outs


def l2_tables():
    f = np.float32
    t = np.arange(SEQ, dtype=f)
    freq = (1.0 / 10000.0 ** (np.arange(0, 8, 2, dtype=f) / f(8))).astype(f)
    angle = np.outer(t, freq).astype(f)
    cos, sin = np.cos(angle).astype(f), np.sin(angle).astype(f)
    cos8 = np.concatenate([cos, cos], 1)
    sin8 = np.concatenate([-sin, sin], 1)
    d = t[:, None] - t[None, :]
    bias = -0.1 * np.log(np.abs(d) + 1.0) + np.log(np.exp(-np.maximum(d, 0.0) * 0.01) + 1e-9)
    return {"rope_cos": np.tile(cos8, (BPT, H)).astype(f), "rope_sin": np.tile(sin8, (BPT, H)).astype(f),
            "distance_bias": np.tile(bias, (BPT, 1)).astype(f)}


def head_constants(env, st):
    k = env.k
    hm, sh = k.sb(st, "head_mask", [P, H]), k.sb(st, "same_head", [P, P])
    a = k.pool(lambda e, i: e.memset(hm[:, :], 1.0))
    b = k.pool(lambda e, i: e.affine_select(out=hm[:, :], in_=hm[:, :], compare_op=ALU.is_ge, fill=0.0, base=0,
                                            pattern=[[-8, H]], channel_multiplier=1), a)
    c = k.pool(lambda e, i: e.affine_select(out=hm[:, :], in_=hm[:, :], compare_op=ALU.is_ge, fill=0.0, base=7,
                                            pattern=[[8, H]], channel_multiplier=-1), b)
    d = k.dve(lambda e, i: e.tensor_copy(sh[:, :].rearrange("p (h j) -> p h j", h=H), hm[:, :].unsqueeze(2).to_broadcast([P, H, 8])), c)
    return hm, sh, d


def l2_attention(env, w, tables):
    k, bank = env.k, env.bank
    DL = 32
    with ExitStack() as st:
        sb = lambda name, shape, dt=F32: k.sb(st, name, shape, dt)
        k.straight()
        Wq, _ = rows(k, st, "Wq", w["Wq"])
        Wd, _ = rows(k, st, "Wd", w["Wkv_down"])
        Wo, _ = rows(k, st, "Wo", w["Wo"])
        bd, _ = columns(k, st, "bd", w["bkv_down"], DL)
        bias = sb("bias", [P, 3 * P])
        k.dma("w", lambda e, i: e.dma_start(bias[:, 0:P], w["bq"].partition_broadcast(P)))
        for t in range(2):
            k.dma("w", lambda e, i, t=t: e.dma_start(
                bias[:, (1 + t) * P:(2 + t) * P].rearrange("p (h j) -> p h j", h=H),
                w["bkv_up"].rearrange("(h two j) -> two h j", two=2, h=H)[t].partition_broadcast(P)))
        Wup = sb("Wup", [DL, 2 * P])
        for t in range(2):
            k.dma("w", lambda e, i, t=t: e.dma_start(
                Wup[:, t * P:(t + 1) * P].rearrange("l (h j) -> l h j", h=H),
                w["Wkv_up"].rearrange("l (h two j) -> l h two j", two=2, h=H)[:, :, t]))
        bo, _ = broadcast_row(k, st, "bo", w["bo"])
        cos, sin, dist = sb("cos", [P, P]), sb("sin", [P, P]), sb("dist", [P, SEQ])
        for t, n in ((cos, "rope_cos"), (sin, "rope_sin"), (dist, "distance_bias")):
            k.dma("w", lambda e, i, t=t, n=n: e.dma_start(t[:, :], tables[n]))
        norm_tiles(env)
        hm, sh, _ = head_constants(env, st)
        mean = sb("mean", [P, BPT])
        a = k.dve(lambda e, i: e.memset(mean[:, :], 0.0))
        for b in range(BPT):
            k.dve(lambda e, i, b=b: e.memset(mean[b * SEQ:(b + 1) * SEQ, b:b + 1], 1.0 / SEQ), a)
        attn = HeadAttention(env, st, hm)
        ys, lat = sb("ys", [P, R4]), sb("lat", [DL, R4])
        q, kk, v, t1, t2 = (sb(n, [P, R4]) for n in ("q", "kk", "v", "t1", "t2"))
        qT, kT, o, oT, gate, rot = (sb(n, [P, R4]) for n in ("qT", "kT", "o", "oT", "gate", "rot"))
        mem = sb("mem", [P, 8 * BPT])
        f_ys, f_lat, f_q, f_k, f_v, f_t1, f_t2, f_qT, f_kT, f_o, f_oT, f_g, f_mem = (Buffer() for _ in range(13))
        f_bank = [Buffer() for _ in range(8)]
        k.barrier()
        k.loop(NT // 4)
        yc = k.pool(lambda e, i: e.tensor_copy(ys[:, :], env.yT[:, bass.ts(i, R4)]), f_ys.free)
        mm = k.pe(lambda e, i: e.matmul(bank[0][0:DL, :], Wd[:, :], ys[:, :], start=True, stop=True), yc, f_bank[0].free)
        la = k.act(lambda e, i: e.activation(lat[:, :], bank[0][0:DL, :], ACT.Identity, bias=bd[:, 0:1]), mm, f_lat.free)
        f_bank[0].read_by(la)
        for s in range(4):
            z = 1 + s % 2
            k.pe(lambda e, i, s=s, z=z: e.matmul(bank[z][:, 0:P], ys[:, s * P:(s + 1) * P], Wq[:, :], start=True, stop=True),
                 f_bank[z].free)
            mm = k.pe(lambda e, i, s=s, z=z: e.matmul(bank[z][:, P:3 * P], lat[:, s * P:(s + 1) * P], Wup[:, :], start=True, stop=True), la)
            for n, (t, f) in enumerate(((q, f_q), (kk, f_k), (v, f_v))):
                e3 = k.dve(lambda e, i, n=n, t=t, s=s, z=z: e.tensor_tensor(
                    t[:, s * P:(s + 1) * P], bank[z][:, n * P:(n + 1) * P], bias[:, n * P:(n + 1) * P], ALU.add), mm, f.free)
            f_bank[z].read_by(e3)
        f_ys.read_by(mm)
        f_lat.read_by(mm)
        four = lambda t: t[:, :].rearrange("p (t d) -> p t d", d=P)
        row = lambda t: t[:, :].unsqueeze(1).to_broadcast([P, 4, P])
        halves = lambda t, n: t[:, :].rearrange("p (g two j) -> p g two j", two=2, j=4)[:, :, n]
        swap_sin = lambda n: sin[:, :].rearrange("p (h two j) -> p h two j", two=2, j=4)[:, :, n].unsqueeze(1).to_broadcast([P, 4, H, 4])
        hv = lambda t, n: t[:, :].rearrange("p (s h two j) -> p s h two j", s=4, two=2, j=4)[:, :, :, n]
        roped = []
        for t, f in ((q, f_q), (kk, f_k)):
            swaps = []
            for n in range(2):
                swaps.append(k.pool(lambda e, i, t=t, n=n: e.tensor_tensor(hv(t1, n), hv(t, 1 - n), swap_sin(n), ALU.mult), e3, f_t1.free))
            a = k.dve(lambda e, i, t=t: e.tensor_tensor(four(t2), four(t), row(cos), ALU.mult), e3, f_t2.free)
            b = k.dve(lambda e, i, t=t: e.tensor_tensor(t[:, :], t1[:, :], t2[:, :], ALU.add), a, swaps)
            f_t1.read_by(b)
            f_t2.read_by(b)
            roped.append(b)
        for s in range(4):
            k.pe(lambda e, i, s=s: e.transpose(bank[3][:, s * P:(s + 1) * P], q[:, s * P:(s + 1) * P], env.ident[:, :]),
                 roped, f_bank[3].free)
            t = k.pe(lambda e, i, s=s: e.transpose(bank[4][:, s * P:(s + 1) * P], kk[:, s * P:(s + 1) * P], env.ident[:, :]),
                     f_bank[4].free)
        c1 = k.act(lambda e, i: e.copy(qT[:, :], bank[3][:, :]), t, f_qT.free)
        c2 = k.act(lambda e, i: e.copy(kT[:, :], bank[4][:, :]), t, f_kT.free)
        f_bank[3].read_by(c1)
        f_bank[4].read_by(c2)
        f_q.read_by(t)
        for s in range(4):
            k.pe(lambda e, i, s=s: e.matmul(bank[7][:, s * BPT:(s + 1) * BPT], kk[:, s * P:(s + 1) * P], mean[:, :], start=True, stop=True),
                 f_bank[7].free)
            mm = k.pe(lambda e, i, s=s: e.matmul(bank[7][:, (4 + s) * BPT:(5 + s) * BPT], v[:, s * P:(s + 1) * P], mean[:, :],
                                                 start=True, stop=True))
        f_k.read_by(mm)
        mc = k.dve(lambda e, i: e.tensor_copy(mem[:, :], bank[7][:, 0:8 * BPT]), mm, f_mem.free)
        f_bank[7].read_by(mc)
        outs = attn(qT, kT, v, o, [c2], f_bank, (5, 6), (1, 2), 8 ** -0.5, dist, f_o.free)
        f_v.read_by(mm, outs[-1])
        f_kT.read_by(outs[-1])
        bq_ = lambda t: t[:, :].rearrange("p (b q) -> p b q", q=SEQ)
        a = k.dve(lambda e, i: e.tensor_tensor(bq_(gate), bq_(qT), mem[:, 0:16].unsqueeze(2).to_broadcast([P, 16, SEQ]), ALU.mult),
                  c1, mc, f_g.free)
        mm = k.pe(lambda e, i: e.matmul(bank[3][:, :], sh[:, :], gate[:, :], start=True, stop=True), a, f_bank[3].free)
        x = k.act(lambda e, i: e.activation(gate[:, :], bank[3][:, :], ACT.Tanh, scale=0.5), mm)
        f_bank[3].read_by(x)
        a = k.dve(lambda e, i: e.scalar_tensor_tensor(bq_(gate), bq_(gate), 1.0, mem[:, 16:32].unsqueeze(2).to_broadcast([P, 16, SEQ]),
                                                      ALU.add, ALU.mult), x)
        f_qT.read_by(a)
        f_mem.read_by(a)
        for s in range(4):
            t = k.pe(lambda e, i, s=s: e.transpose(bank[4][:, s * P:(s + 1) * P], o[:, s * P:(s + 1) * P], env.ident[:, :]),
                     outs, f_bank[4].free)
        f_o.read_by(t)
        a = k.dve(lambda e, i: e.scalar_tensor_tensor(oT[:, :], gate[:, :], 0.5 * 0.2, bank[4][:, :], ALU.mult, ALU.add), a, t, f_oT.free)
        f_bank[4].read_by(a)
        f_g.read_by(a)
        for s in range(4):
            mm = k.pe(lambda e, i, s=s: e.matmul(bank[0][:, s * P:(s + 1) * P], oT[:, s * P:(s + 1) * P], Wo[:, :], start=True, stop=True),
                      a, f_bank[0].free)
        f_oT.read_by(mm)
        xs = lambda i: env.X[:, bass.ts(i, R4)]
        a = k.dve(lambda e, i: e.tensor_tensor(xs(i), xs(i), bank[0][:, :], ALU.add), mm)
        f_bank[0].read_by(a)
        k.dve(lambda e, i: e.tensor_tensor(xs(i).rearrange("p (t d) -> p t d", d=P), xs(i).rearrange("p (t d) -> p t d", d=P), row(bo), ALU.add), a)
        k.barrier()


def l3_attention(env, w):
    k, bank = env.k, env.bank
    R, TOP = 64, 6
    with ExitStack() as st:
        sb = lambda name, shape, dt=F32: k.sb(st, name, shape, dt)
        y = sb("y", [P, NTOK])
        k.straight()
        in_rows, _ = rows(k, st, "in_rows", w["in_proj_w"])
        QK_rows = sb("QK_rows", [P, P])
        k.dma("w", lambda e, i: e.dma_start(QK_rows[0:R, :], w["Qp_w"]))
        k.dma("w", lambda e, i: e.dma_start(QK_rows[R:2 * R, :], w["Kp_w"]))
        out_rows, _ = rows(k, st, "out_rows", w["out_proj_w"])
        V_rows, _ = rows(k, st, "V_rows", w["Vp_w"])
        f1_rows, _ = rows(k, st, "f1_rows", w["ff1_w"])
        f2_rows, _ = rows(k, st, "f2_rows", w["ff2_w"])
        b_qk, _ = columns(k, st, "b_qk", w["in_proj_b"][0:2 * P])
        b_Q, _ = columns(k, st, "b_Q", w["Qp_b"], R)
        b_K, _ = columns(k, st, "b_K", w["Kp_b"], R)
        b_f1, _ = columns(k, st, "b_f1", w["ff1_b"])
        b_vV = sb("b_vV", [P, 2 * P])
        k.dma("w", lambda e, i: e.dma_start(b_vV[:, 0:P], w["in_proj_b"][2 * P:3 * P].partition_broadcast(P)))
        k.dma("w", lambda e, i: e.dma_start(b_vV[:, P:2 * P], w["Vp_b"].partition_broadcast(P)))
        b_out, _ = broadcast_row(k, st, "b_out", w["out_proj_b"])
        b_f2, _ = broadcast_row(k, st, "b_f2", w["ff2_b"])
        lam, _ = broadcast_row(k, st, "lam", w["lam"])
        g1, _ = broadcast_row(k, st, "g1", w["ln1_g"])
        be1, _ = broadcast_row(k, st, "be1", w["ln1_b"])
        g2, _ = broadcast_row(k, st, "g2", w["ln2_g"])
        be2, l = broadcast_row(k, st, "be2", w["ln2_b"])
        norm_tiles(env, y)
        inT, outT, QKT, vVT, f1T, f2T = (sb(n, [P, c * P]) for n, c in
                                         (("inT", 2), ("outT", 1), ("QKT", 1), ("vVT", 2), ("f1T", 4), ("f2T", 4)))
        transpose_blocks(env, in_rows, inT, 2, l)
        transpose_blocks(env, None, vVT, 2, l, src_at=lambda n: in_rows[:, 2 * P:3 * P] if n == 0 else V_rows[:, :], first_bank=1)
        transpose_blocks(env, out_rows, outT, 1, l, first_bank=2)
        transpose_blocks(env, QK_rows, QKT, 1, l, first_bank=3)
        transpose_blocks(env, f1_rows, f1T, 4, l)
        transpose_blocks(env, f2_rows, f2T, 4, l, first_bank=1)
        sig = k.act(lambda e, i: e.activation(lam[:, :], lam[:, :], ACT.Sigmoid), l)
        one_minus = sb("one_minus", [P, 1])
        k.dve(lambda e, i: e.tensor_scalar(one_minus[:, :], lam[:, :], -1.0, 1.0, ALU.mult, ALU.add), sig)
        hm, _, _ = head_constants(env, st)
        attn = HeadAttention(env, st, hm)
        norm = Norm4(env, st)
        ys, v, V2, o, oT, s1, x1T, mix = (sb(n, [P, R4]) for n in ("ys", "v", "V2", "o", "oT", "s1", "x1T", "mix"))
        qk = [sb("qT", [P, R4]), sb("kT", [P, R4])]
        QK = [sb("QT", [R, R4]), sb("KT", [R, R4])]
        W34 = SEQ + 2
        aw, rest, top = sb("aw", [P, 4 * W34]), sb("rest", [P, 4 * W34]), sb("top", [P, 32])
        amx, asm, sp = sb("amx", [P, 4]), sb("asm", [P, 4]), sb("sp", [P, 4 * SEQ])
        spT = sb("spT", [P, R4])
        hT = sb("hT", [P, 4 * R4])
        k.dve(lambda e, i: e.memset(aw[:, :], 2.0))
        k.dve(lambda e, i: e.memset(spT[:, :], 0.0))
        names = "ys v V2 o oT s1 x1T mix q k Q K aw rest top amx asm sp spT hT".split()
        f = {n: Buffer() for n in names}
        f_bank = [Buffer() for _ in range(8)]
        four = lambda t: t[:, :].rearrange("p (t d) -> p t d", d=P)
        row = lambda t: t[:, :].unsqueeze(1).to_broadcast([P, 4, P])
        k.barrier()
        k.loop(NT // 4)
        yc = k.pool(lambda e, i: e.tensor_copy(ys[:, :], env.yT[:, bass.ts(i, R4)]), f["ys"].free)
        made = []
        for n in range(4):
            wide = n < 2
            rows_ = P if wide else R
            lhs = inT[:, n * P:(n + 1) * P] if wide else QKT[:, (n - 2) * R:(n - 1) * R]
            dst = qk[n] if wide else QK[n - 2]
            b = b_qk[:, n:n + 1] if wide else (b_Q, b_K)[n - 2][:, 0:1]
            mm = k.pe(lambda e, i, n=n, lhs=lhs, rows_=rows_: e.matmul(bank[n][0:rows_, :], lhs, ys[:, :], start=True, stop=True),
                      yc, f_bank[n].free)
            a = k.act(lambda e, i, n=n, dst=dst, b=b, rows_=rows_: e.activation(dst[:, :], bank[n][0:rows_, :], ACT.Identity, bias=b),
                      mm, f["qkQK"[n]].free)
            f_bank[n].read_by(a)
            made.append(a)
        for s in range(4):
            z = 4 + s % 2
            mm = k.pe(lambda e, i, s=s, z=z: e.matmul(bank[z][:, 0:2 * P], ys[:, s * P:(s + 1) * P], vVT[:, :], start=True, stop=True),
                      f_bank[z].free)
            for n, t in ((0, v), (1, V2)):
                vb = k.dve(lambda e, i, s=s, z=z, n=n, t=t: e.tensor_tensor(
                    t[:, s * P:(s + 1) * P], bank[z][:, n * P:(n + 1) * P], b_vV[:, n * P:(n + 1) * P], ALU.add), mm,
                    f["v" if n == 0 else "V2"].free)
            f_bank[z].read_by(vb)
        f["ys"].read_by(mm)
        for s in range(4):
            for b in range(BPT):
                c = s * P + b * SEQ
                mm = k.pe(lambda e, i, s=s, b=b, c=c: e.matmul(
                    bank[3][b * SEQ:(b + 1) * SEQ, s * SEQ:(s + 1) * SEQ], QK[0][:, c:c + SEQ], QK[1][:, c:c + SEQ],
                    start=True, stop=True, tile_position=(0, b * SEQ)), made, f_bank[3].free, alone=True)
        f["Q"].read_by(mm)
        f["K"].read_by(mm)
        S3 = bank[3][:, 0:P].rearrange("p (s k) -> p s k", s=4)
        A3 = aw[:, :].rearrange("p (s k) -> p s k", s=4)[:, :, 0:SEQ]
        R3 = rest[:, :].rearrange("p (s k) -> p s k", s=4)[:, :, 0:SEQ]
        P3 = sp[:, :].rearrange("p (s k) -> p s k", s=4)
        wide4 = lambda t: t[:, :].unsqueeze(2).to_broadcast([P, 4, SEQ])
        a = k.dve(lambda e, i: e.tensor_reduce(amx[:, :], S3, AX.X, ALU.max), mm, f["amx"].free)
        a = k.dve(lambda e, i: e.tensor_tensor(A3, S3, wide4(amx), ALU.subtract), a, f["aw"].free)
        f_bank[3].read_by(a)
        f["amx"].read_by(a)
        a = k.act(lambda e, i: e.activation(A3, A3, ACT.Exp, scale=R ** -0.5), a)
        a = k.dve(lambda e, i: e.tensor_reduce(asm[:, :], A3, AX.X, ALU.add), a, f["asm"].free)
        a = k.dve(lambda e, i: e.reciprocal(asm[:, :], asm[:, :]), a)
        a = k.dve(lambda e, i: e.tensor_tensor(A3, A3, wide4(asm), ALU.mult), a)
        for s in range(4):
            t = k.dve(lambda e, i, s=s: e.max(top[:, 8 * s:8 * s + 8], aw[:, s * W34:(s + 1) * W34]), a, f["top"].free, alone=True)
        for s in range(4):
            m = k.dve(lambda e, i, s=s: e.match_replace(rest[:, s * W34:(s + 1) * W34], top[:, 8 * s:8 * s + 8],
                                                        aw[:, s * W34:(s + 1) * W34], 0.0), t, f["rest"].free, alone=True)
        f["top"].read_by(m)
        a = k.dve(lambda e, i: e.tensor_tensor(P3, A3, R3, ALU.subtract), m, f["sp"].free)
        f["aw"].read_by(a)
        f["rest"].read_by(a)
        a = k.dve(lambda e, i: e.tensor_reduce(asm[:, :], P3, AX.X, ALU.add), a)
        a = k.dve(lambda e, i: e.tensor_scalar(asm[:, :], asm[:, :], 1e-9, None, ALU.add), a)
        a = k.dve(lambda e, i: e.reciprocal(asm[:, :], asm[:, :]), a)
        a = k.dve(lambda e, i: e.tensor_tensor(P3, P3, wide4(asm), ALU.mult), a)
        f["asm"].read_by(a)
        for b in range(BPT):
            t = k.dve(lambda e, i, b=b: e.transpose(
                spT[:, :].rearrange("p (s b q) -> p b s q", s=4, b=BPT)[b * SEQ:(b + 1) * SEQ, b],
                P3[b * SEQ:(b + 1) * SEQ]), a, f["spT"].free)
        f["sp"].read_by(t)
        outs = attn(qk[0], qk[1], v, o, [made, vb], f_bank, (6, 7), (4, 5), 8 ** -0.5, None, f["o"].free)
        for n in "qkv":
            f[n].read_by(outs[-1])
        for s in range(4):
            mm = k.pe(lambda e, i, s=s: e.matmul(bank[0][:, s * P:(s + 1) * P], spT[:, s * P:(s + 1) * P], V2[:, s * P:(s + 1) * P],
                                                 start=True, stop=True), t, f_bank[0].free)
        f["spT"].read_by(mm)
        f["V2"].read_by(mm)
        for s in range(4):
            t = k.pe(lambda e, i, s=s: e.transpose(bank[1][:, s * P:(s + 1) * P], o[:, s * P:(s + 1) * P], env.ident[:, :]),
                     outs, f_bank[1].free)
        f["o"].read_by(t)
        oc = k.act(lambda e, i: e.copy(oT[:, :], bank[1][:, :]), t, f["oT"].free)
        f_bank[1].read_by(oc)
        for s in range(4):
            md = k.pe(lambda e, i, s=s: e.matmul(bank[2][:, s * P:(s + 1) * P], oT[:, s * P:(s + 1) * P], outT[:, :], start=True, stop=True),
                      oc, f_bank[2].free)
        f["oT"].read_by(md)
        a = k.dve(lambda e, i: e.tensor_tensor(four(mix), four(bank[2]), row(b_out), ALU.add), md, f["mix"].free)
        f_bank[2].read_by(a)
        b = k.dve(lambda e, i: e.scalar_tensor_tensor(s1[:, :], bank[0][:, :], one_minus[:, 0:1], y[:, bass.ts(i, R4)], ALU.mult, ALU.add),
                  mm, f["s1"].free)
        f_bank[0].read_by(b)
        a = k.dve(lambda e, i: e.scalar_tensor_tensor(s1[:, :], mix[:, :], lam[:, 0:1], s1[:, :], ALU.mult, ALU.add), a, b)
        f["mix"].read_by(a)
        n1 = norm(s1, s1, g1, be1, a)
        for s in range(4):
            t = k.pe(lambda e, i, s=s: e.transpose(bank[1][:, s * P:(s + 1) * P], s1[:, s * P:(s + 1) * P], env.ident[:, :]),
                     n1, f_bank[1].free)
        xc = k.act(lambda e, i: e.copy(x1T[:, :], bank[1][:, :]), t, f["x1T"].free)
        f_bank[1].read_by(xc)
        for c in range(4):
            n = 4 + c % 2
            mm = k.pe(lambda e, i, c=c, n=n: e.matmul(bank[n][:, :], f1T[:, c * P:(c + 1) * P], x1T[:, :], start=True, stop=True),
                      xc, f_bank[n].free)
            re = k.act(lambda e, i, c=c, n=n: e.activation(hT[:, c * R4:(c + 1) * R4], bank[n][:, :], ACT.Relu, bias=b_f1[:, c:c + 1]),
                       mm, f["hT"].free)
            f_bank[n].read_by(re)
        f["x1T"].read_by(mm)
        for s in range(4):
            for c in range(4):
                mm = k.pe(lambda e, i, s=s, c=c: e.matmul(bank[6][:, s * P:(s + 1) * P], hT[:, c * R4 + s * P:c * R4 + (s + 1) * P],
                                                          f2T[:, c * P:(c + 1) * P], start=c == 0, stop=c == 3), re, f_bank[6].free)
        f["hT"].read_by(mm)
        a = k.dve(lambda e, i: e.tensor_tensor(s1[:, :], bank[6][:, :], s1[:, :], ALU.add), mm)
        f_bank[6].read_by(a)
        a = k.dve(lambda e, i: e.tensor_tensor(four(s1), four(s1), row(b_f2), ALU.add), a)
        n2 = norm(s1, s1, g2, be2, a)
        f["s1"].read_by(k.dve(lambda e, i: e.tensor_tensor(env.X[:, bass.ts(i, R4)], env.X[:, bass.ts(i, R4)], s1[:, :], ALU.add), n2))
        k.barrier()


def l2_ffn(env, w, tables):
    k, bank = env.k, env.bank
    E, SETS, F = 32, 4, 32
    ES = E * SETS
    with ExitStack() as st:
        sb = lambda name, shape, dt=F32: k.sb(st, name, shape, dt)
        y = sb("y", [P, NTOK])
        k.straight()
        Wc, _ = rows(k, st, "Wc", w["Wc"].rearrange("d e s -> d (e s)"))
        bc = sb("bc", [P, 1])
        k.dma("w", lambda e, i: e.dma_start(bc[:, :], w["bc"].rearrange("e (s a) -> (e s) a", a=1)))
        b1 = sb("b1", [P, E])
        k.dma("w", lambda e, i: e.dma_start(b1[:, :], w["b1"].rearrange("e s f -> (s f) e")))
        b2 = sb("b2", [P, P])
        k.dma("w", lambda e, i: e.dma_start(b2[:, :], w["b2"].rearrange("e s d -> (e s) d")))
        tie = sb("tie", [P, SEQ])
        k.dma("w", lambda e, i: e.dma_start(tie[:, :], tables["tie"].partition_broadcast(P)))
        norm_tiles(env, y)
        pick = sb("pick", [P, NTOK])
        G = sb("G", [P, ES * BATCH])
        G3 = G[:, :].rearrange("p (x b) -> p x b", b=BATCH)
        lg, mx = sb("lg", [P, R4]), sb("mx", [P, 16])
        pk = sb("pk", [P, R4])
        pick_tok, ys = sb("pick_tok", [P, R4]), sb("ys", [P, R4])
        f_lg, f_mx, f_pk, f_pt, f_ys = (Buffer() for _ in range(5))
        f_bank = [Buffer() for _ in range(8)]
        k.barrier()
        k.loop(NT // 4)
        b32 = lambda t: t[:, :].rearrange("p (b t) -> p b t", t=SEQ)
        mm = k.pe(lambda e, i: e.matmul(bank[0][:, :], Wc[:, :], env.yT[:, bass.ts(i, R4)], start=True, stop=True), f_bank[0].free)
        a = k.dve(lambda e, i: e.tensor_scalar(lg[:, :], bank[0][:, :], bc[:, 0:1], None, ALU.add), mm, f_lg.free)
        f_bank[0].read_by(a)
        a = k.dve(lambda e, i: e.tensor_tensor(b32(lg), b32(lg), tie[:, :].unsqueeze(1).to_broadcast([P, 16, SEQ]), ALU.add), a)
        a = k.dve(lambda e, i: e.tensor_reduce(mx[:, :], b32(lg), AX.X, ALU.max), a, f_mx.free)
        a = k.dve(lambda e, i: e.tensor_tensor(b32(pk), b32(lg), mx[:, :].unsqueeze(2).to_broadcast([P, 16, SEQ]), ALU.is_equal), a, f_pk.free)
        f_lg.read_by(a)
        f_mx.read_by(a)
        pc = k.pool(lambda e, i: e.tensor_copy(pick[:, bass.ts(i, R4)], pk[:, :]), a)
        yc = k.pool(lambda e, i: e.tensor_copy(ys[:, :], y[:, bass.ts(i, R4)]), f_ys.free)
        for s in range(4):
            t = k.pe(lambda e, i, s=s: e.transpose(bank[1][:, s * P:(s + 1) * P], pk[:, s * P:(s + 1) * P], env.ident[:, :]),
                     a, f_bank[1].free)
        f_pk.read_by(t, pc)
        c = k.act(lambda e, i: e.copy(pick_tok[:, :], bank[1][:, :]), t, f_pt.free)
        f_bank[1].read_by(c)
        for s in range(4):
            for b in range(BPT):
                lo = b * SEQ
                mm = k.pe(lambda e, i, s=s, b=b, lo=lo: e.matmul(
                    bank[2 + b][:, s * P:(s + 1) * P], ys[lo:lo + SEQ, s * P:(s + 1) * P], pick_tok[lo:lo + SEQ, s * P:(s + 1) * P],
                    start=True, stop=True), c, yc, f_bank[2 + b].free)
        f_pt.read_by(mm)
        f_ys.read_by(mm)
        for b in range(BPT):
            eng = (k.dve, k.act)[b % 2]
            for s in range(4):
                op = eng(lambda e, i, b=b, s=s: (e.copy if b % 2 else e.tensor_copy)(
                    G3[:, :, bass.ds(16 * i + 4 * s + b, 1)].rearrange("p x a -> p (x a)"), bank[2 + b][:, s * P:(s + 1) * P]), mm)
            f_bank[2 + b].read_by(op)
        k.barrier()
        ND = 2
        dd = lambda n, s: [sb(n, s) for _ in range(ND)]
        W1, W2, W2T, Gs, inner = dd("W1", [P, P]), dd("W2", [P, P]), dd("W2T", [P, P]), dd("Gs", [P, 256]), dd("inner", [P, 256])
        for t in inner:
            k.dve(lambda e, i, t=t: e.memset(t[:, :], 0.0))
        mk = lambda: [Buffer() for _ in range(ND)]
        f_W1, f_W2, f_W2T, f_Gs, f_in = (mk() for _ in range(5))
        f_bank = [Buffer() for _ in range(8)]
        k.barrier()
        k.loop(E // ND)
        for d in range(ND):
            xp = lambda i, d=d: bass.ds(ND * i + d, 1)
            l1 = k.dma(f"kv{d}", lambda e, i, d=d, xp=xp: e.dma_start(
                W1[d][:, :].rearrange("p (s f) -> p s f", s=SETS), w["W1"][xp(i)].rearrange("a s d f -> d (a s) f")), f_W1[d].free)
            l2 = k.dma(f"kv{d}", lambda e, i, d=d, xp=xp: e.dma_start(
                W2[d][:, :].rearrange("p (s f) -> p s f", s=SETS), w["W2"][xp(i)].rearrange("a s d f -> d (a s) f")), f_W2[d].free)
            gc = k.pool(lambda e, i, d=d: e.tensor_copy(Gs[d][:, :], G[:, bass.ts(ND * i + d, 256)]), f_Gs[d].free)
            t = k.pe(lambda e, i, d=d: e.transpose(bank[d][:, 0:P], W2[d][:, :], env.ident[:, :]), l2, f_bank[d].free)
            f_W2[d].read_by(t)
            wc = k.dve(lambda e, i, d=d: e.tensor_copy(W2T[d][:, :], bank[d][:, 0:P]), t, f_W2T[d].free)
            f_bank[d].read_by(wc)
            for s in range(SETS):
                mm = k.pe(lambda e, i, d=d, s=s: e.matmul(
                    bank[2 + d][32 * s:32 * s + 32, 0:BATCH], W1[d][:, s * F:(s + 1) * F], Gs[d][:, s * BATCH:(s + 1) * BATCH],
                    start=True, stop=True, tile_position=(0, 32 * s)), gc, f_bank[2 + d].free)
            f_W1[d].read_by(mm)
            f_Gs[d].read_by(mm)
            for s in range(SETS):
                ra = k.act(lambda e, i, d=d, s=s: e.activation(
                    inner[d][32 * s:32 * s + 32, s * BATCH:(s + 1) * BATCH], bank[2 + d][32 * s:32 * s + 32, 0:BATCH], ACT.Relu,
                    bias=b1[32 * s:32 * s + 32, bass.ds(ND * i + d, 1)]), mm, f_in[d].free)
            f_bank[2 + d].read_by(ra)
            mm = k.pe(lambda e, i, d=d: e.matmul(bank[4 + d][:, 0:256], W2T[d][:, :], inner[d][:, :], start=True, stop=True),
                      ra, wc, f_bank[4 + d].free)
            f_W2T[d].read_by(mm)
            f_in[d].read_by(mm)
            f_bank[4 + d].read_by(k.dve(lambda e, i, d=d: e.tensor_copy(G[:, bass.ts(ND * i + d, 256)], bank[4 + d][:, 0:256]), mm, gc))
        k.barrier()
        Rb, rb, pt = dd("Rb", [P, 512]), dd("rb", [P, 512]), dd("pt", [P, P])
        f_Rb, f_rb, f_pt = (mk() for _ in range(3))
        f_bank = [Buffer() for _ in range(8)]
        k.loop(NT // ND)
        for d in range(ND):
            cps = [k.pool(lambda e, i, d=d: e.tensor_copy(pt[d][:, :], pick[:, bass.ts(ND * i + d, P)]), f_pt[d].free)]
            for b in range(BPT):
                cps.append((k.pool, k.dve)[b % 2](lambda e, i, d=d, b=b: e.tensor_copy(
                    Rb[d][:, b * P:(b + 1) * P], G3[:, :, bass.ds(4 * (ND * i + d) + b, 1)].rearrange("p x a -> p (x a)")), f_Rb[d].free))
            for b in range(BPT):
                t = k.pe(lambda e, i, d=d, b=b: e.transpose(bank[d][:, b * P:(b + 1) * P], Rb[d][:, b * P:(b + 1) * P], env.ident[:, :]),
                         cps, f_bank[d].free)
            f_Rb[d].read_by(t)
            a = k.dve(lambda e, i, d=d: e.tensor_tensor(
                rb[d][:, :].rearrange("p (b d) -> p b d", b=4), bank[d][:, :].rearrange("p (b d) -> p b d", b=4),
                b2[:, :].unsqueeze(1).to_broadcast([P, 4, P]), ALU.add), t, f_rb[d].free)
            f_bank[d].read_by(a)
            for b in range(BPT):
                mm = k.pe(lambda e, i, d=d, b=b: e.matmul(
                    bank[2 + d][b * SEQ:(b + 1) * SEQ, 0:P], pt[d][:, b * SEQ:(b + 1) * SEQ], rb[d][:, b * P:(b + 1) * P],
                    start=True, stop=True, tile_position=(0, b * SEQ)), a, f_bank[2 + d].free)
            f_rb[d].read_by(mm)
            f_pt[d].read_by(mm)
            f_bank[2 + d].read_by(k.dve(lambda e, i, d=d: e.tensor_tensor(
                env.X[:, bass.ts(ND * i + d, P)], env.X[:, bass.ts(ND * i + d, P)], bank[2 + d][:, 0:P], ALU.add), mm))
        k.barrier()


def tie_table():
    return {"tie": np.linspace(0.0, 1e-6, SEQ, dtype=np.float32)}


def l3_ffn(env, w, out):
    k, nc, bank = env.k, env.k.nc, env.bank
    E, F = 8, 256
    HID = E * P
    ex_dram = nc.dram_tensor("x_scratch", (NTOK, P), F32, kind="Internal").ap()
    pos = lambda c: (c % 4) * 2 + c // 4
    k.barrier()
    k.straight()
    a = k.dma("turn", lambda e, i: e.dma_start(ex_dram.rearrange("(t p) d -> p t d", p=P),
                                               env.X[:, :].rearrange("p (t d) -> p t d", d=P)))
    by_time = lambda dram: [dram.rearrange("(b j t) d -> t b j d", b=BATCH, t=2)[t] for t in range(2)]
    tiles = lambda t: env.X[t * BATCH:(t + 1) * BATCH, :].rearrange("b (j d) -> b j d", d=P)
    for t in range(2):
        k.dma("turn", lambda e, i, t=t: e.dma_start(tiles(t), by_time(ex_dram)[t]), a)
    k.barrier()
    norm_tiles(env)
    with ExitStack() as outer:
        slots = SEQ + 1
        s_num, s_expr, s_state = (k.sb(outer, n, [P, slots * 4]) for n in ("s_num", "s_expr", "s_state"))
        gram = k.sb(outer, "gram", [P, slots * 4 * E])
        same = k.sb(outer, "same_token", [P, P])
        same_expert = k.sb(outer, "same_expert", [P, E])
        a = k.pool(lambda e, i: e.memset(same[:, :], 1.0))
        s3 = same[:, :].rearrange("p (b e) -> p b e", e=E)
        a = k.pool(lambda e, i: e.affine_select(out=s3, in_=s3, compare_op=ALU.is_ge, fill=0.0, base=0,
                                                pattern=[[-E, 16], [0, E]], channel_multiplier=1), a)
        a = k.pool(lambda e, i: e.affine_select(out=s3, in_=s3, compare_op=ALU.is_ge, fill=0.0, base=E - 1,
                                                pattern=[[E, 16], [0, E]], channel_multiplier=-1), a)
        k.dve(lambda e, i: e.tensor_reduce(same_expert[:, :], env.ident[:, :].rearrange("p (b e) -> p e b", e=E), AX.X, ALU.add))
        with ExitStack() as st:
            sb = lambda name, shape, dt=F32: k.sb(st, name, shape, dt)
            WhhT = sb("WhhT", [P, E * 3 * HID])
            W3 = WhhT[:, :].rearrange("p (c g) -> p c g", c=E)
            WihT = sb("WihT", [P, 3 * HID])
            ctxT = sb("ctxT", [P, HID])
            ctx_b = sb("ctx_b", [P, E])
            raw = [sb("raw", [P, HID]) for _ in range(2)]
            rawi = [sb("rawi", [P, P]) for _ in range(2)]
            k.straight()
            k.dma("w", lambda e, i: e.dma_start(ctx_b[:, :], w["ctx_b"].rearrange("(c p) -> p c", p=P)))
            f_raw, f_rawi = [Buffer(), Buffer()], [Buffer(), Buffer()]
            f_bank = [Buffer() for _ in range(8)]
            k.loop(3 * E // 2)
            for d in range(2):
                q = lambda i, d=d: 2 * i + d
                l = k.dma(f"kv{d}", lambda e, i, d=d, q=q: e.dma_start(raw[d][:, :], w["gru_w_hh"][bass.ts(q(i), P), :]), f_raw[d].free)
                l = k.dma(f"kv{d}", lambda e, i, d=d, q=q: e.dma_start(rawi[d][:, :], w["gru_w_ih"][bass.ts(q(i), P), :]), f_rawi[d].free)
                for half in range(2):
                    b = 2 * d + half
                    for r in range(4):
                        t = k.pe(lambda e, i, d=d, b=b, r=r, half=half: e.transpose(
                            bank[b][:, r * P:(r + 1) * P], raw[d][:, (4 * half + r) * P:(4 * half + r + 1) * P], env.ident[:, :]),
                            l, f_bank[b].free)
                    eng, op = ((k.dve, "dve"), (k.act, "act"))[half]
                    c = eng(lambda e, i, b=b, half=half, q=q, op=op: (e.tensor_copy if op == "dve" else e.copy)(
                        W3[:, 4 * half:4 * half + 4, bass.ts(q(i), P)], bank[b][:, :].rearrange("p (c g) -> p c g", c=4)), t)
                    f_bank[b].read_by(c)
                f_raw[d].read_by(t)
                t = k.pe(lambda e, i, d=d: e.transpose(bank[4 + d][:, 0:P], rawi[d][:, :], env.ident[:, :]), f_bank[4 + d].free)
                f_rawi[d].read_by(t)
                f_bank[4 + d].read_by(k.dve(lambda e, i, d=d, q=q: e.tensor_copy(WihT[:, bass.ts(q(i), P)], bank[4 + d][:, 0:P]), t))
            k.barrier()
            HALF = HID // 2
            k.straight()
            l = k.dma("w0", lambda e, i: e.dma_start(raw[0][:, :].rearrange("p (c h) -> p c h", c=E),
                                                    w["ctx_w"].rearrange("(c p) h -> p c h", p=P)))
            hb = sb("hb", [P, HALF])
            hT = sb("hT", [P, HID * BATCH // P])
            b0 = sb("b0", [P, HALF])
            for hf in range(2):
                lb = k.dma("w1", lambda e, i, hf=hf: e.dma_start(
                    b0[hf * BATCH:(hf + 1) * BATCH, :], w["ctx_b"][hf * HALF:(hf + 1) * HALF].partition_broadcast(BATCH)))
            done = transpose_blocks(env, raw[0], ctxT, E, l)
            mean = sb("mean", [P, BATCH])
            m = k.dve(lambda e, i: e.tensor_reduce(mean[:, :], env.yT[:, :].rearrange("p (t b) -> p b t", b=BATCH), AX.X, ALU.add))
            m = k.dve(lambda e, i: e.tensor_scalar(mean[:, :], mean[:, :], 1.0 / SEQ, None, ALU.mult), m)
            for hf in range(2):
                mm = k.pe(lambda e, i, hf=hf: e.matmul(bank[5][hf * BATCH:(hf + 1) * BATCH, :], mean[:, :], ctxT[:, hf * HALF:(hf + 1) * HALF],
                                                       start=True, stop=True, tile_position=(0, hf * BATCH)), m, done)
            k.dve(lambda e, i: e.tensor_tensor(hb[:, :], bank[5][:, :], b0[:, :], ALU.add), mm, lb)
            r_, z_, n_, d_, t_ = (sb(nm, [P, HALF]) for nm in ("r", "z", "n", "d", "t"))
            xt = sb("xt", [P, BATCH])
            R, HN, XN, ZA, ZB, TA, TB, GR = range(8)
            f = {nm: Buffer() for nm in ("r", "z", "n", "d", "t", "xt", "xp", "hT", "rb", "dv", "pr", "sq")}
            made = [Buffer(), Buffer()]
            f_bank = [Buffer() for _ in range(8)]
            Q = HALF // 2
            exprT = sb("exprT", [P, HID])
            xp = sb("xp", [P, BATCH])
            rb, dv, pr, sq = (sb(nm, [P, HALF]) for nm in ("rb", "dv", "pr", "sq"))
            l = k.dma("w2", lambda e, i: e.dma_start(raw[1][:, :].rearrange("p (c h) -> p c h", c=E),
                                                    w["expr_w"].rearrange("(c p) h -> p c h", p=P)))
            transpose_blocks(env, raw[1], exprT, E, l)
            k.dve(lambda e, i: e.memset(xt[:, :], 0.0))
            four = lambda t: t[:, :].rearrange("p (c d) -> p c d", c=4)

            def routing_work(made, EX, GR, turned, f_bank, tt):
                done = []
                pc = k.pool(lambda e, i: e.tensor_copy(rb[:, :].rearrange("p (b q) -> p q b", q=E),
                                                       hT[:, :].rearrange("p (q b) -> p q b", q=E)), turned, f["rb"].free, alone=True)
                for hf in range(2):
                    mx = k.pe(lambda e, i, hf=hf: e.matmul(bank[EX][hf * BATCH:(hf + 1) * BATCH, :], xp[:, :], exprT[:, hf * HALF:(hf + 1) * HALF],
                                                           start=True, stop=True, tile_position=(0, hf * BATCH)), xo, turned)
                f["xp"].read_by(mx)
                for g in range(4):
                    mg = k.pe(lambda e, i, g=g: e.matmul(bank[GR][:, g * P:(g + 1) * P], rb[:, g * P:(g + 1) * P], rb[:, g * P:(g + 1) * P],
                                                         start=True, stop=True), pc, f_bank[GR].free)
                f["rb"].read_by(mg)
                a = k.dve(lambda e, i: e.tensor_tensor(pr[:, :], hb[:, :], bank[EX][:, :], ALU.mult), mx, f["pr"].free, [b.free for b in made])
                done.append(a)
                b = k.act(lambda e, i: e.activation(sq[:, :], bank[EX][:, :], ACT.Square), a, f["sq"].free)
                f_bank[EX].read_by(b)
                f["pr"].read_by(k.dve(lambda e, i: e.tensor_reduce(s_num[:, bass.ts(i, 4)], four(pr), AX.X, ALU.add), a))
                b = k.dve(lambda e, i: e.tensor_reduce(s_expr[:, bass.ts(i, 4)], four(sq), AX.X, ALU.add), b)
                b = k.act(lambda e, i: e.activation(sq[:, :], hb[:, :], ACT.Square), b)
                done.append(b)
                f["sq"].read_by(k.dve(lambda e, i: e.tensor_reduce(s_state[:, bass.ts(i, 4)], four(sq), AX.X, ALU.add), b))
                a = k.dve(lambda e, i: e.tensor_tensor(four(dv), four(bank[GR]), same[:, :].unsqueeze(1).to_broadcast([P, 4, P]), ALU.mult),
                          mg, f["dv"].free)
                f_bank[GR].read_by(a)
                f["dv"].read_by(k.dve(lambda e, i: e.tensor_reduce(
                    gram[:, bass.ts(i, 4 * E)].rearrange("p (g f) -> p g f", g=4),
                    dv[:, :].rearrange("p (g b f) -> p g f b", g=4, f=E), AX.X, ALU.add), a))
                return done

            k.barrier()
            k.loop(SEQ)
            xo = k.pool(lambda e, i: e.tensor_copy(xp[:, :], xt[:, :]), f["xt"].free, f["xp"].free, alone=True)
            xc = k.pool(lambda e, i: e.tensor_copy(xt[:, :], env.yT[:, bass.ts(i, BATCH)]), f["xt"].free, xo, alone=True)

            def product(b, gate, kc, cols, start, stop, *waits):
                for hf in range(2):
                    lhs = xt[:, :] if kc is None else hT[:, pos(kc) * BATCH:(pos(kc) + 1) * BATCH]
                    g = gate * HID + hf * HALF
                    rhs = (WihT[:, g + cols.start:g + cols.stop] if kc is None else W3[:, kc, g + cols.start:g + cols.stop])
                    mm = k.pe(lambda e, i, hf=hf, lhs=lhs, rhs=rhs, n=cols.stop - cols.start: e.matmul(
                        bank[b][hf * BATCH:(hf + 1) * BATCH, 0:n], lhs, rhs, start=start, stop=stop, tile_position=(0, hf * BATCH)),
                        *waits)
                return mm

            every, cA, cB = slice(0, HALF), slice(0, Q), slice(Q, HALF)
            xm = product(XN, 2, None, every, True, True, xc, f_bank[XN].free)
            product(R, 0, None, every, True, False, f_bank[R].free)
            product(ZA, 1, None, cA, True, False, f_bank[ZA].free)
            xl = product(ZB, 1, None, cB, True, False, f_bank[ZB].free)
            f["xt"].read_by(xl)
            turned = []
            for half, (b, order) in enumerate(((TA, (0, 4, 1, 5)), (TB, (2, 6, 3, 7)))):
                for c in range(2):
                    tt = k.pe(lambda e, i, b=b, c=c, half=half: e.transpose(
                        bank[b][:, c * P:(c + 1) * P], hb[:, half * Q + c * P:half * Q + (c + 1) * P], env.ident[:, :]),
                        made[half].free, f_bank[b].free)
                ev = k.act(lambda e, i, b=b, half=half: e.copy(hT[:, half * Q:(half + 1) * Q], bank[b][:, 0:Q]), tt,
                           f["hT"].free)
                f_bank[b].read_by(ev)
                turned.append(ev)
                for kc in order:
                    rm = product(R, 0, kc, every, False, kc == 7, ev)
            hb_read = routing_work(made, TA, GR, turned, f_bank, tt)
            for kc in range(E):
                hm = product(HN, 2, kc, every, kc == 0, kc == 7, f_bank[HN].free)
            for kc in range(E):
                zA = product(ZA, 1, kc, cA, False, kc == 7)
            for kc in range(E):
                zB = product(ZB, 1, kc, cB, False, kc == 7)
            f["hT"].read_by(zB)
            a = k.act(lambda e, i: e.activation(r_[:, :], bank[R][:, :], ACT.Tanh, scale=0.5), rm, f["r"].free)
            f_bank[R].read_by(a)
            a = k.dve(lambda e, i: e.scalar_tensor_tensor(t_[:, :], r_[:, :], 1.0, bank[HN][:, :], ALU.add, ALU.mult), a, hm, f["t"].free)
            f_bank[HN].read_by(a)
            f["r"].read_by(a)
            a = k.dve(lambda e, i: e.scalar_tensor_tensor(t_[:, :], t_[:, :], 0.5, bank[XN][:, :], ALU.mult, ALU.add), a, xm)
            f_bank[XN].read_by(a)
            nn = k.act(lambda e, i: e.activation(n_[:, :], t_[:, :], ACT.Tanh), a, f["n"].free)
            f["t"].read_by(nn)
            dd = k.dve(lambda e, i: e.tensor_tensor(d_[:, :], hb[:, :], n_[:, :], ALU.subtract), nn, f["d"].free,
                       [b.free for b in made])
            for half, (b, zm, s) in enumerate(((ZA, zA, cA), (ZB, zB, cB))):
                a = k.act(lambda e, i, s=s, b=b: e.activation(z_[:, s], bank[b][:, 0:Q], ACT.Tanh, scale=0.5), zm, f["z"].free)
                f_bank[b].read_by(a)
                a = k.dve(lambda e, i, s=s: e.scalar_tensor_tensor(d_[:, s], z_[:, s], 1.0, d_[:, s], ALU.add, ALU.mult), a, dd)
                a = k.dve(lambda e, i, s=s: e.scalar_tensor_tensor(hb[:, s], d_[:, s], 0.5, n_[:, s], ALU.mult, ALU.add), a, tt, hb_read)
                made[half].read_by(a)
            for nm in ("z", "n", "d"):
                f[nm].read_by(a)
            k.barrier()
            k.loop(1)
            k.seg.first = SEQ
            for c in range(4):
                tt = k.pe(lambda e, i, c=c: e.transpose(bank[TB][:, c * P:(c + 1) * P], hb[:, c * P:(c + 1) * P], env.ident[:, :]))
            ev = k.act(lambda e, i: e.copy(hT[:, :], bank[TB][:, :]), tt)
            xo = k.pool(lambda e, i: e.tensor_copy(xp[:, :], xt[:, :]))
            f = {nm: Buffer() for nm in f}
            routing_work([Buffer(), Buffer()], TA, GR, [ev], [Buffer() for _ in range(8)], tt)
            k.barrier()
        with ExitStack() as st:
            sb = lambda name, shape, dt=F32: k.sb(st, name, shape, dt)
            k.straight()
            NE = NT * E
            NG = SEQ * 4
            nm = {n: sb(n, [P, NE]) for n in ("num", "den", "tmp", "cos", "key", "pick", "one", "order", "expr2", "state2")}
            sm = {n: sb(n, [P, NT]) for n in ("top", "first", "second")}
            pen = {n: sb(n, [P, NG]) for n in ("inv", "dev2", "pb")}
            gw = {n: sb(n, [P, NG * E]) for n in ("own", "norm")}
            one = sb("pen1", [P, 1])
            A = {n: t[:, :] for n, t in {**nm, **sm, **pen, **gw, "pen1": one}.items()}
            G = gram[:, 4 * E:].rearrange("p (m f) -> p m f", f=E)
            gx = lambda n: A[n].rearrange("p (m f) -> p m f", f=E)
            expert = same_expert[:, :].unsqueeze(1).to_broadcast([P, NG, E])
            by_row = lambda n: A[n].unsqueeze(2).to_broadcast([P, NG, E])
            te = lambda n: A[n].rearrange("p (t e) -> p t e", e=E)
            col = lambda n: A[n].unsqueeze(2).to_broadcast([P, NT, E])
            last = []

            def step(eng, fn):
                last[:] = [eng(fn, last)]

            TS = lambda o, a, s1, s2, p1, p2=None: step(k.dve, lambda e, i: (
                e.tensor_scalar(A[o], A[a], s1, s2, p1, p2) if p2 is not None else e.tensor_scalar(A[o], A[a], s1, s2, p1)))
            TT = lambda o, a, b, p: step(k.dve, lambda e, i: e.tensor_tensor(A[o], A[a], A[b], p))
            TC = lambda o, a, c, p: step(k.dve, lambda e, i: e.tensor_tensor(te(o), te(a), col(c), p))
            RD = lambda o, a, p: step(k.dve, lambda e, i: e.tensor_reduce(A[o], te(a), AX.X, p))
            RC = lambda o: step(k.dve, lambda e, i: e.reciprocal(A[o], A[o]))
            AC = lambda o, a, fn, scale=1.0: step(k.act, lambda e, i: e.activation(A[o], A[a], fn, scale=scale))
            step(k.dve, lambda e, i: e.tensor_tensor(gx("own"), G, expert, ALU.mult))
            step(k.dve, lambda e, i: e.tensor_reduce(A["inv"], gx("own"), AX.X, ALU.add))
            AC("inv", "inv", ACT.Sqrt)
            TS("inv", "inv", 1e-12, None, ALU.max)
            RC("inv")
            step(k.dve, lambda e, i: e.tensor_tensor(gx("own"), by_row("inv"), expert, ALU.mult))
            step(k.dve, lambda e, i: e.tensor_tensor(gx("norm"), G, by_row("inv"), ALU.mult))
            for n in range(2):
                s = slice(n * 512, (n + 1) * 512)
                step(k.pe, lambda e, i, s=s, n=n: e.matmul(bank[n][:, :], same[:, :], A["own"][:, s], start=True, stop=True))
                step(k.dve, lambda e, i, s=s, n=n: e.tensor_tensor(A["norm"][:, s], A["norm"][:, s], bank[n][:, :], ALU.mult))
            step(k.dve, lambda e, i: e.tensor_tensor(gx("norm"), gx("norm"), expert, ALU.subtract))
            AC("norm", "norm", ACT.Square)
            step(k.dve, lambda e, i: e.tensor_reduce(A["dev2"], gx("norm"), AX.X, ALU.add))
            AC("inv", "dev2", ACT.Sqrt)
            TS("inv", "inv", 1e-12, None, ALU.max)
            RC("inv")
            TT("pb", "inv", "inv", ALU.mult)
            TT("pb", "pb", "dev2", ALU.mult)
            step(k.dve, lambda e, i: e.tensor_reduce(A["pen1"], A["pb"], AX.X, ALU.add))
            step(k.pe, lambda e, i: e.matmul(bank[0][:, 0:1], env.ones[:, :], one[:, :], start=True, stop=True))
            step(k.dve, lambda e, i: e.tensor_scalar(one[:, :], bank[0][:, 0:1], 1.0 / NTOK, 1.0, ALU.mult, ALU.add))
            for name, src in (("num", s_num), ("expr2", s_expr), ("state2", s_state)):
                for t in range(2):
                    for hf in range(2):
                        step(k.dve, lambda e, i, name=name, src=src, t=t, hf=hf: e.tensor_copy(
                            te(name)[t * BATCH:(t + 1) * BATCH, :, hf * 4:hf * 4 + 4],
                            src[hf * BATCH:(hf + 1) * BATCH, 4:].rearrange("p (j t c) -> p t j c", t=2, c=4)[:, t]))
            AC("one", "state2", ACT.Sqrt)
            TS("one", "one", 1e-12, None, ALU.max)
            RC("one")
            TT("num", "num", "one", ALU.mult)
            TT("state2", "state2", "one", ALU.mult)
            TT("state2", "state2", "one", ALU.mult)
            for src, dst in (("expr2", "den"), ("state2", "tmp")):
                AC(dst, src, ACT.Sqrt)
                TS(dst, dst, 1e-8, None, ALU.max)
            TT("den", "den", "tmp", ALU.mult)
            RC("den")
            TT("cos", "num", "den", ALU.mult)
            TS("cos", "cos", -1.0, 1.0, ALU.mult, ALU.add)
            step(k.dve, lambda e, i: e.tensor_scalar(A["cos"], A["cos"], one[:, 0:1], None, ALU.mult))
            for n in range(E):
                step(k.dve, lambda e, i, n=n: e.memset(te("order")[:, :, n], float(E - n)))
            for n, name in enumerate(("first", "second")):
                RD(name, "cos", ALU.max)
                TC("key", "cos", name, ALU.is_equal)
                TT("key", "key", "order", ALU.mult)
                RD("top", "key", ALU.max)
                TC("key" if n else "pick", "key", "top", ALU.is_equal)
                if n == 0:
                    TS("tmp", "pick", -3.0e38, None, ALU.mult)
                    TT("cos", "cos", "tmp", ALU.add)
            TT("second", "second", "first", ALU.subtract)
            AC("second", "second", ACT.Exp)
            TC("key", "key", "second", ALU.mult)
            TT("pick", "pick", "key", ALU.add)
            TS("second", "second", 1.0, None, ALU.add)
            RC("second")
            TC("pick", "pick", "second", ALU.mult)
            share = nm["pick"]
            NX = E + 1
            up, gate_, down = (sb(n, [P, NX * F]) for n in ("upT", "gateT", "downT"))
            rawg, rawu, rawd = (sb(n, [P, NX * F]) for n in ("rawg", "rawu", "rawd"))
            for t, a, b in ((rawg, "gate_w", "shared_gate_w"), (rawu, "up_w", "shared_up_w")):
                v = t[:, :].rearrange("p (c h) -> p c h", h=P)
                k.dma("w", lambda e, i, v=v, a=a: e.dma_start(v[:, 0:2 * E], w[a].rearrange("x (c p) h -> p (x c) h", p=P)))
                k.dma("w", lambda e, i, v=v, b=b: e.dma_start(v[:, 2 * E:2 * NX], w[b].rearrange("(c p) h -> p c h", p=P)))
            k.dma("w", lambda e, i: e.dma_start(rawd[:, 0:E * F].rearrange("p (x f) -> p x f", f=F), w["down_w"].rearrange("x p f -> p x f")))
            l = k.dma("w", lambda e, i: e.dma_start(rawd[:, E * F:NX * F], w["shared_down_w"]))
            for src, dst in ((rawg, gate_), (rawu, up), (rawd, down)):
                transpose_blocks(env, src, dst, 2 * NX, [l, last])
            hs = [[sb("h", [P, R4]) for _ in range(2)] for _ in range(2)]
            wt = sb("wt", [P, 4 * E])
            f_h, f_bank, f_wt = [Buffer(), Buffer()], [Buffer() for _ in range(8)], Buffer()
            k.barrier()
            k.loop(NT // 4)
            wc = k.dve(lambda e, i: e.tensor_copy(wt[:, :], share[:, bass.ts(i, 4 * E)]), f_wt.free)
            ad = None
            for x in range(NX):
                z = x % 2
                ms = []
                for c in range(2):
                    o = (2 * x + c) * P
                    g = k.pe(lambda e, i, c=c, o=o: e.matmul(bank[c][:, :], gate_[:, o:o + P], env.yT[:, bass.ts(i, R4)],
                                                             start=True, stop=True), f_bank[c].free)
                    u = k.pe(lambda e, i, c=c, o=o: e.matmul(bank[2 + c][:, :], up[:, o:o + P], env.yT[:, bass.ts(i, R4)],
                                                             start=True, stop=True), f_bank[2 + c].free)
                    a = k.act(lambda e, i, c=c, z=z: e.activation(hs[z][c][:, :], bank[c][:, :], ACT.Silu), g, f_h[z].free)
                    f_bank[c].read_by(a)
                    m = k.dve(lambda e, i, c=c, z=z: e.tensor_tensor(hs[z][c][:, :], hs[z][c][:, :], bank[2 + c][:, :], ALU.mult), a, u)
                    f_bank[2 + c].read_by(m)
                    ms.append(m)
                for s in range(4):
                    for c in range(2):
                        o = (2 * x + c) * P
                        mm = k.pe(lambda e, i, c=c, o=o, z=z, s=s: e.matmul(
                            bank[4 + z][:, s * P:(s + 1) * P], hs[z][c][:, s * P:(s + 1) * P], down[:, o:o + P],
                            start=c == 0, stop=c == 1), ms, f_bank[4 + z].free)
                f_h[z].read_by(mm)
                if x < E:
                    prior = ad
                    for s in range(4):
                        ad = k.dve(lambda e, i, x=x, z=z, s=s: e.scalar_tensor_tensor(
                            env.X[:, bass.ts(4 * i + s, P)], bank[4 + z][:, s * P:(s + 1) * P], wt[:, s * E + x:s * E + x + 1],
                            env.X[:, bass.ts(4 * i + s, P)], ALU.mult, ALU.add), mm, wc, prior)
                else:
                    f_wt.read_by(ad)
                    ad = k.dve(lambda e, i, z=z: e.tensor_tensor(env.X[:, bass.ts(i, R4)], env.X[:, bass.ts(i, R4)], bank[4 + z][:, :], ALU.add), mm, ad)
                f_bank[4 + z].read_by(ad)
            k.barrier()
            k.straight()
            for t in range(2):
                k.dma("out", lambda e, i, t=t: e.dma_start(by_time(out)[t], tiles(t)))




def perceiver(nc, a, out):
    with ExitStack() as ctx:
        ctx.enter_context(nc.allow_non_contiguous_dma(reason="bias columns and head-major weights are small"))
        k = Queues(nc, ctx)
        k.straight()
        env = Env(k, ctx)
        env.constants()
        load_x(env, a["x"].rearrange("b t d -> (b t) d"))
        k.barrier()

        def of(prefix):
            return {name[len(prefix) + 1:]: v for name, v in a.items() if name.startswith(prefix + "_")}

        kv = a["ctx_1024"]
        w = of("L0_xattn")
        softmax_cross_attention(env, kv, 64, w["W_Q"], w["W_K"], w["W_V"], w["W_out"], 64 ** -0.5,
                                w["b_Q"], w["b_K"], w["b_V"], w["b_out"], a["mask_BxSxS2_bk1"], True, -10000.0)
        l0_attention(env, of("L0_attn"))
        l0_ffn(env, of("L0_ffn"))
        w = of("L1_xattn")
        softmax_cross_attention(env, kv, 8, w["Wq"], w["Wk"], w["Wv"], w["Wo"], 8 ** -0.5,
                                w["bq"], w["bk"], w["bv"], w["bo"],
                                a["mask_Bx1xSxS2_bf1"].rearrange("b a q s -> (b a) q s"), False, -1.0e9)
        l1_attention(env, of("L1_attn"))
        l1_ffn(env, of("L1_ffn"))
        l2_cross_attention(env, of("L2_xattn"), kv)
        l2_attention(env, of("L2_attn"), a)
        l2_ffn(env, of("L2_ffn"), a)
        w = of("L3_xattn")
        softmax_cross_attention(env, kv, 8, w["Wq"], w["Wk"], w["Wv"], w["Wp"], 8 ** -0.5, bo=w["bp"], shared=True)
        l3_attention(env, of("L3_attn"))
        l3_ffn(env, of("L3_ffn"), out.rearrange("b t d -> (b t) d"))
        k.finish()


def kernel(**inputs):
    import concourse.bacc as bacc
    from concourse.bass_utils import run_bass_kernel_spmd

    nc = bacc.Bacc("TRN2", target_bir_lowering=False, num_devices=1)
    arrays, args = {}, {}
    for name, v in {**inputs, **l2_tables(), **tie_table()}.items():
        v = np.ascontiguousarray(v)
        if v.ndim == 0:
            v = v.reshape(1)
        arrays["in_" + name] = v
        args[name] = nc.dram_tensor("in_" + name, v.shape, mybir.dt.from_np(v.dtype), kind="ExternalInput").ap()
    out = nc.dram_tensor("out_0", (BATCH, SEQ, P), F32, kind="ExternalOutput").ap()
    perceiver(nc, args, out)
    r = run_bass_kernel_spmd(nc, [arrays], core_ids=[0])
    return r.results[0]["out_0"]
```

```python
from contextlib import ExitStack
import numpy as np
import concourse.bass as bass
from concourse import mybir

F32 = mybir.dt.float32
U8 = mybir.dt.uint8
ALU = mybir.AluOpType
ACT = mybir.ActivationFunctionType
AX = mybir.AxisListType

P = 128
BATCH = 64
SEQ = 32
CTX = 257
NTOK = BATCH * SEQ
NT = NTOK // P
BPT = P // SEQ
H = 16


class Token:

    def __init__(self, seg, sem, unit):
        self.seg, self.sem, self.unit, self.used, self.order = seg, sem, unit, False, None

    def value(self, i):
        return self.seg.base[self.sem] + i * self.seg.per.get(self.sem, 0) + self.order


class Prev:

    def __init__(self, token):
        self.token = token


class Buffer:

    def __init__(self, *readers):
        self.readers, self.by_segment = list(readers), {}

    def read_by(self, *tokens):
        self.readers = [t for t in tokens if t is not None]
        self.by_segment[self.readers[0].seg] = self.readers
        return tokens[0]

    @property
    def free(self):
        return Free(self, self.readers)

    made_by = read_by
    made = free


class Free:
    def __init__(self, buffer, readers):
        self.buffer, self.readers = buffer, readers

    def tokens(self, seg):
        if any(t.seg is seg for t in self.readers):
            return self.readers
        again = self.buffer.by_segment.get(seg, []) if seg.rounds > 1 else []
        return self.readers + [Prev(t) for t in again]


class Segment:
    def __init__(self, rounds):
        self.rounds, self.ops, self.per, self.base = rounds, {}, {}, {}
        self.first = 0


class Queues:

    ENGINES = ("pe", "act", "dve", "pool", "sp")

    def __init__(self, nc, ctx):
        self.nc, self.ctx = nc, ctx
        self.sems, self.segments, self.tokens = {}, [], []
        for e in self.ENGINES:
            self.sems[e] = ctx.enter_context(nc.semaphore("done_" + e))
        self.spare = ctx.enter_context(nc.semaphore("spare"))
        self.seg = None
        self.names = 0

    def sb(self, stack, name, shape, dt=F32):
        self.names += 1
        return stack.enter_context(self.nc.sbuf_tensor(f"{name}_{self.names}", shape, dt))

    def straight(self):
        self.seg = Segment(1)
        self.segments.append(self.seg)

    def loop(self, rounds):
        self.seg = Segment(rounds)
        self.segments.append(self.seg)

    def barrier(self):
        last = {}
        for seg in self.segments:
            for ops in seg.ops.values():
                for _, _, t in ops:
                    if t is not None:
                        last[t.sem] = t
        self.straight()
        for e in self.ENGINES:
            for sem, t in last.items():
                t.used = True
            self.seg.ops.setdefault(e, []).append((None, list(last.values()), None))

    def put(self, engine, fn, waits, sem=None, unit=1, alone=False):
        t = Token(self.seg, sem or engine, unit)
        t.alone = alone
        if unit == 16:
            t.used = True
        flat = self.flat(waits)
        self.seg.ops.setdefault(engine, []).append((fn, flat, t))
        return t

    def flat(self, waits):
        out = []
        for w in waits:
            out += self.flat(w) if isinstance(w, (list, tuple)) else [] if w is None else [w]
        return out

    def pe(self, fn, *w, alone=False):
        return self.put("pe", fn, w, alone=alone)

    def act(self, fn, *w, alone=False):
        return self.put("act", fn, w, alone=alone)

    def dve(self, fn, *w, alone=False):
        return self.put("dve", fn, w, alone=alone)

    def pool(self, fn, *w, alone=False):
        return self.put("pool", fn, w, alone=alone)

    def dma(self, sem, fn, *w, q="sp"):
        if sem not in self.sems:
            self.sems[sem] = self.ctx.enter_context(self.nc.semaphore("dma_" + sem))
        return self.put(q, fn, w, sem=sem, unit=16)

    def finish(self):
        for seg in self.segments:
            for ops in seg.ops.values():
                for n, (fn, waits, t) in enumerate(ops):
                    waits = [x for w in waits for x in (w.tokens(seg) if isinstance(w, Free) else [w])]
                    ops[n] = (fn, waits, t)
                    for w in waits:
                        (w.token if isinstance(w, Prev) else w).used = True
        total = {s: 0 for s in self.sems}
        for seg in self.segments:
            seg.base = dict(total)
            per = {}
            for ops in seg.ops.values():
                for _, _, t in ops:
                    if t is not None and t.used:
                        per[t.sem] = per.get(t.sem, 0) + t.unit
                        t.order = per[t.sem]
            seg.per = per
            for s, n in per.items():
                total[s] += n * seg.rounds
        lead = {s: max([seg.per.get(s, 0) for seg in self.segments]) for s in self.sems}
        owner = {}
        for seg in self.segments:
            for e, ops in seg.ops.items():
                for _, _, t in ops:
                    if t is not None and t.used:
                        owner.setdefault(t.sem, e)

        def emit(name, eng):
            for s in self.sems:
                if owner.get(s) == name and lead[s]:
                    eng.sem_inc(self.sems[s], lead[s])
            known = {}
            for seg in self.segments:
                ops = seg.ops.get(name, [])
                if not ops:
                    continue
                if seg.rounds == 1:
                    self.run(seg, ops, eng, seg.first, lead, known)
                    continue
                for _, waits, _ in ops:
                    for w in waits:
                        if not isinstance(w, Prev) and w.seg is not seg:
                            self.wait(eng, w.sem, lead[w.sem] + w.value(w.seg.rounds - 1), known)
                with eng.Fori(0, seg.rounds) as i:
                    self.run(seg, ops, eng, i, lead, None)
                known.clear()

        block = self.ctx.enter_context(self.nc.Block())

        @block.tensor
        def _(e):
            emit("pe", e)

        @block.scalar
        def _(e):
            emit("act", e)

        @block.vector
        def _(e):
            emit("dve", e)

        @block.gpsimd
        def _(e):
            emit("pool", e)

        @block.sync
        def _(e):
            emit("sp", e)
            for s in self.sems:
                if s not in self.ENGINES and total[s]:
                    e.wait_ge(self.sems[s], lead[s] + total[s])

    def wait(self, eng, sem, value, known):
        if known.get(sem, -1) < value:
            eng.wait_ge(self.sems[sem], value)
            known[sem] = value

    def run(self, seg, ops, eng, i, lead, known):
        inside = {}
        for fn, waits, t in ops:
            need, waited = {}, False
            for w in waits:
                if isinstance(w, Prev):
                    r = w.token.order - seg.per[w.token.sem]
                    need[w.token.sem] = max(need.get(w.token.sem, -1 << 30), r)
                elif w.seg is seg:
                    need[w.sem] = max(need.get(w.sem, -1 << 30), w.order)
                elif seg.rounds == 1:
                    self.wait(eng, w.sem, lead[w.sem] + w.value(w.seg.rounds - 1), known)
            for s, r in need.items():
                if inside.get(s, -1 << 30) < r:
                    inside[s] = r
                    v = lead[s] + seg.base[s] + r
                    if seg.rounds == 1:
                        self.wait(eng, s, v, known)
                    else:
                        eng.wait_ge(self.sems[s], v + i * seg.per[s])
                        waited = True
            if fn is None:
                continue
            if waited and t.alone:
                eng.sem_inc(self.spare, 1)
            ins = fn(eng, i)
            if t is not None and t.used:
                ins.then_inc(self.sems[t.sem], t.unit)


class Env:

    def __init__(self, k, ctx):
        nc = k.nc
        self.k, self.ctx = k, ctx
        self.X = k.sb(ctx, "X", [P, NT * P])
        self.yT = k.sb(ctx, "yT", [P, NTOK])
        self.ident = k.sb(ctx, "ident", [P, P])
        self.ones = k.sb(ctx, "ones", [P, P])
        self.rstd = k.sb(ctx, "rstd", [P, 8])
        self.stats = k.sb(ctx, "stats", [P, 8 * 6])
        self.moments = k.sb(ctx, "moments", [P, 8 * 2])
        self.ytile = k.sb(ctx, "ytile", [P, 8 * P])
        self.prep_banks = [Buffer() for _ in range(8)]
        self.bank = [ctx.enter_context(nc.psum_tensor(f"bank{n}", [P, 512], F32)) for n in range(8)]

    def constants(self):
        k = self.k
        a = k.pool(lambda e, i: e.memset(self.ident[:, :], 0.0))
        k.pool(lambda e, i: e.affine_select(out=self.ident[:, :], in_=self.ident[:, :], compare_op=ALU.not_equal,
                                            fill=1.0, base=0, pattern=[[-1, P]], channel_multiplier=1), a)
        k.dve(lambda e, i: e.memset(self.ones[:, :], 1.0))


def norm_tiles(env, y=None):
    k, X, mv, rstd = env.k, env.X, env.moments, env.rstd
    N = 8
    k.loop(NT // N)
    f_stats, f_mv, f_rstd = Buffer(), Buffer(), Buffer()
    f_tile, f_bank = [Buffer() for _ in range(N)], [Buffer(), Buffer()]
    for u in range(N):
        st = k.dve(lambda e, i, u=u: e.bn_stats(env.stats[:, 6 * u:6 * u + 6], X[:, bass.ts(N * i + u, P)]), f_stats.free)
    for u in range(N):
        ag = k.dve(lambda e, i, u=u: e.bn_aggr(mv[:, 2 * u:2 * u + 2], env.stats[:, 6 * u:6 * u + 6]), st, f_mv.free, alone=True)
    f_stats.read_by(ag)
    var = mv[:, :].rearrange("p (t two) -> p t two", two=2)[:, :, 1]
    a = k.dve(lambda e, i: e.tensor_scalar(rstd[:, :], var, 1e-5, None, ALU.add), ag, f_rstd.free)
    b = k.act(lambda e, i: e.activation(rstd[:, :], rstd[:, :], ACT.Sqrt), a)
    r = k.dve(lambda e, i: e.reciprocal(rstd[:, :], rstd[:, :]), b)
    for q in range(2):
        for v in range(4):
            u = 4 * q + v
            yt = env.ytile[:, u * P:(u + 1) * P]
            n = k.dve(lambda e, i, u=u, yt=yt: e.tensor_scalar(yt, X[:, bass.ts(N * i + u, P)], mv[:, 2 * u:2 * u + 1], rstd[:, u:u + 1],
                                                               ALU.subtract, ALU.mult), r, f_tile[u].free)
            c = None
            if y is not None:
                c = k.pool(lambda e, i, u=u, yt=yt: e.tensor_copy(y[:, bass.ts(N * i + u, P)], yt), n, alone=True)
            t = k.pe(lambda e, i, q=q, v=v, yt=yt: e.transpose(env.bank[q][:, v * P:(v + 1) * P], yt, env.ident[:, :]), n, f_bank[q].free)
            f_tile[u].read_by(t, c)
        f_bank[q].read_by(k.act(lambda e, i, q=q: e.copy(env.yT[:, bass.ts(2 * i + q, 512)], env.bank[q][:, :]), t))
    f_mv.read_by(n)
    f_rstd.read_by(n)
    k.barrier()


def load_x(env, x):
    env.k.dma("x", lambda e, i: e.dma_start(env.X[:, :].rearrange("p (t d) -> p t d", d=P),
                                            x.rearrange("(t p) d -> p t d", p=P)))


def store_x(env, out):
    env.k.barrier()
    env.k.straight()
    env.k.dma("out", lambda e, i: e.dma_start(out.rearrange("(t p) d -> p t d", p=P),
                                              env.X[:, :].rearrange("p (t d) -> p t d", d=P)))


def heads_last(w):
    return w.rearrange("(h j) d -> j h d", h=H)


def softmax_cross_attention(env, ctx_kv, dk, Wq, Wk, Wv, Wo, scale, bq=None, bk=None, bv=None, bo=None,
                            mask=None, masked_where=None, masked_to=None, shared=False):
    k, nc = env.k, env.k.nc
    bank = env.bank
    with ExitStack() as st:
        sb = lambda name, shape, dt=F32: k.sb(st, name, shape, dt)
        A = sb("A", [P, H * P])
        M = sb("M", [P, H * P])
        bo_eff = sb("bo_eff", [1, P])
        last_rows, last_T, v_rows = sb("last_rows", [BATCH, P]), sb("last_T", [P, BATCH]), sb("v_rows", [BATCH, H * P])
        if bq is not None:
            c = sb("c", [P, H])
            g = sb("g", [P, H])
            g0 = sb("g0", [P, H // 4])
        k.straight()
        with ExitStack() as pre:
            wsb = lambda name, shape: k.sb(pre, name, shape)
            wq, wk, wv, wo = (wsb(n, [dk, H * P]) for n in ("wq", "wk", "wv", "wo"))
            as_heads = lambda t: t[:, :].rearrange("j (h d) -> j h d", h=H)
            lw = []
            done = []
            k.dma("last", lambda e, i: e.dma_start(last_rows[:, :], ctx_kv[:, 2 * P:CTX, :].rearrange("b c d -> b (c d)")))
            if not shared:
                for t, src in ((wq, Wq), (wk, Wk), (wv, Wv)):
                    lw.append(k.dma("w", lambda e, i, t=t, src=src: e.dma_start(as_heads(t), heads_last(src))))
                wo_rows = wsb("wo_rows", [P, H * dk])
                lo = k.dma("w", lambda e, i: e.dma_start(wo_rows[:, :], Wo))
                brow = wsb("brow", [1, P])
                bcol = [wsb("bcol", [dk, H]) for _ in range(3)]
                lb = [k.dma("w", lambda e, i: e.dma_start(brow[:, :], bo.rearrange("(a d) -> a d", a=1)))]
                for t, src in zip(bcol, (bq, bk, bv)):
                    lb.append(k.dma("w", lambda e, i, t=t, src=src: e.dma_start(
                        t[:, :], src.rearrange("(h j) -> j h", h=H))))
                lw = [lb[-1]]
                norm_tiles(env)
                for q in range(4):
                    for r in range(4):
                        h = 4 * q + r
                        tt = k.pe(lambda e, i, q=q, r=r, h=h: e.transpose(
                            bank[q][0:dk, r * P:(r + 1) * P], wo_rows[:, h * dk:(h + 1) * dk], env.ident[:, :]), lb[-1])
                    cp = k.act(lambda e, i, q=q: e.copy(wo[:, q * 512:(q + 1) * 512], bank[q][0:dk, :]), tt)
                    done.append(cp)
                wkh = lambda h: wk[:, h * P:(h + 1) * P]
                wvh = lambda h: wv[:, h * P:(h + 1) * P]
            else:
                rows = [wsb("rows", [P, w]) for w in (P, dk, dk)]
                for t, src in zip(rows, (Wq, Wk, Wv)):
                    k.dma("w", lambda e, i, t=t, src=src: e.dma_start(t[:, :], src))
                brow = wsb("brow", [1, P])
                k.dma("w", lambda e, i: e.dma_start(brow[:, :], bo.rearrange("(a d) -> a d", a=1)))
                lw = [k.dma("w", lambda e, i: e.dma_start(as_heads(wo), heads_last(Wo)))]
                norm_tiles(env)
                for q in range(4):
                    for r in range(4):
                        h = 4 * q + r
                        tt = k.pe(lambda e, i, q=q, r=r, h=h: e.transpose(
                            bank[q][0:dk, r * P:(r + 1) * P], rows[0][:, h * dk:(h + 1) * dk], env.ident[:, :]), lw)
                    done.append(k.act(lambda e, i, q=q: e.copy(wq[:, q * 512:(q + 1) * 512], bank[q][0:dk, :]), tt))
                for n, t in ((1, wk), (2, wv)):
                    tt = k.pe(lambda e, i, n=n: e.transpose(bank[3 + n][0:dk, 0:P], rows[n][:, :], env.ident[:, :]), lw)
                    done.append(k.act(lambda e, i, n=n, t=t: e.copy(t[:, 0:P], bank[3 + n][0:dk, 0:P]), tt))
                wkh = lambda h: wk[:, 0:P]
                wvh = lambda h: wv[:, 0:P]
            wqh = lambda h: wq[:, h * P:(h + 1) * P]
            woh = lambda h: wo[:, h * P:(h + 1) * P]
            for dst, left, right, first in ((A, wqh, wkh, 0), (M, wvh, woh, 4)):
                for q in range(4):
                    for r in range(4):
                        h = 4 * q + r
                        mm = k.pe(lambda e, i, h=h, r=r, b=bank[first + q], left=left, right=right: e.matmul(
                            b[:, r * P:(r + 1) * P], left(h), right(h), start=True, stop=True), done, lw)
                    cp = k.dve(lambda e, i, q=q, b=bank[first + q], dst=dst: e.tensor_copy(
                        dst[:, q * 512:(q + 1) * 512], b[:, :]), mm)
                    last = cp
                    if first == 0 and q == 0:
                        free0 = cp
                    if first == 0 and q == 1:
                        free1 = cp
            free = [free0, free1]
            if bq is not None:
                for h in range(H):
                    k.pe(lambda e, i, h=h: e.matmul(bank[0][:, h:h + 1], wkh(h), bcol[0][:, h:h + 1], start=True, stop=True), free)
                    mm = k.pe(lambda e, i, h=h: e.matmul(bank[0][:, H + h:H + h + 1], wqh(h), bcol[1][:, h:h + 1], start=True, stop=True))
                c1 = k.dve(lambda e, i: e.tensor_copy(c[:, :], bank[0][:, 0:H]), mm)
                c2 = k.dve(lambda e, i: e.tensor_copy(g[:, :], bank[0][:, H:2 * H]), mm)
                m1 = k.dve(lambda e, i: e.tensor_tensor(bcol[0][:, :], bcol[0][:, :], bcol[1][:, :], ALU.mult), mm)
                gq = bcol[0][:, :].rearrange("j (g f) -> j g f", f=4)
                for f in range(4):
                    mm = k.pe(lambda e, i, f=f: e.matmul(bank[2][32 * f:32 * f + 32, 0:4], env.ones[0:dk, 0:32], gq[:, :, f],
                                                         start=True, stop=True, tile_position=(0, 32 * f)), m1, done)
                c3 = k.dve(lambda e, i: e.tensor_copy(g0[:, :], bank[2][:, 0:4]), mm)
            mm = k.pe(lambda e, i: e.matmul(bank[1][0:1, 0:P], env.ones[0:1, 0:1], brow[:, :], start=True, stop=bq is None), free, lw)
            if bq is not None:
                for h in range(H):
                    mm = k.pe(lambda e, i, h=h: e.matmul(bank[1][0:1, 0:P], bcol[2][:, h:h + 1], woh(h),
                                                         start=False, stop=h == H - 1))
            k.dve(lambda e, i: e.tensor_copy(bo_eff[:, :], bank[1][0:1, 0:P]), mm)
            k.barrier()
        v_dram = nc.dram_tensor(f"v_last_{k.names}", (BATCH * 4, 4 * P), F32, kind="Internal").ap()
        t = k.pe(lambda e, i: e.transpose(bank[3][:, 0:BATCH], last_rows[:, :], env.ident[0:BATCH, 0:BATCH]))
        lT = k.act(lambda e, i: e.copy(last_T[:, :], bank[3][:, 0:BATCH]), t)
        v_made = []
        for q in range(4):
            mm = k.pe(lambda e, i, q=q: e.matmul(bank[4 + q][0:BATCH, :], last_T[:, :], M[:, q * 512:(q + 1) * 512], start=True, stop=True), lT)
            v_made.append(k.dve(lambda e, i, q=q: e.tensor_copy(v_rows[:, q * 512:(q + 1) * 512], bank[4 + q][0:BATCH, :]), mm))
        v_stored = k.dma("w3", lambda e, i: e.dma_start(v_dram.rearrange("(b n) d -> b (n d)", n=4), v_rows[:, :]), v_made)
        AHEAD, RING = 3, 4
        UNITS = 2 * BPT
        G = 2 * P
        qh = [sb("qh", [P, BPT * H * SEQ]) for _ in range(2)]
        p_last = [sb("p_last", [P, BPT * 4]) for _ in range(2)]
        p_diag = sb("p_diag", [P, P])
        of_batch = sb("of_batch", [BPT * 4, P])
        v_last = [sb("v_last", [P, P]) for _ in range(2)]
        bo_rows = sb("bo_rows", [P, P])
        with_bo = [sb("with_bo", [P, P]) for _ in range(2)]
        kv = [sb("kv", [P, 2 * P]) for _ in range(BPT)]
        kv_last = [sb("kv_last", [1, P]) for _ in range(BPT)]
        kvT = [sb("kvT", [P, CTX]) for _ in range(2)]
        maxes, nbias, rows_sum, rinv = ([sb(n, [P, 2]) for _ in range(RING)] for n in ("maxes", "nbias", "rows_sum", "rinv"))
        probs = [sb("probs", [P, 2 * CTX]) for _ in range(RING)]
        pT = [sb("pT", [P, 2 * G]) for _ in range(2)]
        U = sb("U", [P, H * P])
        if bq is not None:
            y_tile = sb("y_tile", [P, P])
            r_all = [sb("r_all", [P, BPT * 4]) for _ in range(2)]
        if mask is not None:
            mask_u8 = sb("mask_u8", [P, BPT * CTX], U8)
            keep, fill = ([sb(n, [P, BPT * CTX]) for _ in range(2)] for n in ("keep", "fill"))
        pair = lambda: [Buffer(), Buffer()]
        ring = lambda: [Buffer() for _ in range(RING)]
        f_q, f_r, f_keep, f_plast, f_vlast, f_kvT, f_pT, f_wb = (pair() for _ in range(8))
        f_mx, f_nb, f_rs, f_ri, f_pr = (ring() for _ in range(5))
        f_y, f_mask, f_U, f_diag = (Buffer() for _ in range(4))
        f_kv = [Buffer() for _ in range(BPT)]
        f_bank = [Buffer() for _ in range(8)]
        bm = k.pe(lambda e, i: e.matmul(bank[2][:, 0:P], env.ones[0:1, :], bo_eff[:, :], start=True, stop=True))
        bo_made = k.dve(lambda e, i: e.tensor_copy(bo_rows[:, :], bank[2][:, 0:P]), bm)
        f_bank[2].read_by(bo_made)
        f_bank[3].read_by(lT)
        for q in range(4):
            f_bank[4 + q].read_by(v_made[q])
        m_q, m_r, m_keep, m_vlast, m_kvT, m_plast, m_pT = (pair() for _ in range(7))
        m_exp, m_prob, m_aside = (ring() for _ in range(3))
        m_mask = Buffer()
        m_kv = [Buffer() for _ in range(BPT)]
        S_BANK, T_BANK, AV, X_BANK = 1, 5, 7, 0
        zeroed = [k.pool(lambda e, i, t=t: e.memset(t[:, :], 0.0)) for t in (p_diag, *v_last)]
        ob = of_batch[:, :].rearrange("p (b q) -> p b q", b=BPT)
        a = k.pool(lambda e, i: e.memset(of_batch[:, :], 1.0))
        a = k.pool(lambda e, i: e.affine_select(out=ob, in_=ob, compare_op=ALU.is_ge, fill=0.0, base=0,
                                                pattern=[[-4, BPT], [0, SEQ]], channel_multiplier=1), a)
        a = k.pool(lambda e, i: e.affine_select(out=ob, in_=ob, compare_op=ALU.is_ge, fill=0.0, base=3,
                                                pattern=[[4, BPT], [0, SEQ]], channel_multiplier=-1), a)
        ob_made = a

        def load_context(tile, b):
            p, at = tile
            l = k.dma(f"kv{b}", lambda e, i: e.dma_start(kv[b][:, :].rearrange("p (c d) -> p c d", c=2),
                      ctx_kv[bass.ds(BPT * at(i) + b, 1), 0:2 * P, :].rearrange("a (c p) d -> p (a c) d", p=P)), f_kv[b].free)
            l = k.dma(f"kv{b}", lambda e, i: e.dma_start(kv_last[b][:, :],
                      ctx_kv[bass.ds(BPT * at(i) + b, 1), 2 * P:CTX, :].rearrange("a c d -> a (c d)")), f_kv[b].free)
            m_kv[b].made_by(l)

        def load_mask(tile):
            p, at = tile
            if mask is not None:
                for f in range(4):
                    lm = k.dma("mask", lambda e, i, f=f: e.dma_start(
                        mask_u8[32 * f:32 * f + 32, :].rearrange("q (b s) -> q b s", b=BPT),
                        mask[bass.ts(at(i), BPT), :, :].rearrange("b q s -> q b s")), f_mask.free)
                m_mask.made_by(lm)

        def map_mask(tile):
            p = tile[0]
            if mask is not None:
                lm = m_mask.made
                keep_mul, keep_add = (-1.0, 1.0) if masked_where else (1.0, 0.0)
                fill_mul, fill_add = (masked_to / scale, 0.0) if masked_where else (-masked_to / scale, masked_to / scale)
                k.pool(lambda e, i: e.tensor_scalar(keep[p][:, :], mask_u8[:, :], keep_mul, keep_add, ALU.mult, ALU.add),
                       lm, f_keep[p].free, alone=True)
                mapped = k.pool(lambda e, i: e.tensor_scalar(fill[p][:, :], mask_u8[:, :], fill_mul, fill_add, ALU.mult, ALU.add),
                                lm, f_keep[p].free, alone=True)
                f_mask.read_by(mapped)
                m_keep[p].made_by(mapped)

        def load_values(tile):
            p, at = tile
            for r in range(4):
                l = k.dma(f"v{p}", lambda e, i, r=r: e.dma_start(
                    v_last[p][32 * r:32 * r + BPT * 4, :], v_dram[bass.ts(at(i), BPT * 4), r * P:(r + 1) * P]),
                    f_vlast[p].free, v_stored, zeroed)
            m_vlast[p].made_by(l)

        def fold_queries(tile, n):
            p, at = tile
            for r in range(4):
                h = 4 * n + r
                mm = k.pe(lambda e, i, r=r, h=h: e.matmul(bank[X_BANK][:, r * P:(r + 1) * P], A[:, h * P:(h + 1) * P],
                                                          env.yT[:, bass.ts(at(i), P)], start=True, stop=True), f_bank[X_BANK].free)
            out = qh[p][:, :].rearrange("p (b h q) -> p h b q", b=BPT, h=H)[:, 4 * n:4 * n + 4]
            src = bank[X_BANK][:, :].rearrange("p (h b q) -> p h b q", h=4, b=BPT)
            if bq is not None:
                cp = k.dve(lambda e, i: e.tensor_tensor(
                    out, src, c[:, 4 * n:4 * n + 4].unsqueeze(2).unsqueeze(3).to_broadcast([P, 4, BPT, SEQ]), ALU.add), mm, f_q[p].free)
            else:
                cp = k.dve(lambda e, i: e.tensor_copy(out, src), mm, f_q[p].free)
            f_bank[X_BANK].read_by(cp)
            m_q[p].made_by(cp)

        def offsets(tile):
            p, at = tile
            yc = k.dve(lambda e, i: e.tensor_copy(y_tile[:, :], env.yT[:, bass.ts(at(i), P)]), f_y.free)
            gf = g[:, :].rearrange("p (g f) -> p g f", f=4)
            for b in range(BPT):
                for f in range(4):
                    mm = k.pe(lambda e, i, b=b, f=f: e.matmul(
                        bank[X_BANK][32 * f:32 * f + 32, 4 * b:4 * b + 4], y_tile[:, 32 * b:32 * b + 32], gf[:, :, f],
                        start=True, stop=True, tile_position=(0, 32 * f)), yc, f_bank[X_BANK].free)
            f_y.read_by(mm)
            rr = k.dve(lambda e, i: e.tensor_tensor(
                r_all[p][:, :].rearrange("p (b g) -> p b g", b=BPT), bank[X_BANK][:, 0:16].rearrange("p (b g) -> p b g", b=BPT),
                g0[:, :].unsqueeze(1).to_broadcast([P, BPT, 4]), ALU.add), mm, f_r[p].free)
            f_bank[X_BANK].read_by(rr)
            m_r[p].made_by(rr)

        def turn_context(b):
            z, w = b % 2, m_kv[b].made
            k.pe(lambda e, i: e.transpose(bank[X_BANK][:, 0:P], kv[b][:, 0:P], env.ident[:, :]), w, f_bank[X_BANK].free)
            k.pe(lambda e, i: e.transpose(bank[X_BANK][:, P:2 * P], kv[b][:, P:2 * P], env.ident[:, :]))
            t = k.pe(lambda e, i: e.transpose(bank[X_BANK][:, 2 * P:CTX], kv_last[b][:, :], env.ident[0:1, 0:1]))
            ct = k.act(lambda e, i: e.copy(kvT[z][:, :], bank[X_BANK][:, 0:CTX]), t, f_kvT[z].free)
            f_bank[X_BANK].read_by(ct)
            m_kvT[z].made_by(ct)

        def scores(tile, u):
            p, b, z = tile[0], u // 2, u % 2
            made = []
            for j in range(2):
                n = 2 * z + j
                bk_ = bank[S_BANK + 2 * z + j]
                mm = k.pe(lambda e, i, n=n, bk_=bk_: e.matmul(
                    bk_[:, 0:CTX], qh[p][:, (4 * b + n) * P:(4 * b + n + 1) * P], kvT[b % 2][:, :], start=True, stop=True),
                    m_kvT[b % 2].made, m_q[p].made, f_bank[S_BANK + 2 * z + j].free)
                made.append(mm)
            if u == UNITS - 1:
                f_q[p].read_by(mm)
            if z:
                f_kvT[b % 2].read_by(mm)
            return made

        def exponentials(tile, u, made):
            p, b, z, v = tile[0], u // 2, u % 2, u % RING
            banks = [bank[S_BANK + 2 * z + j] for j in range(2)]
            top = lambda j: maxes[v][:, j:j + 1]
            if mask is not None:
                kept = [k.dve(lambda e, i, j=j: e.scalar_tensor_tensor(
                    banks[j][:, 0:CTX], banks[j][:, 0:CTX], r_all[p][:, 4 * b + 2 * z + j:4 * b + 2 * z + j + 1], keep[p][:, b * CTX:(b + 1) * CTX],
                    ALU.add, ALU.mult), made[j], m_r[p].made, m_keep[p].made) for j in range(2)]
                mx = [k.dve(lambda e, i, j=j: e.tensor_tensor_reduce(
                    banks[j][:, 0:CTX], banks[j][:, 0:CTX], fill[p][:, b * CTX:(b + 1) * CTX], 1.0, -3.0e38, ALU.add, ALU.max,
                    top(j)), kept[j], f_mx[v].free if j == 0 else None, alone=True) for j in range(2)]
                if u == UNITS - 1:
                    f_r[p].read_by(kept[1])
                    f_keep[p].read_by(mx[1])
            else:
                mx = [k.dve(lambda e, i, j=j: e.tensor_reduce(top(j), banks[j][:, 0:CTX], AX.X, ALU.max),
                            made[j], f_mx[v].free if j == 0 else None) for j in range(2)]
            nb = k.dve(lambda e, i: e.tensor_scalar(nbias[v][:, :], maxes[v][:, :], -scale, None, ALU.mult), mx, f_nb[v].free)
            f_mx[v].read_by(nb)
            for j in range(2):
                ex = k.act(lambda e, i, j=j: e.activation(
                    probs[v][:, j * CTX:(j + 1) * CTX], banks[j][:, 0:CTX], ACT.Exp, bias=nbias[v][:, j:j + 1], scale=scale,
                    accum_out=rows_sum[v][:, j:j + 1]), nb, [f_pr[v].free, m_aside[v].made] if j == 0 else None, f_rs[v].free if j == 0 else None)
                f_bank[S_BANK + 2 * z + j].read_by(ex)
            f_nb[v].read_by(ex)
            m_exp[v].made_by(ex)

        def normalise(tile, u):
            p, v = tile[0], u % RING
            ri = k.dve(lambda e, i: e.reciprocal(rinv[v][:, :], rows_sum[v][:, :]), m_exp[v].made, f_ri[v].free)
            f_rs[v].read_by(ri)
            for j in range(2):
                nm = k.pool(lambda e, i, j=j: e.tensor_scalar(
                    probs[v][:, j * CTX:(j + 1) * CTX], probs[v][:, j * CTX:(j + 1) * CTX], rinv[v][:, j:j + 1], 1.0,
                    ALU.mult, ALU.mult), ri, alone=True)
            f_ri[v].read_by(nm)
            pl = k.pool(lambda e, i: e.tensor_copy(p_last[p][:, 2 * u:2 * u + 2],
                                                   probs[v][:, :].rearrange("p (j s) -> p j s", j=2)[:, :, CTX - 1]), nm, f_plast[p].free, alone=True)
            m_prob[v].made_by(nm)
            m_plast[p].made_by(pl)
            m_aside[v].made_by(pl)

        def turn_probs(u):
            z, v = u % 2, u % RING
            for c_ in range(2):
                for j in range(2):
                    t = k.pe(lambda e, i, c_=c_, j=j: e.transpose(
                        bank[T_BANK + z][:, c_ * G + j * P:c_ * G + (j + 1) * P], probs[v][:, j * CTX + c_ * P:j * CTX + (c_ + 1) * P],
                        env.ident[:, :]), m_prob[v].made, f_bank[T_BANK + z].free)
            f_pr[v].read_by(t)
            cp = k.dve(lambda e, i: e.tensor_copy(pT[z][:, :], bank[T_BANK + z][:, :]), t, f_pT[z].free)
            f_bank[T_BANK + z].read_by(cp)
            m_pT[z].made_by(cp)

        def attend(tile, u):
            b, z = u // 2, u % 2
            k.pe(lambda e, i: e.matmul(bank[AV][:, 0:G], kv[b][:, 0:P], pT[z][:, 0:G], start=True, stop=False), m_pT[z].made, f_bank[AV].free)
            mm = k.pe(lambda e, i: e.matmul(bank[AV][:, 0:G], kv[b][:, P:2 * P], pT[z][:, G:2 * G], start=False, stop=True))
            f_pT[z].read_by(mm)
            if z:
                f_kv[b].read_by(mm)
            uo = k.act(lambda e, i: e.copy(
                U[:, :].rearrange("p (h b q) -> p h b q", h=H, b=BPT)[:, 8 * z:8 * z + 8, b], bank[AV][:, 0:G].rearrange("p (h q) -> p h q", h=8)),
                mm, f_U.free if u < 2 else None)
            f_bank[AV].read_by(uo)
            return uo

        def turn_last(tile):
            p = tile[0]
            t = k.pe(lambda e, i: e.transpose(bank[X_BANK][0:BPT * 4, 0:P], p_last[p][:, :], env.ident[:, :]), m_plast[p].made, f_bank[X_BANK].free)
            f_plast[p].read_by(t)
            for r in range(4):
                d = k.dve(lambda e, i, r=r: e.tensor_tensor(
                    p_diag[32 * r:32 * r + BPT * 4, :].rearrange("p (b q) -> p b q", b=BPT),
                    bank[X_BANK][0:BPT * 4, r * SEQ:(r + 1) * SEQ].unsqueeze(1).to_broadcast([BPT * 4, BPT, SEQ]),
                    ob, ALU.mult), t, ob_made, zeroed, f_diag.free)
            f_bank[X_BANK].read_by(d)
            return d

        def output(tile, uo, diag):
            p, at = tile
            for h in range(H):
                k.pe(lambda e, i, h=h: e.matmul(bank[X_BANK][:, 0:P], U[:, h * P:(h + 1) * P], M[:, h * P:(h + 1) * P],
                                                start=h == 0, stop=False), uo[h // 8], f_bank[X_BANK].free)
            mm = k.pe(lambda e, i: e.matmul(bank[X_BANK][:, 0:P], p_diag[:, :], v_last[p][:, :], start=False, stop=True), diag, m_vlast[p].made)
            f_U.read_by(mm)
            f_diag.read_by(mm)
            f_vlast[p].read_by(mm)
            wb = k.dve(lambda e, i: e.tensor_tensor(with_bo[p][:, :], bank[X_BANK][:, 0:P], bo_rows[:, :], ALU.add), mm, bo_made, f_wb[p].free)
            f_bank[X_BANK].read_by(wb)
            f_wb[p].read_by(k.pool(lambda e, i: e.tensor_tensor(env.X[:, bass.ts(at(i), P)], env.X[:, bass.ts(at(i), P)], with_bo[p][:, :],
                                                                ALU.add), wb, alone=True))

        def attention(tile, following):
            uo = [None, None]
            for u in range(UNITS):
                ahead = [(tile, u + d) if u + d < UNITS else (following, u + d - UNITS) for d in range(AHEAD + 2)]
                if u == UNITS - 1:
                    diag = turn_last(tile)
                made = scores(*ahead[AHEAD]) if ahead[AHEAD][0] else None
                if u % 2 == 0 and ahead[AHEAD + 1][0]:
                    turn_context(ahead[AHEAD + 1][1] // 2)
                uo[u % 2] = attend(tile, u)
                if made:
                    exponentials(*ahead[AHEAD], made)
                if ahead[2][0]:
                    normalise(*ahead[2])
                if ahead[1][0]:
                    turn_probs(ahead[1][1])
                if following:
                    if u == 0:
                        load_mask(following)
                        load_values(following)
                    if u == 2:
                        map_mask(following)
                    if u < 4:
                        fold_queries(following, u)
                    if u == 4 and bq is not None:
                        offsets(following)
                    if u % 2:
                        load_context(following, u // 2)
            output(tile, uo, diag)

        first = (0, lambda i: 0)
        load_mask(first)
        for b in range(BPT):
            load_context(first, b)
        load_values(first)
        map_mask(first)
        for n in range(4):
            fold_queries(first, n)
        if bq is not None:
            offsets(first)
        for u in range(AHEAD):
            if u % 2 == 0:
                turn_context(u // 2)
            exponentials(first, u, scores(first, u))
            if u < 2:
                normalise(first, u)
        turn_probs(0)
        even, odd = (0, lambda i: 2 * i), (1, lambda i: 2 * i + 1)
        k.loop(NT // 2 - 1)
        attention(even, odd)
        attention(odd, (0, lambda i: 2 * i + 2))
        k.loop(1)
        k.seg.first = NT // 2 - 1
        attention(even, odd)
        attention(odd, None)
        k.barrier()

R4 = 4 * P


def columns(k, st, name, src, width=P):
    n = src.shape[0] // width
    t = k.sb(st, name, [width, n])
    return t, k.dma("w", lambda e, i: e.dma_start(t[:, :], src.rearrange("(c p) -> p c", p=width)))


def broadcast_row(k, st, name, src):
    t = k.sb(st, name, [P, src.shape[0]])
    return t, k.dma("w", lambda e, i: e.dma_start(t[:, :], src.partition_broadcast(P)))


def rows(k, st, name, src):
    c = src.shape[0] // P
    t = k.sb(st, name, [P, c * src.shape[1]])
    return t, k.dma("w", lambda e, i: e.dma_start(t[:, :].rearrange("p (c n) -> p c n", c=c),
                                                  src.rearrange("(c p) n -> p c n", p=P)))


def transpose_blocks(env, src, dst, count, ready, src_at=None, dst_at=None, first_bank=0):
    k = env.k
    src_at = src_at or (lambda n: src[:, n * P:(n + 1) * P])
    out = []
    for q in range(0, count, 4):
        b = first_bank + (q // 4) % 4
        m = min(4, count - q)
        for r in range(m):
            t = k.pe(lambda e, i, q=q, r=r, b=b: e.transpose(env.bank[b][:, r * P:(r + 1) * P], src_at(q + r),
                                                             env.ident[:, :]), ready, env.prep_banks[b].free)
        if dst_at is None:
            c = k.dve(lambda e, i, q=q, m=m, b=b: e.tensor_copy(dst[:, q * P:(q + m) * P], env.bank[b][:, 0:m * P]), t)
        else:
            c = k.dve(lambda e, i, q=q, m=m, b=b: e.tensor_copy(dst_at(q, m), env.bank[b][:, 0:m * P]), t)
        env.prep_banks[b].read_by(c)
        out.append(c)
    return out


def block_diagonal(env, st, value):
    k = env.k
    t = k.sb(st, "same_batch", [P, P])
    a = k.dve(lambda e, i: e.memset(t[:, :], 0.0))
    for b in range(BPT):
        a2 = k.dve(lambda e, i, b=b: e.memset(t[b * SEQ:(b + 1) * SEQ, b * SEQ:(b + 1) * SEQ], value), a)
    return t


def together(*streams):
    streams = list(streams)
    while streams:
        streams = [s for s in streams if next(s, streams) is not streams]
        yield


def alternate(*streams):
    for _ in together(*streams):
        pass


def stagger(streams):
    streams, running = list(streams), []
    while streams or running:
        if streams:
            running.append(streams.pop(0))
        running = [s for s in running if next(s, running) is not running]
        yield


def staggered(streams):
    alternate(stagger(streams))


class Norm4:

    def __init__(self, env, st):
        self.env, k = env, env.k
        self.stats = k.sb(st, "stats4", [P, 4 * 6])
        self.mv = k.sb(st, "mv4", [P, 8])
        self.rstd = k.sb(st, "rstd4", [P, 4])
        self.f_stats, self.f_mv, self.f_rstd = Buffer(), Buffer(), Buffer()

    def __call__(self, src, dst, gain, offset, ready):
        k = self.env.k
        s = []
        for u in range(4):
            s.append(k.dve(lambda e, i, u=u: e.bn_stats(self.stats[:, u * 6:u * 6 + 6], src[:, u * P:(u + 1) * P]), ready,
                           self.f_stats.free))
        for u in range(4):
            a = k.dve(lambda e, i, u=u: e.bn_aggr(self.mv[:, 2 * u:2 * u + 2], self.stats[:, u * 6:u * 6 + 6]), s[-1],
                      self.f_mv.free, alone=True)
        self.f_stats.read_by(a)
        var = self.mv[:, :].rearrange("p (t two) -> p t two", two=2)[:, :, 1]
        v = k.dve(lambda e, i: e.tensor_scalar(self.rstd[:, :], var, 1e-5, None, ALU.add), a, self.f_rstd.free)
        q = k.act(lambda e, i: e.activation(self.rstd[:, :], self.rstd[:, :], ACT.Sqrt), v)
        r = k.dve(lambda e, i: e.reciprocal(self.rstd[:, :], self.rstd[:, :]), q)
        for u in range(4):
            n = k.dve(lambda e, i, u=u: e.tensor_scalar(
                dst[:, u * P:(u + 1) * P], src[:, u * P:(u + 1) * P], self.mv[:, 2 * u:2 * u + 1],
                self.rstd[:, u:u + 1], ALU.subtract, ALU.mult), r)
        self.f_mv.read_by(n)
        self.f_rstd.read_by(n)
        self.last_read = n
        four = lambda t: t[:, :].rearrange("p (t d) -> p t d", d=P)
        row = lambda t: t[:, :].unsqueeze(1).to_broadcast([P, 4, P])
        g = k.dve(lambda e, i: e.tensor_tensor(four(dst), four(dst), row(gain), ALU.mult), n)
        return k.dve(lambda e, i: e.tensor_tensor(four(dst), four(dst), row(offset), ALU.add), g)


def l0_attention(env, w):
    k, bank = env.k, env.bank
    DH, C = 64, 8
    with ExitStack() as st:
        sb = lambda name, shape, dt=F32: k.sb(st, name, shape, dt)
        y = sb("y", [P, NTOK])
        k.straight()
        Wq, _ = rows(k, st, "Wq", w["Wq"])
        Wk, _ = rows(k, st, "Wk", w["Wk"])
        Wv, _ = rows(k, st, "Wv", w["Wv"])
        Wo, _ = rows(k, st, "Wo", w["Wo"])
        W1, _ = rows(k, st, "W1", w["W1"])
        W2, _ = rows(k, st, "W2", w["W2"])
        bq, _ = columns(k, st, "bq", w["bq"])
        bk, _ = columns(k, st, "bk", w["bk"])
        b1, _ = columns(k, st, "b1", w["b1"])
        bv, _ = broadcast_row(k, st, "bv", w["bv"])
        bo, _ = broadcast_row(k, st, "bo", w["bo"])
        b2, _ = broadcast_row(k, st, "b2", w["b2"])
        g1, _ = broadcast_row(k, st, "g1", w["g1"])
        be1, _ = broadcast_row(k, st, "be1", w["be1"])
        g2, _ = broadcast_row(k, st, "g2", w["g2"])
        be2, _ = broadcast_row(k, st, "be2", w["be2"])
        norm_tiles(env, y)
        same = block_diagonal(env, st, 1.0)
        y_static = sb("y_static", [P, R4])
        feat = [sb("qf", [P, C * R4]), sb("kf", [P, C * R4])]
        ex = [sb("ex", [P, R4]) for _ in range(2)]
        vext, o_tok = ([sb(n, [P, wd]) for _ in range(2)] for n, wd in (("vext", H * (DH + 1)), ("o_tok", H * DH)))
        att = [[sb("att", [P, 512]) for _ in range(2)] for _ in range(2)]
        rec = [sb("rec", [P, H]) for _ in range(2)]
        oT = [sb("oT", [P, H * DH]) for _ in range(2)]
        s1, x1T, s2 = (sb(n, [P, R4]) for n in ("s1", "x1T", "s2"))
        hT = sb("hT", [P, 4 * R4])
        for t in vext:
            k.dve(lambda e, i, t=t: e.memset(t[:, :], 1.0))
        norm = Norm4(env, st)
        k.barrier()
        f_ys, f_s1, f_x1T, f_hT, f_s2 = (Buffer() for _ in range(5))
        pair = lambda: [Buffer(), Buffer()]
        f_feat, f_ex, f_v, f_ot, f_oT, f_rec = (pair() for _ in range(6))
        f_att = [pair(), pair()]
        f_bank = [Buffer() for _ in range(8)]
        m_feat, m_ys = pair(), Buffer()

        def features(at):
            yc = k.pool(lambda e, i: e.tensor_copy(y_static[:, :], env.yT[:, bass.ts(at(i), R4)]), f_ys.free, alone=True)
            m_ys.made_by(yc)
            for c in range(C):
                for t, (W, b) in enumerate(((Wq, bq), (Wk, bk))):
                    n = t
                    mm = k.pe(lambda e, i, c=c, W=W, n=n: e.matmul(bank[n][:, :], W[:, c * P:(c + 1) * P], y_static[:, :],
                                                                   start=True, stop=True), yc, f_bank[n].free)
                    a = k.act(lambda e, i, c=c, b=b, n=n: e.activation(ex[n][:, :], bank[n][:, :], ACT.Exp, bias=b[:, c:c + 1]),
                              mm, f_ex[n].free)
                    if t:
                        r = k.act(lambda e, i, c=c, b=b, n=n: e.activation(bank[n][:, :], bank[n][:, :], ACT.Relu, bias=b[:, c:c + 1]), a)
                    else:
                        r = k.dve(lambda e, i, c=c, b=b, n=n: e.tensor_scalar(bank[n][:, :], bank[n][:, :], b[:, c:c + 1], 0.0, ALU.add, ALU.max), a)
                    m = k.dve(lambda e, i, c=c, t=t, n=n: e.scalar_tensor_tensor(
                        feat[t][:, c * R4:(c + 1) * R4], ex[n][:, :], 1.0, bank[n][:, :], ALU.min, ALU.add), r, f_feat[t].free)
                    f_bank[n].read_by(m)
                    f_ex[n].read_by(m)
                    m_feat[t].made_by(m)
                yield

        def values(s):
            z = s % 2
            for n in range(2):
                mm = k.pe(lambda e, i, s=s, n=n: e.matmul(bank[2 + n][:, :], y_static[:, s * P:(s + 1) * P],
                                                          Wv[:, n * 512:(n + 1) * 512], start=True, stop=True), m_ys.made, f_bank[2 + n].free)
                va = k.dve(lambda e, i, z=z, n=n: e.tensor_tensor(
                    vext[z][:, :].rearrange("p (h j) -> p h j", h=H)[:, 8 * n:8 * n + 8, 0:DH],
                    bank[2 + n][:, :].rearrange("p (h j) -> p h j", h=8),
                    bv[:, n * 512:(n + 1) * 512].rearrange("p (h j) -> p h j", h=8), ALU.add), mm, f_v[z].free)
                f_bank[2 + n].read_by(va)
            f_ys.read_by(mm)
            return va

        def weights(u):
            s, j = u // 2, u % 2
            for r in range(4):
                for odd in range(2):
                    lo, col = odd * DH, (4 * j + r) * R4 + s * P
                    mm = k.pe(lambda e, i, r=r, lo=lo, col=col, odd=odd: e.matmul(
                        bank[4 + odd][:, r * P:(r + 1) * P], feat[1][lo:lo + DH, col:col + P], feat[0][lo:lo + DH, col:col + P],
                        start=True, stop=True), [m.made for m in m_feat], f_bank[4 + odd].free)
            if u == 7:
                for f in f_feat:
                    f.read_by(mm)
            return mm

        def within_batch(u, mm):
            out = []
            for odd in range(2):
                ma = k.dve(lambda e, i, odd=odd, t=att[u % 2][odd]: e.tensor_tensor(
                    t[:, :].rearrange("p (h q) -> p h q", h=4), bank[4 + odd][:, :].rearrange("p (h q) -> p h q", h=4),
                    same[:, :].unsqueeze(1).to_broadcast([P, 4, P]), ALU.mult), mm, f_att[u % 2][odd].free)
                f_bank[4 + odd].read_by(ma)
                out.append(ma)
            return out

        def apply(u, ma, va):
            s, j, z = u // 2, u % 2, (u // 2) % 2
            outs = []
            for odd in range(2):
                for r in range(4):
                    h = 8 * j + 2 * r + odd
                    mo = k.pe(lambda e, i, r=r, h=h, odd=odd: e.matmul(
                        bank[6 + odd][:, r * 65:(r + 1) * 65], att[u % 2][odd][:, r * P:(r + 1) * P], vext[z][:, h * 65:(h + 1) * 65],
                        start=True, stop=True), ma[odd], va, f_bank[6 + odd].free)
                f_att[u % 2][odd].read_by(mo)
                outs.append(mo)
            if j:
                f_v[z].read_by(mo)
            return outs

        def over_sums(u, outs):
            s, j, z = u // 2, u % 2, (u // 2) % 2
            views = [bank[6 + odd][:, 0:4 * 65].rearrange("p (h j) -> p h j", h=4) for odd in range(2)]
            at = lambda odd: slice(4 * (2 * j + odd), 4 * (2 * j + odd) + 4)
            for odd in range(2):
                r1 = k.dve(lambda e, i, odd=odd: e.tensor_scalar(rec[z][:, at(odd)], views[odd][:, :, DH], 1e-6, None, ALU.add),
                           outs[odd], f_rec[z].free)
            r2 = k.dve(lambda e, i: e.reciprocal(rec[z][:, 8 * j:8 * j + 8], rec[z][:, 8 * j:8 * j + 8]), r1)
            for odd in range(2):
                oo = k.dve(lambda e, i, odd=odd: e.tensor_tensor(
                    o_tok[z][:, :].rearrange("p (j r o d) -> p j o r d", j=2, r=4, o=2)[:, j, odd], views[odd][:, :, 0:DH],
                    rec[z][:, at(odd)].unsqueeze(2).to_broadcast([P, 4, DH]), ALU.mult), r2, f_ot[z].free)
                f_bank[6 + odd].read_by(oo)
            if j:
                f_rec[z].read_by(oo)
            return oo

        def project(s, oo):
            z = s % 2
            for n in range(2):
                for r in range(4):
                    t = k.pe(lambda e, i, n=n, r=r: e.transpose(bank[n][:, r * P:(r + 1) * P],
                                                                o_tok[z][:, (4 * n + r) * P:(4 * n + r + 1) * P], env.ident[:, :]),
                             oo, f_bank[n].free)
                ec = k.act(lambda e, i, n=n: e.copy(oT[z][:, n * 512:(n + 1) * 512], bank[n][:, :]), t, f_oT[z].free)
                f_bank[n].read_by(ec)
            f_ot[z].read_by(t)
            return ec

        def onto_y(s, ec, at):
            z = s % 2
            for c in range(8):
                mm = k.pe(lambda e, i, c=c: e.matmul(bank[0][:, 0:P], oT[z][:, c * P:(c + 1) * P], Wo[:, c * P:(c + 1) * P],
                                                     start=c == 0, stop=c == 7), ec, f_bank[0].free)
            f_oT[z].read_by(mm)
            a1 = k.dve(lambda e, i: e.tensor_tensor(s1[:, s * P:(s + 1) * P], bank[0][:, 0:P], bo[:, :], ALU.add), mm, f_s1.free)
            f_bank[0].read_by(a1)
            return k.dve(lambda e, i: e.tensor_tensor(s1[:, s * P:(s + 1) * P], s1[:, s * P:(s + 1) * P],
                                                      y[:, bass.ts(4 * at(i) + s, P)], ALU.add), a1)

        def attention(at):
            va = {0: values(0)}
            mm = weights(0)
            ma = within_batch(0, mm)
            turned = done = None
            for u in range(8):
                s, j = u // 2, u % 2
                if u < 7:
                    mm = weights(u + 1)
                if j == 1 and s < 3:
                    va[s + 1] = values(s + 1)
                if turned:
                    done = onto_y(s - 1, turned, at)
                    turned = None
                outs = apply(u, ma, va[s])
                if u < 7:
                    ma = within_batch(u + 1, mm)
                oo = over_sums(u, outs)
                if j == 0 and s:
                    turned = project(s - 1, before)
                if j:
                    before = oo
            return onto_y(3, project(3, before), at)

        def mlp(at, done):
            n1 = norm(s1, s1, g1, be1, done)
            yield
            for s in range(4):
                t = k.pe(lambda e, i, s=s: e.transpose(bank[2][:, s * P:(s + 1) * P], s1[:, s * P:(s + 1) * P], env.ident[:, :]),
                         n1, f_bank[2].free)
            xc = k.act(lambda e, i: e.copy(x1T[:, :], bank[2][:, :]), t, f_x1T.free)
            f_bank[2].read_by(xc)
            yield
            for c in range(4):
                n = 4 + c
                mm = k.pe(lambda e, i, c=c, n=n: e.matmul(bank[n][:, :], W1[:, c * P:(c + 1) * P], x1T[:, :], start=True, stop=True),
                          xc, f_bank[n].free)
                ge = k.act(lambda e, i, c=c, n=n: e.activation(hT[:, c * R4:(c + 1) * R4], bank[n][:, :], ACT.Gelu, bias=b1[:, c:c + 1]),
                           mm, f_hT.free)
                f_bank[n].read_by(ge)
            f_x1T.read_by(mm)
            yield
            for s in range(4):
                for c in range(4):
                    mm = k.pe(lambda e, i, s=s, c=c: e.matmul(bank[3][:, s * P:(s + 1) * P], hT[:, c * R4 + s * P:c * R4 + (s + 1) * P],
                                                              W2[:, c * P:(c + 1) * P], start=c == 0, stop=c == 3), ge, f_bank[3].free)
            f_hT.read_by(mm)
            a = k.dve(lambda e, i: e.tensor_tensor(s2[:, :], bank[3][:, :], s1[:, :], ALU.add), mm, f_s2.free)
            f_bank[3].read_by(a)
            f_s1.read_by(a)
            yield
            a = k.dve(lambda e, i: e.tensor_tensor(s2[:, :].rearrange("p (t d) -> p t d", d=P), s2[:, :].rearrange("p (t d) -> p t d", d=P),
                                                   b2[:, :].unsqueeze(1).to_broadcast([P, 4, P]), ALU.add), a)
            n2 = norm(s2, s2, g2, be2, a)
            yield
            f_s2.read_by(k.dve(lambda e, i: e.tensor_tensor(env.X[:, bass.ts(at(i), R4)], env.X[:, bass.ts(at(i), R4)], s2[:, :], ALU.add), n2))

        k.straight()
        alternate(features(lambda i: 0))
        k.loop(NT // 4 - 1)
        same_round, next_round = (lambda i: i), (lambda i: i + 1)
        alternate(features(next_round), mlp(same_round, attention(same_round)))
        k.loop(1)
        k.seg.first = NT // 4 - 1
        alternate(mlp(same_round, attention(same_round)))
        k.barrier()


def l0_ffn(env, w):
    k, bank = env.k, env.bank
    FC = 4
    with ExitStack() as st:
        sb = lambda name, shape, dt=F32: k.sb(st, name, shape, dt)
        k.straight()
        raw = [sb(f"k{n}", [P, c * wd], U8) for n, c, wd in ((0, 2, 512), (1, 4, 512), (2, 4, 128))]
        W = [sb(f"W{n}", [P, c * wd]) for n, c, wd in ((0, 2, 512), (1, 4, 512), (2, 4, 128))]
        scales = sb("scales", [P, 3])
        for n, c in ((0, 2), (1, 4), (2, 4)):
            k.dma("w", lambda e, i, n=n, c=c: e.dma_start(raw[n][:, :].rearrange("p (c n) -> p c n", c=c),
                                                          w[f"k{n}"].rearrange("(c p) n -> p c n", p=P)))
        for n in range(3):
            l = k.dma("w", lambda e, i, n=n: e.dma_start(scales[:, n:n + 1], w[f"s{n}"].partition_broadcast(P)))
        norm_tiles(env)
        for n in range(3):
            c = k.dve(lambda e, i, n=n: e.tensor_scalar(W[n][:, :], raw[n][:, :], 2.0, -1.0, ALU.mult, ALU.add), l)
        k.dve(lambda e, i: e.tensor_tensor(W[0][:, 0:512], W[0][:, 0:512], W[0][:, 512:1024], ALU.subtract), c)
        k.dve(lambda e, i: e.tensor_scalar(scales[:, 1:3], scales[:, 1:3], 2.0, None, ALU.mult), l)
        h = [sb("h0", [P, FC * R4]), sb("h1", [P, FC * R4])]
        f_h = [Buffer(), Buffer()]
        f_bank = [Buffer() for _ in range(8)]
        k.barrier()
        k.loop(NT // 4)
        r0 = []
        for c in range(FC):
            n = c % 2
            mm = k.pe(lambda e, i, c=c, n=n: e.matmul(bank[n][:, :], W[0][:, c * P:(c + 1) * P], env.yT[:, bass.ts(i, R4)],
                                                      start=True, stop=True), f_bank[n].free)
            a = k.act(lambda e, i, c=c, n=n: e.activation(h[0][:, c * R4:(c + 1) * R4], bank[n][:, :], ACT.Relu, scale=scales[:, 0:1]),
                      mm, f_h[0].free)
            f_bank[n].read_by(a)
        r0 = a
        for c in range(FC):
            n = 2 + c % 2
            for kc in range(FC):
                mm = k.pe(lambda e, i, c=c, kc=kc, n=n: e.matmul(bank[n][:, :], W[1][:, kc * 512 + c * P:kc * 512 + (c + 1) * P],
                                                                 h[0][:, kc * R4:(kc + 1) * R4], start=kc == 0, stop=kc == FC - 1),
                          r0, f_bank[n].free)
            a = k.act(lambda e, i, c=c, n=n: e.activation(h[1][:, c * R4:(c + 1) * R4], bank[n][:, :], ACT.Relu, scale=scales[:, 1:2]),
                      mm, f_h[1].free)
            f_bank[n].read_by(a)
        f_h[0].read_by(mm)
        for s in range(4):
            for c in range(FC):
                mm = k.pe(lambda e, i, s=s, c=c: e.matmul(bank[4][:, s * P:(s + 1) * P], h[1][:, c * R4 + s * P:c * R4 + (s + 1) * P],
                                                          W[2][:, c * P:(c + 1) * P], start=c == 0, stop=c == FC - 1), a, f_bank[4].free)
        f_h[1].read_by(mm)
        f_bank[4].read_by(k.dve(lambda e, i: e.scalar_tensor_tensor(
            env.X[:, bass.ts(i, R4)], bank[4][:, :], scales[:, 2:3], env.X[:, bass.ts(i, R4)], ALU.mult, ALU.add), mm))
        k.barrier()


def l1_attention(env, w):
    k, bank = env.k, env.bank
    with ExitStack() as st:
        sb = lambda name, shape, dt=F32: k.sb(st, name, shape, dt)
        y = sb("y", [P, NTOK])
        k.straight()
        qkv_rows, _ = rows(k, st, "qkv_rows", w["qkv_w"])
        proj_rows, _ = rows(k, st, "proj_rows", w["proj_w"])
        bqk, _ = columns(k, st, "bqk", w["qkv_b"][0:2 * P])
        bv, _ = broadcast_row(k, st, "bv", w["qkv_b"][2 * P:3 * P])
        bp, _ = broadcast_row(k, st, "bp", w["proj_b"])
        gw, _ = broadcast_row(k, st, "gw", w["norm_w"])
        gb, l = broadcast_row(k, st, "gb", w["norm_b"])
        norm_tiles(env, y)
        qkvT = sb("qkvT", [P, 3 * P])
        projT = sb("projT", [P, P])
        transpose_blocks(env, qkv_rows, qkvT, 3, l)
        transpose_blocks(env, proj_rows, projT, 1, l, first_bank=1)
        same = block_diagonal(env, st, P ** -0.5)
        norm = Norm4(env, st)
        f_bank = [Buffer() for _ in range(8)]

        def group(d):
            hn, hT, v, att, oT, t1 = (sb(n, [P, R4]) for n in ("hn", "hT", "v", "att", "oT", "t1"))
            qk = [sb("qT", [P, R4]), sb("kT", [P, R4])]
            f_hn, f_hT, f_v, f_att, f_oT, f_t1 = (Buffer() for _ in range(6))
            f_qk = [Buffer(), Buffer()]
            ycp = k.dve(lambda e, i: e.tensor_copy(t1[:, :], y[:, bass.ts(2 * i + d, R4)]), f_t1.free)
            n1 = norm(t1, hn, gw, gb, [ycp, f_hn.free])
            yield
            for s in range(4):
                t = k.pe(lambda e, i, s=s: e.transpose(bank[0][:, s * P:(s + 1) * P], hn[:, s * P:(s + 1) * P], env.ident[:, :]),
                         n1, f_bank[0].free)
            f_hn.read_by(t)
            hc = k.act(lambda e, i: e.copy(hT[:, :], bank[0][:, :]), t, f_hT.free)
            f_bank[0].read_by(hc)
            yield
            for n in range(2):
                mm = k.pe(lambda e, i, n=n: e.matmul(bank[1 + n][:, :], qkvT[:, n * P:(n + 1) * P], hT[:, :], start=True, stop=True),
                          hc, f_bank[1 + n].free)
                qa = k.act(lambda e, i, n=n: e.activation(qk[n][:, :], bank[1 + n][:, :], ACT.Identity, bias=bqk[:, n:n + 1]),
                           mm, f_qk[n].free)
                f_bank[1 + n].read_by(qa)
            for s in range(4):
                mm = k.pe(lambda e, i, s=s: e.matmul(bank[3][:, s * P:(s + 1) * P], hT[:, s * P:(s + 1) * P], qkvT[:, 2 * P:3 * P],
                                                     start=True, stop=True), f_bank[3].free)
            f_hT.read_by(mm)
            four = lambda t: t[:, :].rearrange("p (t d) -> p t d", d=P)
            row = lambda t: t[:, :].unsqueeze(1).to_broadcast([P, 4, P])
            va = k.dve(lambda e, i: e.tensor_tensor(four(v), four(bank[3]), row(bv), ALU.add), mm, f_v.free)
            f_bank[3].read_by(va)
            yield
            for s in range(4):
                mm = k.pe(lambda e, i, s=s: e.matmul(bank[4][:, s * P:(s + 1) * P], qk[1][:, s * P:(s + 1) * P], qk[0][:, s * P:(s + 1) * P],
                                                     start=True, stop=True), qa, f_bank[4].free)
            f_qk[0].read_by(mm)
            f_qk[1].read_by(mm)
            aa = k.dve(lambda e, i: e.tensor_tensor(four(att), four(bank[4]), row(same), ALU.mult), mm, f_att.free)
            f_bank[4].read_by(aa)
            yield
            for s in range(4):
                mm = k.pe(lambda e, i, s=s: e.matmul(bank[5][:, s * P:(s + 1) * P], v[:, s * P:(s + 1) * P], att[:, s * P:(s + 1) * P],
                                                     start=True, stop=True), aa, va, f_bank[5].free)
            f_v.read_by(mm)
            f_att.read_by(mm)
            oc = k.act(lambda e, i: e.copy(oT[:, :], bank[5][:, :]), mm, f_oT.free)
            f_bank[5].read_by(oc)
            yield
            for s in range(4):
                mm = k.pe(lambda e, i, s=s: e.matmul(bank[6][:, s * P:(s + 1) * P], oT[:, s * P:(s + 1) * P], projT[:, :],
                                                     start=True, stop=True), oc, f_bank[6].free)
            f_oT.read_by(mm)
            a = k.dve(lambda e, i: e.tensor_tensor(t1[:, :], bank[6][:, :], t1[:, :], ALU.add), mm)
            f_bank[6].read_by(a)
            yield
            a = k.dve(lambda e, i: e.tensor_tensor(four(t1), four(t1), row(bp), ALU.add), a)
            f_t1.read_by(k.dve(lambda e, i: e.tensor_tensor(env.X[:, bass.ts(2 * i + d, R4)], env.X[:, bass.ts(2 * i + d, R4)], t1[:, :], ALU.add), a))

        k.barrier()
        k.loop(NT // 8)
        alternate(group(0), group(1))
        k.barrier()


def l1_ffn(env, w):
    k, bank = env.k, env.bank
    E, I = 8, 128
    CENTER, LOWER, UPPER = 1.0 / np.e, 0.5 - np.log(4.0 / 3.0), 0.5
    with ExitStack() as st:
        sb = lambda name, shape, dt=F32: k.sb(st, name, shape, dt)
        k.straight()
        Wg, Wu, Wd = (sb(n, [P, E * P]) for n in ("Wg", "Wu", "Wd"))
        for t, s in ((Wg, "Wg"), (Wu, "Wu"), (Wd, "Wd")):
            k.dma("w", lambda e, i, t=t, s=s: e.dma_start(t[:, :].rearrange("p (e n) -> p e n", e=E), w[s].rearrange("e p n -> p e n")))
        Wr, _ = rows(k, st, "Wr", w["Wr"])
        temp, l = broadcast_row(k, st, "temp", w["temperature"])
        norm_tiles(env)
        last = [k.dve(lambda e, i: e.reciprocal(temp[:, :], temp[:, :]), l)]
        for t in range(NT):
            mm = k.pe(lambda e, i, t=t: e.matmul(bank[0][:, t * E:(t + 1) * E], env.yT[:, t * P:(t + 1) * P], Wr[:, :],
                                                 start=True, stop=True), l)
        NE = NT * E
        names = {n: sb(n, [P, NE]) for n in ("inh", "dist", "zone", "hot", "wz", "fb", "left", "key", "pick", "order")}
        small = {n: sb(n, [P, NT]) for n in ("wsum", "none", "top", "fsum")}
        A = {n: t[:, :] for n, t in {**names, **small}.items()}
        te = lambda n: A[n].rearrange("p (t e) -> p t e", e=E)
        col = lambda n: A[n].unsqueeze(2).to_broadcast([P, NT, E])
        last.append(mm)

        def step(eng, fn):
            last[:] = [eng(fn, last)]

        TS = lambda o, a, s1, s2, p1, p2=None: step(k.dve, lambda e, i: (
            e.tensor_scalar(A[o], A[a], s1, s2, p1, p2) if p2 is not None else e.tensor_scalar(A[o], A[a], s1, s2, p1)))
        TT = lambda o, a, b, p: step(k.dve, lambda e, i: e.tensor_tensor(A[o], A[a], A[b], p))
        TC = lambda o, a, c, p: step(k.dve, lambda e, i: e.tensor_tensor(te(o), te(a), col(c), p))
        RD = lambda o, a, p: step(k.dve, lambda e, i: e.tensor_reduce(A[o], te(a), AX.X, p))
        for n in range(E):
            step(k.dve, lambda e, i, n=n: e.memset(te("order")[:, :, n], float(E - n)))
        step(k.act, lambda e, i: e.activation(A["inh"], bank[0][:, 0:NE], ACT.Sigmoid, scale=temp[:, 0:1]))
        TS("zone", "inh", LOWER, None, ALU.is_ge)
        TS("hot", "inh", UPPER, None, ALU.is_le)
        TT("zone", "zone", "hot", ALU.mult)
        TS("dist", "inh", CENTER, None, ALU.subtract)
        step(k.act, lambda e, i: e.activation(A["dist"], A["dist"], ACT.Abs))
        step(k.act, lambda e, i: e.activation(A["wz"], A["dist"], ACT.Exp, scale=-1.0 / 0.1))
        step(k.act, lambda e, i: e.activation(A["fb"], A["dist"], ACT.Exp, scale=-1.0 / 0.3))
        TT("wz", "wz", "zone", ALU.mult)
        RD("wsum", "wz", ALU.add)
        TS("none", "wsum", 1e-8, None, ALU.is_lt)
        TS("left", "fb", 1.0, None, ALU.mult)
        TS("pick", "fb", 0.0, None, ALU.mult)
        for _ in range(2):
            RD("top", "left", ALU.max)
            TC("key", "left", "top", ALU.is_equal)
            TT("key", "key", "order", ALU.mult)
            RD("top", "key", ALU.max)
            TC("key", "key", "top", ALU.is_equal)
            TT("pick", "pick", "key", ALU.add)
            TS("key", "key", -4.0, None, ALU.mult)
            TT("left", "left", "key", ALU.add)
        TT("fb", "fb", "pick", ALU.mult)
        RD("fsum", "fb", ALU.add)
        TS("fsum", "fsum", 1e-8, None, ALU.max)
        step(k.dve, lambda e, i: e.reciprocal(A["fsum"], A["fsum"]))
        TC("fb", "fb", "fsum", ALU.mult)
        TT("fb", "fb", "wz", ALU.subtract)
        TC("fb", "fb", "none", ALU.mult)
        TT("wz", "wz", "fb", ALU.add)
        RD("wsum", "wz", ALU.add)
        TS("wsum", "wsum", 1e-8, None, ALU.max)
        step(k.dve, lambda e, i: e.reciprocal(A["wsum"], A["wsum"]))
        TC("wz", "wz", "wsum", ALU.mult)
        weights = names["wz"]
        hs = [sb("h", [P, R4]) for _ in range(2)]
        wt = sb("wt", [P, 4 * E])
        f_h, f_bank, f_wt = [Buffer(), Buffer()], [Buffer() for _ in range(8)], Buffer()
        k.barrier()
        k.loop(NT // 4)
        wc = k.dve(lambda e, i: e.tensor_copy(wt[:, :], weights[:, bass.ts(i, 4 * E)]), f_wt.free)
        for x in range(E):
            z = x % 2
            g = k.pe(lambda e, i, x=x, z=z: e.matmul(bank[z][:, :], Wg[:, x * P:(x + 1) * P], env.yT[:, bass.ts(i, R4)],
                                                     start=True, stop=True), f_bank[z].free)
            u = k.pe(lambda e, i, x=x, z=z: e.matmul(bank[2 + z][:, :], Wu[:, x * P:(x + 1) * P], env.yT[:, bass.ts(i, R4)],
                                                     start=True, stop=True), f_bank[2 + z].free)
            a = k.act(lambda e, i, z=z: e.activation(hs[z][:, :], bank[z][:, :], ACT.Silu), g, f_h[z].free)
            f_bank[z].read_by(a)
            m = k.dve(lambda e, i, z=z: e.tensor_tensor(hs[z][:, :], hs[z][:, :], bank[2 + z][:, :], ALU.mult), a, u)
            f_bank[2 + z].read_by(m)
            for s in range(4):
                mm = k.pe(lambda e, i, x=x, z=z, s=s: e.matmul(bank[4 + z][:, s * P:(s + 1) * P], hs[z][:, s * P:(s + 1) * P],
                                                               Wd[:, x * P:(x + 1) * P], start=True, stop=True), m, f_bank[4 + z].free)
            f_h[z].read_by(mm)
            for s in range(4):
                prior = f_bank[4 + (x + 1) % 2].readers if x else None
                ad = k.dve(lambda e, i, x=x, z=z, s=s: e.scalar_tensor_tensor(
                    env.X[:, bass.ts(4 * i + s, P)], bank[4 + z][:, s * P:(s + 1) * P], wt[:, s * E + x:s * E + x + 1],
                    env.X[:, bass.ts(4 * i + s, P)], ALU.mult, ALU.add), mm, wc, prior)
            f_bank[4 + z].read_by(ad)
        f_wt.read_by(ad)
        k.barrier()


def l2_cross_attention(env, w, ctx_kv):
    k, bank = env.k, env.bank
    DQ = 32
    with ExitStack() as st:
        sb = lambda name, shape, dt=F32: k.sb(st, name, shape, dt)
        k.straight()
        Wq, Wk, Wv = sb("Wq", [DQ, P]), sb("Wk", [DQ, P]), sb("Wv", [P, P])
        for t, n in ((Wq, "Wq"), (Wk, "Wk"), (Wv, "Wv")):
            k.dma("w", lambda e, i, t=t, n=n: e.dma_start(t[:, :], w[n]))
        bq, _ = columns(k, st, "bq", w["bq"], DQ)
        bk, _ = columns(k, st, "bk", w["bk"], DQ)
        bv, _ = broadcast_row(k, st, "bv", w["bv"])
        norm_tiles(env)
        A, WvT, cg, g0, bq_all = sb("A", [P, P]), sb("WvT", [P, P]), sb("cg", [P, 2]), sb("g0", [P, 1]), sb("bq_all", [DQ, P])
        c0 = k.dve(lambda e, i: e.tensor_copy(bq_all[:, :], bq[:, 0:1].to_broadcast([DQ, P])))
        k.pe(lambda e, i: e.matmul(bank[0][:, 0:P], Wq[:, :], Wk[:, :], start=True, stop=True))
        k.pe(lambda e, i: e.matmul(bank[0][:, P:P + 1], Wk[:, :], bq[:, :], start=True, stop=True))
        k.pe(lambda e, i: e.matmul(bank[0][:, P + 1:P + 2], Wq[:, :], bk[:, :], start=True, stop=True))
        k.pe(lambda e, i: e.matmul(bank[0][:, P + 2:P + 3], bq_all[:, :], bk[:, :], start=True, stop=True), c0)
        t = k.pe(lambda e, i: e.transpose(bank[0][:, 2 * P:3 * P], Wv[:, :], env.ident[:, :]))
        k.dve(lambda e, i: e.tensor_copy(A[:, :], bank[0][:, 0:P]), t)
        cc = k.dve(lambda e, i: e.tensor_copy(cg[:, :], bank[0][:, P:P + 2]), t)
        gc = k.dve(lambda e, i: e.tensor_copy(g0[:, :], bank[0][:, P + 2:P + 3]), t)
        k.dve(lambda e, i: e.tensor_copy(WvT[:, :], bank[0][:, 2 * P:3 * P]), t)
        scale = DQ ** -0.5
        r_all = sb("r_all", [P, NT])
        for t in range(NT):
            mm = k.pe(lambda e, i, t=t: e.matmul(bank[1][:, t:t + 1], env.yT[:, t * P:(t + 1) * P], cg[:, 1:2], start=True, stop=True), cc)
        k.dve(lambda e, i: e.tensor_scalar(r_all[:, :], bank[1][:, 0:NT], g0[:, 0:1], scale, ALU.add, ALU.mult), mm, gc)
        of_batch = sb("of_batch", [P, BPT])
        a = k.dve(lambda e, i: e.memset(of_batch[:, :], 0.0))
        for b in range(BPT):
            k.dve(lambda e, i, b=b: e.memset(of_batch[b * SEQ:(b + 1) * SEQ, b:b + 1], 1.0), a)
        TILES = 8
        kv = [sb("kv", [P, BPT * 2 * P]) for _ in range(TILES)]
        kv_last = [sb("kv_last", [BPT, P]) for _ in range(TILES)]
        pair = lambda n, s: [sb(n, s) for _ in range(2)]
        zsum = sb("zsum", [P, TILES])
        kvT, qf, zt, z4 = (pair(n, [P, c]) for n, c in (("kvT", BPT * CTX), ("qf", P), ("z", CTX), ("z4", BPT)))
        zT, zT_last, U, UT, t1 = (pair(n, [p, c]) for n, p, c in
                                  (("zT", P, 2 * P), ("zT_last", BPT, P), ("U", P, P), ("UT", P, P), ("t1", P, P)))
        f = {n: [Buffer(), Buffer()] for n in ("kvT", "qf", "z", "z4", "zT", "zT_last", "U", "UT", "t1")}
        f_kv, f_zsum = ([Buffer() for _ in range(TILES)] for _ in range(2))
        f_bank = [Buffer() for _ in range(8)]

        def work(j):
            z, at = j % 2, lambda i: TILES * i + j
            for c in range(2):
                k.dma(f"kv{j}", lambda e, i, c=c: e.dma_start(
                    kv[j][:, :].rearrange("p (c b d) -> p c b d", b=BPT, c=2)[:, c],
                    ctx_kv[bass.ts(at(i), BPT), c * P:(c + 1) * P, :].rearrange("b p d -> p b d")), f_kv[j].free)
            ld = k.dma(f"kv{j}", lambda e, i: e.dma_start(
                kv_last[j][:, :], ctx_kv[bass.ts(at(i), BPT), 2 * P:CTX, :].rearrange("b c d -> b (c d)")), f_kv[j].free)
            yield
            yield
            T = kvT[z][:, :].rearrange("p (b s) -> p b s", b=BPT)
            evs = []
            for n in range(2):
                for r in range(2):
                    for c in range(2):
                        t = k.pe(lambda e, i, n=n, r=r, c=c: e.transpose(
                            bank[n][:, (2 * r + c) * P:(2 * r + c + 1) * P], kv[j][:, (c * BPT + 2 * n + r) * P:(c * BPT + 2 * n + r + 1) * P],
                            env.ident[:, :]), ld, f_bank[n].free)
                eng, op = ((k.dve, "tensor_copy"), (k.act, "copy"))[n]
                ev = eng(lambda e, i, n=n: (e.copy if n else e.tensor_copy)(
                    T[:, 2 * n:2 * n + 2, 0:2 * P], bank[n][:, :].rearrange("p (b s) -> p b s", b=2)), t, f["kvT"][z].free)
                f_bank[n].read_by(ev)
                evs.append(ev)
            k.pe(lambda e, i: e.transpose(bank[2][:, P:P + BPT], kv_last[j][:, :], env.ident[0:BPT, 0:BPT]), ld, f_bank[2].free, alone=True)
            mm = k.pe(lambda e, i: e.matmul(bank[2][:, 0:P], A[:, :], env.yT[:, bass.ts(at(i), P)], start=True, stop=True))
            evs.append(k.dve(lambda e, i: e.tensor_copy(T[:, :, 2 * P], bank[2][:, P:P + BPT]), mm))
            q = k.dve(lambda e, i: e.tensor_scalar(qf[z][:, :], bank[2][:, 0:P], cg[:, 0:1], None, ALU.add), mm, f["qf"][z].free)
            f_bank[2].read_by(q)
            yield
            for b in range(BPT):
                mm = k.pe(lambda e, i, b=b: e.matmul(
                    bank[3][b * SEQ:(b + 1) * SEQ, 0:CTX], qf[z][:, b * SEQ:(b + 1) * SEQ], kvT[z][:, b * CTX:(b + 1) * CTX],
                    start=True, stop=True, tile_position=(0, b * SEQ)), q, evs, f_bank[3].free)
            f["kvT"][z].read_by(mm)
            f["qf"][z].read_by(mm)
            sg = k.act(lambda e, i: e.activation(zt[z][:, :], bank[3][:, 0:CTX], ACT.Sigmoid, bias=r_all[:, bass.ds(at(i), 1)], scale=scale,
                                                 accum_out=zsum[:, j:j + 1]), mm, f["z"][z].free, f_zsum[j].free)
            f_bank[3].read_by(sg)
            zc = k.dve(lambda e, i: e.tensor_scalar(z4[z][:, :], of_batch[:, :], zt[z][:, 2 * P:CTX], None, ALU.mult), sg, f["z4"][z].free)
            yield
            for c in range(2):
                t = k.pe(lambda e, i, c=c: e.transpose(bank[4][:, c * P:(c + 1) * P], zt[z][:, c * P:(c + 1) * P], env.ident[:, :]),
                         sg, f_bank[4].free)
            t4 = k.pe(lambda e, i: e.transpose(bank[4][0:BPT, 2 * P:3 * P], z4[z][:, :], env.ident[:, :]), zc, alone=True)
            f["z"][z].read_by(t)
            f["z4"][z].read_by(t4)
            c1 = k.dve(lambda e, i: e.tensor_copy(zT[z][:, :], bank[4][:, 0:2 * P]), t4, f["zT"][z].free)
            c2 = k.dve(lambda e, i: e.tensor_copy(zT_last[z][:, :], bank[4][0:BPT, 2 * P:3 * P]), t4, f["zT_last"][z].free)
            f_bank[4].read_by(c2)
            yield
            k.pe(lambda e, i: e.matmul(bank[5][:, 0:P], zT_last[z][:, :], kv_last[j][:, :], start=True, stop=False), c2, f_bank[5].free)
            for b in range(BPT):
                for c in range(2):
                    mm = k.pe(lambda e, i, b=b, c=c: e.matmul(
                        bank[5][b * SEQ:(b + 1) * SEQ, 0:P], zT[z][:, c * P + b * SEQ:c * P + (b + 1) * SEQ],
                        kv[j][:, (c * BPT + b) * P:(c * BPT + b + 1) * P], start=False, stop=c == 1, tile_position=(0, b * SEQ)), c1)
            f["zT"][z].read_by(mm)
            f["zT_last"][z].read_by(mm)
            f_kv[j].read_by(mm)
            uc = k.act(lambda e, i: e.copy(U[z][:, :], bank[5][:, 0:P]), mm, f["U"][z].free)
            f_bank[5].read_by(uc)
            yield
            t = k.pe(lambda e, i: e.transpose(bank[6][:, 0:P], U[z][:, :], env.ident[:, :]), uc, f_bank[6].free)
            f["U"][z].read_by(t)
            uc = k.act(lambda e, i: e.copy(UT[z][:, :], bank[6][:, 0:P]), t, f["UT"][z].free)
            f_bank[6].read_by(uc)
            yield
            mm = k.pe(lambda e, i: e.matmul(bank[7][:, 0:P], UT[z][:, :], WvT[:, :], start=True, stop=True), uc, f_bank[7].free)
            f["UT"][z].read_by(mm)
            a = k.dve(lambda e, i: e.scalar_tensor_tensor(t1[z][:, :], bv[:, :], zsum[:, j:j + 1], bank[7][:, 0:P], ALU.mult, ALU.add),
                      mm, f["t1"][z].free)
            f_zsum[j].read_by(a)
            f_bank[7].read_by(a)
            f["t1"][z].read_by(k.pool(lambda e, i: e.tensor_tensor(
                env.X[:, bass.ts(at(i), P)], env.X[:, bass.ts(at(i), P)], t1[z][:, :], ALU.add), a, alone=True))

        k.barrier()
        k.loop(NT // TILES)
        staggered([work(j) for j in range(TILES)])
        k.barrier()


class HeadAttention:

    def __init__(self, env, st, head_mask):
        k = env.k
        self.env, self.head_mask = env, head_mask
        sb = lambda n, s: k.sb(st, n, s)
        self.kh = [sb("kh", [P, BPT * H * SEQ]) for _ in range(2)]
        self.s = [sb("s", [P, 512]) for _ in range(2)]
        self.mx = [sb("mx", [P, H]) for _ in range(2)]
        self.sum = [sb("sum", [P, P]) for _ in range(2)]
        self.pT = [sb("pT", [P, H * P]) for _ in range(2)]
        for t in self.pT:
            k.pool(lambda e, i, t=t: e.memset(t[:, :], 0.0))
        self.ones4 = self.four_copies(st, "ones4")
        self.ones_made = k.pool(lambda e, i: e.memset(self.own_columns(self.ones4[:, :]), 1.0), self.cleared)
        self.scored, self.applied = {}, {}
        self.f = {n: [Buffer(), Buffer()] for n in ("kh", "s", "mx", "sum", "pT")}

    V4 = 4 * (P + 8)

    def four_copies(self, st, name):
        t = self.env.k.sb(st, name, [P, self.V4])
        self.cleared = self.env.k.pool(lambda e, i: e.memset(t[:, :], 0.0))
        return t

    def own_columns(self, t):
        return t.rearrange("p (m x) -> p m x", m=4)[:, :, 0:P].rearrange("p m (r c) -> p m r c", r=4)[:, :, :, 0:8]

    def work(self, j, qT, kT, v4, out, ready, v_ready, f_bank, score_banks, out_bank, scale, made, table=None, out_free=None):
        k, bank, f, z = self.env.k, self.env.bank, self.f, j % 2
        hb = lambda t: t.rearrange("p (h q) -> p h q", h=H)
        wide = lambda t, n=SEQ: t[:, :].unsqueeze(2).to_broadcast([P, H, n])
        sbank, kh, S, mx, sm, pT = score_banks[z], self.kh[z], self.s[z], self.mx[z], self.sum[z], self.pT[z]
        k4 = kh[:, :].rearrange("p (b h q) -> p b h q", b=BPT, h=H)
        kb = kT.rearrange("p (b q) -> p b q", b=BPT)
        masked = [k.pool(lambda e, i: e.tensor_tensor(
            k4[:, 2:4], kb[:, 2:4].unsqueeze(2).to_broadcast([P, 2, H, SEQ]),
            self.head_mask[:, :].unsqueeze(1).unsqueeze(3).to_broadcast([P, 2, H, SEQ]), ALU.mult), ready, f["kh"][z].free)]
        for h in range(H):
            m = k.act(lambda e, i, h=h: e.activation(k4[:, 0:2, h], kb[:, 0:2], ACT.Copy, scale=self.head_mask[:, h:h + 1]), ready, f["kh"][z].free)
        masked.append(m)
        yield
        for b in range(BPT):
            mm = k.pe(lambda e, i, b=b: e.matmul(
                bank[sbank][b * SEQ:(b + 1) * SEQ, :], qT[:, b * SEQ:(b + 1) * SEQ], kh[:, b * 512:(b + 1) * 512],
                start=True, stop=True, tile_position=(0, b * SEQ)), masked, f_bank[sbank].free)
        f["kh"][z].read_by(mm)
        self.scored[j] = mm
        yield
        if table is not None:
            a = k.dve(lambda e, i: e.scalar_tensor_tensor(hb(bank[sbank][:, :]), hb(bank[sbank][:, :]), scale,
                                                          table[:, :].unsqueeze(1).to_broadcast([P, H, SEQ]), ALU.mult, ALU.add), mm)
        else:
            a = mm
        m = k.dve(lambda e, i: e.tensor_reduce(mx[:, :], hb(bank[sbank][:, :]), AX.X, ALU.max), a, f["mx"][z].free)
        d = k.dve(lambda e, i: e.tensor_tensor(hb(S[:, :]), hb(bank[sbank][:, :]), wide(mx), ALU.subtract), m, f["s"][z].free)
        f["mx"][z].read_by(d)
        f_bank[sbank].read_by(d)
        x = k.act(lambda e, i: e.activation(S[:, :], S[:, :], ACT.Exp, scale=scale if table is None else 1.0), d)
        yield
        for b in range(BPT):
            t = k.dve(lambda e, i, b=b: e.transpose(
                pT[:, :].rearrange("p (h b q) -> p b h q", h=H, b=BPT)[b * SEQ:(b + 1) * SEQ, b],
                hb(S[:, :])[b * SEQ:(b + 1) * SEQ]), x, f["pT"][z].free)
        f["s"][z].read_by(t)
        yield
        col = lambda t, m, r: t[:, m * P + 32 * r:m * P + 32 * r + 32]
        for n, left in enumerate((v4, self.ones4)):
            for m in range(4):
                for r in range(4):
                    mm = k.pe(lambda e, i, n=n, m=m, r=r, left=left: e.matmul(
                        bank[out_bank][32 * r:32 * r + 32, n * P:(n + 1) * P], col(left, m, r), pT[:, (4 * r + m) * P:(4 * r + m + 1) * P],
                        start=m == 0, stop=m == 3, tile_position=(0, 32 * r)), t, v_ready, f_bank[out_bank].free)
        f["pT"][z].read_by(mm)
        self.applied[j] = mm
        yield
        rc = k.dve(lambda e, i: e.reciprocal(sm[:, :], bank[out_bank][:, P:2 * P]), mm, f["sum"][z].free)
        o = k.dve(lambda e, i: e.tensor_tensor(out, bank[out_bank][:, 0:P], sm[:, :], ALU.mult), rc, out_free)
        f["sum"][z].read_by(o)
        f_bank[out_bank].read_by(o)
        made.append(o)


def l2_tables():
    f = np.float32
    t = np.arange(SEQ, dtype=f)
    freq = (1.0 / 10000.0 ** (np.arange(0, 8, 2, dtype=f) / f(8))).astype(f)
    angle = np.outer(t, freq).astype(f)
    cos, sin = np.cos(angle).astype(f), np.sin(angle).astype(f)
    cos8 = np.concatenate([cos, cos], 1)
    sin8 = np.concatenate([-sin, sin], 1)
    d = t[:, None] - t[None, :]
    bias = -0.1 * np.log(np.abs(d) + 1.0) + np.log(np.exp(-np.maximum(d, 0.0) * 0.01) + 1e-9)
    return {"rope_cos": np.tile(cos8, (1, H)).T.astype(f), "rope_sin": np.tile(sin8, (1, H)).T.astype(f),
            "distance_bias": np.tile(bias, (BPT, 1)).astype(f)}


def head_constants(env, st):
    k = env.k
    hm, sh = k.sb(st, "head_mask", [P, H]), k.sb(st, "same_head", [P, P])
    a = k.pool(lambda e, i: e.memset(hm[:, :], 1.0))
    b = k.pool(lambda e, i: e.affine_select(out=hm[:, :], in_=hm[:, :], compare_op=ALU.is_ge, fill=0.0, base=0,
                                            pattern=[[-8, H]], channel_multiplier=1), a)
    c = k.pool(lambda e, i: e.affine_select(out=hm[:, :], in_=hm[:, :], compare_op=ALU.is_ge, fill=0.0, base=7,
                                            pattern=[[8, H]], channel_multiplier=-1), b)
    d = k.dve(lambda e, i: e.tensor_copy(sh[:, :].rearrange("p (h j) -> p h j", h=H), hm[:, :].unsqueeze(2).to_broadcast([P, H, 8])), c)
    return hm, sh, d


def l2_attention(env, w, tables):
    k, bank = env.k, env.bank
    DL = 32
    with ExitStack() as st:
        sb = lambda name, shape, dt=F32: k.sb(st, name, shape, dt)
        k.straight()
        Wq, _ = rows(k, st, "Wq", w["Wq"])
        Wd, _ = rows(k, st, "Wd", w["Wkv_down"])
        Wo, _ = rows(k, st, "Wo", w["Wo"])
        bd, _ = columns(k, st, "bd", w["bkv_down"], DL)
        b_qk = [sb("b_qk", [P, 1]) for _ in range(4)]
        Wqs = sb("Wqs", [P, P])
        Wk, Wks, Wv = (sb(n, [DL, P]) for n in ("Wk", "Wks", "Wv"))
        bv = sb("bv", [P, P])
        swapped = lambda src, n: src.rearrange("(g two j) -> two g j", two=2, j=4)[n]
        up_b = w["bkv_up"].rearrange("(h two j) -> two h j", two=2, h=H)
        bv_col = sb("bv_col", [P, 1])
        k.dma("w", lambda e, i: e.dma_start(bv_col[:, :], up_b[1].rearrange("h (j a) -> h j a", a=1)))
        for n, src in ((0, w["bq"].rearrange("(h j) -> h j", h=H)), (2, up_b[0])):
            k.dma("w", lambda e, i, n=n, src=src: e.dma_start(b_qk[n][:, :], src.rearrange("h (j a) -> h j a", a=1)))
        for t, src in ((bv, up_b[1]),):
            k.dma("w", lambda e, i, t=t, src=src: e.dma_start(t[:, :].rearrange("p (h j) -> p h j", h=H), src.partition_broadcast(P)))
        up_w = w["Wkv_up"].rearrange("l (h two j) -> l h two j", two=2, h=H)
        for t, n in ((Wk, 0), (Wv, 1)):
            k.dma("w", lambda e, i, t=t, n=n: e.dma_start(t[:, :].rearrange("l (h j) -> l h j", h=H), up_w[:, :, n]))
        bo, _ = broadcast_row(k, st, "bo", w["bo"])
        cos, sin, dist = sb("cos", [P, SEQ]), sb("sin", [P, SEQ]), sb("dist", [P, SEQ])
        for t, n in ((cos, "rope_cos"), (sin, "rope_sin"), (dist, "distance_bias")):
            k.dma("w", lambda e, i, t=t, n=n: e.dma_start(t[:, :], tables[n]))
        norm_tiles(env)
        halves = lambda t, n: t[:, :].rearrange("p (g two j) -> p g two j", two=2, j=4)[:, :, n]
        for src, dst in ((Wq, Wqs), (Wk, Wks)):
            for n in range(2):
                k.dve(lambda e, i, src=src, dst=dst, n=n: e.tensor_copy(halves(dst, n), halves(src, 1 - n)))
        perm = sb("perm", [P, P])
        pd = [k.dve(lambda e, i, n=n: e.tensor_copy(halves(perm, n), halves(env.ident, 1 - n))) for n in range(2)]
        for n in (0, 2):
            t = k.pe(lambda e, i, n=n: e.matmul(bank[0][:, n:n + 1], perm[:, :], b_qk[n][:, :], start=True, stop=True), pd)
        for n in (0, 2):
            k.dve(lambda e, i, n=n: e.tensor_copy(b_qk[n + 1][:, :], bank[0][:, n:n + 1]), t)
        hm, sh, _ = head_constants(env, st)
        attn = HeadAttention(env, st, hm)
        TILES = RING = 8
        ring = {n: [sb(n, [P, c]) for _ in range(RING)] for n, c in
                (("q", P), ("qs", P), ("k", P), ("ks", P), ("v4", HeadAttention.V4), ("o", P), ("oT", P), ("gate", P), ("mem", 2 * BPT), ("sum", P))}
        ring["lat"] = [sb("lat", [DL, P]) for _ in range(RING)]
        f = {n: [Buffer() for _ in range(RING)] for n in ring}
        for t in ring["v4"]:
            k.pool(lambda e, i, t=t: e.memset(t[:, :], 0.0))
        f_bank = [Buffer() for _ in range(8)]
        bq_ = lambda t: t[:, :].rearrange("p (b q) -> p b q", q=SEQ)

        def work(j):
            r, at = j % RING, lambda i: TILES * i + j
            T = {n: t[r] for n, t in ring.items()}
            F = {n: t[r] for n, t in f.items()}
            for n, W in enumerate((Wq, Wqs)):
                mq = k.pe(lambda e, i, n=n, W=W: e.matmul(bank[0][:, n * P:(n + 1) * P], W[:, :], env.yT[:, bass.ts(at(i), P)],
                                                          start=True, stop=True), f_bank[0].free)
            ml = k.pe(lambda e, i: e.matmul(bank[0][0:DL, 2 * P:3 * P], Wd[:, :], env.yT[:, bass.ts(at(i), P)], start=True, stop=True))

            def rotary(name, b, at_col, banks, mm):
                for n, (t, table) in enumerate(((name, cos), (name + "s", sin))):
                    a = k.dve(lambda e, i, n=n, t=t, table=table: e.scalar_tensor_tensor(
                        bq_(T[t]), bank[banks][:, at_col + n * P:at_col + (n + 1) * P].rearrange("p (b q) -> p b q", q=SEQ),
                        b_qk[b + n][:, 0:1], table[:, :].unsqueeze(1).to_broadcast([P, BPT, SEQ]), ALU.add, ALU.mult), mm, F[t].free)
                f_bank[banks].read_by(a)
                both = k.pool(lambda e, i: e.tensor_tensor(T[name][:, :], T[name][:, :], T[name + "s"][:, :], ALU.add), a)
                F[name + "s"].read_by(both)
                return both

            yield
            la = k.dve(lambda e, i: e.tensor_scalar(T["lat"][:, :], bank[0][0:DL, 2 * P:3 * P], bd[:, 0:1], None, ALU.add), ml, F["lat"].free)
            rq = rotary("q", 0, 0, 0, ml)
            yield
            for n, W in enumerate((Wk, Wks)):
                k.pe(lambda e, i, n=n, W=W: e.matmul(bank[1][:, n * P:(n + 1) * P], W[:, :], T["lat"][:, :], start=True, stop=True), la, f_bank[1].free)
            k.pe(lambda e, i: e.matmul(bank[1][:, 3 * P:4 * P], Wv[:, :], T["lat"][:, :], start=True, stop=True))
            mkv = k.pe(lambda e, i: e.matmul(bank[1][:, 2 * P:3 * P], T["lat"][:, :], Wv[:, :], start=True, stop=True))
            F["lat"].read_by(mkv)
            yield
            va = k.dve(lambda e, i: e.tensor_tensor(
                attn.own_columns(T["v4"][:, :]), bank[1][:, 2 * P:3 * P].rearrange("p (r m j) -> p m r j", r=4, m=4),
                bv[:, :].rearrange("p (r m j) -> p m r j", r=4, m=4), ALU.add), mkv, F["v4"].free)
            vs = k.dve(lambda e, i: e.tensor_reduce(T["mem"][:, BPT:2 * BPT], bank[1][:, 3 * P:4 * P].rearrange("p (b q) -> p b q", q=SEQ),
                                                    AX.X, ALU.add), mkv, F["mem"].free)
            rk = rotary("k", 2, 0, 1, mkv)
            yield
            made = []
            head = attn.work(j, T["q"][:, :], T["k"][:, :], T["v4"][:, :], T["o"][:, :], [rq, rk], va, f_bank, (3, 4), 5, 8 ** -0.5, made, dist, F["o"].free)
            next(head)
            m1 = k.dve(lambda e, i: e.tensor_reduce(T["mem"][:, 0:BPT], bq_(T["k"]), AX.X, ALU.add), rk)
            m2 = k.dve(lambda e, i: e.tensor_scalar(T["mem"][:, BPT:2 * BPT], T["mem"][:, BPT:2 * BPT], 1.0 / SEQ, bv_col[:, 0:1],
                                                    ALU.mult, ALU.add), vs)
            yield
            next(head)
            F["k"].read_by(attn.scored[j], m1)
            ga = k.dve(lambda e, i: e.scalar_tensor_tensor(bq_(T["gate"]), bq_(T["q"]), 1.0 / SEQ, T["mem"][:, 0:BPT].unsqueeze(2).to_broadcast([P, BPT, SEQ]),
                                                           ALU.mult, ALU.mult), rq, m1, F["gate"].free)
            F["q"].read_by(attn.scored[j], ga)
            yield
            next(head)
            yield
            next(head)
            mg = k.pe(lambda e, i: e.matmul(bank[2][:, 0:P], sh[:, :], T["gate"][:, :], start=True, stop=True), ga, f_bank[2].free)
            x = k.act(lambda e, i: e.activation(T["gate"][:, :], bank[2][:, 0:P], ACT.Tanh, scale=0.5), mg)
            f_bank[2].read_by(x)
            yield
            next(head)
            F["v4"].read_by(attn.applied[j])
            gb = k.dve(lambda e, i: e.scalar_tensor_tensor(bq_(T["gate"]), bq_(T["gate"]), 1.0, T["mem"][:, BPT:2 * BPT].unsqueeze(2).to_broadcast([P, BPT, SEQ]),
                                                           ALU.add, ALU.mult), x, m2)
            F["mem"].read_by(gb)
            yield
            next(head, None)
            yield
            oa = k.dve(lambda e, i: e.scalar_tensor_tensor(T["oT"][:, :], T["gate"][:, :], 0.5 * 0.2, T["o"][:, :], ALU.mult, ALU.add),
                       gb, made, F["oT"].free)
            F["o"].read_by(oa)
            F["gate"].read_by(oa)
            mo = k.pe(lambda e, i: e.matmul(bank[7][:, 0:P], T["oT"][:, :], Wo[:, :], start=True, stop=True), oa, f_bank[7].free)
            F["oT"].read_by(mo)
            a = k.dve(lambda e, i: e.tensor_tensor(T["sum"][:, :], bank[7][:, 0:P], bo[:, :], ALU.add), mo, F["sum"].free)
            f_bank[7].read_by(a)
            xs = lambda i: env.X[:, bass.ts(at(i), P)]
            F["sum"].read_by(k.pool(lambda e, i: e.tensor_tensor(xs(i), xs(i), T["sum"][:, :], ALU.add), a, alone=True))

        k.barrier()
        k.loop(NT // TILES)
        staggered([work(j) for j in range(TILES)])
        k.barrier()


def l3_attention(env, w):
    k, bank = env.k, env.bank
    R, TOP = 64, 6
    with ExitStack() as st:
        sb = lambda name, shape, dt=F32: k.sb(st, name, shape, dt)
        y = sb("y", [P, NTOK])
        k.straight()
        in_rows, _ = rows(k, st, "in_rows", w["in_proj_w"])
        QK_rows = sb("QK_rows", [P, P])
        k.dma("w", lambda e, i: e.dma_start(QK_rows[0:R, :], w["Qp_w"]))
        k.dma("w", lambda e, i: e.dma_start(QK_rows[R:2 * R, :], w["Kp_w"]))
        out_rows, _ = rows(k, st, "out_rows", w["out_proj_w"])
        V_rows, _ = rows(k, st, "V_rows", w["Vp_w"])
        f1_rows, _ = rows(k, st, "f1_rows", w["ff1_w"])
        f2_rows, _ = rows(k, st, "f2_rows", w["ff2_w"])
        b_qk, _ = columns(k, st, "b_qk", w["in_proj_b"][0:2 * P])
        b_Q, _ = columns(k, st, "b_Q", w["Qp_b"], R)
        b_K, _ = columns(k, st, "b_K", w["Kp_b"], R)
        b_f1, _ = columns(k, st, "b_f1", w["ff1_b"])
        b_vV = sb("b_vV", [P, 2 * P])
        k.dma("w", lambda e, i: e.dma_start(b_vV[:, 0:P], w["in_proj_b"][2 * P:3 * P].partition_broadcast(P)))
        k.dma("w", lambda e, i: e.dma_start(b_vV[:, P:2 * P], w["Vp_b"].partition_broadcast(P)))
        b_out, _ = broadcast_row(k, st, "b_out", w["out_proj_b"])
        b_f2, _ = broadcast_row(k, st, "b_f2", w["ff2_b"])
        lam, _ = broadcast_row(k, st, "lam", w["lam"])
        g1, _ = broadcast_row(k, st, "g1", w["ln1_g"])
        be1, _ = broadcast_row(k, st, "be1", w["ln1_b"])
        g2, _ = broadcast_row(k, st, "g2", w["ln2_g"])
        be2, l = broadcast_row(k, st, "be2", w["ln2_b"])
        norm_tiles(env, y)
        inT, outT, QKT, vVT, f1T, f2T = (sb(n, [P, c * P]) for n, c in
                                         (("inT", 2), ("outT", 1), ("QKT", 1), ("vVT", 2), ("f1T", 4), ("f2T", 4)))
        transpose_blocks(env, in_rows, inT, 2, l)
        transpose_blocks(env, None, vVT, 2, l, src_at=lambda n: in_rows[:, 2 * P:3 * P] if n == 0 else V_rows[:, :], first_bank=1)
        transpose_blocks(env, out_rows, outT, 1, l, first_bank=2)
        transpose_blocks(env, QK_rows, QKT, 1, l, first_bank=3)
        transpose_blocks(env, f1_rows, f1T, 4, l)
        transpose_blocks(env, f2_rows, f2T, 4, l, first_bank=1)
        sig = k.act(lambda e, i: e.activation(lam[:, :], lam[:, :], ACT.Sigmoid), l)
        one_minus = sb("one_minus", [P, 1])
        k.dve(lambda e, i: e.tensor_scalar(one_minus[:, :], lam[:, :], -1.0, 1.0, ALU.mult, ALU.add), sig)
        hm, _, _ = head_constants(env, st)
        attn = HeadAttention(env, st, hm)
        norm = Norm4(env, st)
        ys, V2, oT, s1, s2, x1T, mix = (sb(n, [P, R4]) for n in ("ys", "V2", "oT", "s1", "s2", "x1T", "mix"))
        v = sb("v4", [P, 4 * attn.V4])
        k.dve(lambda e, i: e.memset(v[:, :], 0.0))
        qk = [sb("qT", [P, R4]), sb("kT", [P, R4])]
        QK = [sb("QT", [R, R4]), sb("KT", [R, R4])]
        W34 = SEQ + 2
        aw, rest, top = sb("aw", [P, 4 * W34]), sb("rest", [P, 4 * W34]), sb("top", [P, 32])
        amx, asm, sp = sb("amx", [P, 4]), sb("asm", [P, 4]), sb("sp", [P, 4 * SEQ])
        spT = sb("spT", [P, R4])
        hT = sb("hT", [P, 4 * R4])
        k.dve(lambda e, i: e.memset(aw[:, :], 2.0))
        k.dve(lambda e, i: e.memset(spT[:, :], 0.0))
        names = "ys v V2 o oT s1 s2 x1T mix q k Q K aw rest top amx asm sp spT hT".split()
        f = {n: Buffer() for n in names}
        f_bank = [Buffer() for _ in range(8)]
        four = lambda t: t[:, :].rearrange("p (t d) -> p t d", d=P)
        row = lambda t: t[:, :].unsqueeze(1).to_broadcast([P, 4, P])
        k.barrier()
        m_s1 = Buffer()

        def sparse_weights(ready, result):
            for s in range(4):
                for b in range(BPT):
                    c = s * P + b * SEQ
                    mm = k.pe(lambda e, i, s=s, b=b, c=c: e.matmul(
                        bank[3][b * SEQ:(b + 1) * SEQ, s * SEQ:(s + 1) * SEQ], QK[0][:, c:c + SEQ], QK[1][:, c:c + SEQ],
                        start=True, stop=True, tile_position=(0, b * SEQ)), ready, f_bank[3].free, alone=True)
            f["Q"].read_by(mm)
            f["K"].read_by(mm)
            S3 = bank[3][:, 0:P].rearrange("p (s k) -> p s k", s=4)
            A3 = aw[:, :].rearrange("p (s k) -> p s k", s=4)[:, :, 0:SEQ]
            R3 = rest[:, :].rearrange("p (s k) -> p s k", s=4)[:, :, 0:SEQ]
            P3 = sp[:, :].rearrange("p (s k) -> p s k", s=4)
            wide4 = lambda t: t[:, :].unsqueeze(2).to_broadcast([P, 4, SEQ])
            a = k.dve(lambda e, i: e.tensor_reduce(amx[:, :], S3, AX.X, ALU.max), mm, f["amx"].free)
            a = k.dve(lambda e, i: e.tensor_tensor(A3, S3, wide4(amx), ALU.subtract), a, f["aw"].free)
            f_bank[3].read_by(a)
            f["amx"].read_by(a)
            yield
            a = k.act(lambda e, i: e.activation(A3, A3, ACT.Exp, scale=R ** -0.5), a)
            a = k.dve(lambda e, i: e.tensor_reduce(asm[:, :], A3, AX.X, ALU.add), a, f["asm"].free)
            a = k.dve(lambda e, i: e.reciprocal(asm[:, :], asm[:, :]), a)
            a = k.dve(lambda e, i: e.tensor_tensor(A3, A3, wide4(asm), ALU.mult), a)
            for s in range(4):
                t = k.dve(lambda e, i, s=s: e.max(top[:, 8 * s:8 * s + 8], aw[:, s * W34:(s + 1) * W34]), a, f["top"].free, alone=True)
            for s in range(4):
                m = k.dve(lambda e, i, s=s: e.match_replace(rest[:, s * W34:(s + 1) * W34], top[:, 8 * s:8 * s + 8],
                                                            aw[:, s * W34:(s + 1) * W34], 0.0), t, f["rest"].free, alone=True)
            f["top"].read_by(m)
            yield
            a = k.dve(lambda e, i: e.tensor_tensor(P3, A3, R3, ALU.subtract), m, f["sp"].free)
            f["aw"].read_by(a)
            f["rest"].read_by(a)
            a = k.dve(lambda e, i: e.tensor_reduce(asm[:, :], P3, AX.X, ALU.add), a)
            a = k.dve(lambda e, i: e.tensor_scalar(asm[:, :], asm[:, :], 1e-9, None, ALU.add), a)
            a = k.dve(lambda e, i: e.reciprocal(asm[:, :], asm[:, :]), a)
            a = k.dve(lambda e, i: e.tensor_tensor(P3, P3, wide4(asm), ALU.mult), a)
            f["asm"].read_by(a)
            for b in range(BPT):
                t = k.dve(lambda e, i, b=b: e.transpose(
                    spT[:, :].rearrange("p (s b q) -> p b s q", s=4, b=BPT)[b * SEQ:(b + 1) * SEQ, b],
                    P3[b * SEQ:(b + 1) * SEQ]), a, f["spT"].free)
            f["sp"].read_by(t)
            result.append(t)

        def attention(at):
            yc = k.pool(lambda e, i: e.tensor_copy(ys[:, :], env.yT[:, bass.ts(at(i), R4)]), f["ys"].free, alone=True)
            made = []
            for n in range(4):
                wide = n < 2
                rows_ = P if wide else R
                lhs = inT[:, n * P:(n + 1) * P] if wide else QKT[:, (n - 2) * R:(n - 1) * R]
                dst = qk[n] if wide else QK[n - 2]
                b = b_qk[:, n:n + 1] if wide else (b_Q, b_K)[n - 2][:, 0:1]
                mm = k.pe(lambda e, i, n=n, lhs=lhs, rows_=rows_: e.matmul(bank[n][0:rows_, :], lhs, ys[:, :], start=True, stop=True),
                          yc, f_bank[n].free)
                a = k.act(lambda e, i, n=n, dst=dst, b=b, rows_=rows_: e.activation(dst[:, :], bank[n][0:rows_, :], ACT.Identity, bias=b),
                          mm, f["qkQK"[n]].free)
                f_bank[n].read_by(a)
                made.append(a)
            yield
            for s in range(4):
                z = 4 + s % 2
                mm = k.pe(lambda e, i, s=s, z=z: e.matmul(bank[z][:, 0:2 * P], ys[:, s * P:(s + 1) * P], vVT[:, :], start=True, stop=True),
                          f_bank[z].free)
                heads = lambda t: t.rearrange("p (r m j) -> p m r j", r=4, m=4)
                vb = k.dve(lambda e, i, s=s, z=z, heads=heads: e.tensor_tensor(
                    attn.own_columns(v[:, s * attn.V4:(s + 1) * attn.V4]), heads(bank[z][:, 0:P]), heads(b_vV[:, 0:P]), ALU.add), mm, f["v"].free)
                vb = k.dve(lambda e, i, s=s, z=z: e.tensor_tensor(
                    V2[:, s * P:(s + 1) * P], bank[z][:, P:2 * P], b_vV[:, P:2 * P], ALU.add), mm, f["V2"].free)
                f_bank[z].read_by(vb)
            f["ys"].read_by(mm)
            yield
            outs = []
            tile = lambda t, s, n=P: t[:, s * n:(s + 1) * n]
            turned = []
            yield from together(sparse_weights(made, turned), stagger([attn.work(s, tile(qk[0], s), tile(qk[1], s), tile(v, s, attn.V4), tile(oT, s), made, vb, f_bank, (6, 7), 4, 8 ** -0.5, outs,
                                 None, f["oT"].free) for s in range(4)]))
            for n in "qkv":
                f[n].read_by(outs[-1])
            for s in range(4):
                mm = k.pe(lambda e, i, s=s: e.matmul(bank[0][:, s * P:(s + 1) * P], spT[:, s * P:(s + 1) * P], V2[:, s * P:(s + 1) * P],
                                                     start=True, stop=True), turned, f_bank[0].free)
            f["spT"].read_by(mm)
            f["V2"].read_by(mm)
            for s in range(4):
                md = k.pe(lambda e, i, s=s: e.matmul(bank[2][:, s * P:(s + 1) * P], oT[:, s * P:(s + 1) * P], outT[:, :], start=True, stop=True),
                          outs, f_bank[2].free)
            f["oT"].read_by(md)
            a = k.dve(lambda e, i: e.tensor_tensor(four(mix), four(bank[2]), row(b_out), ALU.add), md, f["mix"].free)
            f_bank[2].read_by(a)
            b = k.dve(lambda e, i: e.scalar_tensor_tensor(s1[:, :], bank[0][:, :], one_minus[:, 0:1], y[:, bass.ts(at(i), R4)], ALU.mult, ALU.add),
                      mm, f["s1"].free)
            f_bank[0].read_by(b)
            a = k.dve(lambda e, i: e.scalar_tensor_tensor(s1[:, :], mix[:, :], lam[:, 0:1], s1[:, :], ALU.mult, ALU.add), a, b)
            f["mix"].read_by(a)
            m_s1.made_by(a)

        def mlp(at):
            n1 = norm(s1, s2, g1, be1, [m_s1.made, f["s2"].free])
            f["s1"].read_by(norm.last_read)
            yield
            for s in range(4):
                t = k.pe(lambda e, i, s=s: e.transpose(bank[5][:, s * P:(s + 1) * P], s2[:, s * P:(s + 1) * P], env.ident[:, :]),
                         n1, f_bank[5].free)
            xc = k.act(lambda e, i: e.copy(x1T[:, :], bank[5][:, :]), t, f["x1T"].free)
            f_bank[5].read_by(xc)
            yield
            for c in range(4):
                n = (5, 0)[c % 2]
                mm = k.pe(lambda e, i, c=c, n=n: e.matmul(bank[n][:, :], f1T[:, c * P:(c + 1) * P], x1T[:, :], start=True, stop=True),
                          xc, f_bank[n].free)
                re = k.act(lambda e, i, c=c, n=n: e.activation(hT[:, c * R4:(c + 1) * R4], bank[n][:, :], ACT.Relu, bias=b_f1[:, c:c + 1]),
                           mm, f["hT"].free)
                f_bank[n].read_by(re)
            f["x1T"].read_by(mm)
            yield
            for s in range(4):
                for c in range(4):
                    mm = k.pe(lambda e, i, s=s, c=c: e.matmul(bank[1][:, s * P:(s + 1) * P], hT[:, c * R4 + s * P:c * R4 + (s + 1) * P],
                                                              f2T[:, c * P:(c + 1) * P], start=c == 0, stop=c == 3), re, f_bank[1].free)
            f["hT"].read_by(mm)
            a = k.dve(lambda e, i: e.tensor_tensor(s2[:, :], bank[1][:, :], s2[:, :], ALU.add), mm)
            f_bank[1].read_by(a)
            yield
            a = k.dve(lambda e, i: e.tensor_tensor(four(s2), four(s2), row(b_f2), ALU.add), a)
            n2 = norm(s2, s2, g2, be2, a)
            yield
            f["s2"].read_by(k.dve(lambda e, i: e.tensor_tensor(env.X[:, bass.ts(at(i), R4)], env.X[:, bass.ts(at(i), R4)], s2[:, :], ALU.add), n2))

        k.straight()
        alternate(attention(lambda i: 0))
        k.loop(NT // 4 - 1)
        alternate(attention(lambda i: i + 1), mlp(lambda i: i))
        k.loop(1)
        k.seg.first = NT // 4 - 1
        alternate(mlp(lambda i: i))
        k.barrier()


def l2_ffn(env, w, tables):
    k, bank = env.k, env.bank
    E, SETS, F = 32, 4, 32
    ES = E * SETS
    with ExitStack() as st:
        sb = lambda name, shape, dt=F32: k.sb(st, name, shape, dt)
        y = sb("y", [P, NTOK])
        k.straight()
        Wc, _ = rows(k, st, "Wc", w["Wc"].rearrange("d e s -> d (e s)"))
        bc = sb("bc", [P, 1])
        k.dma("w", lambda e, i: e.dma_start(bc[:, :], w["bc"].rearrange("e (s a) -> (e s) a", a=1)))
        b1 = sb("b1", [P, E])
        k.dma("w", lambda e, i: e.dma_start(b1[:, :], w["b1"].rearrange("e s f -> (s f) e")))
        b2 = sb("b2", [P, P])
        k.dma("w", lambda e, i: e.dma_start(b2[:, :], w["b2"].rearrange("e s d -> (e s) d")))
        tie = sb("tie", [P, SEQ])
        k.dma("w", lambda e, i: e.dma_start(tie[:, :], tables["tie"].partition_broadcast(P)))
        norm_tiles(env, y)
        pick = sb("pick", [P, NTOK])
        G = sb("G", [P, ES * BATCH])
        G3 = G[:, :].rearrange("p (x b) -> p x b", b=BATCH)
        b32 = lambda t: t[:, :].rearrange("p (b t) -> p b t", t=SEQ)
        dd = lambda n, sh, c=2: [sb(n, sh) for _ in range(c)]
        mk = lambda c=2: [Buffer() for _ in range(c)]
        f_bank = mk(8)
        k.barrier()
        with ExitStack() as first:
            two = lambda n, c: [k.sb(first, n, [P, c]) for _ in range(2)]
            lgs, mxs, pks, pick_toks, yss = two("lg", R4), two("mx", 16), two("pk", R4), two("pick_tok", R4), two("ys", R4)
            f_lg, f_mx, f_pk, f_pt, f_ys = (mk() for _ in range(5))

            def picks(d):
                lg, mx, pk, pick_tok, ys = lgs[d], mxs[d], pks[d], pick_toks[d], yss[d]
                at = lambda i: 2 * i + d
                mm = k.pe(lambda e, i: e.matmul(bank[0][:, :], Wc[:, :], env.yT[:, bass.ts(at(i), R4)], start=True, stop=True), f_bank[0].free)
                a = k.dve(lambda e, i: e.tensor_scalar(lg[:, :], bank[0][:, :], bc[:, 0:1], None, ALU.add), mm, f_lg[d].free)
                f_bank[0].read_by(a)
                yc = k.pool(lambda e, i: e.tensor_copy(ys[:, :], y[:, bass.ts(at(i), R4)]), f_ys[d].free, alone=True)
                a = k.dve(lambda e, i: e.tensor_tensor(b32(lg), b32(lg), tie[:, :].unsqueeze(1).to_broadcast([P, 16, SEQ]), ALU.add), a)
                a = k.dve(lambda e, i: e.tensor_reduce(mx[:, :], b32(lg), AX.X, ALU.max), a, f_mx[d].free)
                a = k.dve(lambda e, i: e.tensor_tensor(b32(pk), b32(lg), mx[:, :].unsqueeze(2).to_broadcast([P, 16, SEQ]), ALU.is_equal), a, f_pk[d].free)
                f_lg[d].read_by(a)
                f_mx[d].read_by(a)
                yield
                pc = k.pool(lambda e, i: e.tensor_copy(pick[:, bass.ts(at(i), R4)], pk[:, :]), a, alone=True)
                for s in range(4):
                    t = k.pe(lambda e, i, s=s: e.transpose(bank[1][:, s * P:(s + 1) * P], pk[:, s * P:(s + 1) * P], env.ident[:, :]),
                             a, f_bank[1].free)
                f_pk[d].read_by(t, pc)
                c = k.act(lambda e, i: e.copy(pick_tok[:, :], bank[1][:, :]), t, f_pt[d].free)
                f_bank[1].read_by(c)
                yield
                for s in range(4):
                    for b in range(BPT):
                        lo = b * SEQ
                        mm = k.pe(lambda e, i, s=s, b=b, lo=lo: e.matmul(
                            bank[2 + b][:, s * P:(s + 1) * P], ys[lo:lo + SEQ, s * P:(s + 1) * P], pick_tok[lo:lo + SEQ, s * P:(s + 1) * P],
                            start=True, stop=True), c, yc, f_bank[2 + b].free)
                f_pt[d].read_by(mm)
                f_ys[d].read_by(mm)
                for b in range(BPT):
                    eng = (k.dve, k.act)[b % 2]
                    for s in range(4):
                        op = eng(lambda e, i, b=b, s=s: (e.copy if b % 2 else e.tensor_copy)(
                            G3[:, :, bass.ds(16 * at(i) + 4 * s + b, 1)].rearrange("p x a -> p (x a)"), bank[2 + b][:, s * P:(s + 1) * P]), mm)
                    f_bank[2 + b].read_by(op)

            k.loop(NT // 8)
            staggered([picks(d) for d in range(2)])
            k.barrier()
        N = 8
        with ExitStack() as second:
            per = lambda n, c: [k.sb(second, n, [P, c]) for _ in range(N)]
            W1, W2, W2T, Gs, inner = per("W1", P), per("W2", P), per("W2T", P), per("Gs", 256), per("inner", 256)
            for t in inner:
                k.pool(lambda e, i, t=t: e.memset(t[:, :], 0.0))
            f_W1, f_W2, f_W2T, f_Gs, f_in = (mk(N) for _ in range(5))
            f_bank = mk(8)

            def expert(d):
                z, at = d % 2, lambda i: N * i + d
                xp = lambda i: bass.ds(at(i), 1)
                k.dma(f"kv{d}", lambda e, i: e.dma_start(
                    W1[d][:, :].rearrange("p (s f) -> p s f", s=SETS), w["W1"][xp(i)].rearrange("a s d f -> d (a s) f")), f_W1[d].free)
                l2 = k.dma(f"kv{d}", lambda e, i: e.dma_start(
                    W2[d][:, :].rearrange("p (s f) -> p s f", s=SETS), w["W2"][xp(i)].rearrange("a s d f -> d (a s) f")), f_W2[d].free)
                gc = k.pool(lambda e, i: e.tensor_copy(Gs[d][:, :], G[:, bass.ts(at(i), 256)]), f_Gs[d].free, alone=True)
                yield
                yield
                t = k.pe(lambda e, i: e.transpose(bank[z][:, 0:P], W2[d][:, :], env.ident[:, :]), l2, f_bank[z].free)
                f_W2[d].read_by(t)
                for s in range(SETS):
                    mm = k.pe(lambda e, i, s=s: e.matmul(
                        bank[2 + z][32 * s:32 * s + 32, 0:BATCH], W1[d][:, s * F:(s + 1) * F], Gs[d][:, s * BATCH:(s + 1) * BATCH],
                        start=True, stop=True, tile_position=(0, 32 * s)), gc, l2, f_bank[2 + z].free)
                f_W1[d].read_by(mm)
                f_Gs[d].read_by(mm)
                yield
                wc = k.dve(lambda e, i: e.tensor_copy(W2T[d][:, :], bank[z][:, 0:P]), t, f_W2T[d].free)
                f_bank[z].read_by(wc)
                for s in range(SETS):
                    ra = k.act(lambda e, i, s=s: e.activation(
                        inner[d][32 * s:32 * s + 32, s * BATCH:(s + 1) * BATCH], bank[2 + z][32 * s:32 * s + 32, 0:BATCH], ACT.Relu,
                        bias=b1[32 * s:32 * s + 32, bass.ds(at(i), 1)]), mm, f_in[d].free)
                f_bank[2 + z].read_by(ra)
                yield
                mm = k.pe(lambda e, i: e.matmul(bank[4 + z][:, 0:256], W2T[d][:, :], inner[d][:, :], start=True, stop=True),
                          ra, wc, f_bank[4 + z].free)
                f_W2T[d].read_by(mm)
                f_in[d].read_by(mm)
                yield
                f_bank[4 + z].read_by(k.dve(lambda e, i: e.tensor_copy(G[:, bass.ts(at(i), 256)], bank[4 + z][:, 0:256]), mm, gc))

            k.barrier()
            k.loop(E // N)
            staggered([expert(d) for d in range(N)])
            k.barrier()
        N, R = 8, 4
        Rb, rb, pt = dd("Rb", [P, 512], R), dd("rb", [P, 512], R), dd("pt", [P, P], R)
        f_Rb, f_rb, f_pt = (mk(R) for _ in range(3))
        f_bank = mk(8)

        def results(d):
            r, z, at = d % R, d % 2, lambda i: N * i + d
            cps = [k.pool(lambda e, i: e.tensor_copy(pt[r][:, :], pick[:, bass.ts(at(i), P)]), f_pt[r].free, alone=True)]
            for b in range(BPT):
                if b == 0:
                    cps.append(k.pool(lambda e, i: e.tensor_copy(
                        Rb[r][:, 0:P], G3[:, :, bass.ds(4 * at(i), 1)].rearrange("p x a -> p (x a)")), f_Rb[r].free, alone=True))
                elif b == 1:
                    cps.append(k.dve(lambda e, i: e.tensor_copy(
                        Rb[r][:, P:2 * P], G3[:, :, bass.ds(4 * at(i) + 1, 1)].rearrange("p x a -> p (x a)")), f_Rb[r].free))
                else:
                    cps.append(k.act(lambda e, i, b=b: e.copy(
                        Rb[r][:, b * P:(b + 1) * P], G3[:, :, bass.ds(4 * at(i) + b, 1)].rearrange("p x a -> p (x a)")), f_Rb[r].free))
            yield
            for b in range(BPT):
                t = k.pe(lambda e, i, b=b: e.transpose(bank[z][:, b * P:(b + 1) * P], Rb[r][:, b * P:(b + 1) * P], env.ident[:, :]),
                         cps, f_bank[z].free)
            f_Rb[r].read_by(t)
            yield
            a = k.dve(lambda e, i: e.tensor_tensor(
                rb[r][:, :].rearrange("p (b d) -> p b d", b=4), bank[z][:, :].rearrange("p (b d) -> p b d", b=4),
                b2[:, :].unsqueeze(1).to_broadcast([P, 4, P]), ALU.add), t, f_rb[r].free)
            f_bank[z].read_by(a)
            yield
            for b in range(BPT):
                mm = k.pe(lambda e, i, b=b: e.matmul(
                    bank[2 + z][b * SEQ:(b + 1) * SEQ, 0:P], pt[r][:, b * SEQ:(b + 1) * SEQ], rb[r][:, b * P:(b + 1) * P],
                    start=True, stop=True, tile_position=(0, b * SEQ)), a, f_bank[2 + z].free)
            f_rb[r].read_by(mm)
            f_pt[r].read_by(mm)
            yield
            f_bank[2 + z].read_by(k.dve(lambda e, i: e.tensor_tensor(
                env.X[:, bass.ts(at(i), P)], env.X[:, bass.ts(at(i), P)], bank[2 + z][:, 0:P], ALU.add), mm))

        k.loop(NT // N)
        staggered([results(d) for d in range(N)])
        k.barrier()


def tie_table():
    return {"tie": np.linspace(0.0, 1e-6, SEQ, dtype=np.float32)}


def l3_ffn(env, w, out):
    k, nc, bank = env.k, env.k.nc, env.bank
    E, F = 8, 256
    HID = E * P
    ex_dram = nc.dram_tensor("x_scratch", (NTOK, P), F32, kind="Internal").ap()
    pos = lambda c: (c % 4) * 2 + c // 4
    k.barrier()
    k.straight()
    a = k.dma("turn", lambda e, i: e.dma_start(ex_dram.rearrange("(t p) d -> p t d", p=P),
                                               env.X[:, :].rearrange("p (t d) -> p t d", d=P)))
    by_time = lambda dram: [dram.rearrange("(b j t) d -> t b j d", b=BATCH, t=2)[t] for t in range(2)]
    tiles = lambda t: env.X[t * BATCH:(t + 1) * BATCH, :].rearrange("b (j d) -> b j d", d=P)
    for t in range(2):
        k.dma("turn", lambda e, i, t=t: e.dma_start(tiles(t), by_time(ex_dram)[t]), a)
    k.barrier()
    norm_tiles(env)
    with ExitStack() as outer:
        slots = SEQ + 1
        s_num, s_expr, s_state = (k.sb(outer, n, [P, slots * 4]) for n in ("s_num", "s_expr", "s_state"))
        gram = k.sb(outer, "gram", [P, slots * 4 * E])
        same = k.sb(outer, "same_token", [P, P])
        same_expert = k.sb(outer, "same_expert", [P, E])
        a = k.pool(lambda e, i: e.memset(same[:, :], 1.0))
        s3 = same[:, :].rearrange("p (b e) -> p b e", e=E)
        a = k.pool(lambda e, i: e.affine_select(out=s3, in_=s3, compare_op=ALU.is_ge, fill=0.0, base=0,
                                                pattern=[[-E, 16], [0, E]], channel_multiplier=1), a)
        a = k.pool(lambda e, i: e.affine_select(out=s3, in_=s3, compare_op=ALU.is_ge, fill=0.0, base=E - 1,
                                                pattern=[[E, 16], [0, E]], channel_multiplier=-1), a)
        k.dve(lambda e, i: e.tensor_reduce(same_expert[:, :], env.ident[:, :].rearrange("p (b e) -> p e b", e=E), AX.X, ALU.add))
        with ExitStack() as st:
            sb = lambda name, shape, dt=F32: k.sb(st, name, shape, dt)
            WhhT = sb("WhhT", [P, E * 3 * HID])
            W3 = WhhT[:, :].rearrange("p (c g) -> p c g", c=E)
            WihT = sb("WihT", [P, 3 * HID])
            ctxT = sb("ctxT", [P, HID])
            ctx_b = sb("ctx_b", [P, E])
            RAW = 4
            raw = [sb("raw", [P, HID]) for _ in range(RAW)]
            rawi = [sb("rawi", [P, P]) for _ in range(RAW)]
            k.straight()
            k.dma("w", lambda e, i: e.dma_start(ctx_b[:, :], w["ctx_b"].rearrange("(c p) -> p c", p=P)))
            f_raw, f_rawi = ([Buffer() for _ in range(RAW)] for _ in range(2))
            f_bank = [Buffer() for _ in range(8)]
            k.loop(3 * E // RAW)
            for d in range(RAW):
                q = lambda i, d=d: RAW * i + d
                l = k.dma(f"kv{d}", lambda e, i, d=d, q=q: e.dma_start(raw[d][:, :], w["gru_w_hh"][bass.ts(q(i), P), :]), f_raw[d].free)
                l = k.dma(f"kv{d}", lambda e, i, d=d, q=q: e.dma_start(rawi[d][:, :], w["gru_w_ih"][bass.ts(q(i), P), :]), f_rawi[d].free)
                for half in range(2):
                    b = 2 * (d % 2) + half
                    for r in range(4):
                        t = k.pe(lambda e, i, d=d, b=b, r=r, half=half: e.transpose(
                            bank[b][:, r * P:(r + 1) * P], raw[d][:, (4 * half + r) * P:(4 * half + r + 1) * P], env.ident[:, :]),
                            l, f_bank[b].free)
                    eng, op = ((k.dve, "dve"), (k.act, "act"))[half]
                    c = eng(lambda e, i, b=b, half=half, q=q, op=op: (e.tensor_copy if op == "dve" else e.copy)(
                        W3[:, 4 * half:4 * half + 4, bass.ts(q(i), P)], bank[b][:, :].rearrange("p (c g) -> p c g", c=4)), t)
                    f_bank[b].read_by(c)
                f_raw[d].read_by(t)
                t = k.pe(lambda e, i, d=d: e.transpose(bank[4 + d % 2][:, 0:P], rawi[d][:, :], env.ident[:, :]), f_bank[4 + d % 2].free)
                f_rawi[d].read_by(t)
                f_bank[4 + d % 2].read_by(k.dve(lambda e, i, d=d, q=q: e.tensor_copy(WihT[:, bass.ts(q(i), P)], bank[4 + d % 2][:, 0:P]), t))
            k.barrier()
            HALF = HID // 2
            k.straight()
            l = k.dma("w0", lambda e, i: e.dma_start(raw[0][:, :].rearrange("p (c h) -> p c h", c=E),
                                                    w["ctx_w"].rearrange("(c p) h -> p c h", p=P)))
            hb = sb("hb", [P, HALF])
            hT = sb("hT", [P, HID * BATCH // P])
            b0 = sb("b0", [P, HALF])
            for hf in range(2):
                lb = k.dma("w1", lambda e, i, hf=hf: e.dma_start(
                    b0[hf * BATCH:(hf + 1) * BATCH, :], w["ctx_b"][hf * HALF:(hf + 1) * HALF].partition_broadcast(BATCH)))
            done = transpose_blocks(env, raw[0], ctxT, E, l)
            mean = sb("mean", [P, BATCH])
            m = k.dve(lambda e, i: e.tensor_reduce(mean[:, :], env.yT[:, :].rearrange("p (t b) -> p b t", b=BATCH), AX.X, ALU.add))
            m = k.dve(lambda e, i: e.tensor_scalar(mean[:, :], mean[:, :], 1.0 / SEQ, None, ALU.mult), m)
            for hf in range(2):
                mm = k.pe(lambda e, i, hf=hf: e.matmul(bank[5][hf * BATCH:(hf + 1) * BATCH, :], mean[:, :], ctxT[:, hf * HALF:(hf + 1) * HALF],
                                                       start=True, stop=True, tile_position=(0, hf * BATCH)), m, done)
            k.dve(lambda e, i: e.tensor_tensor(hb[:, :], bank[5][:, :], b0[:, :], ALU.add), mm, lb)
            r_, z_, n_, d_, t_ = (sb(nm, [P, HALF]) for nm in ("r", "z", "n", "d", "t"))
            xt = sb("xt", [P, BATCH])
            R, HN, XN, ZA, ZB, TA, TB, GR = range(8)
            f = {nm: Buffer() for nm in ("r", "z", "n", "d", "t", "xt", "xp", "hT", "rb", "dv", "pr", "sq")}
            made = [Buffer(), Buffer()]
            f_bank = [Buffer() for _ in range(8)]
            Q = HALF // 2
            exprT = sb("exprT", [P, HID])
            xp = sb("xp", [P, BATCH])
            rb, dv, pr, sq = (sb(nm, [P, HALF]) for nm in ("rb", "dv", "pr", "sq"))
            l = k.dma("w2", lambda e, i: e.dma_start(raw[1][:, :].rearrange("p (c h) -> p c h", c=E),
                                                    w["expr_w"].rearrange("(c p) h -> p c h", p=P)))
            transpose_blocks(env, raw[1], exprT, E, l)
            k.dve(lambda e, i: e.memset(xt[:, :], 0.0))
            four = lambda t: t[:, :].rearrange("p (c d) -> p c d", c=4)

            def routing_work(made, EX, GR, turned, f_bank, tt):
                done = []
                pc = k.pool(lambda e, i: e.tensor_copy(rb[:, :].rearrange("p (b q) -> p q b", q=E),
                                                       hT[:, :].rearrange("p (q b) -> p q b", q=E)), turned, f["rb"].free, alone=True)
                for hf in range(2):
                    mx = k.pe(lambda e, i, hf=hf: e.matmul(bank[EX][hf * BATCH:(hf + 1) * BATCH, :], xp[:, :], exprT[:, hf * HALF:(hf + 1) * HALF],
                                                           start=True, stop=True, tile_position=(0, hf * BATCH)), xo, turned)
                f["xp"].read_by(mx)
                for g in range(4):
                    mg = k.pe(lambda e, i, g=g: e.matmul(bank[GR][:, g * P:(g + 1) * P], rb[:, g * P:(g + 1) * P], rb[:, g * P:(g + 1) * P],
                                                         start=True, stop=True), pc, f_bank[GR].free)
                f["rb"].read_by(mg)
                a = k.dve(lambda e, i: e.tensor_tensor(pr[:, :], hb[:, :], bank[EX][:, :], ALU.mult), mx, f["pr"].free, [b.free for b in made])
                done.append(a)
                b = k.act(lambda e, i: e.activation(sq[:, :], bank[EX][:, :], ACT.Square), a, f["sq"].free)
                f_bank[EX].read_by(b)
                f["pr"].read_by(k.dve(lambda e, i: e.tensor_reduce(s_num[:, bass.ts(i, 4)], four(pr), AX.X, ALU.add), a))
                b = k.dve(lambda e, i: e.tensor_reduce(s_expr[:, bass.ts(i, 4)], four(sq), AX.X, ALU.add), b)
                b = k.act(lambda e, i: e.activation(sq[:, :], hb[:, :], ACT.Square), b)
                done.append(b)
                f["sq"].read_by(k.dve(lambda e, i: e.tensor_reduce(s_state[:, bass.ts(i, 4)], four(sq), AX.X, ALU.add), b))
                a = k.dve(lambda e, i: e.tensor_tensor(four(dv), four(bank[GR]), same[:, :].unsqueeze(1).to_broadcast([P, 4, P]), ALU.mult),
                          mg, f["dv"].free)
                f_bank[GR].read_by(a)
                f["dv"].read_by(k.dve(lambda e, i: e.tensor_reduce(
                    gram[:, bass.ts(i, 4 * E)].rearrange("p (g f) -> p g f", g=4),
                    dv[:, :].rearrange("p (g b f) -> p g f b", g=4, f=E), AX.X, ALU.add), a))
                return done

            k.barrier()
            k.loop(SEQ)
            xo = k.pool(lambda e, i: e.tensor_copy(xp[:, :], xt[:, :]), f["xt"].free, f["xp"].free, alone=True)
            xc = k.pool(lambda e, i: e.tensor_copy(xt[:, :], env.yT[:, bass.ts(i, BATCH)]), f["xt"].free, xo, alone=True)

            def product(b, gate, kc, cols, start, stop, *waits):
                for hf in range(2):
                    lhs = xt[:, :] if kc is None else hT[:, pos(kc) * BATCH:(pos(kc) + 1) * BATCH]
                    g = gate * HID + hf * HALF
                    rhs = (WihT[:, g + cols.start:g + cols.stop] if kc is None else W3[:, kc, g + cols.start:g + cols.stop])
                    mm = k.pe(lambda e, i, hf=hf, lhs=lhs, rhs=rhs, n=cols.stop - cols.start: e.matmul(
                        bank[b][hf * BATCH:(hf + 1) * BATCH, 0:n], lhs, rhs, start=start, stop=stop, tile_position=(0, hf * BATCH)),
                        *waits)
                return mm

            every, cA, cB = slice(0, HALF), slice(0, Q), slice(Q, HALF)
            xm = product(XN, 2, None, every, True, True, xc, f_bank[XN].free)
            product(R, 0, None, every, True, False, f_bank[R].free)
            product(ZA, 1, None, cA, True, False, f_bank[ZA].free)
            xl = product(ZB, 1, None, cB, True, False, f_bank[ZB].free)
            f["xt"].read_by(xl)
            turned = []
            for half, (b, order) in enumerate(((TA, (0, 4, 1, 5)), (TB, (2, 6, 3, 7)))):
                for c in range(2):
                    tt = k.pe(lambda e, i, b=b, c=c, half=half: e.transpose(
                        bank[b][:, c * P:(c + 1) * P], hb[:, half * Q + c * P:half * Q + (c + 1) * P], env.ident[:, :]),
                        made[half].free, f_bank[b].free)
                ev = k.act(lambda e, i, b=b, half=half: e.copy(hT[:, half * Q:(half + 1) * Q], bank[b][:, 0:Q]), tt,
                           f["hT"].free)
                f_bank[b].read_by(ev)
                turned.append(ev)
                for kc in order:
                    rm = product(R, 0, kc, every, False, kc == 7, ev)
            hb_read = routing_work(made, TA, GR, turned, f_bank, tt)
            for kc in range(E):
                hm = product(HN, 2, kc, every, kc == 0, kc == 7, f_bank[HN].free)
            for kc in range(E):
                zA = product(ZA, 1, kc, cA, False, kc == 7)
            for kc in range(E):
                zB = product(ZB, 1, kc, cB, False, kc == 7)
            f["hT"].read_by(zB)
            a = k.act(lambda e, i: e.activation(r_[:, :], bank[R][:, :], ACT.Tanh, scale=0.5), rm, f["r"].free)
            f_bank[R].read_by(a)
            a = k.dve(lambda e, i: e.scalar_tensor_tensor(t_[:, :], r_[:, :], 1.0, bank[HN][:, :], ALU.add, ALU.mult), a, hm, f["t"].free)
            f_bank[HN].read_by(a)
            f["r"].read_by(a)
            a = k.dve(lambda e, i: e.scalar_tensor_tensor(t_[:, :], t_[:, :], 0.5, bank[XN][:, :], ALU.mult, ALU.add), a, xm)
            f_bank[XN].read_by(a)
            nn = k.act(lambda e, i: e.activation(n_[:, :], t_[:, :], ACT.Tanh), a, f["n"].free)
            f["t"].read_by(nn)
            dd = k.dve(lambda e, i: e.tensor_tensor(d_[:, :], hb[:, :], n_[:, :], ALU.subtract), nn, f["d"].free,
                       [b.free for b in made])
            for half, (b, zm, s) in enumerate(((ZA, zA, cA), (ZB, zB, cB))):
                a = k.act(lambda e, i, s=s, b=b: e.activation(z_[:, s], bank[b][:, 0:Q], ACT.Tanh, scale=0.5), zm, f["z"].free)
                f_bank[b].read_by(a)
                a = k.dve(lambda e, i, s=s: e.scalar_tensor_tensor(d_[:, s], z_[:, s], 1.0, d_[:, s], ALU.add, ALU.mult), a, dd)
                a = k.dve(lambda e, i, s=s: e.scalar_tensor_tensor(hb[:, s], d_[:, s], 0.5, n_[:, s], ALU.mult, ALU.add), a, tt, hb_read)
                made[half].read_by(a)
            for nm in ("z", "n", "d"):
                f[nm].read_by(a)
            k.barrier()
            k.loop(1)
            k.seg.first = SEQ
            for c in range(4):
                tt = k.pe(lambda e, i, c=c: e.transpose(bank[TB][:, c * P:(c + 1) * P], hb[:, c * P:(c + 1) * P], env.ident[:, :]))
            ev = k.act(lambda e, i: e.copy(hT[:, :], bank[TB][:, :]), tt)
            xo = k.pool(lambda e, i: e.tensor_copy(xp[:, :], xt[:, :]))
            f = {nm: Buffer() for nm in f}
            routing_work([Buffer(), Buffer()], TA, GR, [ev], [Buffer() for _ in range(8)], tt)
            k.barrier()
        with ExitStack() as st:
            sb = lambda name, shape, dt=F32: k.sb(st, name, shape, dt)
            k.straight()
            NE = NT * E
            NG = SEQ * 4
            nm = {n: sb(n, [P, NE]) for n in ("num", "den", "tmp", "cos", "key", "pick", "one", "order", "expr2", "state2")}
            sm = {n: sb(n, [P, NT]) for n in ("top", "first", "second")}
            pen = {n: sb(n, [P, NG]) for n in ("inv", "dev2", "pb")}
            gw = {n: sb(n, [P, NG * E]) for n in ("own", "norm")}
            one = sb("pen1", [P, 1])
            A = {n: t[:, :] for n, t in {**nm, **sm, **pen, **gw, "pen1": one}.items()}
            G = gram[:, 4 * E:].rearrange("p (m f) -> p m f", f=E)
            gx = lambda n: A[n].rearrange("p (m f) -> p m f", f=E)
            expert = same_expert[:, :].unsqueeze(1).to_broadcast([P, NG, E])
            by_row = lambda n: A[n].unsqueeze(2).to_broadcast([P, NG, E])
            te = lambda n: A[n].rearrange("p (t e) -> p t e", e=E)
            col = lambda n: A[n].unsqueeze(2).to_broadcast([P, NT, E])
            last = []

            def step(eng, fn):
                last[:] = [eng(fn, last)]

            TS = lambda o, a, s1, s2, p1, p2=None: step(k.dve, lambda e, i: (
                e.tensor_scalar(A[o], A[a], s1, s2, p1, p2) if p2 is not None else e.tensor_scalar(A[o], A[a], s1, s2, p1)))
            TT = lambda o, a, b, p: step(k.dve, lambda e, i: e.tensor_tensor(A[o], A[a], A[b], p))
            TC = lambda o, a, c, p: step(k.dve, lambda e, i: e.tensor_tensor(te(o), te(a), col(c), p))
            RD = lambda o, a, p: step(k.dve, lambda e, i: e.tensor_reduce(A[o], te(a), AX.X, p))
            RC = lambda o: step(k.dve, lambda e, i: e.reciprocal(A[o], A[o]))
            AC = lambda o, a, fn, scale=1.0: step(k.act, lambda e, i: e.activation(A[o], A[a], fn, scale=scale))
            step(k.dve, lambda e, i: e.tensor_tensor(gx("own"), G, expert, ALU.mult))
            step(k.dve, lambda e, i: e.tensor_reduce(A["inv"], gx("own"), AX.X, ALU.add))
            AC("inv", "inv", ACT.Sqrt)
            TS("inv", "inv", 1e-12, None, ALU.max)
            RC("inv")
            step(k.dve, lambda e, i: e.tensor_tensor(gx("own"), by_row("inv"), expert, ALU.mult))
            step(k.dve, lambda e, i: e.tensor_tensor(gx("norm"), G, by_row("inv"), ALU.mult))
            for n in range(2):
                s = slice(n * 512, (n + 1) * 512)
                step(k.pe, lambda e, i, s=s, n=n: e.matmul(bank[n][:, :], same[:, :], A["own"][:, s], start=True, stop=True))
                step(k.dve, lambda e, i, s=s, n=n: e.tensor_tensor(A["norm"][:, s], A["norm"][:, s], bank[n][:, :], ALU.mult))
            step(k.dve, lambda e, i: e.tensor_tensor(gx("norm"), gx("norm"), expert, ALU.subtract))
            AC("norm", "norm", ACT.Square)
            step(k.dve, lambda e, i: e.tensor_reduce(A["dev2"], gx("norm"), AX.X, ALU.add))
            AC("inv", "dev2", ACT.Sqrt)
            TS("inv", "inv", 1e-12, None, ALU.max)
            RC("inv")
            TT("pb", "inv", "inv", ALU.mult)
            TT("pb", "pb", "dev2", ALU.mult)
            step(k.dve, lambda e, i: e.tensor_reduce(A["pen1"], A["pb"], AX.X, ALU.add))
            step(k.pe, lambda e, i: e.matmul(bank[0][:, 0:1], env.ones[:, :], one[:, :], start=True, stop=True))
            step(k.dve, lambda e, i: e.tensor_scalar(one[:, :], bank[0][:, 0:1], 1.0 / NTOK, 1.0, ALU.mult, ALU.add))
            for name, src in (("num", s_num), ("expr2", s_expr), ("state2", s_state)):
                for t in range(2):
                    for hf in range(2):
                        step(k.dve, lambda e, i, name=name, src=src, t=t, hf=hf: e.tensor_copy(
                            te(name)[t * BATCH:(t + 1) * BATCH, :, hf * 4:hf * 4 + 4],
                            src[hf * BATCH:(hf + 1) * BATCH, 4:].rearrange("p (j t c) -> p t j c", t=2, c=4)[:, t]))
            AC("one", "state2", ACT.Sqrt)
            TS("one", "one", 1e-12, None, ALU.max)
            RC("one")
            TT("num", "num", "one", ALU.mult)
            TT("state2", "state2", "one", ALU.mult)
            TT("state2", "state2", "one", ALU.mult)
            for src, dst in (("expr2", "den"), ("state2", "tmp")):
                AC(dst, src, ACT.Sqrt)
                TS(dst, dst, 1e-8, None, ALU.max)
            TT("den", "den", "tmp", ALU.mult)
            RC("den")
            TT("cos", "num", "den", ALU.mult)
            TS("cos", "cos", -1.0, 1.0, ALU.mult, ALU.add)
            step(k.dve, lambda e, i: e.tensor_scalar(A["cos"], A["cos"], one[:, 0:1], None, ALU.mult))
            for n in range(E):
                step(k.dve, lambda e, i, n=n: e.memset(te("order")[:, :, n], float(E - n)))
            for n, name in enumerate(("first", "second")):
                RD(name, "cos", ALU.max)
                TC("key", "cos", name, ALU.is_equal)
                TT("key", "key", "order", ALU.mult)
                RD("top", "key", ALU.max)
                TC("key" if n else "pick", "key", "top", ALU.is_equal)
                if n == 0:
                    TS("tmp", "pick", -3.0e38, None, ALU.mult)
                    TT("cos", "cos", "tmp", ALU.add)
            TT("second", "second", "first", ALU.subtract)
            AC("second", "second", ACT.Exp)
            TC("key", "key", "second", ALU.mult)
            TT("pick", "pick", "key", ALU.add)
            TS("second", "second", 1.0, None, ALU.add)
            RC("second")
            TC("pick", "pick", "second", ALU.mult)
            share = nm["pick"]
            NX = E + 1
            up, gate_, down = (sb(n, [P, NX * F]) for n in ("upT", "gateT", "downT"))
            rawg, rawu, rawd = (sb(n, [P, NX * F]) for n in ("rawg", "rawu", "rawd"))
            for t, a, b in ((rawg, "gate_w", "shared_gate_w"), (rawu, "up_w", "shared_up_w")):
                v = t[:, :].rearrange("p (c h) -> p c h", h=P)
                k.dma("w", lambda e, i, v=v, a=a: e.dma_start(v[:, 0:2 * E], w[a].rearrange("x (c p) h -> p (x c) h", p=P)))
                k.dma("w", lambda e, i, v=v, b=b: e.dma_start(v[:, 2 * E:2 * NX], w[b].rearrange("(c p) h -> p c h", p=P)))
            k.dma("w", lambda e, i: e.dma_start(rawd[:, 0:E * F].rearrange("p (x f) -> p x f", f=F), w["down_w"].rearrange("x p f -> p x f")))
            l = k.dma("w", lambda e, i: e.dma_start(rawd[:, E * F:NX * F], w["shared_down_w"]))
            for src, dst in ((rawg, gate_), (rawu, up), (rawd, down)):
                transpose_blocks(env, src, dst, 2 * NX, [l, last])
            hs = [[sb("h", [P, R4]) for _ in range(2)] for _ in range(2)]
            wt = sb("wt", [P, 4 * E])
            f_h, f_bank, f_wt = [Buffer(), Buffer()], [Buffer() for _ in range(8)], Buffer()
            k.barrier()
            k.loop(NT // 4)
            wc = k.dve(lambda e, i: e.tensor_copy(wt[:, :], share[:, bass.ts(i, 4 * E)]), f_wt.free)
            ad = None
            for x in range(NX):
                z = x % 2
                ms = []
                for c in range(2):
                    o = (2 * x + c) * P
                    g = k.pe(lambda e, i, c=c, o=o: e.matmul(bank[c][:, :], gate_[:, o:o + P], env.yT[:, bass.ts(i, R4)],
                                                             start=True, stop=True), f_bank[c].free)
                    u = k.pe(lambda e, i, c=c, o=o: e.matmul(bank[2 + c][:, :], up[:, o:o + P], env.yT[:, bass.ts(i, R4)],
                                                             start=True, stop=True), f_bank[2 + c].free)
                    a = k.act(lambda e, i, c=c, z=z: e.activation(hs[z][c][:, :], bank[c][:, :], ACT.Silu), g, f_h[z].free)
                    f_bank[c].read_by(a)
                    m = k.dve(lambda e, i, c=c, z=z: e.tensor_tensor(hs[z][c][:, :], hs[z][c][:, :], bank[2 + c][:, :], ALU.mult), a, u)
                    f_bank[2 + c].read_by(m)
                    ms.append(m)
                for s in range(4):
                    for c in range(2):
                        o = (2 * x + c) * P
                        mm = k.pe(lambda e, i, c=c, o=o, z=z, s=s: e.matmul(
                            bank[4 + z][:, s * P:(s + 1) * P], hs[z][c][:, s * P:(s + 1) * P], down[:, o:o + P],
                            start=c == 0, stop=c == 1), ms, f_bank[4 + z].free)
                f_h[z].read_by(mm)
                if x < E:
                    prior = ad
                    for s in range(4):
                        ad = k.dve(lambda e, i, x=x, z=z, s=s: e.scalar_tensor_tensor(
                            env.X[:, bass.ts(4 * i + s, P)], bank[4 + z][:, s * P:(s + 1) * P], wt[:, s * E + x:s * E + x + 1],
                            env.X[:, bass.ts(4 * i + s, P)], ALU.mult, ALU.add), mm, wc, prior)
                else:
                    f_wt.read_by(ad)
                    ad = k.dve(lambda e, i, z=z: e.tensor_tensor(env.X[:, bass.ts(i, R4)], env.X[:, bass.ts(i, R4)], bank[4 + z][:, :], ALU.add), mm, ad)
                f_bank[4 + z].read_by(ad)
            k.barrier()
            k.straight()
            for t in range(2):
                k.dma("out", lambda e, i, t=t: e.dma_start(by_time(out)[t], tiles(t)))




def perceiver(nc, a, out):
    with ExitStack() as ctx:
        ctx.enter_context(nc.allow_non_contiguous_dma(reason="bias columns and head-major weights are small"))
        k = Queues(nc, ctx)
        k.straight()
        env = Env(k, ctx)
        env.constants()
        load_x(env, a["x"].rearrange("b t d -> (b t) d"))
        k.barrier()

        def of(prefix):
            return {name[len(prefix) + 1:]: v for name, v in a.items() if name.startswith(prefix + "_")}

        kv = a["ctx_1024"]
        w = of("L0_xattn")
        softmax_cross_attention(env, kv, 64, w["W_Q"], w["W_K"], w["W_V"], w["W_out"], 64 ** -0.5,
                                w["b_Q"], w["b_K"], w["b_V"], w["b_out"], a["mask_BxSxS2_bk1"], True, -10000.0)
        l0_attention(env, of("L0_attn"))
        l0_ffn(env, of("L0_ffn"))
        w = of("L1_xattn")
        softmax_cross_attention(env, kv, 8, w["Wq"], w["Wk"], w["Wv"], w["Wo"], 8 ** -0.5,
                                w["bq"], w["bk"], w["bv"], w["bo"],
                                a["mask_Bx1xSxS2_bf1"].rearrange("b a q s -> (b a) q s"), False, -1.0e9)
        l1_attention(env, of("L1_attn"))
        l1_ffn(env, of("L1_ffn"))
        l2_cross_attention(env, of("L2_xattn"), kv)
        l2_attention(env, of("L2_attn"), a)
        l2_ffn(env, of("L2_ffn"), a)
        w = of("L3_xattn")
        softmax_cross_attention(env, kv, 8, w["Wq"], w["Wk"], w["Wv"], w["Wp"], 8 ** -0.5, bo=w["bp"], shared=True)
        l3_attention(env, of("L3_attn"))
        l3_ffn(env, of("L3_ffn"), out.rearrange("b t d -> (b t) d"))
        k.finish()


def kernel(**inputs):
    import concourse.bacc as bacc
    from concourse.bass_utils import run_bass_kernel_spmd

    nc = bacc.Bacc("TRN2", target_bir_lowering=False, num_devices=1)
    arrays, args = {}, {}
    for name, v in {**inputs, **l2_tables(), **tie_table()}.items():
        v = np.ascontiguousarray(v)
        if v.ndim == 0:
            v = v.reshape(1)
        arrays["in_" + name] = v
        args[name] = nc.dram_tensor("in_" + name, v.shape, mybir.dt.from_np(v.dtype), kind="ExternalInput").ap()
    out = nc.dram_tensor("out_0", (BATCH, SEQ, P), F32, kind="ExternalOutput").ap()
    perceiver(nc, args, out)
    r = run_bass_kernel_spmd(nc, [arrays], core_ids=[0])
    return r.results[0]["out_0"]
```
